# Optimizing a Trainium2 kernel written in Bass

```python
import numpy as np
import jax
import jax.numpy as jnp

def _softmax(x, axis=-1):
    return jax.nn.softmax(x, axis=axis)

def _gelu(x):
    return jax.nn.gelu(x, approximate=True)

def _silu(x):
    return jax.nn.silu(x)

def _sigmoid(x):
    return jax.nn.sigmoid(x)

def _layernorm(x, axis=-1, eps=1e-05):
    m = jnp.mean(x, axis=axis, keepdims=True)
    v = jnp.var(x, axis=axis, keepdims=True)
    return (x - m) / jnp.sqrt(v + eps)

def _scatter_add(tgt, idx, src, axis=0):
    return tgt.at[idx].add(src)

def _segment_sum(src, seg, n):
    return jax.ops.segment_sum(src, seg, n)
kernel_name = 'mk_decoder_postln_d4_seqx_r4_43de13'

def setup_inputs(seed: int=0):
    np.random.seed(seed)
    _w = jnp.asarray

    def _rec_inputs():
        import jax
        import jax.numpy as jnp
        _rk = jax.random.key(seed)
        x = 7.22e-05 + 1 * jax.random.normal(jax.random.fold_in(_rk, 1), (2, 1024, 256), jnp.float32)
        _lenS = 1024 - jax.random.randint(jax.random.fold_in(_rk, 7), (2,), 0, max(1, 1024 // 4) + 1, jnp.int32)
        _lenS2 = 154 - jax.random.randint(jax.random.fold_in(_rk, 8), (2,), 0, max(1, 154 // 4) + 1, jnp.int32)
        _ctx_1024P = jax.random.normal(jax.random.fold_in(_rk, 11), (2, 16, 256), jnp.float32)
        _ctx_1024c = jax.random.dirichlet(jax.random.fold_in(_rk, 511), 0.3 * jnp.ones((16,), jnp.float32), (2, 154))
        _ctx_1024t = jnp.einsum('bsk,bkd->bsd', _ctx_1024c, _ctx_1024P)
        _ctx_1024t = _ctx_1024t * jax.lax.rsqrt(jnp.mean(jnp.square(_ctx_1024t)) + 1e-12) * 0.953939
        ctx_1024 = 4.13588e-05 + 0.999923 * (_ctx_1024t + 0.3 * jax.random.normal(jax.random.fold_in(_rk, 611), (2, 154, 256), jnp.float32))
        _validS = jnp.arange(1024)[None, :] < _lenS[:, None]
        _validS2 = jnp.arange(154)[None, :] < _lenS2[:, None]
        _causal = jnp.tril(jnp.ones((1024, 1024), dtype=bool))
        mask_1xSxS2_ff0 = jnp.where(jnp.ones((1, 1024, 154), dtype=bool), 0.0, -1000000000.0).astype(jnp.float32)
        return (x, ctx_1024, mask_1xSxS2_ff0)
    x, ctx_1024, mask_1xSxS2_ff0 = _rec_inputs()

    def _L0_attn_setup():
        import jax, jax.numpy as jnp
        import numpy as np
        HID = 256
        NH = 4
        HD = HID // NH
        KS = 4
        C = 64
        EPS = 1e-05
        B = 4
        L = 1024

        def _causal_dwconv(x, w):
            xc = jnp.moveaxis(x, 1, 2)
            y = jax.lax.conv_general_dilated(xc, w, window_strides=(1,), padding=[(w.shape[-1] - 1, 0)], dimension_numbers=('NCH', 'OIH', 'NCH'), feature_group_count=w.shape[0])
            return jnp.moveaxis(jax.nn.silu(y), 1, 2)

        def _forward(x, Wq, Wk, Wv, Wb, conv_q, conv_k, conv_v, g, Wo):
            Bx, Lx, _ = x.shape
            N = Lx // C
            q = _causal_dwconv(x @ Wq, conv_q).reshape(Bx, Lx, NH, HD)
            k = _causal_dwconv(x @ Wk, conv_k).reshape(Bx, Lx, NH, HD)
            v = _causal_dwconv(x @ Wv, conv_v).reshape(Bx, Lx, NH, HD)
            q = q / jnp.linalg.norm(q, axis=-1, keepdims=True)
            k = k / jnp.linalg.norm(k, axis=-1, keepdims=True)
            beta = jax.nn.sigmoid(x @ Wb)
            Q = q.reshape(Bx, N, C, NH, HD)
            K = k.reshape(Bx, N, C, NH, HD)
            V = v.reshape(Bx, N, C, NH, HD)
            bta = beta.reshape(Bx, N, C, NH, 1)
            Kb = K * bta
            Vb = V * bta
            A = jnp.einsum('bnihd,bnjhd->bnij', Kb, K)
            T0 = jnp.eye(C, dtype=x.dtype) - jnp.tril(A, -1)
            col = jnp.arange(C)

            def body(i, T):
                row = jax.lax.dynamic_slice_in_dim(T, i, 1, axis=2)[:, :, 0]
                acc = jnp.einsum('bnj,bnjc->bnc', row, T)
                new_row = jnp.where(col < i, row + acc, row)
                return jax.lax.dynamic_update_slice_in_dim(T, new_row[:, :, None, :], i, axis=2)
            T = jax.lax.fori_loop(1, C, body, T0)
            W = jnp.einsum('bnij,bnjhd->bnihd', T, Kb)
            U = jnp.einsum('bnij,bnjhd->bnihd', T, Vb)

            def chunk_step(S, inp):
                q_i, k_i, w_i, u0 = inp
                Sd = jnp.diagonal(S, axis1=-2, axis2=-1)
                u_i = u0 - w_i * Sd[:, None]
                o_inter = q_i * Sd[:, None]
                A_i = jnp.tril(jnp.einsum('bchd,bchd->bc', q_i, k_i))
                o_intra = A_i[:, :, None, None] * u_i
                S = S + jnp.einsum('bchd,bche->bhde', k_i, u_i)
                return (S, o_inter + o_intra)
            xs = tuple((jnp.moveaxis(a, 1, 0) for a in (Q, K, W, U)))
            S0 = jnp.zeros((Bx, NH, HD, HD), x.dtype)
            S, O = jax.lax.scan(chunk_step, S0, xs)
            o = jnp.moveaxis(O, 0, 1).reshape(Bx, Lx, NH, HD)
            o = o * jax.lax.rsqrt(jnp.mean(o * o, axis=-1, keepdims=True) + EPS) * g
            out = o.reshape(Bx, Lx, NH * HD) @ Wo
            return (out, S)

        def _reference_tuple_inner(x, Wq, Wk, Wv, Wb, conv_q, conv_k, conv_v, g, Wo):
            return _forward(x, Wq, Wk, Wv, Wb, conv_q, conv_k, conv_v, g, Wo)
        key = jax.random.key(seed)
        ks = jax.random.split(key, 9)
        return {'x': jax.random.normal(ks[0], (B, L, HID), jnp.float32), 'Wq': jax.random.normal(ks[1], (HID, HID), jnp.float32) * 0.02, 'Wk': jax.random.normal(ks[2], (HID, HID), jnp.float32) * 0.02, 'Wv': jax.random.normal(ks[3], (HID, HID), jnp.float32) * 0.02, 'Wb': jax.random.normal(ks[4], (HID, NH), jnp.float32) * 0.02, 'conv_q': jax.random.normal(ks[5], (HID, 1, KS), jnp.float32) * 0.5, 'conv_k': jax.random.normal(ks[6], (HID, 1, KS), jnp.float32) * 0.5, 'conv_v': jax.random.normal(ks[7], (HID, 1, KS), jnp.float32) * 0.5, 'g': jnp.ones((HD,), jnp.float32), 'Wo': jax.random.normal(ks[8], (HID, HID), jnp.float32) * 0.02}
    _L0_attn_all = _L0_attn_setup()
    _L0_attn_in = {k: v for k, v in _L0_attn_all.items() if k in ('Wq', 'Wk', 'Wv', 'Wb', 'conv_q', 'conv_k', 'conv_v', 'g', 'Wo')}
    del _L0_attn_all

    def _L0_xattn_setup():
        import jax, jax.numpy as jnp
        import numpy as np
        EMB = 256
        NH = 16
        HD = EMB // NH
        key = jax.random.key(seed)
        ks = jax.random.split(key, 11)
        B, S = (4, 512)
        s_in = 1.0 / np.sqrt(EMB)
        return {'q': jax.random.normal(ks[0], (B, S, EMB), jnp.float32), 'k': jax.random.normal(ks[1], (B, S, EMB), jnp.float32), 'v': jax.random.normal(ks[2], (B, S, EMB), jnp.float32), 'Wq': jax.random.normal(ks[3], (EMB, NH * HD), jnp.float32) * s_in, 'bq': jnp.zeros((NH * HD,), jnp.float32), 'Wk': jax.random.normal(ks[4], (EMB, HD), jnp.float32) * s_in, 'bk': jnp.zeros((HD,), jnp.float32), 'Wv': jax.random.normal(ks[5], (EMB, HD), jnp.float32) * s_in, 'bv': jnp.zeros((HD,), jnp.float32), 'Wo': jax.random.normal(ks[6], (NH * HD, EMB), jnp.float32) * s_in, 'bo': jnp.zeros((EMB,), jnp.float32)}
    _L0_xattn_all = _L0_xattn_setup()
    _L0_xattn_in = {k: v for k, v in _L0_xattn_all.items() if k in ('Wq', 'bq', 'Wk', 'bk', 'Wv', 'bv', 'Wo', 'bo')}
    del _L0_xattn_all

    def _L0_ffn_setup():
        import jax, jax.numpy as jnp
        import numpy as np
        EPS = 1e-05

        def _ln(x, g, b):
            mu = jnp.mean(x, axis=-1, keepdims=True)
            var = jnp.mean(jnp.square(x - mu), axis=-1, keepdims=True)
            return (x - mu) * jax.lax.rsqrt(var + EPS) * g + b

        def _forward(x, index_b, index_t, sw1, sb1, sw2, sb2, sw3, sb3, s_ln_g, s_ln_b, sg_w, sg_b, eg_w, eg_b, exp_bias, ew1, eb1, ew2, eb2, ew3, eb3, sel_ln_g, sel_ln_b):
            x1 = jnp.einsum('btd,hd->bth', x, sw1) + sb1
            x2 = jnp.einsum('btd,hd->bth', x, sw2) + sb2
            sh = _ln(jax.nn.silu(x1) * x2, s_ln_g, s_ln_b)
            shared_out = jnp.einsum('bth,dh->btd', sh, sw3) + sb3
            x_moe = x[index_b, index_t]
            shared_scores = jax.nn.sigmoid(x_moe @ sg_w.T + sg_b)
            expert_scores = jax.nn.sigmoid(x_moe @ eg_w.T + eg_b)
            top1_idx = jnp.argmax(expert_scores + exp_bias, axis=-1)
            top1_score = jnp.take_along_axis(expert_scores, top1_idx[:, None], axis=-1)
            weights = jax.nn.softmax(jnp.concatenate([shared_scores, top1_score], axis=-1), axis=-1)
            shared_w, expert_w = (weights[:, 0], weights[:, 1])
            shared_moe_out = shared_out[index_b, index_t] * shared_w[:, None]
            h1 = jnp.einsum('md,ehd->meh', x_moe, ew1) + eb1
            h2 = jnp.einsum('md,ehd->meh', x_moe, ew2) + eb2
            z = _ln(jax.nn.silu(h1) * h2, sel_ln_g, sel_ln_b)
            out_all = jnp.einsum('meh,edh->med', z, ew3) + eb3
            expert_out = jnp.take_along_axis(out_all, top1_idx[:, None, None], axis=1)[:, 0]
            expert_moe_out = expert_out * expert_w[:, None]
            final_out = shared_out.at[index_b, index_t].set(shared_moe_out + expert_moe_out)
            return final_out
        B, T, D, E, H, M = (2, 512, 256, 8, 128, 512)
        key = jax.random.key(seed)
        ks = jax.random.split(key, 24)
        s = 0.02
        inp = {}
        inp['x'] = jax.random.normal(ks[0], (B, T, D), jnp.float32)
        flat = jnp.arange(M, dtype=jnp.int32) * 2
        inp['index_b'] = flat // T
        inp['index_t'] = flat % T
        inp['sw1'] = jax.random.normal(ks[1], (H, D), jnp.float32) * s
        inp['sb1'] = jnp.zeros((H,), jnp.float32)
        inp['sw2'] = jax.random.normal(ks[2], (H, D), jnp.float32) * s
        inp['sb2'] = jnp.zeros((H,), jnp.float32)
        inp['sw3'] = jax.random.normal(ks[3], (D, H), jnp.float32) * s
        inp['sb3'] = jnp.zeros((D,), jnp.float32)
        inp['s_ln_g'] = jnp.ones((H,), jnp.float32)
        inp['s_ln_b'] = jnp.zeros((H,), jnp.float32)
        inp['sg_w'] = jax.random.normal(ks[4], (1, D), jnp.float32) * s
        inp['sg_b'] = jnp.zeros((1,), jnp.float32)
        inp['eg_w'] = jax.random.normal(ks[5], (E, D), jnp.float32) * s
        inp['eg_b'] = jnp.zeros((E,), jnp.float32)
        inp['exp_bias'] = jnp.zeros((E,), jnp.float32)
        inp['ew1'] = jax.random.normal(ks[6], (E, H, D), jnp.float32) * s
        inp['eb1'] = jnp.zeros((E, H), jnp.float32)
        inp['ew2'] = jax.random.normal(ks[7], (E, H, D), jnp.float32) * s
        inp['eb2'] = jnp.zeros((E, H), jnp.float32)
        inp['ew3'] = jax.random.normal(ks[8], (E, D, H), jnp.float32) * s
        inp['eb3'] = jnp.zeros((E, D), jnp.float32)
        inp['sel_ln_g'] = jnp.ones((H,), jnp.float32)
        inp['sel_ln_b'] = jnp.zeros((H,), jnp.float32)
        return inp
    _L0_ffn_all = _L0_ffn_setup()
    _L0_ffn_in = {k: v for k, v in _L0_ffn_all.items() if k in ('index_b', 'index_t', 'sw1', 'sb1', 'sw2', 'sb2', 'sw3', 'sb3', 's_ln_g', 's_ln_b', 'sg_w', 'sg_b', 'eg_w', 'eg_b', 'exp_bias', 'ew1', 'eb1', 'ew2', 'eb2', 'ew3', 'eb3', 'sel_ln_g', 'sel_ln_b')}
    del _L0_ffn_all

    def _L1_attn_setup():
        import jax, jax.numpy as jnp
        import numpy as np
        import math
        D_MODEL = 256
        N_HEADS = 16
        Q_PROJ = D_MODEL // 4
        KV_PROJ = D_MODEL // 4
        DH = D_MODEL // N_HEADS
        LN_EPS = 1e-05

        def _layernorm(x, gamma, beta):
            mu = jnp.mean(x, axis=-1, keepdims=True)
            var = jnp.mean(jnp.square(x - mu), axis=-1, keepdims=True)
            return (x - mu) * jax.lax.rsqrt(var + LN_EPS) * gamma + beta
        key = jax.random.key(seed)
        ks = jax.random.split(key, 7)
        B, S = (2, 512)
        x = jax.random.normal(ks[0], (B, S, D_MODEL), dtype=jnp.float32)
        W_dq = 0.01 * jax.random.normal(ks[1], (D_MODEL, Q_PROJ), dtype=jnp.float32)
        W_uq = 0.01 * jax.random.normal(ks[2], (Q_PROJ, D_MODEL), dtype=jnp.float32)
        W_dkv = 0.01 * jax.random.normal(ks[3], (D_MODEL, KV_PROJ), dtype=jnp.float32)
        W_ukv = 0.01 * jax.random.normal(ks[4], (KV_PROJ, 2 * D_MODEL), dtype=jnp.float32)
        W_o = 0.01 * jax.random.normal(ks[5], (D_MODEL, D_MODEL), dtype=jnp.float32)
        return {'x': x, 'W_dq': W_dq, 'W_uq': W_uq, 'q_ln_g': jnp.ones((Q_PROJ,), jnp.float32), 'q_ln_b': jnp.zeros((Q_PROJ,), jnp.float32), 'W_dkv': W_dkv, 'W_ukv': W_ukv, 'kv_ln_g': jnp.ones((KV_PROJ,), jnp.float32), 'kv_ln_b': jnp.zeros((KV_PROJ,), jnp.float32), 'W_o': W_o}
    _L1_attn_all = _L1_attn_setup()
    _L1_attn_in = {k: v for k, v in _L1_attn_all.items() if k in ('W_dq', 'W_uq', 'q_ln_g', 'q_ln_b', 'W_dkv', 'W_ukv', 'kv_ln_g', 'kv_ln_b', 'W_o')}
    del _L1_attn_all

    def _L1_xattn_setup():
        import jax, jax.numpy as jnp
        import numpy as np
        B, S, D_IN, D_MODEL = (4, 512, 256, 256)
        key = jax.random.key(seed)
        ks = jax.random.split(key, 8)
        glorot = np.sqrt(6.0 / (D_IN + D_MODEL))
        inp = {'q': jax.random.normal(ks[0], (B, S, D_IN), dtype=jnp.float32), 'k': jax.random.normal(ks[1], (B, S, D_IN), dtype=jnp.float32), 'v': jax.random.normal(ks[2], (B, S, D_IN), dtype=jnp.float32), 'mask': jnp.zeros((1, S, S), dtype=jnp.float32), 'kernel_q': jax.random.uniform(ks[3], (1, 1, D_IN, D_MODEL), jnp.float32, -glorot, glorot), 'kernel_k': jax.random.uniform(ks[4], (1, 1, D_IN, D_MODEL), jnp.float32, -glorot, glorot), 'kernel_v': jax.random.uniform(ks[5], (1, 1, D_IN, D_MODEL), jnp.float32, -glorot, glorot), 'bias_q': 0.05 * jax.random.normal(ks[6], (D_MODEL,), dtype=jnp.float32), 'bias_k': 0.05 * jax.random.normal(ks[7], (D_MODEL,), dtype=jnp.float32), 'bias_v': 0.05 * jax.random.normal(jax.random.fold_in(key, 7), (D_MODEL,), dtype=jnp.float32)}
        return inp
    _L1_xattn_all = _L1_xattn_setup()
    _L1_xattn_in = {k: v for k, v in _L1_xattn_all.items() if k in ('kernel_q', 'kernel_k', 'kernel_v', 'bias_q', 'bias_k', 'bias_v')}
    del _L1_xattn_all

    def _L1_ffn_setup():
        import jax, jax.numpy as jnp
        import numpy as np
        HIDDEN = 256
        INNER = 1024

        def _weight_quant(w):
            scale = 1.0 / jnp.clip(jnp.mean(jnp.abs(w)), 1e-05)
            wq = jnp.clip(jnp.round(w * scale), -1.0, 1.0) / scale
            return w + jax.lax.stop_gradient(wq - w)

        def _act_quant(x):
            scale = 127.0 / jnp.clip(jnp.max(jnp.abs(x), axis=-1, keepdims=True), 1e-05)
            xq = jnp.clip(jnp.round(x * scale), -128.0, 127.0) / scale
            return x + jax.lax.stop_gradient(xq - x)

        def _bitlinear(x, w):
            return jnp.einsum('bsi,oi->bso', _act_quant(x), _weight_quant(w))
        key = jax.random.key(seed)
        k0, k1, k2, k3 = jax.random.split(key, 4)
        x = jax.random.normal(k0, (4, 512, HIDDEN), dtype=jnp.float32)
        w_gate = jax.random.normal(k1, (INNER, HIDDEN), dtype=jnp.float32) / np.sqrt(HIDDEN)
        w_up = jax.random.normal(k2, (INNER, HIDDEN), dtype=jnp.float32) / np.sqrt(HIDDEN)
        w_down = jax.random.normal(k3, (HIDDEN, INNER), dtype=jnp.float32) / np.sqrt(INNER)
        return {'x': x, 'w_gate': w_gate, 'w_up': w_up, 'w_down': w_down}
    _L1_ffn_all = _L1_ffn_setup()
    _L1_ffn_in = {k: v for k, v in _L1_ffn_all.items() if k in ('w_gate', 'w_up', 'w_down')}
    del _L1_ffn_all

    def _L2_attn_setup():
        import jax, jax.numpy as jnp
        import numpy as np
        B, L, E, H = (2, 1024, 256, 16)
        D = E // H
        CHUNK = 64

        def _linear_attention(x, W_qkv, W_out):
            Bz, Lz, Ez = x.shape
            scale = D ** (-0.5)
            qkv = x @ W_qkv.T
            qkv = qkv.reshape(Bz, Lz, 3, H, D).transpose(2, 0, 3, 1, 4)
            q, k, v = (qkv[0], qkv[1], qkv[2])
            q = (jax.nn.elu(q) + 1.0) * scale
            k = jax.nn.elu(k) + 1.0
            nc = Lz // CHUNK

            def to_chunks(t):
                return t.reshape(Bz, H, nc, CHUNK, D).transpose(2, 0, 1, 3, 4)
            qc, kc, vc = (to_chunks(q), to_chunks(k), to_chunks(v))
            causal = jnp.tril(jnp.ones((CHUNK, CHUNK), dtype=x.dtype))

            def step(carry, inp):
                S, Z = carry
                qi, ki, vi = inp
                attn = jnp.einsum('bhld,bhmd->bhlm', qi, ki) * causal
                num = jnp.einsum('bhlm,bhme->bhle', attn, vi) + jnp.einsum('bhld,bhde->bhle', qi, S)
                den = attn.sum(-1) + jnp.einsum('bhld,bhd->bhl', qi, Z)
                S = S + jnp.einsum('bhmd,bhme->bhde', ki, vi)
                Z = Z + ki.sum(axis=2)
                return ((S, Z), (num, den))
            S0 = jnp.zeros((Bz, H, D, D), dtype=x.dtype)
            Z0 = jnp.zeros((Bz, H, D), dtype=x.dtype)
            _, (num, den) = jax.lax.scan(step, (S0, Z0), (qc, kc, vc))
            num = num.transpose(1, 2, 0, 3, 4).reshape(Bz, H, Lz, D)
            den = den.transpose(1, 2, 0, 3).reshape(Bz, H, Lz)
            den = jnp.maximum(den, 1e-06)
            out = num / den[..., None]
            out = out.transpose(0, 2, 1, 3).reshape(Bz, Lz, Ez)
            return out @ W_out.T
        key = jax.random.key(seed)
        k1, k2, k3 = jax.random.split(key, 3)
        x = jax.random.normal(k1, (B, L, E), dtype=jnp.float32)
        W_qkv = jax.random.normal(k2, (3 * E, E), dtype=jnp.float32) * 0.02
        W_out = jax.random.normal(k3, (E, E), dtype=jnp.float32) * 0.02
        return {'x': x, 'W_qkv': W_qkv, 'W_out': W_out}
    _L2_attn_all = _L2_attn_setup()
    _L2_attn_in = {k: v for k, v in _L2_attn_all.items() if k in ('W_qkv', 'W_out')}
    del _L2_attn_all

    def _L2_xattn_setup():
        import jax, jax.numpy as jnp
        import numpy as np
        D = 256
        key = jax.random.key(seed)
        ks = jax.random.split(key, 11)
        B, Sq, Skv = (4, 512, 512)
        s = 0.02
        return {'query': jax.random.normal(ks[0], (B, Sq, D), jnp.float32), 'key': jax.random.normal(ks[1], (B, Skv, D), jnp.float32), 'value': jax.random.normal(ks[2], (B, Skv, D), jnp.float32), 'Wq': jax.random.normal(ks[3], (D, D), jnp.float32) * s, 'bq': jnp.zeros((D,), jnp.float32), 'Wk': jax.random.normal(ks[4], (D, D), jnp.float32) * s, 'bk': jnp.zeros((D,), jnp.float32), 'Wv': jax.random.normal(ks[5], (D, D), jnp.float32) * s, 'bv': jnp.zeros((D,), jnp.float32), 'Wo': jax.random.normal(ks[6], (D, D), jnp.float32) * s, 'bo': jnp.zeros((D,), jnp.float32)}
    _L2_xattn_all = _L2_xattn_setup()
    _L2_xattn_in = {k: v for k, v in _L2_xattn_all.items() if k in ('Wq', 'bq', 'Wk', 'bk', 'Wv', 'bv', 'Wo', 'bo')}
    del _L2_xattn_all

    def _L2_ffn_setup():
        import jax, jax.numpy as jnp
        import numpy as np
        DIM = 256
        DEPTH = 2
        HEADS = 8
        DIM_HEAD = 64
        WINDOW = 128
        INNER = HEADS * DIM_HEAD
        HID = int(DIM * 4 * 2 / 3)
        B, N = (2, 2048)
        QK_SCALE = 8.0

        def shift_token(t):
            t1, t2 = jnp.split(t, 2, axis=-1)
            t2 = jnp.pad(t2, ((0, 0), (1, 0), (0, 0)))[:, :-1]
            return jnp.concatenate([t1, t2], axis=-1)

        def l2norm(t):
            return t / jnp.clip(jnp.linalg.norm(t, axis=-1, keepdims=True), 1e-12)

        def rotate_half(x):
            x1, x2 = jnp.split(x, 2, axis=-1)
            return jnp.concatenate([-x2, x1], axis=-1)

        def rotary_xpos(q, k):
            n = q.shape[-2]
            half_idx = jnp.arange(0, DIM_HEAD, 2, dtype=jnp.float32)
            inv_freq = 1.0 / 10000.0 ** (half_idx / DIM_HEAD)
            t = jnp.arange(n, dtype=jnp.float32)
            freqs = t[:, None] * inv_freq[None, :]
            freqs = jnp.concatenate([freqs, freqs], axis=-1)
            base = (half_idx + 0.4 * DIM_HEAD) / (1.4 * DIM_HEAD)
            power = (t - n // 2) / float(WINDOW // 2)
            scale = base[None, :] ** power[:, None]
            scale = jnp.concatenate([scale, scale], axis=-1)
            cos, sin = (jnp.cos(freqs), jnp.sin(freqs))
            q = q * cos * scale + rotate_half(q) * sin * scale
            k = k * cos / scale + rotate_half(k) * sin / scale
            return (q, k)

        def local_attention(q, k, v):
            b, h, n, d = q.shape
            w = n // WINDOW
            bq = q.reshape(b, h, w, WINDOW, d) * QK_SCALE
            bk = k.reshape(b, h, w, WINDOW, d)
            bv = v.reshape(b, h, w, WINDOW, d)

            def look_around(t):
                p = jnp.pad(t, ((0, 0), (0, 0), (1, 0), (0, 0), (0, 0)))
                return jnp.concatenate([p[:, :, :w], p[:, :, 1:]], axis=3)
            bk, bv = (look_around(bk), look_around(bv))
            bt = jnp.arange(n).reshape(w, WINDOW)
            btp = jnp.pad(bt, ((1, 0), (0, 0)), constant_values=-1)
            btk = jnp.concatenate([btp[:w], btp[1:]], axis=1)
            sim = jnp.einsum('bhwid,bhwjd->bhwij', bq, bk)
            i = bt[:, :, None]
            j = btk[:, None, :]
            mask = (i < j) | (i > j + WINDOW) | (j == -1)
            sim = jnp.where(mask, -jnp.finfo(sim.dtype).max, sim)
            attn = jax.nn.softmax(sim, axis=-1)
            out = jnp.einsum('bhwij,bhwjd->bhwid', attn, bv)
            return out.reshape(b, h, n, d)

        def _layer(x, wqkv, qs, ksc, wo, lg, lb, w1, b1, w2, b2):
            b, n, _ = x.shape
            h = shift_token(x)
            qkv = h @ wqkv
            q, k, v = jnp.split(qkv, 3, axis=-1)
            to_heads = lambda t: t.reshape(b, n, HEADS, DIM_HEAD).transpose(0, 2, 1, 3)
            q, k, v = (to_heads(q), to_heads(k), to_heads(v))
            q = l2norm(q) * qs
            k = l2norm(k) * ksc
            q, k = rotary_xpos(q, k)
            o = local_attention(q, k, v)
            o = o.transpose(0, 2, 1, 3).reshape(b, n, INNER)
            x = x + o @ wo
            h = shift_token(x)
            mu = h.mean(-1, keepdims=True)
            var = h.var(-1, keepdims=True)
            h = (h - mu) / jnp.sqrt(var + 1e-05) * lg + lb
            h = h @ w1 + b1
            a, g = jnp.split(h, 2, axis=-1)
            h = a * jax.nn.gelu(g, approximate=False)
            x = x + h @ w2 + b2
            return x
        key = jax.random.key(seed)
        ks = jax.random.split(key, 6)
        return {'x': jax.random.normal(ks[0], (B, N, DIM), jnp.float32), 'wqkv': jax.random.normal(ks[1], (DEPTH, DIM, 3 * INNER), jnp.float32) * 0.02, 'q_scale': jnp.ones((DEPTH, DIM_HEAD), jnp.float32), 'k_scale': jnp.ones((DEPTH, DIM_HEAD), jnp.float32), 'wo': jax.random.normal(ks[2], (DEPTH, INNER, DIM), jnp.float32) * 0.02, 'ln_g': jnp.ones((DEPTH, DIM), jnp.float32), 'ln_b': jnp.zeros((DEPTH, DIM), jnp.float32), 'w1': jax.random.normal(ks[3], (DEPTH, DIM, 2 * HID), jnp.float32) * 0.02, 'b1': jnp.zeros((DEPTH, 2 * HID), jnp.float32), 'w2': jax.random.normal(ks[4], (DEPTH, HID, DIM), jnp.float32) * 0.02, 'b2': jnp.zeros((DEPTH, DIM), jnp.float32)}
    _L2_ffn_all = _L2_ffn_setup()
    _L2_ffn_in = {k: v for k, v in _L2_ffn_all.items() if k in ('wqkv', 'q_scale', 'k_scale', 'wo', 'ln_g', 'ln_b', 'w1', 'b1', 'w2', 'b2')}
    del _L2_ffn_all

    def _L3_attn_setup():
        import jax, jax.numpy as jnp
        import numpy as np
        from jax import lax
        B, L, D = (4, 1024, 256)
        EXPAND, K = (2, 4)
        INNER = D * EXPAND
        key = jax.random.key(seed)
        k0, k1, k2, k3, k4 = jax.random.split(key, 5)
        s = 0.02
        return {'x': jax.random.normal(k0, (B, L, D), jnp.float32), 'W_in': jax.random.normal(k1, (D, 2 * INNER), jnp.float32) * s, 'conv_w': jax.random.normal(k2, (INNER, 1, K), jnp.float32) * s, 'conv_b': jax.random.normal(k3, (INNER,), jnp.float32) * s, 'W_out': jax.random.normal(k4, (INNER, D), jnp.float32) * s}
    _L3_attn_all = _L3_attn_setup()
    _L3_attn_in = {k: v for k, v in _L3_attn_all.items() if k in ('W_in', 'conv_w', 'conv_b', 'W_out')}
    del _L3_attn_all

    def _L3_xattn_setup():
        import jax, jax.numpy as jnp
        import numpy as np
        import math
        EMBED = 256
        HEADS = 16
        HEAD_DIM = EMBED // HEADS

        def alibi_slopes(heads: int) -> jnp.ndarray:
            return jnp.asarray([2.0 ** (-8.0 * (h + 1) / heads) for h in range(heads)], dtype=jnp.float32)
        key = jax.random.key(seed)
        ks = jax.random.split(key, 8)
        B, Nq, Nk = (2, 512, 512)
        s = 0.02
        return {'query': jax.random.normal(ks[0], (B, Nq, EMBED), jnp.float32), 'kv': jax.random.normal(ks[1], (B, Nk, EMBED), jnp.float32), 'Wq': jax.random.normal(ks[2], (EMBED, EMBED), jnp.float32) * s, 'bq': jnp.zeros((EMBED,), jnp.float32), 'Wkv': jax.random.normal(ks[3], (EMBED, 2 * EMBED), jnp.float32) * s, 'bkv': jnp.zeros((2 * EMBED,), jnp.float32), 'Wo': jax.random.normal(ks[4], (EMBED, EMBED), jnp.float32) * s, 'bo': jnp.zeros((EMBED,), jnp.float32)}
    _L3_xattn_all = _L3_xattn_setup()
    _L3_xattn_in = {k: v for k, v in _L3_xattn_all.items() if k in ('Wq', 'bq', 'Wkv', 'bkv', 'Wo', 'bo')}
    del _L3_xattn_all

    def _L3_ffn_setup():
        import jax, jax.numpy as jnp
        import numpy as np
        HIDDEN = 256
        INTER = 1024
        N_EXPERTS = 8
        TOP_K = 2
        INIT_STD = 0.02
        key = jax.random.key(seed)
        ks = jax.random.split(key, 6)
        x = jax.random.normal(ks[0], (2, 256, HIDDEN), dtype=jnp.float32)
        Wg = jax.random.normal(ks[1], (N_EXPERTS, HIDDEN), dtype=jnp.float32) * INIT_STD
        W1 = jax.random.normal(ks[2], (N_EXPERTS, HIDDEN, INTER), dtype=jnp.float32) * INIT_STD
        b1 = jnp.zeros((N_EXPERTS, INTER), dtype=jnp.float32)
        W2 = jax.random.normal(ks[3], (N_EXPERTS, INTER, HIDDEN), dtype=jnp.float32) * INIT_STD
        b2 = jnp.zeros((N_EXPERTS, HIDDEN), dtype=jnp.float32)
        return {'x': x, 'Wg': Wg, 'W1': W1, 'b1': b1, 'W2': W2, 'b2': b2}
    _L3_ffn_all = _L3_ffn_setup()
    _L3_ffn_in = {k: v for k, v in _L3_ffn_all.items() if k in ('Wg', 'W1', 'b1', 'W2', 'b2')}
    del _L3_ffn_all
    return {'x': x, 'ctx_1024': ctx_1024, 'mask_1xSxS2_ff0': mask_1xSxS2_ff0, 'L0_attn_Wq': _L0_attn_in['Wq'], 'L0_attn_Wk': _L0_attn_in['Wk'], 'L0_attn_Wv': _L0_attn_in['Wv'], 'L0_attn_Wb': _L0_attn_in['Wb'], 'L0_attn_conv_q': _L0_attn_in['conv_q'], 'L0_attn_conv_k': _L0_attn_in['conv_k'], 'L0_attn_conv_v': _L0_attn_in['conv_v'], 'L0_attn_g': _L0_attn_in['g'], 'L0_attn_Wo': _L0_attn_in['Wo'], 'L0_xattn_Wq': _L0_xattn_in['Wq'], 'L0_xattn_bq': _L0_xattn_in['bq'], 'L0_xattn_Wk': _L0_xattn_in['Wk'], 'L0_xattn_bk': _L0_xattn_in['bk'], 'L0_xattn_Wv': _L0_xattn_in['Wv'], 'L0_xattn_bv': _L0_xattn_in['bv'], 'L0_xattn_Wo': _L0_xattn_in['Wo'], 'L0_xattn_bo': _L0_xattn_in['bo'], 'L0_ffn_index_b': _L0_ffn_in['index_b'], 'L0_ffn_index_t': _L0_ffn_in['index_t'], 'L0_ffn_sw1': _L0_ffn_in['sw1'], 'L0_ffn_sb1': _L0_ffn_in['sb1'], 'L0_ffn_sw2': _L0_ffn_in['sw2'], 'L0_ffn_sb2': _L0_ffn_in['sb2'], 'L0_ffn_sw3': _L0_ffn_in['sw3'], 'L0_ffn_sb3': _L0_ffn_in['sb3'], 'L0_ffn_s_ln_g': _L0_ffn_in['s_ln_g'], 'L0_ffn_s_ln_b': _L0_ffn_in['s_ln_b'], 'L0_ffn_sg_w': _L0_ffn_in['sg_w'], 'L0_ffn_sg_b': _L0_ffn_in['sg_b'], 'L0_ffn_eg_w': _L0_ffn_in['eg_w'], 'L0_ffn_eg_b': _L0_ffn_in['eg_b'], 'L0_ffn_exp_bias': _L0_ffn_in['exp_bias'], 'L0_ffn_ew1': _L0_ffn_in['ew1'], 'L0_ffn_eb1': _L0_ffn_in['eb1'], 'L0_ffn_ew2': _L0_ffn_in['ew2'], 'L0_ffn_eb2': _L0_ffn_in['eb2'], 'L0_ffn_ew3': _L0_ffn_in['ew3'], 'L0_ffn_eb3': _L0_ffn_in['eb3'], 'L0_ffn_sel_ln_g': _L0_ffn_in['sel_ln_g'], 'L0_ffn_sel_ln_b': _L0_ffn_in['sel_ln_b'], 'L1_attn_W_dq': _L1_attn_in['W_dq'], 'L1_attn_W_uq': _L1_attn_in['W_uq'], 'L1_attn_q_ln_g': _L1_attn_in['q_ln_g'], 'L1_attn_q_ln_b': _L1_attn_in['q_ln_b'], 'L1_attn_W_dkv': _L1_attn_in['W_dkv'], 'L1_attn_W_ukv': _L1_attn_in['W_ukv'], 'L1_attn_kv_ln_g': _L1_attn_in['kv_ln_g'], 'L1_attn_kv_ln_b': _L1_attn_in['kv_ln_b'], 'L1_attn_W_o': _L1_attn_in['W_o'], 'L1_xattn_kernel_q': _L1_xattn_in['kernel_q'], 'L1_xattn_kernel_k': _L1_xattn_in['kernel_k'], 'L1_xattn_kernel_v': _L1_xattn_in['kernel_v'], 'L1_xattn_bias_q': _L1_xattn_in['bias_q'], 'L1_xattn_bias_k': _L1_xattn_in['bias_k'], 'L1_xattn_bias_v': _L1_xattn_in['bias_v'], 'L1_ffn_w_gate': _L1_ffn_in['w_gate'], 'L1_ffn_w_up': _L1_ffn_in['w_up'], 'L1_ffn_w_down': _L1_ffn_in['w_down'], 'L2_attn_W_qkv': _L2_attn_in['W_qkv'], 'L2_attn_W_out': _L2_attn_in['W_out'], 'L2_xattn_Wq': _L2_xattn_in['Wq'], 'L2_xattn_bq': _L2_xattn_in['bq'], 'L2_xattn_Wk': _L2_xattn_in['Wk'], 'L2_xattn_bk': _L2_xattn_in['bk'], 'L2_xattn_Wv': _L2_xattn_in['Wv'], 'L2_xattn_bv': _L2_xattn_in['bv'], 'L2_xattn_Wo': _L2_xattn_in['Wo'], 'L2_xattn_bo': _L2_xattn_in['bo'], 'L2_ffn_wqkv': _L2_ffn_in['wqkv'], 'L2_ffn_q_scale': _L2_ffn_in['q_scale'], 'L2_ffn_k_scale': _L2_ffn_in['k_scale'], 'L2_ffn_wo': _L2_ffn_in['wo'], 'L2_ffn_ln_g': _L2_ffn_in['ln_g'], 'L2_ffn_ln_b': _L2_ffn_in['ln_b'], 'L2_ffn_w1': _L2_ffn_in['w1'], 'L2_ffn_b1': _L2_ffn_in['b1'], 'L2_ffn_w2': _L2_ffn_in['w2'], 'L2_ffn_b2': _L2_ffn_in['b2'], 'L3_attn_W_in': _L3_attn_in['W_in'], 'L3_attn_conv_w': _L3_attn_in['conv_w'], 'L3_attn_conv_b': _L3_attn_in['conv_b'], 'L3_attn_W_out': _L3_attn_in['W_out'], 'L3_xattn_Wq': _L3_xattn_in['Wq'], 'L3_xattn_bq': _L3_xattn_in['bq'], 'L3_xattn_Wkv': _L3_xattn_in['Wkv'], 'L3_xattn_bkv': _L3_xattn_in['bkv'], 'L3_xattn_Wo': _L3_xattn_in['Wo'], 'L3_xattn_bo': _L3_xattn_in['bo'], 'L3_ffn_Wg': _L3_ffn_in['Wg'], 'L3_ffn_W1': _L3_ffn_in['W1'], 'L3_ffn_b1': _L3_ffn_in['b1'], 'L3_ffn_W2': _L3_ffn_in['W2'], 'L3_ffn_b2': _L3_ffn_in['b2']}

def reference(x, ctx_1024, mask_1xSxS2_ff0, L0_attn_Wq, L0_attn_Wk, L0_attn_Wv, L0_attn_Wb, L0_attn_conv_q, L0_attn_conv_k, L0_attn_conv_v, L0_attn_g, L0_attn_Wo, L0_xattn_Wq, L0_xattn_bq, L0_xattn_Wk, L0_xattn_bk, L0_xattn_Wv, L0_xattn_bv, L0_xattn_Wo, L0_xattn_bo, L0_ffn_index_b, L0_ffn_index_t, L0_ffn_sw1, L0_ffn_sb1, L0_ffn_sw2, L0_ffn_sb2, L0_ffn_sw3, L0_ffn_sb3, L0_ffn_s_ln_g, L0_ffn_s_ln_b, L0_ffn_sg_w, L0_ffn_sg_b, L0_ffn_eg_w, L0_ffn_eg_b, L0_ffn_exp_bias, L0_ffn_ew1, L0_ffn_eb1, L0_ffn_ew2, L0_ffn_eb2, L0_ffn_ew3, L0_ffn_eb3, L0_ffn_sel_ln_g, L0_ffn_sel_ln_b, L1_attn_W_dq, L1_attn_W_uq, L1_attn_q_ln_g, L1_attn_q_ln_b, L1_attn_W_dkv, L1_attn_W_ukv, L1_attn_kv_ln_g, L1_attn_kv_ln_b, L1_attn_W_o, L1_xattn_kernel_q, L1_xattn_kernel_k, L1_xattn_kernel_v, L1_xattn_bias_q, L1_xattn_bias_k, L1_xattn_bias_v, L1_ffn_w_gate, L1_ffn_w_up, L1_ffn_w_down, L2_attn_W_qkv, L2_attn_W_out, L2_xattn_Wq, L2_xattn_bq, L2_xattn_Wk, L2_xattn_bk, L2_xattn_Wv, L2_xattn_bv, L2_xattn_Wo, L2_xattn_bo, L2_ffn_wqkv, L2_ffn_q_scale, L2_ffn_k_scale, L2_ffn_wo, L2_ffn_ln_g, L2_ffn_ln_b, L2_ffn_w1, L2_ffn_b1, L2_ffn_w2, L2_ffn_b2, L3_attn_W_in, L3_attn_conv_w, L3_attn_conv_b, L3_attn_W_out, L3_xattn_Wq, L3_xattn_bq, L3_xattn_Wkv, L3_xattn_bkv, L3_xattn_Wo, L3_xattn_bo, L3_ffn_Wg, L3_ffn_W1, L3_ffn_b1, L3_ffn_W2, L3_ffn_b2):
    import jax
    import jax.numpy as jnp

    def _L0_attn_ref(x, Wq, Wk, Wv, Wb, conv_q, conv_k, conv_v, g, Wo):
        import jax, jax.numpy as jnp
        import numpy as np
        HID = 256
        NH = 4
        HD = HID // NH
        KS = 4
        C = 64
        EPS = 1e-05
        B = 4
        L = 1024

        def _causal_dwconv(x, w):
            xc = jnp.moveaxis(x, 1, 2)
            y = jax.lax.conv_general_dilated(xc, w, window_strides=(1,), padding=[(w.shape[-1] - 1, 0)], dimension_numbers=('NCH', 'OIH', 'NCH'), feature_group_count=w.shape[0])
            return jnp.moveaxis(jax.nn.silu(y), 1, 2)

        def _forward(x, Wq, Wk, Wv, Wb, conv_q, conv_k, conv_v, g, Wo):
            Bx, Lx, _ = x.shape
            N = Lx // C
            q = _causal_dwconv(x @ Wq, conv_q).reshape(Bx, Lx, NH, HD)
            k = _causal_dwconv(x @ Wk, conv_k).reshape(Bx, Lx, NH, HD)
            v = _causal_dwconv(x @ Wv, conv_v).reshape(Bx, Lx, NH, HD)
            q = q / jnp.linalg.norm(q, axis=-1, keepdims=True)
            k = k / jnp.linalg.norm(k, axis=-1, keepdims=True)
            beta = jax.nn.sigmoid(x @ Wb)
            Q = q.reshape(Bx, N, C, NH, HD)
            K = k.reshape(Bx, N, C, NH, HD)
            V = v.reshape(Bx, N, C, NH, HD)
            bta = beta.reshape(Bx, N, C, NH, 1)
            Kb = K * bta
            Vb = V * bta
            A = jnp.einsum('bnihd,bnjhd->bnij', Kb, K)
            T0 = jnp.eye(C, dtype=x.dtype) - jnp.tril(A, -1)
            col = jnp.arange(C)

            def body(i, T):
                row = jax.lax.dynamic_slice_in_dim(T, i, 1, axis=2)[:, :, 0]
                acc = jnp.einsum('bnj,bnjc->bnc', row, T)
                new_row = jnp.where(col < i, row + acc, row)
                return jax.lax.dynamic_update_slice_in_dim(T, new_row[:, :, None, :], i, axis=2)
            T = jax.lax.fori_loop(1, C, body, T0)
            W = jnp.einsum('bnij,bnjhd->bnihd', T, Kb)
            U = jnp.einsum('bnij,bnjhd->bnihd', T, Vb)

            def chunk_step(S, inp):
                q_i, k_i, w_i, u0 = inp
                Sd = jnp.diagonal(S, axis1=-2, axis2=-1)
                u_i = u0 - w_i * Sd[:, None]
                o_inter = q_i * Sd[:, None]
                A_i = jnp.tril(jnp.einsum('bchd,bchd->bc', q_i, k_i))
                o_intra = A_i[:, :, None, None] * u_i
                S = S + jnp.einsum('bchd,bche->bhde', k_i, u_i)
                return (S, o_inter + o_intra)
            xs = tuple((jnp.moveaxis(a, 1, 0) for a in (Q, K, W, U)))
            S0 = jnp.zeros((Bx, NH, HD, HD), x.dtype)
            S, O = jax.lax.scan(chunk_step, S0, xs)
            o = jnp.moveaxis(O, 0, 1).reshape(Bx, Lx, NH, HD)
            o = o * jax.lax.rsqrt(jnp.mean(o * o, axis=-1, keepdims=True) + EPS) * g
            out = o.reshape(Bx, Lx, NH * HD) @ Wo
            return (out, S)

        def _reference_tuple_inner(x, Wq, Wk, Wv, Wb, conv_q, conv_k, conv_v, g, Wo):
            return _forward(x, Wq, Wk, Wv, Wb, conv_q, conv_k, conv_v, g, Wo)
        return _reference_tuple_inner(x, Wq, Wk, Wv, Wb, conv_q, conv_k, conv_v, g, Wo)[0]

    def _L0_xattn_ref(q, k, v, Wq, bq, Wk, bk, Wv, bv, Wo, bo):
        import jax, jax.numpy as jnp
        import numpy as np
        EMB = 256
        NH = 16
        HD = EMB // NH
        B, S, _ = q.shape
        scale = HD ** (-0.5)
        Q = (q @ Wq + bq).reshape(B, S, NH, HD).transpose(0, 2, 1, 3)
        K = k @ Wk + bk
        V = v @ Wv + bv
        scores = jnp.einsum('bhqd,bkd->bhqk', Q, K) * scale
        attn = jax.nn.softmax(scores, axis=-1)
        out = jnp.einsum('bhqk,bkd->bhqd', attn, V)
        out = out.transpose(0, 2, 1, 3).reshape(B, S, NH * HD)
        return out @ Wo + bo

    def _L0_ffn_ref(x, index_b, index_t, sw1, sb1, sw2, sb2, sw3, sb3, s_ln_g, s_ln_b, sg_w, sg_b, eg_w, eg_b, exp_bias, ew1, eb1, ew2, eb2, ew3, eb3, sel_ln_g, sel_ln_b):
        import jax, jax.numpy as jnp
        import numpy as np
        EPS = 1e-05

        def _ln(x, g, b):
            mu = jnp.mean(x, axis=-1, keepdims=True)
            var = jnp.mean(jnp.square(x - mu), axis=-1, keepdims=True)
            return (x - mu) * jax.lax.rsqrt(var + EPS) * g + b

        def _forward(x, index_b, index_t, sw1, sb1, sw2, sb2, sw3, sb3, s_ln_g, s_ln_b, sg_w, sg_b, eg_w, eg_b, exp_bias, ew1, eb1, ew2, eb2, ew3, eb3, sel_ln_g, sel_ln_b):
            x1 = jnp.einsum('btd,hd->bth', x, sw1) + sb1
            x2 = jnp.einsum('btd,hd->bth', x, sw2) + sb2
            sh = _ln(jax.nn.silu(x1) * x2, s_ln_g, s_ln_b)
            shared_out = jnp.einsum('bth,dh->btd', sh, sw3) + sb3
            x_moe = x[index_b, index_t]
            shared_scores = jax.nn.sigmoid(x_moe @ sg_w.T + sg_b)
            expert_scores = jax.nn.sigmoid(x_moe @ eg_w.T + eg_b)
            top1_idx = jnp.argmax(expert_scores + exp_bias, axis=-1)
            top1_score = jnp.take_along_axis(expert_scores, top1_idx[:, None], axis=-1)
            weights = jax.nn.softmax(jnp.concatenate([shared_scores, top1_score], axis=-1), axis=-1)
            shared_w, expert_w = (weights[:, 0], weights[:, 1])
            shared_moe_out = shared_out[index_b, index_t] * shared_w[:, None]
            h1 = jnp.einsum('md,ehd->meh', x_moe, ew1) + eb1
            h2 = jnp.einsum('md,ehd->meh', x_moe, ew2) + eb2
            z = _ln(jax.nn.silu(h1) * h2, sel_ln_g, sel_ln_b)
            out_all = jnp.einsum('meh,edh->med', z, ew3) + eb3
            expert_out = jnp.take_along_axis(out_all, top1_idx[:, None, None], axis=1)[:, 0]
            expert_moe_out = expert_out * expert_w[:, None]
            final_out = shared_out.at[index_b, index_t].set(shared_moe_out + expert_moe_out)
            return final_out
        return _forward(x, index_b, index_t, sw1, sb1, sw2, sb2, sw3, sb3, s_ln_g, s_ln_b, sg_w, sg_b, eg_w, eg_b, exp_bias, ew1, eb1, ew2, eb2, ew3, eb3, sel_ln_g, sel_ln_b)

    def _L1_attn_ref(x, W_dq, W_uq, q_ln_g, q_ln_b, W_dkv, W_ukv, kv_ln_g, kv_ln_b, W_o):
        import jax, jax.numpy as jnp
        import numpy as np
        import math
        D_MODEL = 256
        N_HEADS = 16
        Q_PROJ = D_MODEL // 4
        KV_PROJ = D_MODEL // 4
        DH = D_MODEL // N_HEADS
        LN_EPS = 1e-05

        def _layernorm(x, gamma, beta):
            mu = jnp.mean(x, axis=-1, keepdims=True)
            var = jnp.mean(jnp.square(x - mu), axis=-1, keepdims=True)
            return (x - mu) * jax.lax.rsqrt(var + LN_EPS) * gamma + beta
        B, S, D = x.shape
        cq = _layernorm(x @ W_dq, q_ln_g, q_ln_b)
        Q = cq @ W_uq
        ckv = _layernorm(x @ W_dkv, kv_ln_g, kv_ln_b)
        KV = ckv @ W_ukv
        K, V = (KV[..., :D], KV[..., D:])
        q = Q.reshape(B, S, N_HEADS, DH)
        k = K.reshape(B, S, N_HEADS, DH)
        v = V.reshape(B, S, N_HEADS, DH)
        scores = jnp.einsum('bqhd,bkhd->bhqk', q, k) / math.sqrt(float(DH))
        mask = jnp.tril(jnp.ones((S, S), dtype=scores.dtype))
        scores = scores * mask
        scores = jnp.where(scores == 0, -jnp.inf, scores)
        attn = jax.nn.softmax(scores, axis=-1)
        out = jnp.einsum('bhqk,bkhd->bqhd', attn, v).reshape(B, S, D)
        return out @ W_o.T

    def _L1_xattn_ref(q, k, v, mask, kernel_q, kernel_k, kernel_v, bias_q, bias_k, bias_v):
        import jax, jax.numpy as jnp
        import numpy as np
        B, S, D_IN, D_MODEL = (4, 512, 256, 256)
        Wq, Wk, Wv = (kernel_q[0, 0], kernel_k[0, 0], kernel_v[0, 0])
        qp = jax.nn.relu(jnp.einsum('bsd,de->bse', q, Wq) + bias_q)
        kp = jax.nn.relu(jnp.einsum('bsd,de->bse', k, Wk) + bias_k)
        vp = jax.nn.relu(jnp.einsum('bsd,de->bse', v, Wv) + bias_v)
        scores = jax.nn.relu(jnp.einsum('bqe,bke->bqk', qp, kp))
        dk = jnp.asarray(kp.shape[-1], dtype=scores.dtype)
        logits = scores / jnp.sqrt(dk) + mask
        out = jax.nn.relu(jnp.einsum('bqk,bke->bqe', logits, vp))
        return out

    def _L1_ffn_ref(x, w_gate, w_up, w_down):
        import jax, jax.numpy as jnp
        import numpy as np
        HIDDEN = 256
        INNER = 1024

        def _weight_quant(w):
            scale = 1.0 / jnp.clip(jnp.mean(jnp.abs(w)), 1e-05)
            wq = jnp.clip(jnp.round(w * scale), -1.0, 1.0) / scale
            return w + jax.lax.stop_gradient(wq - w)

        def _act_quant(x):
            scale = 127.0 / jnp.clip(jnp.max(jnp.abs(x), axis=-1, keepdims=True), 1e-05)
            xq = jnp.clip(jnp.round(x * scale), -128.0, 127.0) / scale
            return x + jax.lax.stop_gradient(xq - x)

        def _bitlinear(x, w):
            return jnp.einsum('bsi,oi->bso', _act_quant(x), _weight_quant(w))
        gate = jax.nn.silu(_bitlinear(x, w_gate))
        up = _bitlinear(x, w_up)
        return _bitlinear(gate * up, w_down)

    def _L2_attn_ref(x, W_qkv, W_out):
        import jax, jax.numpy as jnp
        import numpy as np
        B, L, E, H = (2, 1024, 256, 16)
        D = E // H
        CHUNK = 64

        def _linear_attention(x, W_qkv, W_out):
            Bz, Lz, Ez = x.shape
            scale = D ** (-0.5)
            qkv = x @ W_qkv.T
            qkv = qkv.reshape(Bz, Lz, 3, H, D).transpose(2, 0, 3, 1, 4)
            q, k, v = (qkv[0], qkv[1], qkv[2])
            q = (jax.nn.elu(q) + 1.0) * scale
            k = jax.nn.elu(k) + 1.0
            nc = Lz // CHUNK

            def to_chunks(t):
                return t.reshape(Bz, H, nc, CHUNK, D).transpose(2, 0, 1, 3, 4)
            qc, kc, vc = (to_chunks(q), to_chunks(k), to_chunks(v))
            causal = jnp.tril(jnp.ones((CHUNK, CHUNK), dtype=x.dtype))

            def step(carry, inp):
                S, Z = carry
                qi, ki, vi = inp
                attn = jnp.einsum('bhld,bhmd->bhlm', qi, ki) * causal
                num = jnp.einsum('bhlm,bhme->bhle', attn, vi) + jnp.einsum('bhld,bhde->bhle', qi, S)
                den = attn.sum(-1) + jnp.einsum('bhld,bhd->bhl', qi, Z)
                S = S + jnp.einsum('bhmd,bhme->bhde', ki, vi)
                Z = Z + ki.sum(axis=2)
                return ((S, Z), (num, den))
            S0 = jnp.zeros((Bz, H, D, D), dtype=x.dtype)
            Z0 = jnp.zeros((Bz, H, D), dtype=x.dtype)
            _, (num, den) = jax.lax.scan(step, (S0, Z0), (qc, kc, vc))
            num = num.transpose(1, 2, 0, 3, 4).reshape(Bz, H, Lz, D)
            den = den.transpose(1, 2, 0, 3).reshape(Bz, H, Lz)
            den = jnp.maximum(den, 1e-06)
            out = num / den[..., None]
            out = out.transpose(0, 2, 1, 3).reshape(Bz, Lz, Ez)
            return out @ W_out.T
        return _linear_attention(x, W_qkv, W_out)

    def _L2_xattn_ref(query, key, value, Wq, bq, Wk, bk, Wv, bv, Wo, bo):
        import jax, jax.numpy as jnp
        import numpy as np
        D = 256
        Q = jnp.einsum('bsd,de->bse', query, Wq) + bq
        K = jnp.einsum('bsd,de->bse', key, Wk) + bk
        V = jnp.einsum('bsd,de->bse', value, Wv) + bv
        scale = 1.0 / jnp.sqrt(jnp.asarray(D, Q.dtype))
        scores = jnp.einsum('bqd,bkd->bqk', Q, K) * scale
        attn = jax.nn.softmax(scores, axis=-1)
        out = jnp.einsum('bqk,bkd->bqd', attn, V)
        return jnp.einsum('bsd,de->bse', out, Wo) + bo

    def _L2_ffn_ref(x, wqkv, q_scale, k_scale, wo, ln_g, ln_b, w1, b1, w2, b2):
        import jax, jax.numpy as jnp
        import numpy as np
        DIM = 256
        DEPTH = 2
        HEADS = 8
        DIM_HEAD = 64
        WINDOW = 128
        INNER = HEADS * DIM_HEAD
        HID = int(DIM * 4 * 2 / 3)
        B, N = (2, 2048)
        QK_SCALE = 8.0

        def shift_token(t):
            t1, t2 = jnp.split(t, 2, axis=-1)
            t2 = jnp.pad(t2, ((0, 0), (1, 0), (0, 0)))[:, :-1]
            return jnp.concatenate([t1, t2], axis=-1)

        def l2norm(t):
            return t / jnp.clip(jnp.linalg.norm(t, axis=-1, keepdims=True), 1e-12)

        def rotate_half(x):
            x1, x2 = jnp.split(x, 2, axis=-1)
            return jnp.concatenate([-x2, x1], axis=-1)

        def rotary_xpos(q, k):
            n = q.shape[-2]
            half_idx = jnp.arange(0, DIM_HEAD, 2, dtype=jnp.float32)
            inv_freq = 1.0 / 10000.0 ** (half_idx / DIM_HEAD)
            t = jnp.arange(n, dtype=jnp.float32)
            freqs = t[:, None] * inv_freq[None, :]
            freqs = jnp.concatenate([freqs, freqs], axis=-1)
            base = (half_idx + 0.4 * DIM_HEAD) / (1.4 * DIM_HEAD)
            power = (t - n // 2) / float(WINDOW // 2)
            scale = base[None, :] ** power[:, None]
            scale = jnp.concatenate([scale, scale], axis=-1)
            cos, sin = (jnp.cos(freqs), jnp.sin(freqs))
            q = q * cos * scale + rotate_half(q) * sin * scale
            k = k * cos / scale + rotate_half(k) * sin / scale
            return (q, k)

        def local_attention(q, k, v):
            b, h, n, d = q.shape
            w = n // WINDOW
            bq = q.reshape(b, h, w, WINDOW, d) * QK_SCALE
            bk = k.reshape(b, h, w, WINDOW, d)
            bv = v.reshape(b, h, w, WINDOW, d)

            def look_around(t):
                p = jnp.pad(t, ((0, 0), (0, 0), (1, 0), (0, 0), (0, 0)))
                return jnp.concatenate([p[:, :, :w], p[:, :, 1:]], axis=3)
            bk, bv = (look_around(bk), look_around(bv))
            bt = jnp.arange(n).reshape(w, WINDOW)
            btp = jnp.pad(bt, ((1, 0), (0, 0)), constant_values=-1)
            btk = jnp.concatenate([btp[:w], btp[1:]], axis=1)
            sim = jnp.einsum('bhwid,bhwjd->bhwij', bq, bk)
            i = bt[:, :, None]
            j = btk[:, None, :]
            mask = (i < j) | (i > j + WINDOW) | (j == -1)
            sim = jnp.where(mask, -jnp.finfo(sim.dtype).max, sim)
            attn = jax.nn.softmax(sim, axis=-1)
            out = jnp.einsum('bhwij,bhwjd->bhwid', attn, bv)
            return out.reshape(b, h, n, d)

        def _layer(x, wqkv, qs, ksc, wo, lg, lb, w1, b1, w2, b2):
            b, n, _ = x.shape
            h = shift_token(x)
            qkv = h @ wqkv
            q, k, v = jnp.split(qkv, 3, axis=-1)
            to_heads = lambda t: t.reshape(b, n, HEADS, DIM_HEAD).transpose(0, 2, 1, 3)
            q, k, v = (to_heads(q), to_heads(k), to_heads(v))
            q = l2norm(q) * qs
            k = l2norm(k) * ksc
            q, k = rotary_xpos(q, k)
            o = local_attention(q, k, v)
            o = o.transpose(0, 2, 1, 3).reshape(b, n, INNER)
            x = x + o @ wo
            h = shift_token(x)
            mu = h.mean(-1, keepdims=True)
            var = h.var(-1, keepdims=True)
            h = (h - mu) / jnp.sqrt(var + 1e-05) * lg + lb
            h = h @ w1 + b1
            a, g = jnp.split(h, 2, axis=-1)
            h = a * jax.nn.gelu(g, approximate=False)
            x = x + h @ w2 + b2
            return x
        for l in range(DEPTH):
            x = _layer(x, wqkv[l], q_scale[l], k_scale[l], wo[l], ln_g[l], ln_b[l], w1[l], b1[l], w2[l], b2[l])
        return x

    def _L3_attn_ref(x, W_in, conv_w, conv_b, W_out):
        import jax, jax.numpy as jnp
        import numpy as np
        from jax import lax
        B, L, D = (4, 1024, 256)
        EXPAND, K = (2, 4)
        INNER = D * EXPAND
        h = jnp.einsum('bld,df->blf', x, W_in)
        a, g = jnp.split(h, 2, axis=-1)
        h = a * jax.nn.sigmoid(g)
        hc = jnp.transpose(h, (0, 2, 1))
        y = lax.conv_general_dilated(hc, conv_w, window_strides=(1,), padding=[(K - 1, 0)], dimension_numbers=('NCH', 'OIH', 'NCH'), feature_group_count=INNER) + conv_b[None, :, None]
        y = jax.nn.silu(y)
        y = jnp.transpose(y, (0, 2, 1))
        return jnp.einsum('blf,fd->bld', y, W_out)

    def _L3_xattn_ref(query, kv, Wq, bq, Wkv, bkv, Wo, bo):
        import jax, jax.numpy as jnp
        import numpy as np
        import math
        EMBED = 256
        HEADS = 16
        HEAD_DIM = EMBED // HEADS

        def alibi_slopes(heads: int) -> jnp.ndarray:
            return jnp.asarray([2.0 ** (-8.0 * (h + 1) / heads) for h in range(heads)], dtype=jnp.float32)
        B, Nq, E = query.shape
        Nk = kv.shape[1]
        H, D = (HEADS, HEAD_DIM)
        q = query @ Wq + bq
        kvp = kv @ Wkv + bkv
        k, v = jnp.split(kvp, 2, axis=-1)
        q = q.reshape(B, Nq, H, D).transpose(0, 2, 1, 3)
        k = k.reshape(B, Nk, H, D).transpose(0, 2, 1, 3)
        v = v.reshape(B, Nk, H, D).transpose(0, 2, 1, 3)
        slopes = alibi_slopes(H)
        rel = jnp.abs(jnp.arange(Nk)[None, :] - jnp.arange(Nq)[:, None] - (Nk - Nq))
        bias = -slopes[:, None, None] * rel.astype(jnp.float32)
        scale = 1.0 / math.sqrt(D)
        scores = jnp.einsum('bhqd,bhkd->bhqk', q, k) * scale + bias[None]
        attn = jax.nn.softmax(scores, axis=-1)
        out = jnp.einsum('bhqk,bhkd->bhqd', attn, v)
        out = out.transpose(0, 2, 1, 3).reshape(B, Nq, E)
        return out @ Wo + bo

    def _L3_ffn_ref(x, Wg, W1, b1, W2, b2):
        import jax, jax.numpy as jnp
        import numpy as np
        HIDDEN = 256
        INTER = 1024
        N_EXPERTS = 8
        TOP_K = 2
        INIT_STD = 0.02
        orig_shape = x.shape
        xt = x.reshape(-1, HIDDEN)
        T = xt.shape[0]
        logits = xt @ Wg.T
        topk_logits, topk_idx = jax.lax.top_k(logits, TOP_K)
        w = jax.nn.softmax(topk_logits, axis=-1)
        rows = jnp.arange(T)[:, None]
        gates = jnp.zeros((T, N_EXPERTS), xt.dtype).at[rows, topk_idx].add(w)
        h = jnp.einsum('th,ehi->tei', xt, W1) + b1
        h = jax.nn.gelu(h, approximate=False)
        o = jnp.einsum('tei,eih->teh', h, W2) + b2
        y = jnp.einsum('te,teh->th', gates, o)
        return y.reshape(orig_shape)
    x = _layernorm(x + _L0_attn_ref(x, L0_attn_Wq, L0_attn_Wk, L0_attn_Wv, L0_attn_Wb, L0_attn_conv_q, L0_attn_conv_k, L0_attn_conv_v, L0_attn_g, L0_attn_Wo), axis=-1)
    x = _layernorm(x + _L0_xattn_ref(x, ctx_1024, ctx_1024, L0_xattn_Wq, L0_xattn_bq, L0_xattn_Wk, L0_xattn_bk, L0_xattn_Wv, L0_xattn_bv, L0_xattn_Wo, L0_xattn_bo), axis=-1)
    x = _layernorm(x + _L0_ffn_ref(x, L0_ffn_index_b, L0_ffn_index_t, L0_ffn_sw1, L0_ffn_sb1, L0_ffn_sw2, L0_ffn_sb2, L0_ffn_sw3, L0_ffn_sb3, L0_ffn_s_ln_g, L0_ffn_s_ln_b, L0_ffn_sg_w, L0_ffn_sg_b, L0_ffn_eg_w, L0_ffn_eg_b, L0_ffn_exp_bias, L0_ffn_ew1, L0_ffn_eb1, L0_ffn_ew2, L0_ffn_eb2, L0_ffn_ew3, L0_ffn_eb3, L0_ffn_sel_ln_g, L0_ffn_sel_ln_b), axis=-1)
    x = _layernorm(x + _L1_attn_ref(x, L1_attn_W_dq, L1_attn_W_uq, L1_attn_q_ln_g, L1_attn_q_ln_b, L1_attn_W_dkv, L1_attn_W_ukv, L1_attn_kv_ln_g, L1_attn_kv_ln_b, L1_attn_W_o), axis=-1)
    x = _layernorm(x + _L1_xattn_ref(x, ctx_1024, ctx_1024, mask_1xSxS2_ff0, L1_xattn_kernel_q, L1_xattn_kernel_k, L1_xattn_kernel_v, L1_xattn_bias_q, L1_xattn_bias_k, L1_xattn_bias_v), axis=-1)
    x = _layernorm(x + _L1_ffn_ref(x, L1_ffn_w_gate, L1_ffn_w_up, L1_ffn_w_down), axis=-1)
    x = _layernorm(x + _L2_attn_ref(x, L2_attn_W_qkv, L2_attn_W_out), axis=-1)
    x = _layernorm(x + _L2_xattn_ref(x, ctx_1024, ctx_1024, L2_xattn_Wq, L2_xattn_bq, L2_xattn_Wk, L2_xattn_bk, L2_xattn_Wv, L2_xattn_bv, L2_xattn_Wo, L2_xattn_bo), axis=-1)
    x = _layernorm(x + _L2_ffn_ref(x, L2_ffn_wqkv, L2_ffn_q_scale, L2_ffn_k_scale, L2_ffn_wo, L2_ffn_ln_g, L2_ffn_ln_b, L2_ffn_w1, L2_ffn_b1, L2_ffn_w2, L2_ffn_b2), axis=-1)
    x = _layernorm(x + _L3_attn_ref(x, L3_attn_W_in, L3_attn_conv_w, L3_attn_conv_b, L3_attn_W_out), axis=-1)
    x = _layernorm(x + _L3_xattn_ref(x, ctx_1024, L3_xattn_Wq, L3_xattn_bq, L3_xattn_Wkv, L3_xattn_bkv, L3_xattn_Wo, L3_xattn_bo), axis=-1)
    x = _layernorm(x + _L3_ffn_ref(x, L3_ffn_Wg, L3_ffn_W1, L3_ffn_b1, L3_ffn_W2, L3_ffn_b2), axis=-1)
    return x

_drawn_inputs = setup_inputs


def setup_inputs(seed=0):
    import zlib

    import numpy as np

    out = dict(_drawn_inputs(seed))
    spreads = {'L0_attn_g': (1.0, 0.6),
     'L0_xattn_bq': (0.0, 0.8),
     'L0_xattn_bk': (0.0, 0.8),
     'L0_xattn_bv': (0.0, 0.8),
     'L0_xattn_bo': (0.0, 0.8),
     'L0_ffn_sb1': (0.0, 0.8),
     'L0_ffn_sb2': (0.0, 0.8),
     'L0_ffn_sb3': (0.0, 0.8),
     'L0_ffn_s_ln_g': (1.0, 0.6),
     'L0_ffn_s_ln_b': (0.0, 0.8),
     'L0_ffn_eg_b': (0.0, 0.8),
     'L0_ffn_exp_bias': (0.0, 0.8),
     'L0_ffn_eb1': (0.0, 0.8),
     'L0_ffn_eb2': (0.0, 0.8),
     'L0_ffn_eb3': (0.0, 0.8),
     'L0_ffn_sel_ln_g': (1.0, 0.6),
     'L0_ffn_sel_ln_b': (0.0, 0.8),
     'L1_attn_q_ln_g': (1.0, 0.6),
     'L1_attn_q_ln_b': (0.0, 0.8),
     'L1_attn_kv_ln_g': (1.0, 0.6),
     'L1_attn_kv_ln_b': (0.0, 0.8),
     'L2_xattn_bq': (0.0, 0.8),
     'L2_xattn_bk': (0.0, 0.8),
     'L2_xattn_bv': (0.0, 0.1),
     'L2_xattn_bo': (0.0, 0.1),
     'L2_ffn_q_scale': (1.0, 0.6),
     'L2_ffn_k_scale': (1.0, 0.6),
     'L2_ffn_ln_g': (1.0, 0.6),
     'L2_ffn_ln_b': (0.0, 0.8),
     'L2_ffn_b1': (0.0, 0.8),
     'L2_ffn_b2': (0.0, 0.1),
     'L3_xattn_bq': (0.0, 0.8),
     'L3_xattn_bkv': (0.0, 0.285),
     'L3_xattn_bo': (0.0, 0.1),
     'L3_ffn_b1': (0.0, 0.323),
     'L3_ffn_b2': (0.0, 0.1)}
    factors = {'L0_attn_Wq': 3.473,
     'L0_attn_Wk': 3.681,
     'L0_attn_Wv': 3.781,
     'L0_attn_Wb': 8.0,
     'L0_attn_conv_q': 3.217,
     'L0_attn_conv_k': 3.578,
     'L0_attn_conv_v': 3.47,
     'L0_attn_Wo': 3.406,
     'L0_xattn_Wq': 4.865,
     'L0_xattn_Wk': 4.878,
     'L0_ffn_sw1': 4.769,
     'L0_ffn_sw2': 4.913,
     'L0_ffn_sw3': 4.675,
     'L0_ffn_sg_w': 8.0,
     'L0_ffn_eg_w': 8.0,
     'L0_ffn_ew1': 8.0,
     'L0_ffn_ew2': 8.0,
     'L0_ffn_ew3': 8.0,
     'L1_attn_W_dq': 8.0,
     'L1_attn_W_uq': 8.0,
     'L1_attn_W_dkv': 8.0,
     'L1_attn_W_ukv': 8.0,
     'L1_attn_W_o': 8.0,
     'L1_xattn_bias_q': 8.0,
     'L1_xattn_bias_k': 8.0,
     'L2_xattn_Wq': 8.0,
     'L2_xattn_Wk': 8.0,
     'L3_attn_W_in': 8.0,
     'L3_attn_conv_w': 8.0,
     'L3_attn_conv_b': 8.0,
     'L3_attn_W_out': 8.0,
     'L3_xattn_Wq': 8.0}
    for name, (base, spread) in spreads.items():
        noise = np.random.default_rng([zlib.crc32(name.encode()), seed]).standard_normal(out[name].shape)
        drawn = base * np.exp(spread * noise) if base else spread * noise
        out[name] = jnp.asarray(drawn.astype(out[name].dtype))
    for name, factor in factors.items():
        out[name] = (out[name] * factor).astype(out[name].dtype)
    return out
```

```python
from contextlib import ExitStack, contextmanager

import numpy as np

import concourse.bass as bass
from concourse import mybir

F32 = mybir.dt.float32
BF16 = mybir.dt.bfloat16
I32 = mybir.dt.int32
U32 = mybir.dt.uint32
ALU = mybir.AluOpType
ACT = mybir.ActivationFunctionType
AX = mybir.AxisListType.X

P = 128
B = 2
S = 1024
D = 256
DC = D // P
TOK = B * S
NT = TOK // P
BLK = 512
NB = TOK // BLK
TPB = BLK // P
CTX = 154
LN_EPS = 1e-5
NEG = -1e30
SEM_LIMIT = 100


class Fixed:
    pass


@contextmanager
def phase(nc, pool, names):
    names = names.split()
    if len(pool) + len(names) > SEM_LIMIT:
        nc.clear_and_free_semaphores(list(pool))
        nc.all_engine_barrier()
        pool.clear()
    sems = {n: nc.alloc_semaphore(f"{n}_{nc.next_id()}") for n in names}
    pool.extend(sems.values())
    with nc.Block() as block:
        yield block, sems


def sbuf(es, nc, name, shape, dt=F32):
    return es.enter_context(nc.sbuf_tensor(f"{name}_{nc.next_id()}", shape, dt))


def spread(v, parts=P):
    return v.rearrange("(o n) -> o n", o=1).broadcast_to((parts, v.shape[0]))



def rows(a):
    a = np.asarray(a)
    return np.ascontiguousarray(a.reshape(a.shape[0] // P, P, -1).transpose(1, 0, 2))


def cols(v):
    return np.ascontiguousarray(np.asarray(v).reshape(-1, P).T)


def pad(a, axis, n):
    width = [(0, 0)] * a.ndim
    width[axis] = (0, n - a.shape[axis])
    return np.pad(np.asarray(a), width)


def setup(nc, K, w):
    with phase(nc, K.sems, "loaded ones_set masks_set") as (block, s):
        @block.sync
        def _(sp):
            sp.dma_start(K.XT[0][:], w["xT"]).then_inc(s["loaded"], 16)
            sp.dma_start(K.ctxT[:], w["ctxT"]).then_inc(s["loaded"], 16)
            sp.dma_start(K.Xtok[:], w["xtok"]).then_inc(s["loaded"], 16)
            sp.wait_ge(s["loaded"], 16 * 3)

        @block.gpsimd
        def _(pool):
            pool.memset(K.eps[:], LN_EPS)
            pool.memset(K.ones[:], 1.0).then_inc(s["ones_set"], 1)
            pool.wait_ge(s["ones_set"], 1)

            def select(out, op, base, pattern, mult, fill=0.0, src=None):
                return pool.affine_select(out=out, in_=out if src is None else src, compare_op=op, fill=fill,
                                          base=base, pattern=pattern, channel_multiplier=mult)
            ones = K.ones[:, 0:P]
            select(K.ident[:], ALU.is_equal, 0, [[-1, P]], 1, src=ones).then_inc(s["masks_set"], 1)
            select(K.identb[:], ALU.is_equal, 0, [[-1, P]], 1, src=ones).then_inc(s["masks_set"], 1)
            select(K.causal_T[:], ALU.is_ge, 0, [[1, P]], -1, src=ones).then_inc(s["masks_set"], 1)
            o8 = K.ones[:, 0:8 * P].rearrange("p (h j) -> p h j", h=8)
            select(K.head_cols[:], ALU.is_ge, 0, [[-16, 8], [1, P]], 0, src=o8).then_inc(s["masks_set"], 1)
            pool.wait_ge(s["masks_set"], 4)
            select(K.head_cols[:], ALU.is_ge, 15, [[16, 8], [-1, P]], 0).then_inc(s["masks_set"], 1)
            select(K.head_rows[:], ALU.is_ge, 0, [[-16, 8]], 1, src=K.ones[:, 0:8]).then_inc(s["masks_set"], 1)
            pool.wait_ge(s["masks_set"], 6)
            select(K.head_rows[:], ALU.is_ge, 15, [[16, 8]], -1).then_inc(s["masks_set"], 1)
            pool.memset(K.above[:], 0.0).then_inc(s["masks_set"], 1)
            pool.memset(K.below[:], 0.0).then_inc(s["masks_set"], 1)
            pool.wait_ge(s["masks_set"], 9)
            select(K.above[:], ALU.is_ge, 0, [[-1, P]], 1, fill=NEG).then_inc(s["masks_set"], 1)
            select(K.below[:], ALU.is_ge, 0, [[1, P]], -1, fill=NEG).then_inc(s["masks_set"], 1)
            select(K.live_keys[:], ALU.is_ge, CTX - P - 1, [[0, 1]], -1, src=K.ones[:, 0:1]).then_inc(s["masks_set"], 1)


def ln_stats(dve, st, r):
    dve.bn_stats(st[:, 2:8], r)
    dve.drain()
    return dve.bn_aggr(st[:, 0:2], st[:, 2:8])


def ln_std(act, K, st):
    return act.activation(st[:, 8:9], st[:, 1:2], ACT.Sqrt, bias=K.eps[:, 0:1])


def ln_apply(dve, st, r, out):
    dve.reciprocal(st[:, 8:9], st[:, 8:9])
    dve.drain()
    return dve.tensor_scalar(out, r, st[:, 0:1], st[:, 8:9], ALU.subtract, ALU.mult)


def finish(nc, K, wt, src, n_k, bias=None, relu=False, res=None):
    xi, xo = K.XT[K.cur], K.XT[1 - K.cur]
    res = res or xi
    with ExitStack() as es, phase(nc, K.sems, "y_done sum_done turned stats_done std_done tok_done back_turned copied") as (block, s):
        rT = sbuf(es, nc, "rT", [P, 2, DC, BLK])
        st = sbuf(es, nc, "ln_stats", [P, NT, 9])

        @block.tensor
        def _(pe):
            def product(j):
                if j >= 2:
                    pe.wait_ge(s["sum_done"], j - 1)
                for h in range(DC):
                    for k in range(n_k):
                        last = pe.matmul(K.bank[2 * (j % 2) + h][:], wt(k, h, j), src(k, j), start=(k == 0), stop=(k == n_k - 1))
                last.then_inc(s["y_done"], 1)

            def turn_back(t):
                pe.wait_ge(s["tok_done"], t + 1)
                if t >= 2:
                    pe.wait_ge(s["copied"], t - 1)
                for h in range(DC):
                    last = pe.transpose(K.bank[6 + t % 2][:, h * P:(h + 1) * P], K.Xtok[:, t, h * P:(h + 1) * P], K.ident[:])
                last.then_inc(s["back_turned"], 1)

            product(0)
            for j in range(NB):
                if j + 1 < NB:
                    product(j + 1)
                pe.wait_ge(s["sum_done"], j + 1)
                for t in range(TPB * j, TPB * (j + 1)):
                    if t >= 2:
                        pe.wait_ge(s["tok_done"], t - 1)
                    for h in range(DC):
                        last = pe.transpose(K.bank[4 + t % 2][:, h * P:(h + 1) * P],
                                            rT[:, j % 2, h, (t % TPB) * P:(t % TPB + 1) * P], K.ident[:])
                    last.then_inc(s["turned"], 1)
                    if t > 0:
                        turn_back(t - 1)
            turn_back(NT - 1)

        @block.vector
        def _(dve):
            def add(j):
                dve.wait_ge(s["y_done"], j + 1)
                for h in range(DC):
                    y = K.bank[2 * (j % 2) + h][:]
                    old = res[:, h, j * BLK:(j + 1) * BLK]
                    if relu:
                        last = dve.scalar_tensor_tensor(out=rT[:, j % 2, h, :], in0=y, scalar=0.0, in1=old, op0=ALU.max, op1=ALU.add)
                    elif bias is not None:
                        last = dve.scalar_tensor_tensor(out=rT[:, j % 2, h, :], in0=y, scalar=bias[:, h:h + 1], in1=old,
                                                        op0=ALU.add, op1=ALU.add)
                    else:
                        last = dve.tensor_tensor(rT[:, j % 2, h, :], y, old, ALU.add)
                    if h == 0:
                        dve.drain()
                last.then_inc(s["sum_done"], 1)

            def normalise(t):
                dve.wait_ge(s["std_done"], t + 1)
                ln_apply(dve, st[:, t, :], K.bank[4 + t % 2][:, 0:D], K.Xtok[:, t, :]).then_inc(s["tok_done"], 1)

            add(0)
            for j in range(NB):
                for t in range(TPB * j, TPB * (j + 1)):
                    dve.wait_ge(s["turned"], t + 1)
                    ln_stats(dve, st[:, t, :], K.bank[4 + t % 2][:, 0:D]).then_inc(s["stats_done"], 1)
                    if t > 0:
                        normalise(t - 1)
                    if t % TPB == 1 and j + 1 < NB:
                        add(j + 1)
            normalise(NT - 1)

        @block.scalar
        def _(act):
            for t in range(NT + 1):
                if t < NT:
                    act.wait_ge(s["stats_done"], t + 1)
                    ln_std(act, K, st[:, t, :]).then_inc(s["std_done"], 1)
                if t > 0:
                    act.wait_ge(s["back_turned"], t)
                    act.activation(xo[:, :, (t - 1) * P:t * P], K.bank[6 + (t - 1) % 2][:, 0:D].rearrange("p (c k) -> p c k", c=2),
                                   ACT.Copy).then_inc(s["copied"], 1)
    K.cur = 1 - K.cur


def project(nc, K, es, n_m, n_k, wt, src, evac_act, evac_dve, n_blk=NB, loads=(), width=lambda j: BLK):
    with phase(nc, K.sems, "loaded done act_out dve_out") as (block, s):
        steps = [(m, j) for m in range(n_m) for j in range(n_blk)]

        @block.sync
        def _(sp):
            for dst, srcd in loads:
                sp.dma_start(dst, srcd).then_inc(s["loaded"], 16)

        @block.tensor
        def _(pe):
            pe.wait_ge(s["loaded"], 16 * len(loads)) if loads else None
            for n, (m, j) in enumerate(steps):
                if n >= 8:
                    pe.wait_ge(s["act_out"] if n % 2 == 0 else s["dve_out"], (n - 8) // 2 + 1)
                for k in range(n_k):
                    last = pe.matmul(K.bank[n % 8][:, 0:width(j)], wt(k, m), src(k, j), start=(k == 0), stop=(k == n_k - 1))
                last.then_inc(s["done"], 1)

        @block.scalar
        def _(act):
            act.wait_ge(s["loaded"], 16 * len(loads)) if loads else None
            for n, (m, j) in enumerate(steps):
                if n % 2 == 0:
                    act.wait_ge(s["done"], n + 1)
                    evac_act(act, m, j, K.bank[n % 8][:, 0:width(j)]).then_inc(s["act_out"], 1)

        @block.vector
        def _(dve):
            dve.wait_ge(s["loaded"], 16 * len(loads)) if loads else None
            for n, (m, j) in enumerate(steps):
                if n % 2 == 1:
                    dve.wait_ge(s["done"], n + 1)
                    evac_dve(dve, m, j, K.bank[n % 8][:, 0:width(j)]).then_inc(s["dve_out"], 1)


def load(nc, K, *pairs):
    with phase(nc, K.sems, "loaded") as (block, s):
        @block.sync
        def _(sp):
            for dst, src in pairs[0::2]:
                sp.dma_start(dst, src).then_inc(s["loaded"], 16)
            sp.wait_ge(s["loaded"], 16 * len(pairs))

        @block.scalar
        def _(act):
            for dst, src in pairs[1::2]:
                act.dma_start(dst, src).then_inc(s["loaded"], 16)


def copy_to(dst, bias=None, relu=False):
    def by_act(act, m, j, src):
        if bias is None:
            return act.activation(dst(m, j), src, ACT.Copy)
        return act.activation(dst(m, j), src, ACT.Relu if relu else ACT.Identity, bias=bias(m))

    def by_dve(dve, m, j, src):
        if bias is None:
            return dve.tensor_copy(dst(m, j), src)
        if relu:
            return dve.tensor_scalar(dst(m, j), src, bias(m), 0.0, ALU.add, ALU.max)
        return dve.tensor_scalar(dst(m, j), src, bias(m), None, ALU.add)
    return by_act, by_dve


def block_of(xT):
    return lambda k, j: xT[:, k, j * BLK:(j + 1) * BLK]


def ctx_values(nc, K, V, Wv, bias_row, relu, live=True):
    with phase(nc, K.sems, "done summed") as (block, s):
        @block.tensor
        def _(pe):
            for n in range(2 * B):
                b, kt = divmod(n, 2)
                for k in range(DC):
                    last = pe.matmul(K.bank[n][:, 0:D], K.ctxT[:, k, b, kt * P:(kt + 1) * P], Wv[:, k, :], start=(k == 0), stop=(k == DC - 1))
                last.then_inc(s["done"], 1)

        @block.vector
        def _(dve):
            for n in range(2 * B):
                b, kt = divmod(n, 2)
                v = V[:, b, kt, :]
                dve.wait_ge(s["done"], n + 1)
                dve.tensor_tensor(v, K.bank[n][:, 0:D], bias_row, ALU.add)
                dve.drain()
                if relu:
                    dve.tensor_scalar(v, v, 0.0, None, ALU.max)
                    dve.drain()
                if kt == 1:
                    dve.tensor_scalar(v, v, K.live_keys[:, 0:1], None, ALU.mult)
                    dve.drain()


def L1_xattn_layout(i):
    maskT = np.ascontiguousarray(pad(np.asarray(i["mask_1xSxS2_ff0"])[0].T, 0, 2 * P))
    return {"L1x_Wq": rows(i["L1_xattn_kernel_q"][0, 0]), "L1x_Wk": rows(i["L1_xattn_kernel_k"][0, 0]),
            "L1x_Wv": rows(i["L1_xattn_kernel_v"][0, 0]), "L1x_bq": cols(i["L1_xattn_bias_q"]),
            "L1x_bk": cols(i["L1_xattn_bias_k"]), "L1x_bv": np.asarray(i["L1_xattn_bias_v"]), "L1x_maskT": rows(maskT)}


def L1_xattn(nc, K, w):
    with ExitStack() as es:
        Wq, Wk, Wv = (sbuf(es, nc, n, [P, DC, D]) for n in ("Wq", "Wk", "Wv"))
        bq, bk = (sbuf(es, nc, n, [P, DC]) for n in ("bq", "bk"))
        bv = sbuf(es, nc, "bv", [P, D])
        maskT = sbuf(es, nc, "maskT", [P, 2, S])
        QT = sbuf(es, nc, "QT", [P, DC, TOK])
        KT = sbuf(es, nc, "KT", [P, DC, B * 256])
        V = sbuf(es, nc, "V", [P, B, 2, D])
        ST = sbuf(es, nc, "ST", [P, 2, TOK])
        load(nc, K, (Wq[:], w["L1x_Wq"]), (Wk[:], w["L1x_Wk"]), (Wv[:], w["L1x_Wv"]), (bq[:], w["L1x_bq"]),
             (bk[:], w["L1x_bk"]), (bv[:], spread(w["L1x_bv"])), (maskT[:], w["L1x_maskT"]))
        a, v = copy_to(lambda m, j: QT[:, m, j * BLK:(j + 1) * BLK], lambda m: bq[:, m:m + 1], True)
        project(nc, K, es, DC, DC, lambda k, m: Wq[:, k, m * P:(m + 1) * P], block_of(K.XT[K.cur]), a, v)
        a, v = copy_to(lambda m, j: KT[:, m, :], lambda m: bk[:, m:m + 1], True)
        project(nc, K, es, DC, DC, lambda k, m: Wk[:, k, m * P:(m + 1) * P],
                lambda k, j: K.ctxT[:, k].rearrange("p b n -> p (b n)"), a, v, n_blk=1)
        ctx_values(nc, K, V, Wv, bv[:], True)
        with phase(nc, K.sems, "done relued masked") as (block, s):
            @block.tensor
            def _(pe):
                for n in range(2 * NB):
                    j, kt = divmod(n, 2)
                    for k in range(DC):
                        last = pe.matmul(K.bank[n][:], KT[:, k, (j // 2) * 256 + kt * P:(j // 2) * 256 + (kt + 1) * P],
                                         QT[:, k, j * BLK:(j + 1) * BLK], start=(k == 0), stop=(k == DC - 1))
                    last.then_inc(s["done"], 1)

            @block.scalar
            def _(act):
                for n in range(2 * NB):
                    act.wait_ge(s["done"], n + 1)
                    j, kt = divmod(n, 2)
                    act.activation(ST[:, kt, j * BLK:(j + 1) * BLK], K.bank[n][:], ACT.Relu, scale=float(D) ** -0.5).then_inc(s["relued"], 1)

            @block.vector
            def _(dve):
                for n in range(2 * NB):
                    dve.wait_ge(s["relued"], n + 1)
                    j, kt = divmod(n, 2)
                    st = ST[:, kt, j * BLK:(j + 1) * BLK]
                    dve.tensor_tensor(st, st, maskT[:, kt, (j % 2) * BLK:(j % 2 + 1) * BLK], ALU.add)
        finish(nc, K, lambda k, h, j: V[:, j // 2, k, h * P:(h + 1) * P], block_of(ST), 2, relu=True)


HEADS = 16
HD = D // HEADS
HPC = P // HD
HK = HPC * CTX
HKT = -(-HK // P)
GROUPS = [(0, 3), (3, 3), (6, 2)]
ALIBI_OFF = S - CTX


def middle(ap, n):
    return ap.unsqueeze(1).broadcast_to((ap.shape[0], n, ap.shape[1]))


def inner(ap, n):
    return ap.unsqueeze(2).broadcast_to((ap.shape[0], ap.shape[1], n))


def cross_attention(nc, K, w, pre, scale, slopes=None):
    with ExitStack() as es:
        Wo = sbuf(es, nc, "Wo", [P, DC, D])
        bo = sbuf(es, nc, "bo", [P, DC])
        OT = sbuf(es, nc, "OT", [P, DC, TOK])
        with ExitStack() as inside:
            Vb = sbuf(inside, nc, "Vblocks", [P, DC, B, HKT, P])
            Kb = sbuf(inside, nc, "Kblocks", [P, DC, B, HK])
            QT = sbuf(inside, nc, "QT", [P, DC, TOK])
            Pr = sbuf(inside, nc, "probs", [P, 2 * 2 * HK])
            with ExitStack() as temp:
                Wq, Wk, Wv = (sbuf(temp, nc, n, [P, DC, D]) for n in ("Wq", "Wk", "Wv"))
                bq, bk, bv = (sbuf(temp, nc, n, [P, DC]) for n in ("bq", "bk", "bv"))
                KT, VT = (sbuf(temp, nc, n, [P, DC, B * 256]) for n in ("KT", "VT"))
                load(nc, K, (Wq[:], w[pre + "Wq"]), (Wk[:], w[pre + "Wk"]), (Wv[:], w[pre + "Wv"]), (Wo[:], w[pre + "Wo"]),
                     (bq[:], w[pre + "bq"]), (bk[:], w[pre + "bk"]), (bv[:], w[pre + "bv"]), (bo[:], w[pre + "bo"]))
                a, v = copy_to(lambda m, j: QT[:, m, j * BLK:(j + 1) * BLK], lambda m: bq[:, m:m + 1])
                project(nc, K, es, DC, DC, lambda k, m: Wq[:, k, m * P:(m + 1) * P], block_of(K.XT[K.cur]), a, v)
                ctx = lambda k, j: K.ctxT[:, k].rearrange("p b n -> p (b n)")
                a, v = copy_to(lambda m, j: KT[:, m, :], lambda m: bk[:, m:m + 1])
                project(nc, K, es, DC, DC, lambda k, m: Wk[:, k, m * P:(m + 1) * P], ctx, a, v, n_blk=1)
                a, v = copy_to(lambda m, j: VT[:, m, :], lambda m: bv[:, m:m + 1])
                project(nc, K, es, DC, DC, lambda k, m: Wv[:, k, m * P:(m + 1) * P], ctx, a, v, n_blk=1)
                with phase(nc, K.sems, "spread turned out") as (block, s):
                    VbT = Pr[:].rearrange("p (n hk) -> p n hk", hk=HK)

                    @block.vector
                    def _(dve):
                        for n in range(DC * B):
                            c, b = divmod(n, B)
                            dve.tensor_tensor(VbT[:, n, :].rearrange("p (h k) -> p h k", h=HPC), middle(VT[:, c, b * 256:b * 256 + CTX], HPC),
                                              inner(K.head_rows[:], CTX), ALU.mult).then_inc(s["spread"], 1)
                        for n in range(DC * B):
                            c, b = divmod(n, B)
                            dve.tensor_tensor(Kb[:, c, b, :].rearrange("p (h k) -> p h k", h=HPC), middle(KT[:, c, b * 256:b * 256 + CTX], HPC),
                                              inner(K.head_rows[:], CTX), ALU.mult)

                    @block.tensor
                    def _(pe):
                        for n in range(DC * B):
                            pe.wait_ge(s["spread"], n + 1)
                            for g in range(3):
                                if 3 * n + g >= 8:
                                    pe.wait_ge(s["out"], 3 * n + g - 7)
                                for i in range(4 * g, min(4 * g + 4, HKT)):
                                    r = min(P, HK - i * P)
                                    last = pe.transpose(K.bank[(3 * n + g) % 8][0:r, (i % 4) * P:(i % 4 + 1) * P],
                                                        VbT[:, n, i * P:i * P + r], K.ident[:])
                                last.then_inc(s["turned"], 1)

                    @block.scalar
                    def _(act):
                        for n in range(DC * B):
                            c, b = divmod(n, B)
                            for g in range(3):
                                act.wait_ge(s["turned"], 3 * n + g + 1)
                                src = K.bank[(3 * n + g) % 8]
                                if g < 2:
                                    act.activation(Vb[:, c, b, 4 * g:4 * g + 4, :], src[:].rearrange("p (i k) -> p i k", i=4), ACT.Copy).then_inc(s["out"], 1)
                                else:
                                    act.activation(Vb[:, c, b, 8, :], src[:, 0:P], ACT.Copy)
                                    act.activation(Vb[0:HK - 9 * P, c, b, 9, :], src[0:HK - 9 * P, P:2 * P], ACT.Copy).then_inc(s["out"], 1)

            PT = sbuf(inside, nc, "probsT", [P, HKT, P])
            stat = sbuf(inside, nc, "stat", [P, 2, 3, HPC])
            Rx = sbuf(inside, nc, "recip_spread", [P, 2, P])
            RT = sbuf(inside, nc, "recipT", [P, 2, P])
            names = "recip_spread scored biased max_done exp_done recip_done turned probs_out recip_out pv_done out"
            with phase(nc, K.sems, names) as (block, s):
                steps = NT * DC
                sc = lambda n, g: K.bank[3 * (n % 2) + g]
                probs = lambda n: Pr[:].rearrange("p (n hk) -> p n hk", hk=HK)[:, n % 2, :]
                st = lambda n, i: stat[:, n % 2, i, :]

                @block.gpsimd
                def _(pool):
                    for n in range(steps):
                        pool.wait_ge(s["recip_done"], n + 1)
                        pool.tensor_copy(Rx[:, n % 2, :].rearrange("p (h d) -> p h d", h=HPC), inner(st(n, 2), HD)).then_inc(s["recip_spread"], 1)

                @block.tensor
                def _(pe):
                    def score(n):
                        t, c = divmod(n, DC)
                        if n >= 2:
                            pe.wait_ge(s["probs_out"], 3 * (n - 1))
                            pe.wait_ge(s["recip_out"], n - 1)
                        for g, (h0, nh) in enumerate(GROUPS):
                            last = pe.matmul(sc(n, g)[:, 0:nh * CTX], QT[:, c, t * P:(t + 1) * P],
                                             Kb[:, c, t // 8, h0 * CTX:(h0 + nh) * CTX], start=True, stop=True)
                        last.then_inc(s["scored"], 1)

                    score(0)
                    for n in range(steps):
                        t, c = divmod(n, DC)
                        if n + 1 < steps:
                            score(n + 1)
                        pe.wait_ge(s["exp_done"], n + 1)
                        for g in range(3):
                            for i in range(4 * g, min(4 * g + 4, HKT)):
                                r = min(P, HK - i * P)
                                last = pe.transpose(sc(n, g)[0:r, (i % 4) * P:(i % 4 + 1) * P], probs(n)[:, i * P:i * P + r], K.ident[:])
                            if g == 2:
                                pe.wait_ge(s["recip_spread"], n + 1)
                                last = pe.transpose(sc(n, 2)[:, 2 * P:3 * P], Rx[:, n % 2, :], K.ident[:])
                            last.then_inc(s["turned"], 1)
                        if n >= 2:
                            pe.wait_ge(s["out"], n - 1)
                        for i in range(HKT):
                            r = min(P, HK - i * P)
                            if i % 4 == 0:
                                pe.wait_ge(s["probs_out"], 3 * n + i // 4 + 1)
                            last = pe.matmul(K.bank[6 + n % 2][:, 0:P], Vb[0:r, c, t // 8, i, :], PT[0:r, i, :], start=(i == 0), stop=(i == HKT - 1))
                        last.then_inc(s["pv_done"], 1)

                @block.vector
                def _(dve):
                    def maxima(n):
                        t, c = divmod(n, DC)
                        dve.wait_ge(s["scored"], n + 1)
                        if slopes:
                            if n >= 2:
                                dve.wait_ge(s["turned"], 3 * (n - 1))
                            for g, (h0, nh) in enumerate(GROUPS):
                                for h in range(h0, h0 + nh):
                                    dve.scalar_tensor_tensor(out=probs(n)[:, h * CTX:(h + 1) * CTX], in0=K.rel[:, t % 8, :],
                                                             scalar=-slopes[c * HPC + h] / scale,
                                                             in1=sc(n, g)[:, (h - h0) * CTX:(h - h0 + 1) * CTX], op0=ALU.mult, op1=ALU.add)
                            dve.drain()
                            dve.reduce_max(st(n, 0), probs(n).rearrange("p (h k) -> p h k", h=HPC), AX)
                        else:
                            for g, (h0, nh) in enumerate(GROUPS):
                                dve.reduce_max(st(n, 0)[:, h0:h0 + nh], sc(n, g)[:, 0:nh * CTX].rearrange("p (h k) -> p h k", h=nh), AX)
                        dve.drain()
                        dve.tensor_scalar(st(n, 0), st(n, 0), -scale, None, ALU.mult).then_inc(s["max_done"], 1)

                    def output(n):
                        t, c = divmod(n, DC)
                        dve.wait_ge(s["pv_done"], n + 1)
                        dve.wait_ge(s["recip_out"], n + 1)
                        dve.tensor_tensor(OT[:, c, t * P:(t + 1) * P], K.bank[6 + n % 2][:, 0:P], RT[:, n % 2, :], ALU.mult).then_inc(s["out"], 1)

                    maxima(0)
                    for n in range(steps):
                        if n + 1 < steps:
                            maxima(n + 1)
                        dve.wait_ge(s["exp_done"], n + 1)
                        if n >= 2:
                            dve.wait_ge(s["recip_spread"], n - 1)
                        dve.reciprocal(st(n, 2), st(n, 1)).then_inc(s["recip_done"], 1)
                        if n >= 1:
                            dve.wait_ge(s["pv_done"], n)
                        for g in range(3):
                            dve.wait_ge(s["turned"], 3 * n + g + 1)
                            if g < 2:
                                dve.tensor_copy(PT[:, 4 * g:4 * g + 4, :], sc(n, g)[:].rearrange("p (i k) -> p i k", i=4)).then_inc(s["probs_out"], 1)
                            else:
                                dve.tensor_copy(PT[:, 8, :], sc(n, g)[:, 0:P])
                                dve.tensor_copy(PT[0:HK - 9 * P, 9, :], sc(n, g)[0:HK - 9 * P, P:2 * P]).then_inc(s["probs_out"], 1)
                        if n >= 1:
                            output(n - 1)
                    output(steps - 1)

                @block.scalar
                def _(act):
                    def exps(n):
                        act.wait_ge(s["max_done"], n + 1)
                        if n >= 2:
                            act.wait_ge(s["turned"], 3 * (n - 1))
                            act.wait_ge(s["recip_done"], n - 1)
                        for g, (h0, nh) in enumerate(GROUPS):
                            for h in range(h0, h0 + nh):
                                p = probs(n)[:, h * CTX:(h + 1) * CTX]
                                src = p if slopes else sc(n, g)[:, (h - h0) * CTX:(h - h0 + 1) * CTX]
                                last = act.activation(p, src, ACT.Exp, bias=st(n, 0)[:, h:h + 1], scale=scale, accum_out=st(n, 1)[:, h:h + 1])
                        last.then_inc(s["exp_done"], 1)

                    exps(0)
                    for n in range(steps):
                        if n + 1 < steps:
                            exps(n + 1)
                        act.wait_ge(s["probs_out"], 3 * n + 3)
                        if n >= 2:
                            act.wait_ge(s["out"], n - 1)
                        act.activation(RT[:, n % 2, :], sc(n, 2)[:, 2 * P:3 * P], ACT.Copy).then_inc(s["recip_out"], 1)
        finish(nc, K, lambda k, h, j: Wo[:, k, h * P:(h + 1) * P], block_of(OT), DC, bias=bo)


def L0_xattn_layout(i):
    return {"L0x_Wq": rows(i["L0_xattn_Wq"]), "L0x_Wk": rows(np.tile(i["L0_xattn_Wk"], (1, HEADS))),
            "L0x_Wv": rows(np.tile(i["L0_xattn_Wv"], (1, HEADS))), "L0x_Wo": rows(i["L0_xattn_Wo"]),
            "L0x_bq": cols(i["L0_xattn_bq"]), "L0x_bk": cols(np.tile(i["L0_xattn_bk"], HEADS)),
            "L0x_bv": cols(np.tile(i["L0_xattn_bv"], HEADS)), "L0x_bo": cols(i["L0_xattn_bo"])}


def L0_xattn(nc, K, w):
    cross_attention(nc, K, w, "L0x_", float(HD) ** -0.5)


def L3_xattn_layout(i):
    Wkv, bkv = np.asarray(i["L3_xattn_Wkv"]), np.asarray(i["L3_xattn_bkv"])
    rel = np.abs(np.arange(CTX)[None, :] - np.arange(S)[:, None] - (CTX - S)).astype(np.float32)
    return {"L3x_Wq": rows(i["L3_xattn_Wq"]), "L3x_Wk": rows(Wkv[:, :D]), "L3x_Wv": rows(Wkv[:, D:]), "L3x_Wo": rows(i["L3_xattn_Wo"]),
            "L3x_bq": cols(i["L3_xattn_bq"]), "L3x_bk": cols(bkv[:D]), "L3x_bv": cols(bkv[D:]), "L3x_bo": cols(i["L3_xattn_bo"]),
            "L3x_rel": rows(rel)}


def L3_xattn(nc, K, w):
    with ExitStack() as es:
        K.rel = sbuf(es, nc, "rel", [P, S // P, CTX])
        load(nc, K, (K.rel[:], w["L3x_rel"]))
        cross_attention(nc, K, w, "L3x_", float(HD) ** -0.5, [2.0 ** (-8.0 * (h + 1) / HEADS) for h in range(HEADS)])


def L2_xattn_layout(i):
    g = lambda n: i["L2_xattn_" + n]
    return {"L2x_Wq": rows(g("Wq")), "L2x_Wk": rows(g("Wk")), "L2x_Wv": rows(g("Wv")), "L2x_Wo": rows(g("Wo")),
            "L2x_bq": cols(g("bq")), "L2x_bk": cols(g("bk")), "L2x_bv": np.asarray(g("bv")), "L2x_bo": cols(g("bo"))}


def L2_xattn(nc, K, w):
    with ExitStack() as es:
        Wq, Wk, Wv, Wo = (sbuf(es, nc, n, [P, DC, D]) for n in ("Wq", "Wk", "Wv", "Wo"))
        bq, bk, bo = (sbuf(es, nc, n, [P, DC]) for n in ("bq", "bk", "bo"))
        bv = sbuf(es, nc, "bv", [P, D])
        QT, OT = (sbuf(es, nc, n, [P, DC, TOK]) for n in ("QT", "OT"))
        KT = sbuf(es, nc, "KT", [P, DC, B * 256])
        V = sbuf(es, nc, "V", [P, B, 2, D])
        load(nc, K, *[(dst[:], w["L2x_" + n]) for n, dst in (("Wq", Wq), ("Wk", Wk), ("Wv", Wv), ("Wo", Wo), ("bq", bq), ("bk", bk), ("bo", bo))],
             (bv[:], spread(w["L2x_bv"])))
        a, v = copy_to(lambda m, j: QT[:, m, j * BLK:(j + 1) * BLK], lambda m: bq[:, m:m + 1])
        project(nc, K, es, DC, DC, lambda k, m: Wq[:, k, m * P:(m + 1) * P], block_of(K.XT[K.cur]), a, v)
        a, v = copy_to(lambda m, j: KT[:, m, :], lambda m: bk[:, m:m + 1])
        project(nc, K, es, DC, DC, lambda k, m: Wk[:, k, m * P:(m + 1) * P],
                lambda k, j: K.ctxT[:, k].rearrange("p b n -> p (b n)"), a, v, n_blk=1)
        ctx_values(nc, K, V, Wv, bv[:], False)
        scale = float(D) ** -0.5
        Pr = sbuf(es, nc, "probs", [P, 2, CTX])
        PT = sbuf(es, nc, "probsT", [P, 2, BLK])
        stat = sbuf(es, nc, "stat", [P, 2, 3])
        with phase(nc, K.sems, "zeroed scored max_done exp_done normed turned probs_out pv_done out") as (block, s):
            @block.gpsimd
            def _(pool):
                pool.memset(PT[:, 1, :], 0.0).then_inc(s["zeroed"], 1)

            @block.tensor
            def _(pe):
                def score(t):
                    if t >= 2:
                        pe.wait_ge(s["exp_done"], t - 1)
                    for k in range(DC):
                        last = pe.matmul(K.bank[t % 2][:, 0:CTX], QT[:, k, t * P:(t + 1) * P], KT[:, k, (t // 8) * 256:(t // 8) * 256 + CTX],
                                         start=(k == 0), stop=(k == DC - 1))
                    last.then_inc(s["scored"], 1)

                score(0)
                for t in range(NT):
                    if t + 1 < NT:
                        score(t + 1)
                    pe.wait_ge(s["normed"], t + 1)
                    if t >= 2:
                        pe.wait_ge(s["probs_out"], t - 1)
                    pe.transpose(K.bank[2 + t % 2][:, 0:P], Pr[:, t % 2, 0:P], K.ident[:])
                    pe.transpose(K.bank[2 + t % 2][0:CTX - P, P:2 * P], Pr[:, t % 2, P:CTX], K.ident[:]).then_inc(s["turned"], 1)
                    if t % TPB == TPB - 1:
                        j = t // TPB
                        pe.wait_ge(s["probs_out"], t + 1)
                        if j >= 2:
                            pe.wait_ge(s["out"], 2 * (j - 1))
                        for h in range(DC):
                            for kt in range(2):
                                last = pe.matmul(K.bank[4 + 2 * (j % 2) + h][:], V[:, j // 2, kt, h * P:(h + 1) * P], PT[:, kt, :],
                                                 start=(kt == 0), stop=(kt == 1))
                        last.then_inc(s["pv_done"], 1)

            @block.vector
            def _(dve):
                def maximum(t):
                    dve.wait_ge(s["scored"], t + 1)
                    if t >= 2:
                        dve.wait_ge(s["exp_done"], t - 1)
                    dve.reduce_max(stat[:, t % 2, 0:1], K.bank[t % 2][:, 0:CTX], AX)
                    dve.drain()
                    dve.tensor_scalar(stat[:, t % 2, 0:1], stat[:, t % 2, 0:1], -scale, None, ALU.mult).then_inc(s["max_done"], 1)

                maximum(0)
                for t in range(NT):
                    if t + 1 < NT:
                        maximum(t + 1)
                    dve.wait_ge(s["exp_done"], t + 1)
                    dve.reciprocal(stat[:, t % 2, 2:3], stat[:, t % 2, 1:2])
                    dve.drain()
                    dve.tensor_scalar(Pr[:, t % 2, :], Pr[:, t % 2, :], stat[:, t % 2, 2:3], None, ALU.mult).then_inc(s["normed"], 1)

            @block.scalar
            def _(act):
                def exp(t):
                    act.wait_ge(s["max_done"], t + 1)
                    if t >= 2:
                        act.wait_ge(s["turned"], t - 1)
                    act.activation(Pr[:, t % 2, :], K.bank[t % 2][:, 0:CTX], ACT.Exp, bias=stat[:, t % 2, 0:1], scale=scale,
                                   accum_out=stat[:, t % 2, 1:2]).then_inc(s["exp_done"], 1)

                act.wait_ge(s["zeroed"], 1)
                exp(0)
                for t in range(NT):
                    if t + 1 < NT:
                        exp(t + 1)
                    act.wait_ge(s["turned"], t + 1)
                    if t % TPB == 0 and t:
                        act.wait_ge(s["pv_done"], t // TPB)
                    cols_ = slice((t % TPB) * P, (t % TPB + 1) * P)
                    act.activation(PT[:, 0, cols_], K.bank[2 + t % 2][:, 0:P], ACT.Copy)
                    act.activation(PT[0:CTX - P, 1, cols_], K.bank[2 + t % 2][0:CTX - P, P:2 * P], ACT.Copy).then_inc(s["probs_out"], 1)
                    if t % TPB == TPB - 1:
                        j = t // TPB
                        act.wait_ge(s["pv_done"], j + 1)
                        for h in range(DC):
                            act.activation(OT[:, h, j * BLK:(j + 1) * BLK], K.bank[4 + 2 * (j % 2) + h][:], ACT.Copy).then_inc(s["out"], 1)
        finish(nc, K, lambda k, h, j: Wo[:, k, h * P:(h + 1) * P], block_of(OT), DC, bias=bo)


def finish_tokens(nc, K, r, last=False):
    xo = K.XT[1 - K.cur]
    with ExitStack() as es, phase(nc, K.sems, "stats_done std_done tok_done turned") as (block, s):
        st = sbuf(es, nc, "ln_stats", [P, NT, 9])

        @block.vector
        def _(dve):
            for t in range(NT):
                dve.bn_stats(st[:, t, 2:8], r[:, t, :])
            dve.drain()
            for t in range(NT):
                ins = dve.bn_aggr(st[:, t, 0:2], st[:, t, 2:8])
            ins.then_inc(s["stats_done"], 1)
            dve.wait_ge(s["std_done"], 1)
            dve.reciprocal(st[:, :, 8:9], st[:, :, 8:9])
            dve.drain()
            for t in range(NT):
                dve.tensor_scalar(K.Xtok[:, t, :], r[:, t, :], st[:, t, 0:1], st[:, t, 8:9], ALU.subtract, ALU.mult).then_inc(s["tok_done"], 1)

        @block.scalar
        def _(act):
            act.wait_ge(s["stats_done"], 1)
            act.activation(st[:, :, 8:9], st[:, :, 1:2], ACT.Sqrt, bias=K.eps[:, 0:1]).then_inc(s["std_done"], 1)
            for t in range(0 if last else NT):
                act.wait_ge(s["turned"], t + 1)
                act.activation(xo[:, :, t * P:(t + 1) * P], K.bank[t % 4][:, 0:D].rearrange("p (c k) -> p c k", c=2), ACT.Copy).then_inc(s["std_done"], 1)

        @block.tensor
        def _(pe):
            for t in range(0 if last else NT):
                pe.wait_ge(s["tok_done"], t + 1)
                if t >= 4:
                    pe.wait_ge(s["std_done"], 1 + t - 3)
                for h in range(DC):
                    ins = pe.transpose(K.bank[t % 4][:, h * P:(h + 1) * P], K.Xtok[:, t, h * P:(h + 1) * P], K.ident[:])
                ins.then_inc(s["turned"], 1)
    K.cur = 1 - K.cur


TAPS = 4
L3A_M = 4


def L3_attn_layout(i):
    cw = np.asarray(i["L3_attn_conv_w"]).reshape(4, P, TAPS).transpose(1, 0, 2)
    return {"L3a_Win": rows(i["L3_attn_W_in"]), "L3a_cw": np.ascontiguousarray(cw), "L3a_cb": cols(i["L3_attn_conv_b"]),
            "L3a_Wout": rows(i["L3_attn_W_out"])}


def L3_attn(nc, K, w):
    with ExitStack() as es:
        Wout = sbuf(es, nc, "Wout", [P, L3A_M, D])
        Y = sbuf(es, nc, "Y", [P, L3A_M, TOK])
        with ExitStack() as inside:
            Win = sbuf(inside, nc, "Win", [P, DC, 2 * L3A_M * P])
            cw = sbuf(inside, nc, "cw", [P, L3A_M, TAPS])
            cb = sbuf(inside, nc, "cb", [P, L3A_M])
            H = sbuf(inside, nc, "H", [P, L3A_M, B, TAPS - 1 + S])
            sg = sbuf(inside, nc, "sigmoid", [P, 2, BLK])
            acc = sbuf(inside, nc, "conv", [P, 2, BLK])
            load(nc, K, (Win[:], w["L3a_Win"]), (cw[:], w["L3a_cw"]), (cb[:], w["L3a_cb"]), (Wout[:], w["L3a_Wout"]))
            steps = [(m, j) for m in range(L3A_M) for j in range(NB)]
            with phase(nc, K.sems, "padded done gated h_done conv_done silu_done") as (block, s):
                @block.gpsimd
                def _(pool):
                    pool.memset(H[:, :, :, 0:TAPS - 1], 0.0).then_inc(s["padded"], 1)

                @block.tensor
                def _(pe):
                    for n, (m, j) in enumerate(steps):
                        if n >= 4:
                            pe.wait_ge(s["h_done"], n - 3)
                        for part in range(2):
                            for k in range(DC):
                                col = (part * L3A_M + m) * P
                                last = pe.matmul(K.bank[2 * (n % 4) + part][:], Win[:, k, col:col + P], K.XT[K.cur][:, k, j * BLK:(j + 1) * BLK],
                                                 start=(k == 0), stop=(k == DC - 1))
                        last.then_inc(s["done"], 1)

                @block.scalar
                def _(act):
                    for n in range(len(steps)):
                        act.wait_ge(s["done"], n + 1)
                        if n >= 2:
                            act.wait_ge(s["h_done"], n - 1)
                        act.activation(sg[:, n % 2, :], K.bank[2 * (n % 4) + 1][:], ACT.Sigmoid).then_inc(s["gated"], 1)
                    for n, (m, j) in enumerate(steps):
                        act.wait_ge(s["conv_done"], n + 1)
                        act.activation(Y[:, m, j * BLK:(j + 1) * BLK], acc[:, n % 2, :], ACT.Silu).then_inc(s["silu_done"], 1)

                @block.vector
                def _(dve):
                    for n, (m, j) in enumerate(steps):
                        dve.wait_ge(s["gated"], n + 1)
                        b, o = divmod(j * BLK, S)
                        dve.tensor_tensor(H[:, m, b, TAPS - 1 + o:TAPS - 1 + o + BLK], K.bank[2 * (n % 4)][:], sg[:, n % 2, :],
                                          ALU.mult).then_inc(s["h_done"], 1)
                    dve.wait_ge(s["padded"], 1)
                    dve.drain()
                    for n, (m, j) in enumerate(steps):
                        b, o = divmod(j * BLK, S)
                        if n >= 2:
                            dve.wait_ge(s["silu_done"], n - 1)
                        dve.tensor_scalar(acc[:, n % 2, :], H[:, m, b, o:o + BLK], cw[:, m, 0:1], cb[:, m:m + 1], ALU.mult, ALU.add)
                        for tap in range(1, TAPS):
                            dve.drain()
                            ins = dve.scalar_tensor_tensor(out=acc[:, n % 2, :], in0=H[:, m, b, o + tap:o + tap + BLK], scalar=cw[:, m, tap:tap + 1],
                                                           in1=acc[:, n % 2, :], op0=ALU.mult, op1=ALU.add)
                        ins.then_inc(s["conv_done"], 1)
        finish(nc, K, lambda k, h, j: Wout[:, k, h * P:(h + 1) * P], block_of(Y), L3A_M)


EXPERTS = 8
INTER = 1024
IC = INTER // P


def L3_ffn_layout(i):
    W1, W2 = np.asarray(i["L3_ffn_W1"]), np.asarray(i["L3_ffn_W2"])
    b1 = np.asarray(i["L3_ffn_b1"]).reshape(EXPERTS, IC, P).transpose(0, 2, 1)
    return {"L3f_Wg": rows(np.asarray(i["L3_ffn_Wg"]).T), "L3f_W1": np.stack([rows(a) for a in W1]), "L3f_W2": np.stack([rows(a) for a in W2]),
            "L3f_b1": np.ascontiguousarray(b1), "L3f_b2": np.asarray(i["L3_ffn_b2"])}


def number_experts(nc, K, es, dst, n):
    ints = sbuf(es, nc, "ints", [P, n], I32)
    with phase(nc, K.sems, "counted") as (block, s):
        @block.gpsimd
        def _(pool):
            pool.iota(ints[:], pattern=[[1, n]], base=0, channel_multiplier=0).then_inc(s["counted"], 1)

        @block.vector
        def _(dve):
            dve.wait_ge(s["counted"], 1)
            dve.tensor_copy(dst, ints[:])


def L3_ffn(nc, K, w):
    xT = K.XT[K.cur]
    with ExitStack() as es:
        Wg = sbuf(es, nc, "Wg", [P, DC, EXPERTS])
        b2 = sbuf(es, nc, "b2", [EXPERTS, D])
        num = sbuf(es, nc, "expert_number", [P, EXPERTS])
        gates = sbuf(es, nc, "gates", [P, EXPERTS, NT])
        acc = sbuf(es, nc, "acc", [P, NT, D])
        W1 = [sbuf(es, nc, f"W1_{q}", [P, DC, INTER]) for q in range(2)]
        W2 = [sbuf(es, nc, f"W2_{q}", [P, IC, D]) for q in range(2)]
        b1 = [sbuf(es, nc, f"b1_{q}", [P, IC]) for q in range(2)]
        hT = sbuf(es, nc, "hiddenT", [P, 2, IC, BLK])
        load(nc, K, (Wg[:], w["L3f_Wg"]), (b2[:], w["L3f_b2"]))
        number_experts(nc, K, es, num[:], EXPERTS)

        with ExitStack() as inside, phase(nc, K.sems, "scored ready exp_done gates_done turned turned_out bias_done bias_out") as (block, s):
            L = sbuf(inside, nc, "logits", [P, NT, EXPERTS])
            top = sbuf(inside, nc, "top", [P, NT, 8])
            at = sbuf(inside, nc, "top_index", [P, NT, 8], U32)
            atf = sbuf(inside, nc, "top_index_f", [P, NT, 8])
            ew = sbuf(inside, nc, "weights", [P, 4, NT])
            one = sbuf(inside, nc, "one_hot", [P, 2, NT, EXPERTS])
            gT = sbuf(inside, nc, "gatesT", [EXPERTS, 2, P])

            @block.tensor
            def _(pe):
                for t in range(NT):
                    for k in range(DC):
                        ins = pe.matmul(K.bank[0][:, t * EXPERTS:(t + 1) * EXPERTS], xT[:, k, t * P:(t + 1) * P], Wg[:, k, :], start=(k == 0), stop=(k == DC - 1))
                ins.then_inc(s["scored"], 1)
                pe.wait_ge(s["gates_done"], 1)
                for t in range(NT):
                    if t >= 2:
                        pe.wait_ge(s["turned_out"], t - 1)
                    pe.transpose(K.bank[1 + t % 2][0:EXPERTS, 0:P], one[:, 0, t, :], K.ident[:]).then_inc(s["turned"], 1)
                    if t >= 2:
                        pe.wait_ge(s["bias_out"], t - 1)
                    pe.wait_ge(s["turned_out"], t + 1)
                    pe.matmul(K.bank[3 + t % 2][:, 0:D], gT[:, t % 2, :], b2[:], start=True, stop=True).then_inc(s["bias_done"], 1)

            @block.scalar
            def _(act):
                act.wait_ge(s["ready"], 1)
                act.activation(ew[:, 1, :], ew[:, 0, :], ACT.Exp).then_inc(s["exp_done"], 1)
                for t in range(NT):
                    act.wait_ge(s["turned"], t + 1)
                    if t >= 2:
                        act.wait_ge(s["bias_done"], t - 1)
                    act.activation(gT[:, t % 2, :], K.bank[1 + t % 2][0:EXPERTS, 0:P], ACT.Copy).then_inc(s["turned_out"], 1)

            @block.vector
            def _(dve):
                dve.wait_ge(s["scored"], 1)
                dve.tensor_copy(L[:], K.bank[0][:, 0:NT * EXPERTS].rearrange("p (t e) -> p t e", e=EXPERTS))
                dve.drain()
                for t in range(NT):
                    dve.max(top[:, t, :], L[:, t, :])
                dve.drain()
                for t in range(NT):
                    dve.max_index(at[:, t, :], top[:, t, :], L[:, t, :])
                dve.tensor_tensor(ew[:, 0, :], top[:, :, 1], top[:, :, 0], ALU.subtract).then_inc(s["ready"], 1)
                dve.drain()
                dve.tensor_copy(atf[:], at[:])
                dve.drain()
                dve.wait_ge(s["exp_done"], 1)
                dve.tensor_scalar(ew[:, 2, :], ew[:, 1, :], 1.0, None, ALU.add)
                dve.drain()
                dve.reciprocal(ew[:, 2, :], ew[:, 2, :])
                dve.drain()
                dve.tensor_tensor(ew[:, 3, :], ew[:, 1, :], ew[:, 2, :], ALU.mult)
                for i in range(2):
                    dve.tensor_tensor(one[:, i], middle(num[:], NT), inner(atf[:, :, i], EXPERTS), ALU.is_equal)
                dve.drain()
                for i in range(2):
                    dve.tensor_tensor(one[:, i], one[:, i], inner(ew[:, 2 + i, :], EXPERTS), ALU.mult)
                dve.drain()
                dve.tensor_tensor(one[:, 0], one[:, 0], one[:, 1], ALU.add)
                dve.drain()
                dve.tensor_copy(gates[:].rearrange("p e t -> p t e"), one[:, 0]).then_inc(s["gates_done"], 1)
                for t in range(NT):
                    dve.wait_ge(s["bias_done"], t + 1)
                    dve.tensor_tensor(acc[:, t, :], K.bank[3 + t % 2][:, 0:D], K.Xtok[:, t, :], ALU.add).then_inc(s["bias_out"], 1)

        with phase(nc, K.sems, "w_loaded0 w_loaded1 up_done gelu_done down_done acc_done") as (block, s):
            w_loaded = [s["w_loaded0"], s["w_loaded1"]]
            PAIR = 2 * NB * IC

            @block.sync
            def _(sp):
                for q in range(2):
                    sp.dma_start(W1[q][:], w["L3f_W1"][q]).then_inc(w_loaded[q], 16)
                    sp.dma_start(W2[q][:], w["L3f_W2"][q]).then_inc(w_loaded[q], 16)
                    sp.dma_start(b1[q][:], w["L3f_b1"][q]).then_inc(w_loaded[q], 16)
                with sp.Fori(0, EXPERTS // 2 - 1) as i:
                    for q in range(2):
                        sp.wait_ge(s["down_done"], i * (2 * NB) + NB * (q + 1) + 2)
                        sp.dma_start(W1[q][:], w["L3f_W1"][bass.ds(i * 2 + 2 + q, 1)].rearrange("e p c n -> p (e c) n")).then_inc(w_loaded[q], 16)
                        sp.dma_start(W2[q][:], w["L3f_W2"][bass.ds(i * 2 + 2 + q, 1)].rearrange("e p c n -> p (e c) n")).then_inc(w_loaded[q], 16)
                        sp.dma_start(b1[q][:], w["L3f_b1"][bass.ds(i * 2 + 2 + q, 1)].rearrange("e p c -> p (e c)")).then_inc(w_loaded[q], 16)

            @block.tensor
            def _(pe):
                pe.sem_inc(s["down_done"], 2)
                with pe.Fori(0, EXPERTS // 2) as i:
                    for q in range(2):
                        pe.wait_ge(w_loaded[q], i * 48 + 48)
                        for j in range(NB):
                            n0 = (q * NB + j) * IC
                            for m in range(IC):
                                pe.wait_ge(s["gelu_done"], i * PAIR + n0 + m + 1)
                                for k in range(DC):
                                    ins = pe.matmul(K.bank[m % 4][:], W1[q][:, k, m * P:(m + 1) * P], xT[:, k, j * BLK:(j + 1) * BLK],
                                                    start=(k == 0), stop=(k == DC - 1))
                                ins.then_inc(s["up_done"], 1)
                            pe.wait_ge(s["acc_done"], i * (2 * NB * TPB) + (q * NB + j) * TPB + TPB)
                            for m in range(IC):
                                pe.wait_ge(s["gelu_done"], i * PAIR + n0 + m + 1 + 4)
                                for t in range(TPB):
                                    ins = pe.matmul(K.bank[4 + t][:, 0:D], hT[:, j % 2, m, t * P:(t + 1) * P], W2[q][:, m, :],
                                                    start=(m == 0), stop=(m == IC - 1))
                            ins.then_inc(s["down_done"], 1)

            @block.scalar
            def _(act):
                act.sem_inc(s["gelu_done"], 4)
                with act.Fori(0, EXPERTS // 2) as i:
                    for q in range(2):
                        act.wait_ge(w_loaded[q], i * 48 + 48)
                        for j in range(NB):
                            act.wait_ge(s["down_done"], i * (2 * NB) + q * NB + j + 1)
                            for m in range(IC):
                                act.wait_ge(s["up_done"], i * PAIR + (q * NB + j) * IC + m + 1)
                                act.activation(hT[:, j % 2, m, :], K.bank[m % 4][:], ACT.Gelu,
                                               bias=b1[q][:, m:m + 1]).then_inc(s["gelu_done"], 1)

            @block.vector
            def _(dve):
                dve.sem_inc(s["acc_done"], TPB)
                with dve.Fori(0, EXPERTS // 2) as i:
                    for q in range(2):
                        for j in range(NB):
                            dve.wait_ge(s["down_done"], i * (2 * NB) + q * NB + j + 1 + 2)
                            for t in range(TPB):
                                tile = j * TPB + t
                                dve.scalar_tensor_tensor(out=acc[:, tile, :], in0=K.bank[4 + t][:, 0:D],
                                                         scalar=gates[:].rearrange("p e t -> p (e t)")[:, bass.ds(i * (2 * NT) + q * NT + tile, 1)],
                                                         in1=acc[:, tile, :], op0=ALU.mult, op1=ALU.add).then_inc(s["acc_done"], 1)
        finish_tokens(nc, K, acc, last=True)


INNER = 1024
ROUND = 1.5 * 2.0 ** 23
QCLIP = 1e-5


def L1_ffn_layout(i):
    return {"L1f_Wg": rows(np.asarray(i["L1_ffn_w_gate"]).T), "L1f_Wu": rows(np.asarray(i["L1_ffn_w_up"]).T),
            "L1f_Wd": rows(np.asarray(i["L1_ffn_w_down"]).T)}


def L1_ffn(nc, K, w):
    xT = K.XT[K.cur]
    n_w = INNER * D
    with ExitStack() as es:
        r = sbuf(es, nc, "sum", [P, NT, D])
        Wq = [sbuf(es, nc, f"W{n}_int", [P, n_w // P], BF16) for n in "gud"]
        wsc = sbuf(es, nc, "w_scale", [P, 3, 3])
        xsc = sbuf(es, nc, "x_scale", [P, NT, 4])
        with ExitStack() as inside:
            W = [sbuf(inside, nc, f"W{n}", [P, n_w // P]) for n in "gud"]
            junk = sbuf(inside, nc, "junk", [P, n_w // P])
            with phase(nc, K.sems, "loaded summed total clipped recip stepped") as (block, s):
                @block.sync
                def _(sp):
                    for i, n in enumerate(("L1f_Wg", "L1f_Wu", "L1f_Wd")):
                        sp.dma_start(W[i][:], w[n].rearrange("p c n -> p (c n)")).then_inc(s["loaded"], 16)

                @block.scalar
                def _(act):
                    act.wait_ge(s["loaded"], 48)
                    for i in range(3):
                        act.activation(junk[:], W[i][:], ACT.Abs, accum_out=wsc[:, i, 0:1]).then_inc(s["summed"], 1)
                        act.drain()

                @block.tensor
                def _(pe):
                    pe.wait_ge(s["summed"], 3)
                    pe.matmul(K.bank[0][:, 0:3], K.ones[:, 0:P], wsc[:, :, 0], start=True, stop=True).then_inc(s["total"], 1)

                @block.vector
                def _(dve):
                    dve.wait_ge(s["total"], 1)
                    dve.tensor_scalar(wsc[:, :, 1], K.bank[0][:, 0:3], 1.0 / n_w, QCLIP, ALU.mult, ALU.max)
                    dve.drain()
                    dve.reciprocal(wsc[:, :, 2], wsc[:, :, 1])
                    dve.drain()
                    for i in range(3):
                        dve.tensor_scalar(W[i][:], W[i][:], wsc[:, i, 2:3], 1.0, ALU.mult, ALU.min)
                        dve.drain()
                        dve.tensor_scalar(W[i][:], W[i][:], -1.0, ROUND, ALU.max, ALU.add).then_inc(s["stepped"], 1)

                @block.gpsimd
                def _(pool):
                    for i in range(3):
                        pool.wait_ge(s["stepped"], i + 1)
                        pool.tensor_scalar(Wq[i][:], W[i][:], ROUND, None, ALU.subtract)
        Wg, Wu = (Wq[i][:].rearrange("p (c n) -> p c n", c=DC) for i in range(2))
        Wd = Wq[2][:].rearrange("p (c n) -> p c n", n=D)
        XqT = sbuf(es, nc, "XqT", [P, DC, TOK], BF16)

        def quantise(dve, src, tmp, out, sc):
            dve.tensor_reduce(sc[:, 0:1], src, AX, ALU.max, apply_absolute_value=True)
            dve.drain()
            dve.tensor_scalar(sc[:, 0:1], sc[:, 0:1], QCLIP, None, ALU.max)
            dve.drain()
            dve.reciprocal(sc[:, 1:2], sc[:, 0:1])
            dve.tensor_scalar(sc[:, 2:3], sc[:, 0:1], 1.0 / 127.0, None, ALU.mult)
            dve.drain()
            dve.tensor_scalar(sc[:, 1:2], sc[:, 1:2], 127.0, None, ALU.mult)
            dve.drain()
            dve.tensor_scalar(tmp, src, sc[:, 1:2], ROUND, ALU.mult, ALU.add)
            dve.drain()
            return dve.tensor_scalar(out, tmp, ROUND, 127.0, ALU.subtract, ALU.min)

        with ExitStack() as inside, phase(nc, K.sems, "quantised turned out") as (block, s):
            tmp = sbuf(inside, nc, "tmp", [P, D])
            xq = sbuf(inside, nc, "xq", [P, 2, D], BF16)

            @block.vector
            def _(dve):
                for t in range(NT):
                    if t >= 2:
                        dve.wait_ge(s["turned"], t - 1)
                    quantise(dve, K.Xtok[:, t, :], tmp[:], xq[:, t % 2, :], xsc[:, t, :]).then_inc(s["quantised"], 1)
                    dve.drain()

            @block.tensor
            def _(pe):
                for t in range(NT):
                    pe.wait_ge(s["quantised"], t + 1)
                    if t >= 4:
                        pe.wait_ge(s["out"], t - 3)
                    for h in range(DC):
                        ins = pe.transpose(K.bank[t % 4][:].bitcast(BF16)[:, h * P:(h + 1) * P], xq[:, t % 2, h * P:(h + 1) * P], K.identb[:])
                    ins.then_inc(s["turned"], 1)

            @block.scalar
            def _(act):
                for t in range(NT):
                    act.wait_ge(s["turned"], t + 1)
                    act.activation(XqT[:, :, t * P:(t + 1) * P], K.bank[t % 4][:].bitcast(BF16)[:, 0:D].rearrange("p (c k) -> p c k", c=2),
                                   ACT.Copy).then_inc(s["out"], 1)
        names = "scaled inner_done silu_done h_done hq_done turned turned_out down_done sum_done"
        with phase(nc, K.sems, names) as (block, s):
            hsc = sbuf(es, nc, "h_scale", [P, 2, 4])
            G = sbuf(es, nc, "gate", [P, 2, INNER])
            H = sbuf(es, nc, "h", [P, INNER])
            Hq = sbuf(es, nc, "hq", [P, 2, INNER], BF16)
            HqT = sbuf(es, nc, "hqT", [P, 2, INNER // P, P], BF16)
            wscale = sbuf(es, nc, "both_scales", [P, NT, 2])

            @block.tensor
            def _(pe):
                def inner_product(t):
                    if t >= 1:
                        pe.wait_ge(s["h_done"], t)
                    for part, W_ in enumerate((Wg, Wu)):
                        for c in range(2):
                            for k in range(DC):
                                ins = pe.matmul(K.bank[2 * part + c][:], XqT[:, k, t * P:(t + 1) * P], W_[:, k, c * BLK:(c + 1) * BLK],
                                                start=(k == 0), stop=(k == DC - 1))
                    ins.then_inc(s["inner_done"], 1)

                inner_product(0)
                for t in range(NT):
                    if t + 1 < NT:
                        inner_product(t + 1)
                    pe.wait_ge(s["hq_done"], t + 1)
                    if t >= 2:
                        pe.wait_ge(s["turned_out"], t - 1)
                    for m in range(INNER // P):
                        ins = pe.transpose(K.bank[4 + t % 2][:].bitcast(BF16)[:, m * P:(m + 1) * P], Hq[:, t % 2, m * P:(m + 1) * P], K.identb[:])
                    ins.then_inc(s["turned"], 1)
                    pe.wait_ge(s["turned_out"], t + 1)
                    if t >= 2:
                        pe.wait_ge(s["sum_done"], t - 1)
                    for m in range(INNER // P):
                        ins = pe.matmul(K.bank[6 + t % 2][:, 0:D], HqT[:, t % 2, m, :], Wd[:, m, :], start=(m == 0), stop=(m == INNER // P - 1))
                    ins.then_inc(s["down_done"], 1)

            @block.scalar
            def _(act):
                act.wait_ge(s["scaled"], 1)
                for t in range(NT + 1):
                    if t < NT:
                        act.wait_ge(s["inner_done"], t + 1)
                        if t >= 2:
                            act.wait_ge(s["h_done"], t - 1)
                        for c in range(2):
                            ins = act.activation(G[:, t % 2, c * BLK:(c + 1) * BLK], K.bank[c][:], ACT.Silu, scale=wscale[:, t, 0:1])
                        ins.then_inc(s["silu_done"], 1)
                    if t > 0:
                        act.wait_ge(s["turned"], t)
                        if t >= 3:
                            act.wait_ge(s["down_done"], t - 2)
                        act.activation(HqT[:, (t - 1) % 2].rearrange("p m k -> p (m k)"), K.bank[4 + (t - 1) % 2][:].bitcast(BF16)[:, 0:INNER],
                                       ACT.Copy).then_inc(s["turned_out"], 1)

            @block.vector
            def _(dve):
                for i in range(2):
                    dve.tensor_scalar(wscale[:, :, i], xsc[:, :, 2], wsc[:, i, 1:2], None, ALU.mult)
                dve.drain()
                dve.sem_inc(s["scaled"], 1)

                def total(t):
                    dve.wait_ge(s["down_done"], t + 1)
                    dve.scalar_tensor_tensor(out=r[:, t, :], in0=K.bank[6 + t % 2][:, 0:D], scalar=hsc[:, t % 2, 3:4], in1=K.Xtok[:, t, :],
                                             op0=ALU.mult, op1=ALU.add).then_inc(s["sum_done"], 1)

                for t in range(NT):
                    dve.wait_ge(s["silu_done"], t + 1)
                    for c in range(2):
                        ins = dve.scalar_tensor_tensor(out=H[:, c * BLK:(c + 1) * BLK], in0=K.bank[2 + c][:], scalar=wscale[:, t, 1:2],
                                                       in1=G[:, t % 2, c * BLK:(c + 1) * BLK], op0=ALU.mult, op1=ALU.mult)
                    ins.then_inc(s["h_done"], 1)
                    dve.drain()
                    if t >= 2:
                        dve.wait_ge(s["turned"], t - 1)
                    quantise(dve, H[:], H[:], Hq[:, t % 2, :], hsc[:, t % 2, :]).then_inc(s["hq_done"], 1)
                    dve.tensor_scalar(hsc[:, t % 2, 3:4], hsc[:, t % 2, 2:3], wsc[:, 2, 1:2], None, ALU.mult)
                    dve.drain()
                    if t >= 1:
                        total(t - 1)
                total(NT - 1)
        finish_tokens(nc, K, r)


def L2_attn_layout(i):
    W = np.asarray(i["L2_attn_W_qkv"]).T
    return {"L2a_W": rows(W), "L2a_Wo": rows(np.asarray(i["L2_attn_W_out"]).T)}


def L2_attn(nc, K, w):
    xT = K.XT[K.cur]
    NQ = 2 * DC
    with ExitStack() as es:
        Wo = sbuf(es, nc, "Wo", [P, DC, D])
        OT = sbuf(es, nc, "OT", [P, DC, TOK])
        with ExitStack() as inside:
            W = sbuf(inside, nc, "Wqkv", [P, DC, 3 * D])
            QT, KT, RT = (sbuf(inside, nc, n, [P, DC, TOK]) for n in ("QT", "KT", "recip_den"))
            same = sbuf(inside, nc, "same_head", [P, P])
            load(nc, K, (W[:], w["L2a_W"]), (Wo[:], w["L2a_Wo"]))
            with ExitStack() as inn, phase(nc, K.sems, "done min_done exp_done out") as (block, s):
                low = sbuf(inn, nc, "low", [P, 2, BLK])
                steps = [(m, j) for m in range(NQ) for j in range(NB)]

                @block.tensor
                def _(pe):
                    for n, (m, j) in enumerate(steps):
                        if n >= 8:
                            pe.wait_ge(s["out"], n - 7)
                        for k in range(DC):
                            ins = pe.matmul(K.bank[n % 8][:], W[:, k, m * P:(m + 1) * P], xT[:, k, j * BLK:(j + 1) * BLK], start=(k == 0), stop=(k == DC - 1))
                        ins.then_inc(s["done"], 1)

                @block.vector
                def _(dve):
                    dve.tensor_copy(same[:].rearrange("p (h d) -> p h d", d=HD), inner(K.head_rows[:], HD))
                    for n in range(len(steps) + 1):
                        if n < len(steps):
                            dve.wait_ge(s["done"], n + 1)
                            if n >= 2:
                                dve.drain()
                            dve.tensor_scalar(low[:, n % 2, :], K.bank[n % 8][:], 0.0, None, ALU.min).then_inc(s["min_done"], 1)
                        if n > 0:
                            m, j = steps[n - 1]
                            dve.wait_ge(s["exp_done"], n)
                            dst = (QT if m < DC else KT)[:, m % DC, j * BLK:(j + 1) * BLK]
                            dve.scalar_tensor_tensor(out=dst, in0=K.bank[(n - 1) % 8][:], scalar=0.0, in1=low[:, (n - 1) % 2, :],
                                                     op0=ALU.max, op1=ALU.add)
                            dve.drain()
                            if m < DC:
                                dve.tensor_scalar(dst, dst, float(HD) ** -0.5, None, ALU.mult).then_inc(s["out"], 1)
                            else:
                                dve.sem_inc(s["out"], 1)

                @block.scalar
                def _(act):
                    for n in range(len(steps)):
                        act.wait_ge(s["min_done"], n + 1)
                        act.activation(low[:, n % 2, :], low[:, n % 2, :], ACT.Exp).then_inc(s["exp_done"], 1)

            with ExitStack() as inn, phase(nc, K.sems, "prod_done den_done recip_done") as (block, s):
                run = sbuf(inn, nc, "running", [P, DC, TOK])
                none = sbuf(inn, nc, "zeros", [P, S])

                @block.vector
                def _(dve):
                    dve.memset(none[:], 0.0)
                    dve.drain()
                    for c in range(DC):
                        for b in range(B):
                            dve.tensor_tensor_scan(run[:, c, b * S:(b + 1) * S], KT[:, c, b * S:(b + 1) * S], none[:], 0.0, ALU.add, ALU.add)
                    dve.drain()
                    for c in range(DC):
                        for j in range(NB):
                            z = run[:, c, j * BLK:(j + 1) * BLK]
                            dve.tensor_tensor(z, z, QT[:, c, j * BLK:(j + 1) * BLK], ALU.mult).then_inc(s["prod_done"], 1)
                    for n in range(DC * NB):
                        c, j = divmod(n, NB)
                        z = RT[:, c, j * BLK:(j + 1) * BLK]
                        dve.wait_ge(s["den_done"], n + 1)
                        dve.tensor_scalar(z, K.bank[n][:], 1e-6, None, ALU.max)
                        dve.drain()
                        dve.reciprocal(z, z)

                @block.tensor
                def _(pe):
                    for n in range(DC * NB):
                        c, j = divmod(n, NB)
                        pe.wait_ge(s["prod_done"], n + 1)
                        pe.matmul(K.bank[n][:], same[:], run[:, c, j * BLK:(j + 1) * BLK], start=True, stop=True).then_inc(s["den_done"], 1)

            Qh = sbuf(inside, nc, "Q_heads", [P, HPC, P])
            Vh = sbuf(inside, nc, "V_heads", [P, 2, HPC, P])
            AT = sbuf(inside, nc, "attnT", [P, HPC, P])
            kv = sbuf(inside, nc, "k_v_tokens", [P, 2, 2 * P])
            St = sbuf(inside, nc, "state", [P, P])
            with phase(nc, K.sems, "q_spread kv_done kv_out v_spread attn_done attn_out state_out o_done out") as (block, s):
                steps = NT * DC

                @block.tensor
                def _(pe):
                    for n in range(steps):
                        t, c = divmod(n, DC)
                        ts = slice(t * P, (t + 1) * P)
                        if n >= 1:
                            pe.wait_ge(s["kv_out"], n)
                        for k in range(DC):
                            pe.matmul(K.bank[2][:, 0:P], xT[:, k, ts], W[:, k, 2 * D + c * P:2 * D + (c + 1) * P], start=(k == 0), stop=(k == DC - 1))
                        pe.transpose(K.bank[2][:, P:2 * P], KT[:, c, ts], K.ident[:]).then_inc(s["kv_done"], 1)
                        pe.wait_ge(s["q_spread"], n + 1)
                        if n >= 1:
                            pe.wait_ge(s["attn_out"], n)
                        for g in range(2):
                            ins = pe.matmul(K.bank[g][:], KT[:, c, ts], Qh[:, 4 * g:4 * g + 4, :], start=True, stop=True)
                        ins.then_inc(s["attn_done"], 1)
                        if n >= 1:
                            pe.wait_ge(s["out"], n)
                        first = t % 8 == 0
                        if not first:
                            pe.wait_ge(s["state_out"], n + 1)
                            pe.matmul(K.bank[3][:, 0:P], St[:], QT[:, c, ts], start=True, stop=False)
                        pe.wait_ge(s["v_spread"], n + 1)
                        pe.wait_ge(s["attn_out"], n + 1)
                        for h in range(HPC):
                            ins = pe.matmul(K.bank[3][:, 0:P], Vh[:, n % 2, h, :], AT[:, h, :], start=(first and h == 0), stop=(h == HPC - 1))
                        ins.then_inc(s["o_done"], 1)
                        pe.wait_ge(s["kv_out"], n + 1)
                        pe.wait_ge(s["state_out"], n + 1)
                        pe.matmul(K.bank[4 + 2 * (t // 8) + c][:, 0:P], kv[:, n % 2, P:2 * P], kv[:, n % 2, 0:P], start=first, stop=True,
                                  skip_group_check=True)

                @block.scalar
                def _(act):
                    for n in range(steps):
                        act.wait_ge(s["kv_done"], n + 1)
                        if n >= 2:
                            act.wait_ge(s["o_done"], n)
                        act.activation(kv[:, n % 2, :], K.bank[2][:, 0:2 * P], ACT.Copy).then_inc(s["kv_out"], 1)

                @block.gpsimd
                def _(pool):
                    for n in range(steps):
                        pool.wait_ge(s["kv_out"], n + 1)
                        if n >= 2:
                            pool.wait_ge(s["o_done"], n - 1)
                        pool.tensor_tensor(Vh[:, n % 2], middle(kv[:, n % 2, 0:P], HPC), K.head_cols[:], ALU.mult).then_inc(s["v_spread"], 1)

                @block.vector
                def _(dve):
                    for n in range(steps):
                        t, c = divmod(n, DC)
                        ts = slice(t * P, (t + 1) * P)
                        if n >= 1:
                            dve.wait_ge(s["attn_done"], n)
                        dve.tensor_tensor(Qh[:], middle(QT[:, c, ts], HPC), inner(K.head_rows[:], P), ALU.mult).then_inc(s["q_spread"], 1)
                        if n >= 1:
                            dve.wait_ge(s["o_done"], n)
                            tp, cp = divmod(n - 1, DC)
                            dve.tensor_tensor(OT[:, cp, tp * P:(tp + 1) * P], K.bank[3][:, 0:P], RT[:, cp, tp * P:(tp + 1) * P], ALU.mult).then_inc(s["out"], 1)
                        if t % 8 == 0:
                            dve.sem_inc(s["state_out"], 1)
                        else:
                            dve.wait_ge(s["kv_done"], n + 1)
                            dve.tensor_tensor(St[:], K.bank[4 + 2 * (t // 8) + c][:, 0:P], same[:], ALU.mult).then_inc(s["state_out"], 1)
                        dve.wait_ge(s["attn_done"], n + 1)
                        for g in range(2):
                            ins = dve.tensor_tensor(AT[:, 4 * g:4 * g + 4, :], K.bank[g][:].rearrange("p (h l) -> p h l", h=4), middle(K.causal_T[:], 4), ALU.mult)
                        ins.then_inc(s["attn_out"], 1)
                    dve.wait_ge(s["o_done"], steps)
                    dve.tensor_tensor(OT[:, DC - 1, TOK - P:TOK], K.bank[3][:, 0:P], RT[:, DC - 1, TOK - P:TOK], ALU.mult).then_inc(s["out"], 1)
        finish(nc, K, lambda k, h, j: Wo[:, k, h * P:(h + 1) * P], block_of(OT), DC)


def block_mean(nc, K, out, size):
    with phase(nc, K.sems, "step") as (block, s):
        @block.gpsimd
        def _(pool):
            n = P // size
            pool.memset(out, 1.0 / size).then_inc(s["step"], 1)
            v = out.rearrange("p (n j) -> p n j", n=n)
            pool.wait_ge(s["step"], 1)
            pool.affine_select(out=v, in_=v, compare_op=ALU.is_ge, fill=0.0, base=0, pattern=[[-size, n], [0, size]], channel_multiplier=1).then_inc(s["step"], 1)
            pool.wait_ge(s["step"], 2)
            pool.affine_select(out=v, in_=v, compare_op=ALU.is_ge, fill=0.0, base=size - 1, pattern=[[size, n], [0, size]], channel_multiplier=-1)


def feature_ln(nc, K, J, n, halves_, src, dst, g, b):
    with ExitStack() as es, phase(nc, K.sems, "mean_done centred squared var_done std_done normed out") as (block, s):
        sq = sbuf(es, nc, "squares", [P, 2, halves_, BLK])
        std = sbuf(es, nc, "std", [P, 2, BLK])
        xc = sbuf(es, nc, "centred", [P, 2, halves_, BLK])

        @block.tensor
        def _(pe):
            def mean(j):
                if j >= 2:
                    pe.wait_ge(s["centred"], j - 1)
                for h in range(halves_):
                    ins = pe.matmul(K.bank[j % 2][:], J, src(j, h), start=(h == 0), stop=(h == halves_ - 1))
                ins.then_inc(s["mean_done"], 1)
            mean(0)
            for j in range(n):
                if j + 1 < n:
                    mean(j + 1)
                pe.wait_ge(s["squared"], j + 1)
                if j >= 2:
                    pe.wait_ge(s["std_done"], j - 1)
                for h in range(halves_):
                    ins = pe.matmul(K.bank[2 + j % 2][:], J, sq[:, j % 2, h, :], start=(h == 0), stop=(h == halves_ - 1))
                ins.then_inc(s["var_done"], 1)

        @block.vector
        def _(dve):
            def centre(j):
                dve.wait_ge(s["mean_done"], j + 1)
                if j >= 2:
                    dve.wait_ge(s["out"], j - 1)
                for h in range(halves_):
                    ins = dve.tensor_tensor(xc[:, j % 2, h, :], src(j, h), K.bank[j % 2][:], ALU.subtract)
                ins.then_inc(s["centred"], 1)
            centre(0)
            for j in range(n):
                if j + 1 < n:
                    centre(j + 1)
                dve.wait_ge(s["std_done"], j + 1)
                dve.reciprocal(std[:, j % 2, :], std[:, j % 2, :])
                dve.drain()
                for h in range(halves_):
                    ins = dve.tensor_tensor(xc[:, j % 2, h, :], xc[:, j % 2, h, :], std[:, j % 2, :], ALU.mult)
                ins.then_inc(s["normed"], 1)

        @block.scalar
        def _(act):
            def square(j):
                act.wait_ge(s["centred"], j + 1)
                if j >= 2:
                    act.wait_ge(s["var_done"], j - 1)
                for h in range(halves_):
                    ins = act.activation(sq[:, j % 2, h, :], xc[:, j % 2, h, :], ACT.Square)
                ins.then_inc(s["squared"], 1)
            square(0)
            for j in range(n):
                if j + 1 < n:
                    square(j + 1)
                act.wait_ge(s["var_done"], j + 1)
                if j >= 2:
                    act.wait_ge(s["normed"], j - 1)
                act.activation(std[:, j % 2, :], K.bank[2 + j % 2][:], ACT.Sqrt, bias=K.eps[:, 0:1]).then_inc(s["std_done"], 1)
                act.wait_ge(s["normed"], j + 1)
                for h in range(halves_):
                    ins = act.activation(dst(j, h), xc[:, j % 2, h, :], ACT.Identity, scale=g(j)[:, h:h + 1], bias=b(j)[:, h:h + 1])
                ins.then_inc(s["out"], 1)


LAT = D // 4


def L1_attn_layout(i):
    g = lambda n: np.asarray(i["L1_attn_" + n])
    uq = pad(g("W_uq"), 0, P)
    ukv = np.concatenate([np.zeros((LAT, 2 * D), np.float32), g("W_ukv")])
    return {"L1a_Wd": rows(np.concatenate([g("W_dq"), g("W_dkv")], axis=1)), "L1a_uq": uq, "L1a_ukv": ukv,
            "L1a_g": np.concatenate([g("q_ln_g"), g("kv_ln_g")]).reshape(P, 1), "L1a_b": np.concatenate([g("q_ln_b"), g("kv_ln_b")]).reshape(P, 1),
            "L1a_Wo": rows(g("W_o").T)}


def L1_attn(nc, K, w):
    xT = K.XT[K.cur]
    QT_ = S // P
    with ExitStack() as es:
        Wo = sbuf(es, nc, "Wo", [P, DC, D])
        OT = sbuf(es, nc, "OT", [P, DC * TOK])
        with ExitStack() as inside:
            QT, KT = (sbuf(inside, nc, n, [P, DC * TOK]) for n in ("QT", "KT"))
            V = sbuf(inside, nc, "V", [P, DC, NT, P])
            with ExitStack() as inn:
                Wd = sbuf(inn, nc, "Wd", [P, DC, P])
                uq = sbuf(inn, nc, "uq", [P, D])
                ukv = sbuf(inn, nc, "ukv", [P, 2 * D])
                g, b = (sbuf(inn, nc, n, [P, 1]) for n in ("g", "b"))
                cT = sbuf(inn, nc, "latents", [P, TOK])
                J = sbuf(inn, nc, "J", [P, P])
                load(nc, K, (Wd[:], w["L1a_Wd"]), (uq[:], w["L1a_uq"]), (ukv[:], w["L1a_ukv"]), (g[:], w["L1a_g"]), (b[:], w["L1a_b"]), (Wo[:], w["L1a_Wo"]))
                block_mean(nc, K, J[:], LAT)
                cb = lambda j: cT[:, j * BLK:(j + 1) * BLK]
                project(nc, K, inn, 1, DC, lambda k, m: Wd[:, k, :], block_of(xT), *copy_to(lambda m, j: cb(j)))
                feature_ln(nc, K, J[:], NB, 1, lambda j, h: cb(j), lambda j, h: cb(j), lambda j: g[:], lambda j: b[:])
                for dst, W in ((QT, uq), (KT, ukv)):
                    project(nc, K, inn, DC, 1, lambda k, m: W[:, m * P:(m + 1) * P], lambda k, j: cb(j),
                            *copy_to(lambda m, j: dst[:, m * TOK + j * BLK:m * TOK + (j + 1) * BLK]))
                with phase(nc, K.sems, "done out") as (block, s):
                    @block.tensor
                    def _(pe):
                        for t in range(NT):
                            if t >= 8:
                                pe.wait_ge(s["out"], t - 7)
                            pe.matmul(K.bank[t % 8][:, 0:D], cT[:, t * P:(t + 1) * P], ukv[:, D:2 * D], start=True, stop=True).then_inc(s["done"], 1)

                    @block.vector
                    def _(dve):
                        for t in range(NT):
                            dve.wait_ge(s["done"], t + 1)
                            dve.tensor_copy(V[:, :, t, :], K.bank[t % 8][:, 0:D].rearrange("p (c k) -> p c k", c=DC)).then_inc(s["out"], 1)

            Vh = sbuf(inside, nc, "V_heads", [P, QT_, HPC, P])
            Qh = sbuf(inside, nc, "Q_heads", [P, 2, HPC, P])
            Sc = sbuf(inside, nc, "scores", [P, 2, S])
            zero = sbuf(inside, nc, "zero_marks", [P, S])
            PT = sbuf(inside, nc, "probsT", [P, 2, S])
            mx = sbuf(inside, nc, "max", [P, 2])
            sums = sbuf(inside, nc, "sums", [P, 2, HPC])
            rec = sbuf(inside, nc, "recip", [P, HPC])
            Rx, RT = (sbuf(inside, nc, n, [P, 2, P]) for n in ("recip_spread", "recipT"))
            scale = float(HD) ** -0.5
            N = QT_ * HPC
            names = "q_spread scored max_done exp_done turned pt_out v_spread r_spread pv_done o_done rt_out out"
            with phase(nc, K.sems, names) as (block, s):
                sc = lambda i: K.psum[:, 2 * (i % 2):2 * (i % 2) + 2, :].rearrange("p b k -> p (b k)")
                ob = lambda q: K.bank[6 + q % 2]

                def slot_free(eng, sem, u, per, i):
                    if i >= 2:
                        eng.wait_ge(sem, u * per + i - 1)

                def turn_over(eng, u, *pairs):
                    for sem, per in pairs:
                        eng.wait_ge(sem, u * per + per)

                @block.gpsimd
                def _(pool):
                    with pool.Fori(0, DC * B) as u:
                        for kt in range(QT_):
                            src = V[:].rearrange("p c t k -> p (c t k)")[:, bass.ds(u * (QT_ * P) + kt * P, P)]
                            pool.tensor_tensor(Vh[:, kt], middle(src, HPC), K.head_cols[:], ALU.mult).then_inc(s["v_spread"], 1)
                        turn_over(pool, u, (s["pv_done"], N))

                @block.tensor
                def _(pe):
                    with pe.Fori(0, DC * B) as u:
                        def score(i):
                            q, h = divmod(i, HPC)
                            if h == 0:
                                pe.wait_ge(s["q_spread"], u * QT_ + q + 1)
                            slot_free(pe, s["max_done"], u, N, i)
                            n = (q + 1) * P
                            for o in range(0, n, BLK):
                                e = min(n, o + BLK)
                                pe.matmul(sc(i)[:, o:e], Qh[:, q % 2, h, :], KT[:, bass.ds(u * S + o, e - o)], start=True, stop=(e < n),
                                          skip_group_check=True)
                            pe.matmul(sc(i)[:, n - P:n], K.identb[:], K.above[:], start=False, stop=True, skip_group_check=True).then_inc(s["scored"], 1)

                        def values(i):
                            q, h = divmod(i, HPC)
                            pe.wait_ge(s["pt_out"], u * N + i + 1)
                            if h == 0:
                                pe.wait_ge(s["v_spread"], u * QT_ + q + 1)
                                slot_free(pe, s["out"], u, QT_, q)
                            for kt in range(q + 1):
                                ins = pe.matmul(ob(q)[:, 0:P], Vh[:, kt, h, :], PT[:, i % 2, kt * P:(kt + 1) * P], start=(h == 0 and kt == 0),
                                                stop=(h == HPC - 1 and kt == q))
                            ins.then_inc(s["pv_done"], 1)
                            if h == HPC - 1:
                                pe.wait_ge(s["r_spread"], u * QT_ + q + 1)
                                pe.transpose(ob(q)[:, P:2 * P], Rx[:, q % 2, :], K.ident[:]).then_inc(s["o_done"], 1)

                        score(0)
                        for i in range(N):
                            if i + 1 < N:
                                score(i + 1)
                            pe.wait_ge(s["exp_done"], u * N + i + 1)
                            if i > 0:
                                pe.wait_ge(s["pt_out"], u * N + i)
                            for kt in range(i // HPC + 1):
                                ins = pe.transpose(K.bank[4 + kt // 4][:, (kt % 4) * P:(kt % 4 + 1) * P], Sc[:, i % 2, kt * P:(kt + 1) * P], K.ident[:])
                            ins.then_inc(s["turned"], 1)
                            if i > 0:
                                values(i - 1)
                        values(N - 1)
                        turn_over(pe, u, (s["max_done"], N), (s["out"], QT_))

                @block.vector
                def _(dve):
                    with dve.Fori(0, DC * B) as u:
                        def spread(q):
                            if q >= 2:
                                dve.wait_ge(s["scored"], u * N + (q - 1) * HPC)
                            dve.tensor_tensor(Qh[:, q % 2], middle(QT[:, bass.ds(u * S + q * P, P)], HPC), inner(K.head_rows[:], P), ALU.mult).then_inc(s["q_spread"], 1)

                        def output(q):
                            dve.wait_ge(s["rt_out"], u * QT_ + q + 1)
                            dve.tensor_tensor(OT[:, bass.ds(u * S + q * P, P)], ob(q)[:, 0:P], RT[:, q % 2, :], ALU.mult).then_inc(s["out"], 1)

                        def recip(q):
                            dve.wait_ge(s["exp_done"], u * N + (q + 1) * HPC)
                            slot_free(dve, s["o_done"], u, QT_, q)
                            dve.reciprocal(rec[:], sums[:, q % 2, :])
                            dve.drain()
                            dve.tensor_copy(Rx[:, q % 2, :].rearrange("p (h d) -> p h d", h=HPC), inner(rec[:], HD)).then_inc(s["r_spread"], 1)

                        spread(0)
                        for i in range(N):
                            q, h = divmod(i, HPC)
                            n = (q + 1) * P
                            if h == 2 and q + 1 < QT_:
                                spread(q + 1)
                            slot_free(dve, s["turned"], u, N, i)
                            dve.wait_ge(s["scored"], u * N + i + 1)
                            dve.tensor_scalar(zero[:, 0:n], sc(i)[:, 0:n], 0.0, NEG, ALU.is_equal, ALU.mult)
                            dve.drain()
                            dve.tensor_tensor_reduce(Sc[:, i % 2, 0:n], sc(i)[:, 0:n], zero[:, 0:n], 1.0, NEG, ALU.add, ALU.max, mx[:, i % 2:i % 2 + 1])
                            dve.drain()
                            dve.tensor_scalar(mx[:, i % 2:i % 2 + 1], mx[:, i % 2:i % 2 + 1], -scale, None, ALU.mult).then_inc(s["max_done"], 1)
                            if q > 0 and h == 0:
                                recip(q - 1)
                            if q > 0 and h == 2:
                                output(q - 1)
                        recip(QT_ - 1)
                        output(QT_ - 1)
                        turn_over(dve, u, (s["turned"], N), (s["o_done"], QT_))

                @block.scalar
                def _(act):
                    with act.Fori(0, DC * B) as u:
                        def exp(i):
                            q, h = divmod(i, HPC)
                            act.wait_ge(s["max_done"], u * N + i + 1)
                            if h == 0:
                                slot_free(act, s["r_spread"], u, QT_, q)
                            p = Sc[:, i % 2, 0:(q + 1) * P]
                            act.activation(p, p, ACT.Exp, bias=mx[:, i % 2:i % 2 + 1], scale=scale, accum_out=sums[:, q % 2, h:h + 1]).then_inc(s["exp_done"], 1)

                        def turn_recip(q):
                            act.wait_ge(s["o_done"], u * QT_ + q + 1)
                            act.activation(RT[:, q % 2, :], ob(q)[:, P:2 * P], ACT.Copy).then_inc(s["rt_out"], 1)

                        exp(0)
                        for i in range(N):
                            q, h = divmod(i, HPC)
                            if i + 1 < N:
                                exp(i + 1)
                            n = (q + 1) * P
                            act.wait_ge(s["turned"], u * N + i + 1)
                            slot_free(act, s["pv_done"], u, N, i)
                            act.activation(PT[:, i % 2, 0:n], K.psum[:, 4:6, :].rearrange("p b k -> p (b k)")[:, 0:n], ACT.Copy).then_inc(s["pt_out"], 1)
                            if q > 0 and h == 0:
                                turn_recip(q - 1)
                        turn_recip(QT_ - 1)
                        turn_over(act, u, (s["r_spread"], QT_), (s["pv_done"], N))
        OTv = OT[:].rearrange("p (c t) -> p c t", c=DC)
        finish(nc, K, lambda k, h, j: Wo[:, k, h * P:(h + 1) * P], block_of(OTv), DC)


L0E = 8
PICKED = 512
PT4 = PICKED // P


def L0_ffn_layout(i):
    g = lambda n: np.asarray(i["L0_ffn_" + n])
    up = lambda a, sh: np.concatenate([rows(g(a)[e].T) for e in range(L0E)] + [rows(g(sh).T)], axis=2)
    vec = lambda a, sh: np.ascontiguousarray(np.concatenate([g(a), g(sh)[None]]).T)
    ln = lambda a, sh: np.stack([g(a), g(sh)], axis=1)
    return {"L0f_W1": up("ew1", "sw1"), "L0f_W2": up("ew2", "sw2"), "L0f_b1": vec("eb1", "sb1"), "L0f_b2": vec("eb2", "sb2"),
            "L0f_W3": np.concatenate([g("ew3").transpose(2, 0, 1).reshape(P, L0E * D), g("sw3").T], axis=1),
            "L0f_b3": np.concatenate([g("eb3"), g("sb3")[None]]), "L0f_sb3": cols(g("sb3")),
            "L0f_g": ln("sel_ln_g", "s_ln_g"), "L0f_b": ln("sel_ln_b", "s_ln_b"),
            "L0f_Wgate": rows(np.concatenate([g("eg_w"), g("sg_w")]).T), "L0f_bgate": np.concatenate([g("eg_b"), g("sg_b")]),
            "L0f_ebias": g("exp_bias"), "L0f_ib": cols(g("index_b")), "L0f_it": cols(g("index_t")),
            "L0f_ibr": g("index_b"), "L0f_itr": g("index_t")}


def turn_tokens(nc, K):
    xo = K.XT[K.cur]
    with phase(nc, K.sems, "turned act_out dve_out") as (block, s):
        @block.tensor
        def _(pe):
            for t in range(NT):
                if t >= 8:
                    pe.wait_ge(s["act_out"] if t % 2 == 0 else s["dve_out"], (t - 8) // 2 + 1)
                for h in range(DC):
                    ins = pe.transpose(K.bank[t % 8][:, h * P:(h + 1) * P], K.Xtok[:, t, h * P:(h + 1) * P], K.ident[:])
                ins.then_inc(s["turned"], 1)

        @block.scalar
        def _(act):
            for t in range(0, NT, 2):
                act.wait_ge(s["turned"], t + 1)
                act.activation(xo[:, :, t * P:(t + 1) * P], K.bank[t % 8][:, 0:D].rearrange("p (c k) -> p c k", c=2), ACT.Copy).then_inc(s["act_out"], 1)

        @block.vector
        def _(dve):
            for t in range(1, NT, 2):
                dve.wait_ge(s["turned"], t + 1)
                dve.tensor_copy(xo[:, :, t * P:(t + 1) * P], K.bank[t % 8][:, 0:D].rearrange("p (c k) -> p c k", c=2)).then_inc(s["dve_out"], 1)


def L0_ffn(nc, K, w):
    xT = K.XT[K.cur]
    NJ = L0E + 1 + NB
    expert = lambda n: min(n, L0E)
    pool_of_rows = nc.dram_tensor("L0f_rows", [TOK + PICKED, D], F32, kind="Internal").ap()
    with ExitStack() as es:
        num = sbuf(es, nc, "expert_number", [P, L0E])
        W3 = sbuf(es, nc, "W3", [P, (L0E + 1) * D])
        b3 = sbuf(es, nc, "b3", [L0E + 1, D])
        sb3 = sbuf(es, nc, "sb3", [P, DC])
        Z = sbuf(es, nc, "Z", [P, NJ, BLK])
        Xm = sbuf(es, nc, "picked", [P, PT4, D])
        XmT = sbuf(es, nc, "pickedT", [P, DC, PICKED])
        G = sbuf(es, nc, "gates", [P, PT4, L0E + 1])
        home = sbuf(es, nc, "home_row", [P, NT], U32)
        number_experts(nc, K, es, num[:], L0E)
        with ExitStack() as inn:
            W1, W2 = (sbuf(inn, nc, n, [P, DC, (L0E + 1) * P]) for n in ("W1", "W2"))
            b1, b2 = (sbuf(inn, nc, n, [P, L0E + 1]) for n in ("b1", "b2"))
            lng, lnb = (sbuf(inn, nc, n, [P, 2]) for n in ("lng", "lnb"))
            Wg = sbuf(inn, nc, "Wgate", [P, DC, L0E + 1])
            bg = sbuf(inn, nc, "bgate", [P, L0E + 1])
            eb = sbuf(inn, nc, "ebias", [P, L0E])
            J = sbuf(inn, nc, "J", [P, P])
            load(nc, K, (W1[:], w["L0f_W1"]), (W2[:], w["L0f_W2"]), (W3[:], w["L0f_W3"]), (b3[:], w["L0f_b3"]), (sb3[:], w["L0f_sb3"]), (b1[:], w["L0f_b1"]),
                 (b2[:], w["L0f_b2"]), (lng[:], w["L0f_g"]), (lnb[:], w["L0f_b"]), (Wg[:], w["L0f_Wgate"]), (bg[:], spread(w["L0f_bgate"])),
                 (eb[:], spread(w["L0f_ebias"])))
            block_mean(nc, K, J[:], P)
            with ExitStack() as ix, phase(nc, K.sems, "loaded rows_out counted index_done picked turned out") as (block, s):
                ints = sbuf(ix, nc, "index_cols", [P, 2, PT4], I32)
                intr = sbuf(ix, nc, "index_rows", [P, 2, PICKED], I32)
                fc = sbuf(ix, nc, "index_cols_f", [P, 2, PT4])
                fr = sbuf(ix, nc, "index_rows_f", [P, 2, PICKED])
                at = sbuf(ix, nc, "flat_index", [P, PT4], U32)
                ordi = sbuf(ix, nc, "order_int", [P, PICKED], I32)
                order = sbuf(ix, nc, "order", [P, PICKED])
                toki = sbuf(ix, nc, "token_int", [P, NT], I32)
                tok = sbuf(ix, nc, "token", [P, NT])
                hit = sbuf(ix, nc, "hit", [P, PICKED])
                last = sbuf(ix, nc, "last_hit", [P, NT, 3])

                @block.sync
                def _(sp):
                    sp.dma_start(pool_of_rows[0:TOK].rearrange("(t p) d -> p t d", p=P), K.Xtok[:]).then_inc(s["rows_out"], 16)
                    sp.dma_start(ints[:, 0], w["L0f_ib"]).then_inc(s["loaded"], 16)
                    sp.dma_start(ints[:, 1], w["L0f_it"]).then_inc(s["loaded"], 16)
                    sp.dma_start(intr[:, 0], spread(w["L0f_ibr"])).then_inc(s["loaded"], 16)
                    sp.dma_start(intr[:, 1], spread(w["L0f_itr"])).then_inc(s["loaded"], 16)

                @block.gpsimd
                def _(pool):
                    pool.iota(ordi[:], pattern=[[1, PICKED]], base=1, channel_multiplier=0).then_inc(s["counted"], 1)
                    pool.iota(toki[:], pattern=[[P, NT]], base=0, channel_multiplier=1).then_inc(s["counted"], 1)
                    pool.wait_ge(s["index_done"], 1)
                    pool.wait_ge(s["rows_out"], 16)
                    for q in range(PT4):
                        pool.indirect_dma_start(out=Xm[:, q, :], out_offset=None, in_=pool_of_rows[0:TOK, :],
                                                in_offset=bass.IndirectOffsetOnAxis(ap=at[:, q:q + 1], axis=0)).then_inc(s["picked"], 16)

                @block.vector
                def _(dve):
                    dve.wait_ge(s["loaded"], 64)
                    dve.wait_ge(s["counted"], 2)
                    dve.tensor_copy(fc[:], ints[:])
                    dve.tensor_copy(fr[:], intr[:])
                    dve.tensor_copy(order[:], ordi[:])
                    dve.tensor_copy(tok[:], toki[:])
                    dve.drain()
                    dve.scalar_tensor_tensor(out=at[:], in0=fc[:, 0], scalar=float(S), in1=fc[:, 1], op0=ALU.mult, op1=ALU.add).then_inc(s["index_done"], 1)
                    dve.scalar_tensor_tensor(out=fr[:, 0], in0=fr[:, 0], scalar=float(S), in1=fr[:, 1], op0=ALU.mult, op1=ALU.add)
                    dve.drain()
                    for t in range(NT):
                        dve.scalar_tensor_tensor(out=hit[:], in0=fr[:, 0], scalar=tok[:, t:t + 1], in1=order[:], op0=ALU.is_equal, op1=ALU.mult)
                        dve.drain()
                        dve.reduce_max(last[:, t, 0:1], hit[:], AX)
                        dve.drain()
                    dve.tensor_scalar(last[:, :, 1], last[:, :, 0], 0.0, None, ALU.is_gt)
                    dve.scalar_tensor_tensor(out=last[:, :, 2], in0=last[:, :, 0], scalar=float(TOK - 1), in1=tok[:], op0=ALU.add, op1=ALU.subtract)
                    dve.drain()
                    dve.tensor_tensor(last[:, :, 2], last[:, :, 2], last[:, :, 1], ALU.mult)
                    dve.drain()
                    dve.tensor_tensor(home[:], last[:, :, 2], tok[:], ALU.add)

                @block.tensor
                def _(pe):
                    pe.wait_ge(s["picked"], 16 * PT4)
                    for q in range(PT4):
                        for h in range(DC):
                            ins = pe.transpose(K.bank[q][:, h * P:(h + 1) * P], Xm[:, q, h * P:(h + 1) * P], K.ident[:])
                        ins.then_inc(s["turned"], 1)

                @block.scalar
                def _(act):
                    for q in range(PT4):
                        act.wait_ge(s["turned"], q + 1)
                        act.activation(XmT[:, :, q * P:(q + 1) * P], K.bank[q][:, 0:D].rearrange("p (c k) -> p c k", c=2), ACT.Copy).then_inc(s["out"], 1)

            with ExitStack() as up, phase(nc, K.sems, "done silu_done z_done") as (block, s):
                sl = sbuf(up, nc, "silu", [P, 2, BLK])

                @block.tensor
                def _(pe):
                    for n in range(NJ):
                        e = expert(n)
                        src = XmT if n <= L0E else xT
                        o = 0 if n <= L0E else (n - L0E - 1) * BLK
                        if n >= 4:
                            pe.wait_ge(s["z_done"], n - 3)
                        for part, W in enumerate((W1, W2)):
                            for k in range(DC):
                                ins = pe.matmul(K.bank[2 * (n % 4) + part][:], W[:, k, e * P:(e + 1) * P], src[:, k, o:o + BLK], start=(k == 0), stop=(k == DC - 1))
                        ins.then_inc(s["done"], 1)

                @block.scalar
                def _(act):
                    for n in range(NJ):
                        act.wait_ge(s["done"], n + 1)
                        if n >= 2:
                            act.wait_ge(s["z_done"], n - 1)
                        act.activation(sl[:, n % 2, :], K.bank[2 * (n % 4)][:], ACT.Silu, bias=b1[:, expert(n):expert(n) + 1]).then_inc(s["silu_done"], 1)

                @block.vector
                def _(dve):
                    for n in range(NJ):
                        dve.wait_ge(s["silu_done"], n + 1)
                        dve.scalar_tensor_tensor(out=Z[:, n, :], in0=K.bank[2 * (n % 4) + 1][:], scalar=b2[:, expert(n):expert(n) + 1], in1=sl[:, n % 2, :],
                                                 op0=ALU.add, op1=ALU.mult).then_inc(s["z_done"], 1)

            ln = lambda v: lambda n: v[:, 0:1] if n < L0E else v[:, 1:2]
            feature_ln(nc, K, J[:], NJ, 1, lambda n, h: Z[:, n, :], lambda n, h: Z[:, n, :], ln(lng), ln(lnb))

            with ExitStack() as gt, phase(nc, K.sems, "scored biased sigma_done ready weights_done") as (block, s):
                sc = sbuf(gt, nc, "scores", [P, PT4, L0E + 1])
                v = sbuf(gt, nc, "biased", [P, PT4, L0E])
                top = sbuf(gt, nc, "top", [P, PT4, 8])
                at = sbuf(gt, nc, "top_index", [P, PT4, 8], U32)
                atf = sbuf(gt, nc, "top_index_f", [P, PT4, 8])
                d = sbuf(gt, nc, "difference", [P, 3, PT4])

                @block.tensor
                def _(pe):
                    for q in range(PT4):
                        for k in range(DC):
                            ins = pe.matmul(K.bank[0][:, q * 16:q * 16 + L0E + 1], XmT[:, k, q * P:(q + 1) * P], Wg[:, k, :], start=(k == 0), stop=(k == DC - 1))
                    ins.then_inc(s["scored"], 1)

                @block.vector
                def _(dve):
                    dve.wait_ge(s["scored"], 1)
                    dve.tensor_tensor(sc[:], K.bank[0][:, 0:16 * PT4].rearrange("p (q e) -> p q e", e=16)[:, :, 0:L0E + 1], middle(bg[:], PT4), ALU.add).then_inc(s["biased"], 1)
                    dve.wait_ge(s["sigma_done"], 1)
                    dve.tensor_tensor(v[:], sc[:, :, 0:L0E], middle(eb[:], PT4), ALU.add)
                    dve.drain()
                    for q in range(PT4):
                        dve.max(top[:, q, :], v[:, q, :])
                    dve.drain()
                    for q in range(PT4):
                        dve.max_index(at[:, q, :], top[:, q, :], v[:, q, :])
                    dve.drain()
                    dve.tensor_copy(atf[:], at[:])
                    dve.drain()
                    dve.tensor_tensor(G[:, :, 0:L0E], middle(num[:], PT4), inner(atf[:, :, 0], L0E), ALU.is_equal)
                    dve.drain()
                    dve.tensor_tensor(v[:], G[:, :, 0:L0E], sc[:, :, 0:L0E], ALU.mult)
                    dve.drain()
                    dve.reduce_sum(d[:, 0, :], v[:], AX)
                    dve.drain()
                    dve.tensor_tensor(d[:, 1, :], d[:, 0, :], sc[:, :, L0E], ALU.subtract)
                    dve.drain()
                    dve.tensor_scalar(d[:, 2, :], d[:, 1, :], -1.0, None, ALU.mult).then_inc(s["ready"], 1)
                    dve.wait_ge(s["weights_done"], 1)
                    dve.tensor_tensor(G[:, :, 0:L0E], G[:, :, 0:L0E], inner(d[:, 1, :], L0E), ALU.mult)
                    dve.tensor_copy(G[:, :, L0E], d[:, 2, :])

                @block.scalar
                def _(act):
                    act.wait_ge(s["biased"], 1)
                    act.activation(sc[:], sc[:], ACT.Sigmoid).then_inc(s["sigma_done"], 1)
                    act.wait_ge(s["ready"], 1)
                    act.activation(d[:, 1:3, :], d[:, 1:3, :], ACT.Sigmoid).then_inc(s["weights_done"], 1)

        acc = sbuf(es, nc, "acc", [P, PT4, D])
        st = sbuf(es, nc, "ln_stats", [P, PT4, 9])
        with ExitStack() as gt, phase(nc, K.sems, "turned turned_out bias_done bias_out done added stats_done std_done stored") as (block, s):
            gT = sbuf(gt, nc, "gatesT", [L0E + 1, PICKED])

            @block.tensor
            def _(pe):
                for q in range(PT4):
                    ins = pe.transpose(K.bank[0][0:L0E + 1, q * P:(q + 1) * P], G[:, q, :], K.ident[:])
                ins.then_inc(s["turned"], 1)
                pe.wait_ge(s["turned_out"], 1)
                for q in range(PT4):
                    if q:
                        pe.wait_ge(s["bias_out"], q)
                    pe.matmul(K.bank[1][:, 0:D], gT[:, q * P:(q + 1) * P], b3[:], start=True, stop=True).then_inc(s["bias_done"], 1)
                for n in range(PT4 * (L0E + 1)):
                    q, e = divmod(n, L0E + 1)
                    if n >= 6:
                        pe.wait_ge(s["added"], n - 5)
                    pe.matmul(K.bank[2 + n % 6][:, 0:D], Z[:, e, q * P:(q + 1) * P], W3[:, e * D:(e + 1) * D], start=True, stop=True).then_inc(s["done"], 1)

            @block.scalar
            def _(act):
                act.wait_ge(s["turned"], 1)
                act.activation(gT[:], K.bank[0][0:L0E + 1, :], ACT.Copy).then_inc(s["turned_out"], 1)
                act.wait_ge(s["stats_done"], 1)
                act.activation(st[:, :, 8:9], st[:, :, 1:2], ACT.Sqrt, bias=K.eps[:, 0:1]).then_inc(s["std_done"], 1)

            @block.vector
            def _(dve):
                for q in range(PT4):
                    dve.wait_ge(s["bias_done"], q + 1)
                    dve.tensor_tensor(acc[:, q, :], K.bank[1][:, 0:D], Xm[:, q, :], ALU.add).then_inc(s["bias_out"], 1)
                dve.drain()
                for n in range(PT4 * (L0E + 1)):
                    q, e = divmod(n, L0E + 1)
                    dve.wait_ge(s["done"], n + 1)
                    dve.scalar_tensor_tensor(out=acc[:, q, :], in0=K.bank[2 + n % 6][:, 0:D], scalar=G[:, q, e:e + 1], in1=acc[:, q, :],
                                             op0=ALU.mult, op1=ALU.add).then_inc(s["added"], 1)
                    dve.drain()
                for q in range(PT4):
                    dve.bn_stats(st[:, q, 2:8], acc[:, q, :])
                dve.drain()
                for q in range(PT4):
                    ins = dve.bn_aggr(st[:, q, 0:2], st[:, q, 2:8])
                ins.then_inc(s["stats_done"], 1)
                dve.wait_ge(s["std_done"], 1)
                dve.reciprocal(st[:, :, 8:9], st[:, :, 8:9])
                dve.drain()
                for q in range(PT4):
                    ins = dve.tensor_scalar(acc[:, q, :], acc[:, q, :], st[:, q, 0:1], st[:, q, 8:9], ALU.subtract, ALU.mult)
                ins.then_inc(s["added"], 1)

            @block.sync
            def _(sp):
                sp.wait_ge(s["added"], PT4 * (L0E + 1) + 1)
                sp.dma_start(pool_of_rows[TOK:TOK + PICKED].rearrange("(q p) d -> p q d", p=P), acc[:]).then_inc(s["stored"], 16)
                sp.wait_ge(s["stored"], 16)

        finish(nc, K, lambda k, h, j: W3[:, L0E * D + h * P:L0E * D + (h + 1) * P], lambda k, j: Z[:, L0E + 1 + j, :], 1, bias=sb3)
        with phase(nc, K.sems, "stored gathered") as (block, s):
            @block.sync
            def _(sp):
                sp.dma_start(pool_of_rows[0:TOK].rearrange("(t p) d -> p t d", p=P), K.Xtok[:]).then_inc(s["stored"], 16)

            @block.gpsimd
            def _(pool):
                pool.wait_ge(s["stored"], 16)
                for t in range(NT):
                    pool.indirect_dma_start(out=K.Xtok[:, t, :], out_offset=None, in_=pool_of_rows[:, :],
                                            in_offset=bass.IndirectOffsetOnAxis(ap=home[:, t:t + 1], axis=0)).then_inc(s["gathered"], 16)
                pool.wait_ge(s["gathered"], 16 * NT)
        turn_tokens(nc, K)


L0H = 4
CH = 64
NCH = TOK // CH


def L0_attn_layout(i):
    g = lambda n: np.asarray(i["L0_attn_" + n])
    cw = np.stack([g(n).reshape(DC, P, 4).transpose(1, 0, 2) for n in ("conv_q", "conv_k", "conv_v")], axis=1)
    return {"L0a_W": rows(np.concatenate([g("Wq"), g("Wk"), g("Wv")], axis=1)), "L0a_Wb": rows(g("Wb")), "L0a_cw": np.ascontiguousarray(cw),
            "L0a_g": np.tile(g("g"), L0H), "L0a_Wo": rows(g("Wo"))}


def L0_attn(nc, K, w):
    xT = K.XT[K.cur]
    with ExitStack() as es:
        Wo = sbuf(es, nc, "Wo", [P, DC, D])
        OT = sbuf(es, nc, "OT", [P, DC, TOK])
        g4 = sbuf(es, nc, "g", [P, D])
        with ExitStack() as q_life:
            QK = sbuf(q_life, nc, "q_k_tokens", [P, NT, 2 * D])
            KV = sbuf(q_life, nc, "beta_k_v", [P, NT, 2 * D])
            beta = sbuf(q_life, nc, "beta", [P, NT, L0H])
            with ExitStack() as inn:
                W = sbuf(inn, nc, "W", [P, DC, 3 * D])
                Wb = sbuf(inn, nc, "Wb", [P, DC, L0H])
                cw = sbuf(inn, nc, "cw", [P, 3, DC, TAPS])
                raw = sbuf(inn, nc, "raw", [P, 2, TAPS - 1 + S])
                act_T = sbuf(inn, nc, "act_T", [P, 4, BLK])
                acc = sbuf(inn, nc, "conv", [P, 2, BLK])
                sq = sbuf(inn, nc, "squares", [P, 2, 2 * P])
                nrm = sbuf(inn, nc, "norm", [P, 2, L0H])
                load(nc, K, (W[:], w["L0a_W"]), (Wb[:], w["L0a_Wb"]), (cw[:], w["L0a_cw"]), (g4[:], spread(w["L0a_g"])), (Wo[:], w["L0a_Wo"]))
                names = "padded done raw_out conv_done silu_done turned tok_out"
                with phase(nc, K.sems, names) as (block, s):
                    runs = [(x, c, b) for x in range(3) for c in range(DC) for b in range(B)]
                    NR = len(runs)

                    @block.gpsimd
                    def _(pool):
                        pool.memset(raw[:, :, 0:TAPS - 1], 0.0).then_inc(s["padded"], 1)

                    @block.tensor
                    def _(pe):
                        def projection(r):
                            x, c, b = runs[r]
                            for i in range(2):
                                n = 2 * r + i
                                if n >= 4:
                                    pe.wait_ge(s["raw_out"], n - 3)
                                for k in range(DC):
                                    ins = pe.matmul(K.bank[n % 4][:], W[:, k, x * D + c * P:x * D + (c + 1) * P],
                                                    xT[:, k, b * S + i * BLK:b * S + (i + 1) * BLK], start=(k == 0), stop=(k == DC - 1))
                                ins.then_inc(s["done"], 1)
                        projection(0)
                        for r in range(NR):
                            if r + 1 < NR:
                                projection(r + 1)
                            for i in range(2):
                                n = 2 * r + i
                                pe.wait_ge(s["silu_done"], n + 1)
                                if n >= 4:
                                    pe.wait_ge(s["tok_out"], n - 3)
                                for t in range(TPB):
                                    ins = pe.transpose(K.bank[4 + n % 4][:, t * P:(t + 1) * P], act_T[:, n % 4, t * P:(t + 1) * P], K.ident[:])
                                ins.then_inc(s["turned"], 1)

                    @block.scalar
                    def _(act):
                        act.wait_ge(s["padded"], 1)
                        for n in range(2 * NR + 2):
                            if n < 2 * NR:
                                r, i = divmod(n, 2)
                                act.wait_ge(s["done"], n + 1)
                                if r >= 2:
                                    act.wait_ge(s["conv_done"], 2 * (r - 1))
                                act.activation(raw[:, r % 2, TAPS - 1 + i * BLK:TAPS - 1 + (i + 1) * BLK], K.bank[n % 4][:], ACT.Copy).then_inc(s["raw_out"], 1)
                            if n >= 2:
                                m = n - 2
                                act.wait_ge(s["conv_done"], m + 1)
                                if m >= 4:
                                    act.wait_ge(s["turned"], m - 3)
                                act.activation(act_T[:, m % 4, :], acc[:, m % 2, :], ACT.Silu).then_inc(s["silu_done"], 1)

                    @block.vector
                    def _(dve):
                        def take(m):
                            x, c, b = runs[m // 2]
                            t0 = b * (S // P) + (m % 2) * TPB
                            dve.wait_ge(s["turned"], m + 1)
                            dst = (QK, QK, KV)[x]
                            col = (0, D, D)[x] + c * P
                            dve.tensor_copy(dst[:, t0:t0 + TPB, col:col + P], K.bank[4 + m % 4][:].rearrange("p (t k) -> p t k", t=TPB)).then_inc(s["tok_out"], 1)

                        for n in range(2 * NR):
                            r, i = divmod(n, 2)
                            x, c, b = runs[r]
                            dve.wait_ge(s["raw_out"], n + 1)
                            if n >= 2:
                                dve.wait_ge(s["silu_done"], n - 1)
                            a = acc[:, n % 2, :]
                            dve.tensor_scalar(a, raw[:, r % 2, i * BLK:(i + 1) * BLK], cw[:, x, c, 0:1], None, ALU.mult)
                            for tap in range(1, TAPS):
                                dve.drain()
                                ins = dve.scalar_tensor_tensor(out=a, in0=raw[:, r % 2, i * BLK + tap:(i + 1) * BLK + tap], scalar=cw[:, x, c, tap:tap + 1],
                                                               in1=a, op0=ALU.mult, op1=ALU.add)
                            ins.then_inc(s["conv_done"], 1)
                            if n >= 3:
                                take(n - 3)
                        for m in range(2 * NR - 3, 2 * NR):
                            take(m)

                with phase(nc, K.sems, "done") as (block, s):
                    @block.tensor
                    def _(pe):
                        for t in range(NT):
                            for k in range(DC):
                                ins = pe.matmul(K.bank[0][:, t * L0H:(t + 1) * L0H], xT[:, k, t * P:(t + 1) * P], Wb[:, k, :], start=(k == 0), stop=(k == DC - 1))
                        ins.then_inc(s["done"], 1)

                    @block.scalar
                    def _(act):
                        act.wait_ge(s["done"], 1)
                        act.activation(beta[:], K.bank[0][:, 0:NT * L0H].rearrange("p (t h) -> p t h", h=L0H), ACT.Sigmoid)

                with ExitStack() as nn, phase(nc, K.sems, "squared summed root") as (block, s):
                    sq2 = sbuf(nn, nc, "squares", [P, 2, 2 * D])
                    nr = sbuf(nn, nc, "norms", [P, NT, 2 * L0H])

                    @block.scalar
                    def _(act):
                        for t in range(NT):
                            if t >= 2:
                                act.wait_ge(s["summed"], t - 1)
                            act.activation(sq2[:, t % 2, :], QK[:, t, :], ACT.Square).then_inc(s["squared"], 1)
                        act.wait_ge(s["summed"], NT)
                        act.activation(nr[:], nr[:], ACT.Sqrt).then_inc(s["root"], 1)

                    @block.vector
                    def _(dve):
                        for t in range(NT):
                            dve.wait_ge(s["squared"], t + 1)
                            dve.reduce_sum(nr[:, t, :], sq2[:, t % 2, :].rearrange("p (h d) -> p h d", h=2 * L0H), AX).then_inc(s["summed"], 1)
                        dve.wait_ge(s["root"], 1)
                        dve.reciprocal(nr[:], nr[:])
                        dve.drain()
                        for t in range(NT):
                            v = QK[:, t, :].rearrange("p (h d) -> p h d", h=2 * L0H)
                            dve.tensor_tensor(v, v, inner(nr[:, t, :], D // L0H), ALU.mult)
                        dve.drain()
                        for t in range(NT):
                            b_ = inner(beta[:, t, :], D // L0H)
                            kb, vb = (KV[:, t, o:o + D].rearrange("p (h d) -> p h d", h=L0H) for o in (0, D))
                            dve.tensor_tensor(kb, QK[:, t, D:2 * D].rearrange("p (h d) -> p h d", h=L0H), b_, ALU.mult)
                            dve.tensor_tensor(vb, vb, b_, ALU.mult)

            TT = sbuf(q_life, nc, "T_transposed", [P, NT, P])
            LEVELS = 6
            with ExitStack() as inn:
                masks = sbuf(inn, nc, "masks", [P, LEVELS + 1, P])
                with phase(nc, K.sems, "step") as (block, s):
                    @block.gpsimd
                    def _(pool):
                        n = 0
                        pool.memset(masks[:], 1.0).then_inc(s["step"], 1)
                        for lv in range(LEVELS + 1):
                            z = 1 << lv if lv < LEVELS else 1
                            m = masks[:, lv, :]
                            v = m.rearrange("p (n a j) -> p n a j", a=2, j=z)
                            blocks = P // (2 * z)
                            first, second = (0, 1) if lv < LEVELS else (1, 0)
                            for cmp_base, pat, mul in (
                                    (-z * first, [[-2 * z, blocks], [0, 2], [0, z]], 1),
                                    (z * first + z - 1, [[2 * z, blocks], [0, 2], [0, z]], -1),
                                    (-second if second else 0, [[0, blocks], [1 if second else -1, 2], [0, z]], 0)):
                                n += 1
                                pool.wait_ge(s["step"], n)
                                pool.affine_select(out=v, in_=v, compare_op=ALU.is_ge, fill=0.0, base=cmp_base, pattern=pat,
                                                   channel_multiplier=mul).then_inc(s["step"], 1)

                GT = 4
                kT = sbuf(inn, nc, "kT", [P, 2, 2 * DC * P])
                E = sbuf(inn, nc, "E_T", [P, LEVELS - 1, GT, P])
                M, MT, X = (sbuf(inn, nc, n, [P, GT, P]) for n in ("M", "M_T", "X"))
                four = lambda ap: middle(ap, GT)
                bank4 = lambda i: K.bank[i][:].rearrange("p (t k) -> p t k", t=GT)
                with phase(nc, K.sems, "k_turned k_out a_done m_ready x_done x_out y_done") as (block, s):
                    @block.tensor
                    def _(pe):
                        for gr in range(NT // GT):
                            for i in range(GT):
                                t = gr * GT + i
                                if t >= 2:
                                    pe.wait_ge(s["k_out"], t - 1)
                                for c in range(DC):
                                    pe.transpose(K.bank[t % 2][:, c * P:(c + 1) * P], QK[:, t, D + c * P:D + (c + 1) * P], K.ident[:])
                                    ins = pe.transpose(K.bank[t % 2][:, (2 + c) * P:(3 + c) * P], KV[:, t, c * P:(c + 1) * P], K.ident[:])
                                ins.then_inc(s["k_turned"], 1)
                                if i == 0 and gr:
                                    pe.wait_ge(s["m_ready"], gr * (LEVELS + 1))
                                pe.wait_ge(s["k_out"], t + 1)
                                k_, kb = (lambda c: kT[:, t % 2, c * P:(c + 1) * P]), (lambda c: kT[:, t % 2, (2 + c) * P:(3 + c) * P])
                                for c in range(DC):
                                    pe.matmul(K.bank[2][:, i * P:(i + 1) * P], k_(c), kb(c), start=(c == 0), stop=(c == DC - 1))
                                for c in range(DC):
                                    ins = pe.matmul(K.bank[3][:, i * P:(i + 1) * P], kb(c), k_(c), start=(c == 0), stop=(c == DC - 1))
                                ins.then_inc(s["a_done"], 1)
                            for lv in range(1, LEVELS):
                                pe.wait_ge(s["m_ready"], gr * (LEVELS + 1) + lv)
                                for i in range(GT):
                                    ins = pe.matmul(K.bank[4][:, i * P:(i + 1) * P], E[:, lv - 1, i, :], M[:, i, :], start=True, stop=True)
                                ins.then_inc(s["x_done"], 1)
                                pe.wait_ge(s["x_out"], gr * (LEVELS - 1) + lv)
                                for i in range(GT):
                                    pe.matmul(K.bank[5][:, i * P:(i + 1) * P], MT[:, i, :], X[:, i, :], start=True, stop=True)
                                for i in range(GT):
                                    ins = pe.matmul(K.bank[6][:, i * P:(i + 1) * P], X[:, i, :], MT[:, i, :], start=True, stop=True)
                                ins.then_inc(s["y_done"], 1)

                    @block.scalar
                    def _(act):
                        for gr in range(NT // GT):
                            for i in range(GT):
                                t = gr * GT + i
                                act.wait_ge(s["k_turned"], t + 1)
                                if t >= 2:
                                    act.wait_ge(s["a_done"], t - 1)
                                act.activation(kT[:, t % 2, :], K.bank[t % 2][:], ACT.Copy).then_inc(s["k_out"], 1)
                            for lv in range(1, LEVELS):
                                act.wait_ge(s["x_done"], gr * (LEVELS - 1) + lv)
                                act.activation(X[:], bank4(4), ACT.Copy).then_inc(s["x_out"], 1)

                    @block.vector
                    def _(dve):
                        for gr in range(NT // GT):
                            dve.wait_ge(s["a_done"], GT * (gr + 1))
                            for lv in range(1, LEVELS):
                                dve.tensor_tensor(E[:, lv - 1], bank4(2), four(masks[:, lv, :]), ALU.mult)
                            dve.tensor_tensor(MT[:], bank4(2), four(masks[:, 0, :]), ALU.mult)
                            dve.tensor_tensor(M[:], bank4(3), four(masks[:, LEVELS, :]), ALU.mult)
                            dve.drain()
                            dve.tensor_tensor(MT[:], four(K.ident[:]), MT[:], ALU.subtract)
                            dve.tensor_tensor(M[:], four(K.ident[:]), M[:], ALU.subtract).then_inc(s["m_ready"], 1)
                            dve.drain()
                            for lv in range(1, LEVELS):
                                dve.wait_ge(s["y_done"], gr * (LEVELS - 1) + lv)
                                dve.tensor_tensor(M[:], M[:], bank4(5), ALU.subtract)
                                dve.tensor_tensor(MT[:], MT[:], bank4(6), ALU.subtract).then_inc(s["m_ready"], 1)
                                dve.drain()
                            dve.tensor_scalar(X[:], four(K.ident[:]), -2.0, None, ALU.mult)
                            dve.drain()
                            dve.scalar_tensor_tensor(out=TT[:, gr * GT:(gr + 1) * GT, :], in0=MT[:], scalar=3.0, in1=X[:], op0=ALU.mult, op1=ALU.add).then_inc(s["m_ready"], 1)

            sums = sbuf(q_life, nc, "chunk_sums", [P, 2 * DC, NCH])
            pick = sbuf(q_life, nc, "chunk_of", [P, 2])
            with ExitStack() as inn, phase(nc, K.sems, "step wu_done wu_out prod_done summed") as (block, s):
                prod = sbuf(inn, nc, "k_products", [P, 2, 2 * D])

                @block.gpsimd
                def _(pool):
                    pool.memset(pick[:], 1.0).then_inc(s["step"], 1)
                    pool.wait_ge(s["step"], 1)
                    pool.affine_select(out=pick[:], in_=pick[:], compare_op=ALU.is_ge, fill=0.0, base=0, pattern=[[-CH, 2]], channel_multiplier=1).then_inc(s["step"], 1)
                    pool.wait_ge(s["step"], 2)
                    pool.affine_select(out=pick[:], in_=pick[:], compare_op=ALU.is_ge, fill=0.0, base=CH - 1, pattern=[[CH, 2]], channel_multiplier=-1).then_inc(s["step"], 1)

                @block.tensor
                def _(pe):
                    def products(t):
                        if t >= 2:
                            pe.wait_ge(s["wu_out"], t - 1)
                        pe.matmul(K.bank[t % 2][:], TT[:, t, :], KV[:, t, :], start=True, stop=True).then_inc(s["wu_done"], 1)
                    products(0)
                    pe.wait_ge(s["step"], 3)
                    for t in range(NT):
                        if t + 1 < NT:
                            products(t + 1)
                        pe.wait_ge(s["prod_done"], t + 1)
                        for c in range(2 * DC):
                            ins = pe.matmul(K.bank[2][:, c * NCH + 2 * t:c * NCH + 2 * t + 2], prod[:, t % 2, c * P:(c + 1) * P], pick[:], start=True, stop=True)
                        ins.then_inc(s["summed"], 1)

                @block.scalar
                def _(act):
                    for t in range(NT):
                        act.wait_ge(s["wu_done"], t + 1)
                        act.activation(KV[:, t, :], K.bank[t % 2][:], ACT.Copy).then_inc(s["wu_out"], 1)

                @block.vector
                def _(dve):
                    for t in range(NT):
                        dve.wait_ge(s["wu_out"], t + 1)
                        if t >= 2:
                            dve.wait_ge(s["summed"], t - 1)
                        dve.tensor_tensor(prod[:, t % 2, :].rearrange("p (a d) -> p a d", a=2), middle(QK[:, t, D:2 * D], 2),
                                          KV[:, t, :].rearrange("p (a d) -> p a d", a=2), ALU.mult).then_inc(s["prod_done"], 1)
                    dve.wait_ge(s["summed"], NT)
                    v = K.bank[2][:, 0:2 * DC * NCH].rearrange("p (c n) -> p c n", n=NCH)
                    dve.tensor_scalar(sums[:, 0:DC], v[:, 0:DC], -1.0, 1.0, ALU.mult, ALU.add)
                    dve.tensor_copy(sums[:, DC:2 * DC], v[:, DC:2 * DC])

            diag = sbuf(q_life, nc, "diagonal", [NCH, D])
            sel = sbuf(q_life, nc, "chunk_select", [NCH, TOK])
            rowm = sbuf(q_life, nc, "first_rows", [P, B])
            with ExitStack() as inn, phase(nc, K.sems, "step scanned turned") as (block, s):
                dT = sbuf(inn, nc, "diagonalT", [P, DC, B, NCH // B + 1])
                dC = sbuf(inn, nc, "diagonal_before", [P, DC, NCH])

                @block.gpsimd
                def _(pool):
                    v = sel[:].rearrange("p (n j) -> p n j", j=CH)
                    pool.memset(sel[:], 1.0).then_inc(s["step"], 1)
                    pool.memset(rowm[:], 1.0).then_inc(s["step"], 1)
                    pool.wait_ge(s["step"], 2)
                    pool.affine_select(out=v, in_=v, compare_op=ALU.is_equal, fill=0.0, base=0, pattern=[[-1, NCH], [0, CH]], channel_multiplier=1)
                    pool.affine_select(out=rowm[0:CH], in_=rowm[0:CH], compare_op=ALU.is_ge, fill=0.0, base=0, pattern=[[1, B]], channel_multiplier=-1)
                    pool.affine_select(out=rowm[CH:P], in_=rowm[CH:P], compare_op=ALU.is_ge, fill=0.0, base=0, pattern=[[1, B]], channel_multiplier=-1)

                @block.vector
                def _(dve):
                    dve.memset(dT[:, :, :, 0:1], 0.0)
                    n = NCH // B
                    for c in range(DC):
                        for b in range(B):
                            dve.tensor_tensor_scan(dT[:, c, b, 1:n + 1], sums[:, c, b * n:(b + 1) * n], sums[:, DC + c, b * n:(b + 1) * n], 0.0, ALU.mult, ALU.add)
                    dve.drain()
                    dve.tensor_copy(dC[:].rearrange("p c (b n) -> p (c b) n", b=B), dT[:].rearrange("p c b n -> p (c b) n")[:, :, 0:n]).then_inc(s["scanned"], 1)
                    dve.wait_ge(s["turned"], 1)
                    dve.tensor_copy(diag[:], K.bank[0][0:NCH, 0:D])

                @block.tensor
                def _(pe):
                    pe.wait_ge(s["scanned"], 1)
                    for c in range(DC):
                        ins = pe.transpose(K.bank[0][0:NCH, c * P:(c + 1) * P], dC[:, c, :], K.ident[:])
                    ins.then_inc(s["turned"], 1)

            with ExitStack() as inn, phase(nc, K.sems, "d_done o_done squared summed root o_normed turned out") as (block, s):
                tmp = sbuf(inn, nc, "tmp", [P, 2, D])
                dot = sbuf(inn, nc, "dot", [P, NT])
                sq = sbuf(inn, nc, "squares", [P, 2, D])
                ms = sbuf(inn, nc, "mean_square", [P, NT, L0H])
                O = sbuf(inn, nc, "O", [P, NT, D])

                @block.tensor
                def _(pe):
                    for t in range(NT):
                        if t >= 4:
                            pe.wait_ge(s["o_done"], t - 3)
                        pe.matmul(K.bank[t % 4][:, 0:D], sel[:, t * P:(t + 1) * P], diag[:], start=True, stop=True).then_inc(s["d_done"], 1)
                    for t in range(NT):
                        pe.wait_ge(s["o_normed"], t + 1)
                        if t >= 4:
                            pe.wait_ge(s["out"], t - 3)
                        for c in range(DC):
                            ins = pe.transpose(K.bank[4 + t % 4][:, c * P:(c + 1) * P], O[:, t, c * P:(c + 1) * P], K.ident[:])
                        ins.then_inc(s["turned"], 1)

                @block.vector
                def _(dve):
                    for t in range(NT):
                        q_, k_ = QK[:, t, 0:D], QK[:, t, D:2 * D]
                        a, b_ = tmp[:, 0, :], tmp[:, 1, :]
                        dve.wait_ge(s["d_done"], t + 1)
                        d_ = K.bank[t % 4][:, 0:D]
                        dve.tensor_tensor_reduce(a, q_, k_, 1.0, 0.0, ALU.mult, ALU.add, dot[:, t:t + 1])
                        dve.tensor_tensor(b_, KV[:, t, 0:D], d_, ALU.mult)
                        dve.drain()
                        dve.tensor_tensor(dot[:, t:t + 1], dot[:, t:t + 1], rowm[:, t // 8:t // 8 + 1], ALU.mult)
                        dve.tensor_tensor(b_, KV[:, t, D:2 * D], b_, ALU.subtract)
                        dve.tensor_tensor(a, q_, d_, ALU.mult)
                        dve.drain()
                        dve.scalar_tensor_tensor(out=O[:, t, :], in0=b_, scalar=dot[:, t:t + 1], in1=a, op0=ALU.mult, op1=ALU.add).then_inc(s["o_done"], 1)
                        dve.drain()
                    for t in range(NT):
                        dve.wait_ge(s["squared"], t + 1)
                        dve.reduce_sum(ms[:, t, :], sq[:, t % 2, :].rearrange("p (h d) -> p h d", h=L0H), AX).then_inc(s["summed"], 1)
                    dve.wait_ge(s["root"], 1)
                    dve.reciprocal(ms[:], ms[:])
                    dve.drain()
                    for t in range(NT):
                        v = O[:, t, :].rearrange("p (h d) -> p h d", h=L0H)
                        dve.tensor_tensor(v, v, inner(ms[:, t, :], D // L0H), ALU.mult)
                        dve.drain()
                        dve.tensor_tensor(O[:, t, :], O[:, t, :], g4[:], ALU.mult).then_inc(s["o_normed"], 1)

                @block.scalar
                def _(act):
                    for t in range(NT):
                        act.wait_ge(s["o_done"], t + 1)
                        if t >= 2:
                            act.wait_ge(s["summed"], t - 1)
                        act.activation(sq[:, t % 2, :], O[:, t, :], ACT.Square).then_inc(s["squared"], 1)
                    act.wait_ge(s["summed"], NT)
                    act.activation(ms[:], ms[:], ACT.Sqrt, scale=1.0 / (D // L0H), bias=K.eps[:, 0:1]).then_inc(s["root"], 1)
                    for t in range(NT):
                        act.wait_ge(s["turned"], t + 1)
                        act.activation(OT[:, :, t * P:(t + 1) * P], K.bank[4 + t % 4][:, 0:D].rearrange("p (c k) -> p c k", c=2), ACT.Copy).then_inc(s["out"], 1)
        finish(nc, K, lambda k, h, j: Wo[:, k, h * P:(h + 1) * P], block_of(OT), DC)


L2D = 2
LH, LHD = 8, 64
LM = LH * LHD // P
HIDP = 6 * P
L2HID = 682
WINDOW = 128


def xpos_tables():
    f = np.float32
    half = np.arange(0, LHD, 2, dtype=f)
    inv = f(1.0) / np.power(f(10000.0), half / f(LHD), dtype=f)
    t = np.arange(S, dtype=f)
    ang = t[:, None] * inv[None, :]
    ang = np.concatenate([ang, ang], axis=1)
    base = (half + f(0.4 * LHD)) / f(1.4 * LHD)
    power = (t - f(S // 2)) / f(WINDOW // 2)
    scale = np.power(base[None, :], power[:, None], dtype=f)
    scale = np.concatenate([scale, scale], axis=1)
    cos, sin = np.cos(ang, dtype=f), np.sin(ang, dtype=f)
    tab = np.stack([cos * scale, sin * scale, cos / scale, sin / scale])
    tab = np.tile(tab.transpose(2, 0, 1), (P // LHD, 1, 1))
    rot = np.zeros((P, P), f)
    for p in range(P):
        h, d = divmod(p, LHD)
        if d < LHD // 2:
            rot[h * LHD + d + LHD // 2, p] = -1.0
        else:
            rot[h * LHD + d - LHD // 2, p] = 1.0
    return np.ascontiguousarray(tab), rot


def L2_ffn_layout(i):
    g = lambda n, l: np.asarray(i["L2_ffn_" + n])[l]
    tab, rot = xpos_tables()
    out = {"L2f_tab": tab, "L2f_rot": rot}
    for l in range(L2D):
        two = lambda a, axis: np.concatenate([pad(a[..., :L2HID], axis, HIDP), pad(a[..., L2HID:], axis, HIDP)], axis=axis)
        out.update({f"L2f{l}_Wqkv": rows(g("wqkv", l)), f"L2f{l}_qs": np.tile(g("q_scale", l), P // LHD).reshape(P, 1),
                    f"L2f{l}_ks": np.tile(g("k_scale", l), P // LHD).reshape(P, 1), f"L2f{l}_Wo": rows(g("wo", l)),
                    f"L2f{l}_g": cols(g("ln_g", l)), f"L2f{l}_b": cols(g("ln_b", l)), f"L2f{l}_W1": rows(two(g("w1", l), 1)),
                    f"L2f{l}_b1": cols(two(g("b1", l), 0)), f"L2f{l}_W2": rows(pad(g("w2", l), 0, HIDP)), f"L2f{l}_b2": cols(g("b2", l))})
    return out


def shift_half(nc, K, X, sh):
    with phase(nc, K.sems, "copied") as (block, s):
        v = X[:, 1, :].rearrange("p (b t) -> p b t", b=B)

        @block.scalar
        def _(act):
            act.activation(sh[:, 0, 1:], v[:, 0], ACT.Copy)

        @block.vector
        def _(dve):
            dve.tensor_copy(sh[:, 1, 1:], v[:, 1])


def local_qk(nc, K, b, src, W, col, Rs, sc, cosT, sinT, ones64, out):
    with ExitStack() as es, phase(nc, K.sems, "done raw_out squared turned_done norm_done root_done clipped straight crossed summed out") as (block, s):
        raw, sq, rt, t1, t2 = (sbuf(es, nc, n, [P, 2, BLK]) for n in ("raw", "squares", "norm", "straight", "crossed"))
        steps = [(m, i) for m in range(LM) for i in range(2)]
        N = len(steps)

        @block.tensor
        def _(pe):
            def projection(n):
                m, i = steps[n]
                if n >= 2:
                    pe.wait_ge(s["raw_out"], n - 1)
                for k in range(DC):
                    ins = pe.matmul(K.bank[n % 2][:], W[:, k, col + m * P:col + (m + 1) * P], src(k, i), start=(k == 0), stop=(k == DC - 1))
                ins.then_inc(s["done"], 1)
            projection(0)
            for n in range(N):
                if n + 1 < N:
                    projection(n + 1)
                pe.wait_ge(s["raw_out"], n + 1)
                if n >= 2:
                    pe.wait_ge(s["crossed"], n - 1)
                pe.matmul(K.bank[2 + n % 2][:], Rs, raw[:, n % 2, :], start=True, stop=True).then_inc(s["turned_done"], 1)
                pe.wait_ge(s["squared"], n + 1)
                if n >= 2:
                    pe.wait_ge(s["root_done"], n - 1)
                pe.matmul(K.bank[4 + n % 2][:], ones64, sq[:, n % 2, :], start=True, stop=True).then_inc(s["norm_done"], 1)

        @block.scalar
        def _(act):
            def take(n):
                act.wait_ge(s["done"], n + 1)
                if n >= 2:
                    act.wait_ge(s["turned_done"], n - 1)
                    act.wait_ge(s["straight"], n - 1)
                act.activation(raw[:, n % 2, :], K.bank[n % 2][:], ACT.Copy).then_inc(s["raw_out"], 1)
                act.wait_ge(s["raw_out"], n + 1)
                if n >= 2:
                    act.wait_ge(s["norm_done"], n - 1)
                act.activation(sq[:, n % 2, :], raw[:, n % 2, :], ACT.Square).then_inc(s["squared"], 1)
            take(0)
            for n in range(N):
                if n + 1 < N:
                    take(n + 1)
                act.wait_ge(s["norm_done"], n + 1)
                if n >= 2:
                    act.wait_ge(s["out"], n - 1)
                act.activation(rt[:, n % 2, :], K.bank[4 + n % 2][:], ACT.Sqrt).then_inc(s["root_done"], 1)

        @block.gpsimd
        def _(pool):
            for n in range(N):
                pool.wait_ge(s["crossed"], n + 1)
                pool.tensor_tensor(t1[:, n % 2, :], t1[:, n % 2, :], t2[:, n % 2, :], ALU.add).then_inc(s["summed"], 1)

        @block.vector
        def _(dve):
            def products(n):
                m, i = steps[n]
                dve.wait_ge(s["raw_out"], n + 1)
                if n >= 2:
                    dve.wait_ge(s["summed"], n - 1)
                dve.scalar_tensor_tensor(out=t1[:, n % 2, :], in0=raw[:, n % 2, :], scalar=sc, in1=cosT[:, i * BLK:(i + 1) * BLK],
                                         op0=ALU.mult, op1=ALU.mult).then_inc(s["straight"], 1)
                dve.wait_ge(s["turned_done"], n + 1)
                dve.wait_ge(s["straight"], n + 1)
                dve.tensor_tensor(t2[:, n % 2, :], K.bank[2 + n % 2][:], sinT[:, i * BLK:(i + 1) * BLK], ALU.mult).then_inc(s["crossed"], 1)
            products(0)
            for n in range(N):
                m, i = steps[n]
                if n + 1 < N:
                    products(n + 1)
                dve.wait_ge(s["root_done"], n + 1)
                r = rt[:, n % 2, :]
                dve.tensor_scalar(r, r, 1e-12, None, ALU.max)
                dve.drain()
                dve.reciprocal(r, r)
                dve.drain()
                dve.wait_ge(s["summed"], n + 1)
                dve.tensor_tensor(out[:, m, i * BLK:(i + 1) * BLK], t1[:, n % 2, :], r, ALU.mult).then_inc(s["out"], 1)
                dve.drain()


def local_attention(nc, K, b, QT, KT, V, half, window_mask, OT):
    NTB = S // P
    QK_SCALE = 8.0
    with ExitStack() as es, phase(nc, K.sems, "q_spread scored max_done exp_done recip_done normed turned pt_out pv_done out") as (block, s):
        Qh = sbuf(es, nc, "Q_heads", [P, 2, LM, 2, P])
        Pr = sbuf(es, nc, "probs", [P, 2, LH, 2 * P])
        PT = sbuf(es, nc, "probsT", [P, LM, 4 * P])
        stat = sbuf(es, nc, "stat", [P, 2, 3, LH])
        keys = lambda t: slice(0 if t else P, 2 * P)

        @block.tensor
        def _(pe):
            def score(t):
                pe.wait_ge(s["q_spread"], 2 * (t + 1))
                for g in range(LM):
                    if t:
                        pe.wait_ge(s["exp_done"], LH * (t - 1) + 2 * (g + 1))
                    for hh in range(2):
                        ks = keys(t)
                        o = K.bank[g][:, hh * 2 * P + ks.start:(hh + 1) * 2 * P]
                        pe.matmul(o, Qh[:, t % 2, g, hh, :], KT[:, g, t * P - P + ks.start:(t + 1) * P], start=True, stop=False, skip_group_check=True)
                        ins = pe.matmul(o, K.identb[:], window_mask[:, ks], start=False, stop=True, skip_group_check=True)
                    ins.then_inc(s["scored"], 1)

            score(0)
            for t in range(NTB):
                if t + 1 < NTB:
                    score(t + 1)
                kts = (0, 1) if t else (1,)
                for g in range(LM):
                    n = LM * t + g
                    pe.wait_ge(s["normed"], n + 1)
                    if n >= 2:
                        pe.wait_ge(s["pt_out"], n - 1)
                    for hh in range(2):
                        for kt in kts:
                            ins = pe.transpose(K.bank[4 + n % 2][:, (2 * hh + kt) * P:(2 * hh + kt + 1) * P], Pr[:, t % 2, 2 * g + hh, kt * P:(kt + 1) * P], K.ident[:])
                    ins.then_inc(s["turned"], 1)
                for g in range(LM):
                    pe.wait_ge(s["pt_out"], LM * t + g + 1)
                    if g == 0 and t >= 2:
                        pe.wait_ge(s["out"], t - 1)
                    for hh in range(2):
                        for kt in kts:
                            h = 2 * g + hh
                            ins = pe.matmul(K.bank[6 + t % 2][hh * LHD:(hh + 1) * LHD, g * P:(g + 1) * P], V[:, t - 1 + kt, h * LHD:(h + 1) * LHD],
                                            PT[:, g, (2 * hh + kt) * P:(2 * hh + kt + 1) * P], start=(kt == kts[0]), stop=(kt == 1))
                    ins.then_inc(s["pv_done"], 1)

        @block.vector
        def _(dve):
            def spread(t):
                if t >= 2:
                    dve.wait_ge(s["scored"], LM * (t - 1))
                for hh in range(2):
                    dve.tensor_scalar(Qh[:, t % 2, :, hh, :], QT[:, :, t * P:(t + 1) * P], half[:, hh:hh + 1], None, ALU.mult).then_inc(s["q_spread"], 1)

            spread(0)
            for t in range(NTB):
                if t + 1 < NTB:
                    spread(t + 1)
                ks = keys(t)
                if t >= 2:
                    dve.wait_ge(s["exp_done"], LH * (t - 1))
                for g in range(LM):
                    dve.wait_ge(s["scored"], LM * t + g + 1)
                    mx = stat[:, t % 2, 0, 2 * g:2 * g + 2]
                    dve.reduce_max(mx, K.bank[g][:].rearrange("p (h k) -> p h k", h=2)[:, :, ks], AX)
                    dve.drain()
                    dve.tensor_scalar(mx, mx, -QK_SCALE, None, ALU.mult).then_inc(s["max_done"], 1)
                for g in range(LM):
                    dve.wait_ge(s["exp_done"], LH * t + 2 * (g + 1))
                    if g == 0 and t >= 2:
                        dve.wait_ge(s["normed"], LM * (t - 1))
                    dve.reciprocal(stat[:, t % 2, 2, 2 * g:2 * g + 2], stat[:, t % 2, 1, 2 * g:2 * g + 2]).then_inc(s["recip_done"], 1)
                if t:
                    dve.wait_ge(s["pv_done"], LM * t)
                    dve.tensor_copy(OT[:, :, b * S + (t - 1) * P:b * S + t * P], K.bank[6 + (t - 1) % 2][:].rearrange("p (g k) -> p g k", g=LM)).then_inc(s["out"], 1)
            dve.wait_ge(s["pv_done"], LM * NTB)
            t = NTB
            dve.tensor_copy(OT[:, :, b * S + (t - 1) * P:b * S + t * P], K.bank[6 + (t - 1) % 2][:].rearrange("p (g k) -> p g k", g=LM)).then_inc(s["out"], 1)

        @block.gpsimd
        def _(pool):
            for t in range(NTB):
                ks = keys(t)
                for g in range(LM):
                    pool.wait_ge(s["recip_done"], LM * t + g + 1)
                    v = Pr[:, t % 2, 2 * g:2 * g + 2, ks]
                    pool.tensor_tensor(v, v, inner(stat[:, t % 2, 2, 2 * g:2 * g + 2], ks.stop - ks.start), ALU.mult).then_inc(s["normed"], 1)

        @block.scalar
        def _(act):
            def exps(t):
                ks = keys(t)
                for g in range(LM):
                    act.wait_ge(s["max_done"], LM * t + g + 1)
                    if t >= 2:
                        act.wait_ge(s["turned"], LM * (t - 2) + g + 1)
                        act.wait_ge(s["recip_done"], LM * (t - 2) + g + 1)
                    for hh in range(2):
                        h = 2 * g + hh
                        act.activation(Pr[:, t % 2, h, ks], K.bank[g][:, hh * 2 * P + ks.start:hh * 2 * P + ks.stop], ACT.Exp, bias=stat[:, t % 2, 0, h:h + 1],
                                       scale=QK_SCALE, accum_out=stat[:, t % 2, 1, h:h + 1]).then_inc(s["exp_done"], 1)
            exps(0)
            for t in range(NTB):
                if t + 1 < NTB:
                    exps(t + 1)
                for g in range(LM):
                    n = LM * t + g
                    act.wait_ge(s["turned"], n + 1)
                    if t:
                        act.wait_ge(s["pv_done"], n - LM + 1)
                    src, dst = (v.rearrange("p (h k) -> p h k", h=2)[:, :, keys(t)] for v in (K.bank[4 + n % 2][:], PT[:, g, :]))
                    act.activation(dst, src, ACT.Copy).then_inc(s["pt_out"], 1)


def add_residual(nc, K, n_k, wt, src, bias, old, new):
    with phase(nc, K.sems, "done out") as (block, s):
        steps = [(h, j) for j in range(NB) for h in range(DC)]

        @block.tensor
        def _(pe):
            for n, (h, j) in enumerate(steps):
                for k in range(n_k):
                    ins = pe.matmul(K.bank[n][:], wt(k, h), src(k, j), start=(k == 0), stop=(k == n_k - 1))
                ins.then_inc(s["done"], 1)

        @block.vector
        def _(dve):
            for n, (h, j) in enumerate(steps):
                dve.wait_ge(s["done"], n + 1)
                o, d = (v[:, h, j * BLK:(j + 1) * BLK] for v in (old, new))
                if bias is None:
                    dve.tensor_tensor(d, K.bank[n][:], o, ALU.add)
                else:
                    dve.scalar_tensor_tensor(out=d, in0=K.bank[n][:], scalar=bias[:, h:h + 1], in1=o, op0=ALU.add, op1=ALU.add)


def L2_ffn(nc, K, w):
    x0, x1 = K.XT[K.cur], K.XT[1 - K.cur]
    with ExitStack() as es:
        sh = sbuf(es, nc, "shifted", [P, B, 1 + S])
        half = sbuf(es, nc, "head_half", [P, 2])
        ones64 = sbuf(es, nc, "ones64", [P, P])
        J = sbuf(es, nc, "J", [P, P])
        wm = sbuf(es, nc, "window_mask", [P, 2 * P], BF16)
        block_mean(nc, K, ones64[:], LHD)
        block_mean(nc, K, J[:], P)
        with phase(nc, K.sems, "step") as (block, s):
            @block.vector
            def _(dve):
                dve.tensor_scalar(ones64[:], ones64[:], float(LHD), None, ALU.mult)
                dve.tensor_scalar(J[:], J[:], 0.5, None, ALU.mult)
                dve.tensor_copy(wm[:, 0:P], K.below[:])
                dve.tensor_copy(wm[:, P:2 * P], K.above[:])
                dve.drain()
                for hh in range(2):
                    dve.tensor_copy(half[:, hh:hh + 1], ones64[:, hh * LHD:hh * LHD + 1])
                dve.memset(sh[:, :, 0:1], 0.0)
        h_of = lambda X: lambda k, j: X[:, 0, j * BLK:(j + 1) * BLK] if k == 0 else sh[:, j // 2, (j % 2) * BLK:(j % 2) * BLK + BLK]
        for l in range(L2D):
            X = x0 if l == 0 else x1
            pre = f"L2f{l}_"
            shift_half(nc, K, X, sh)
            with ExitStack() as att:
                OT = sbuf(att, nc, "OT", [P, LM, TOK])
                with ExitStack() as inn:
                    W = sbuf(inn, nc, "Wqkv", [P, DC, 3 * LM * P])
                    tab = sbuf(inn, nc, "tables", [P, 4, S])
                    rot = sbuf(inn, nc, "rotation", [P, 2, P])
                    qs = sbuf(inn, nc, "scales", [P, 2])
                    QT, KT = (sbuf(inn, nc, n, [P, LM, S]) for n in ("QT", "KT"))
                    load(nc, K, (W[:], w[pre + "Wqkv"]), (tab[:], w["L2f_tab"]), (rot[:, 0, :], w["L2f_rot"]), (rot[:, 1, :], w["L2f_rot"]),
                         (qs[:, 0:1], w[pre + "qs"]), (qs[:, 1:2], w[pre + "ks"]))
                    with phase(nc, K.sems, "step") as (block, s):
                        @block.vector
                        def _(dve):
                            for i in range(2):
                                dve.tensor_scalar(rot[:, i, :], rot[:, i, :], qs[:, i:i + 1], None, ALU.mult)
                    for b in range(B):
                        src = lambda k, i: h_of(X)(k, 2 * b + i)
                        for i, dst in enumerate((QT, KT)):
                            local_qk(nc, K, b, src, W, i * LM * P, rot[:, i, :], qs[:, i:i + 1], tab[:, 2 * i, :], tab[:, 2 * i + 1, :], ones64[:], dst)
                        V = K.Xtok[:].rearrange("p (t c) d -> p t (c d)", c=2)
                        with phase(nc, K.sems, "done out") as (block, s):
                            @block.tensor
                            def _(pe):
                                for t in range(S // P):
                                    for k in range(DC):
                                        a = X[:, 0, b * S + t * P:b * S + (t + 1) * P] if k == 0 else sh[:, b, t * P:(t + 1) * P]
                                        ins = pe.matmul(K.bank[t][:], a, W[:, k, 2 * LM * P:3 * LM * P], start=(k == 0), stop=(k == DC - 1))
                                    ins.then_inc(s["done"], 1)

                            @block.scalar
                            def _(act):
                                for t in range(S // P):
                                    act.wait_ge(s["done"], t + 1)
                                    act.activation(V[:, t, :], K.bank[t][:], ACT.Copy)
                        local_attention(nc, K, b, QT, KT, V, half, wm, OT)
                with ExitStack() as inn:
                    Wo = sbuf(inn, nc, "Wo", [P, LM, D])
                    load(nc, K, (Wo[:], w[pre + "Wo"]))
                    add_residual(nc, K, LM, lambda k, h: Wo[:, k, h * P:(h + 1) * P], block_of(OT), None, X, x1)
            shift_half(nc, K, x1, sh)
            with ExitStack() as ff:
                W2 = sbuf(ff, nc, "W2", [P, HIDP // P, D])
                b2 = sbuf(ff, nc, "b2", [P, DC])
                GT = sbuf(ff, nc, "GT", [P, HIDP // P, TOK])
                with ExitStack() as inn:
                    W1 = sbuf(inn, nc, "W1", [P, DC, 2 * HIDP])
                    b1 = sbuf(inn, nc, "b1", [P, 2 * HIDP // P])
                    g, b_ = (sbuf(inn, nc, n, [P, DC]) for n in ("g", "b"))
                    Hn = sbuf(inn, nc, "Hn", [P, DC, TOK])
                    ge = sbuf(inn, nc, "gelu", [P, 2, BLK])
                    load(nc, K, (W1[:], w[pre + "W1"]), (b1[:], w[pre + "b1"]), (g[:], w[pre + "g"]), (b_[:], w[pre + "b"]), (W2[:], w[pre + "W2"]), (b2[:], w[pre + "b2"]))
                    feature_ln(nc, K, J[:], NB, DC, lambda j, h: h_of(x1)(h, j), lambda j, h: Hn[:, h, j * BLK:(j + 1) * BLK], lambda j: g[:], lambda j: b_[:])
                    HC = HIDP // P
                    steps = [(m, j) for m in range(HC) for j in range(NB)]
                    with phase(nc, K.sems, "done gelu_done out") as (block, s):
                        @block.tensor
                        def _(pe):
                            for n, (m, j) in enumerate(steps):
                                if n >= 4:
                                    pe.wait_ge(s["out"], n - 3)
                                for part in range(2):
                                    for k in range(DC):
                                        ins = pe.matmul(K.bank[2 * (n % 4) + part][:], W1[:, k, (part * HC + m) * P:(part * HC + m + 1) * P],
                                                        Hn[:, k, j * BLK:(j + 1) * BLK], start=(k == 0), stop=(k == DC - 1))
                                ins.then_inc(s["done"], 1)

                        @block.scalar
                        def _(act):
                            for n, (m, j) in enumerate(steps):
                                act.wait_ge(s["done"], n + 1)
                                if n >= 2:
                                    act.wait_ge(s["out"], n - 1)
                                act.activation(ge[:, n % 2, :], K.bank[2 * (n % 4) + 1][:], ACT.Gelu, bias=b1[:, HC + m:HC + m + 1]).then_inc(s["gelu_done"], 1)

                        @block.vector
                        def _(dve):
                            for n, (m, j) in enumerate(steps):
                                dve.wait_ge(s["gelu_done"], n + 1)
                                dve.scalar_tensor_tensor(out=GT[:, m, j * BLK:(j + 1) * BLK], in0=K.bank[2 * (n % 4)][:], scalar=b1[:, m:m + 1],
                                                         in1=ge[:, n % 2, :], op0=ALU.add, op1=ALU.mult).then_inc(s["out"], 1)
                if l < L2D - 1:
                    add_residual(nc, K, HIDP // P, lambda k, h: W2[:, k, h * P:(h + 1) * P], block_of(GT), b2, x1, x1)
                else:
                    with phase(nc, K.sems, "step") as (block, s):
                        @block.vector
                        def _(dve):
                            dve.tensor_tensor(x1[:, 0, :], x1[:, 0, :], x0[:, 0, :], ALU.add)

                        @block.gpsimd
                        def _(pool):
                            pool.tensor_tensor(x1[:, 1, :], x1[:, 1, :], x0[:, 1, :], ALU.add)
                    finish(nc, K, lambda k, h, j: W2[:, k, h * P:(h + 1) * P], block_of(GT), HIDP // P, bias=b2, res=x1)


def program(nc, w, out, first=0, last=12):
    stored = nc.alloc_semaphore("stored")
    with ExitStack() as es:
        K = Fixed()
        K.sems, K.cur = [], 0
        K.XT = [sbuf(es, nc, f"XT{i}", [P, DC, TOK]) for i in range(2)]
        K.Xtok = sbuf(es, nc, "Xtok", [P, NT, D])
        K.ctxT = sbuf(es, nc, "ctxT", [P, DC, B, 256])
        K.ones = sbuf(es, nc, "ones", [P, 8 * P])
        K.ident = sbuf(es, nc, "ident", [P, P])
        K.identb = sbuf(es, nc, "identb", [P, P], BF16)
        K.causal_T = sbuf(es, nc, "causal_T", [P, P])
        K.head_cols = sbuf(es, nc, "head_cols", [P, 8, P])
        K.head_rows = sbuf(es, nc, "head_rows", [P, 8])
        K.above = sbuf(es, nc, "above", [P, P], BF16)
        K.below = sbuf(es, nc, "below", [P, P], BF16)
        K.live_keys = sbuf(es, nc, "live_keys", [P, 1])
        K.eps = sbuf(es, nc, "eps", [P, 1])
        K.psum = es.enter_context(nc.psum_tensor("psum", [P, 8, BLK], F32))
        K.bank = [K.psum[:, i, :] for i in range(8)]
        setup(nc, K, w)
        for sublayer in SUBLAYERS[first:last]:
            sublayer(nc, K, w)
        with nc.Block() as block:
            @block.sync
            def _(sp):
                sp.dma_start(out.rearrange("b (t p) d -> p (b t) d", p=P), K.Xtok[:]).then_inc(stored, 16)
                sp.wait_ge(stored, 16)


def layouts(i):
    x = np.asarray(i["x"]).reshape(TOK, D)
    out = {"xT": rows(x.T), "xtok": rows(x)}
    ctx = np.concatenate([pad(np.asarray(i["ctx_1024"])[b].T, 1, 2 * P) for b in range(B)], axis=1)
    out["ctxT"] = rows(ctx).reshape(P, DC, B, 2 * P)
    for f in LAYOUTS:
        out.update(f(i))
    return out


LAYOUTS = (L0_attn_layout, L0_xattn_layout, L0_ffn_layout, L1_attn_layout, L1_xattn_layout, L1_ffn_layout,
           L2_attn_layout, L2_xattn_layout, L2_ffn_layout, L3_attn_layout, L3_xattn_layout, L3_ffn_layout)
SUBLAYERS = (L0_attn, L0_xattn, L0_ffn, L1_attn, L1_xattn, L1_ffn, L2_attn, L2_xattn, L2_ffn, L3_attn, L3_xattn, L3_ffn)


def kernel(**inputs):
    import concourse.bacc as _bacc
    from concourse import mybir as _mybir
    from concourse.bass_utils import run_bass_kernel_spmd as _run

    nc = _bacc.Bacc("TRN2", target_bir_lowering=False, num_devices=1)
    arrays, w = {}, {}
    for name, a in layouts(inputs).items():
        a = np.ascontiguousarray(a)
        arrays[f"in_{name}"] = a
        w[name] = nc.dram_tensor(f"in_{name}", a.shape, _mybir.dt.from_np(a.dtype), kind="ExternalInput").ap()
    out = nc.dram_tensor("out", (B, S, D), _mybir.dt.float32, kind="ExternalOutput").ap()
    program(nc, w, out)
    return _run(nc, [arrays], core_ids=[0]).results[0]["out"]
```

```python
from contextlib import ExitStack, contextmanager

import numpy as np

import concourse.bass as bass
from concourse import mybir

F32 = mybir.dt.float32
BF16 = mybir.dt.bfloat16
I32 = mybir.dt.int32
U32 = mybir.dt.uint32
ALU = mybir.AluOpType
ACT = mybir.ActivationFunctionType
AX = mybir.AxisListType.X

P = 128
B = 2
S = 1024
D = 256
DC = D // P
TOK = B * S
NT = TOK // P
BLK = 512
NB = TOK // BLK
TPB = BLK // P
CTX = 154
LN_EPS = 1e-5
NEG = -1e30
SEM_LIMIT = 100


class Fixed:
    pass


@contextmanager
def phase(nc, pool, names):
    names = names.split()
    if len(pool) + len(names) > SEM_LIMIT:
        nc.clear_and_free_semaphores(list(pool))
        nc.all_engine_barrier()
        pool.clear()
    sems = {n: nc.alloc_semaphore(f"{n}_{nc.next_id()}") for n in names}
    pool.extend(sems.values())
    with nc.Block() as block:
        yield block, sems


def sbuf(es, nc, name, shape, dt=F32):
    return es.enter_context(nc.sbuf_tensor(f"{name}_{nc.next_id()}", shape, dt))


def spread(v, parts=P):
    return v.rearrange("(o n) -> o n", o=1).broadcast_to((parts, v.shape[0]))



def rows(a):
    a = np.asarray(a)
    return np.ascontiguousarray(a.reshape(a.shape[0] // P, P, -1).transpose(1, 0, 2))


def cols(v):
    return np.ascontiguousarray(np.asarray(v).reshape(-1, P).T)


def pad(a, axis, n):
    width = [(0, 0)] * a.ndim
    width[axis] = (0, n - a.shape[axis])
    return np.pad(np.asarray(a), width)


def setup(nc, K, w):
    with phase(nc, K.sems, "loaded ones_set masks_set") as (block, s):
        @block.sync
        def _(sp):
            sp.dma_start(K.XT[0][:], w["xT"]).then_inc(s["loaded"], 16)
            sp.dma_start(K.ctxT[:], w["ctxT"]).then_inc(s["loaded"], 16)
            sp.dma_start(K.Xtok[:], w["xtok"]).then_inc(s["loaded"], 16)
            sp.wait_ge(s["loaded"], 16 * 3)

        @block.gpsimd
        def _(pool):
            pool.memset(K.eps[:], LN_EPS)
            pool.memset(K.ones[:], 1.0).then_inc(s["ones_set"], 1)
            pool.wait_ge(s["ones_set"], 1)

            def select(out, op, base, pattern, mult, fill=0.0, src=None):
                return pool.affine_select(out=out, in_=out if src is None else src, compare_op=op, fill=fill,
                                          base=base, pattern=pattern, channel_multiplier=mult)
            ones = K.ones[:, 0:P]
            select(K.ident[:], ALU.is_equal, 0, [[-1, P]], 1, src=ones).then_inc(s["masks_set"], 1)
            select(K.identb[:], ALU.is_equal, 0, [[-1, P]], 1, src=ones).then_inc(s["masks_set"], 1)
            select(K.causal_T[:], ALU.is_ge, 0, [[1, P]], -1, src=ones).then_inc(s["masks_set"], 1)
            o8 = K.ones[:, 0:8 * P].rearrange("p (h j) -> p h j", h=8)
            select(K.head_cols[:], ALU.is_ge, 0, [[-16, 8], [1, P]], 0, src=o8).then_inc(s["masks_set"], 1)
            pool.wait_ge(s["masks_set"], 4)
            select(K.head_cols[:], ALU.is_ge, 15, [[16, 8], [-1, P]], 0).then_inc(s["masks_set"], 1)
            select(K.head_rows[:], ALU.is_ge, 0, [[-16, 8]], 1, src=K.ones[:, 0:8]).then_inc(s["masks_set"], 1)
            pool.wait_ge(s["masks_set"], 6)
            select(K.head_rows[:], ALU.is_ge, 15, [[16, 8]], -1).then_inc(s["masks_set"], 1)
            pool.memset(K.above[:], 0.0).then_inc(s["masks_set"], 1)
            pool.memset(K.below[:], 0.0).then_inc(s["masks_set"], 1)
            pool.wait_ge(s["masks_set"], 9)
            select(K.above[:], ALU.is_ge, 0, [[-1, P]], 1, fill=NEG).then_inc(s["masks_set"], 1)
            select(K.below[:], ALU.is_ge, 0, [[1, P]], -1, fill=NEG).then_inc(s["masks_set"], 1)
            select(K.live_keys[:], ALU.is_ge, CTX - P - 1, [[0, 1]], -1, src=K.ones[:, 0:1]).then_inc(s["masks_set"], 1)


def ln_stats(dve, st, r):
    dve.bn_stats(st[:, 2:8], r)
    dve.drain()
    return dve.bn_aggr(st[:, 0:2], st[:, 2:8])


def ln_std(act, K, st):
    return act.activation(st[:, 8:9], st[:, 1:2], ACT.Sqrt, bias=K.eps[:, 0:1])


def ln_apply(dve, st, r, out):
    dve.reciprocal(st[:, 8:9], st[:, 8:9])
    dve.drain()
    return dve.tensor_scalar(out, r, st[:, 0:1], st[:, 8:9], ALU.subtract, ALU.mult)


def finish(nc, K, wt, src, n_k, bias=None, relu=False, res=None):
    xi, xo = K.XT[K.cur], K.XT[1 - K.cur]
    res = res or xi
    with ExitStack() as es, phase(nc, K.sems, "y_done sum_done turned stats_done std_done tok_done back_turned copied") as (block, s):
        rT = sbuf(es, nc, "rT", [P, 2, DC, BLK])
        st = sbuf(es, nc, "ln_stats", [P, NT, 9])

        @block.tensor
        def _(pe):
            def product(j):
                if j >= 2:
                    pe.wait_ge(s["sum_done"], j - 1)
                for h in range(DC):
                    for k in range(n_k):
                        last = pe.matmul(K.bank[2 * (j % 2) + h][:], wt(k, h, j), src(k, j), start=(k == 0), stop=(k == n_k - 1))
                last.then_inc(s["y_done"], 1)

            def turn_back(t):
                pe.wait_ge(s["tok_done"], t + 1)
                if t >= 2:
                    pe.wait_ge(s["copied"], t - 1)
                for h in range(DC):
                    last = pe.transpose(K.bank[6 + t % 2][:, h * P:(h + 1) * P], K.Xtok[:, t, h * P:(h + 1) * P], K.ident[:])
                last.then_inc(s["back_turned"], 1)

            product(0)
            for j in range(NB):
                if j + 1 < NB:
                    product(j + 1)
                pe.wait_ge(s["sum_done"], j + 1)
                for t in range(TPB * j, TPB * (j + 1)):
                    if t >= 2:
                        pe.wait_ge(s["tok_done"], t - 1)
                    for h in range(DC):
                        last = pe.transpose(K.bank[4 + t % 2][:, h * P:(h + 1) * P],
                                            rT[:, j % 2, h, (t % TPB) * P:(t % TPB + 1) * P], K.ident[:])
                    last.then_inc(s["turned"], 1)
                    if t > 0:
                        turn_back(t - 1)
            turn_back(NT - 1)

        @block.vector
        def _(dve):
            def add(j):
                dve.wait_ge(s["y_done"], j + 1)
                for h in range(DC):
                    y = K.bank[2 * (j % 2) + h][:]
                    old = res[:, h, j * BLK:(j + 1) * BLK]
                    if relu:
                        last = dve.scalar_tensor_tensor(out=rT[:, j % 2, h, :], in0=y, scalar=0.0, in1=old, op0=ALU.max, op1=ALU.add)
                    elif bias is not None:
                        last = dve.scalar_tensor_tensor(out=rT[:, j % 2, h, :], in0=y, scalar=bias[:, h:h + 1], in1=old,
                                                        op0=ALU.add, op1=ALU.add)
                    else:
                        last = dve.tensor_tensor(rT[:, j % 2, h, :], y, old, ALU.add)
                    if h == 0:
                        dve.drain()
                last.then_inc(s["sum_done"], 1)

            def normalise(t):
                dve.wait_ge(s["std_done"], t + 1)
                ln_apply(dve, st[:, t, :], K.bank[4 + t % 2][:, 0:D], K.Xtok[:, t, :]).then_inc(s["tok_done"], 1)

            add(0)
            for j in range(NB):
                for t in range(TPB * j, TPB * (j + 1)):
                    dve.wait_ge(s["turned"], t + 1)
                    ln_stats(dve, st[:, t, :], K.bank[4 + t % 2][:, 0:D]).then_inc(s["stats_done"], 1)
                    if t > 0:
                        normalise(t - 1)
                    if t % TPB == 1 and j + 1 < NB:
                        add(j + 1)
            normalise(NT - 1)

        @block.scalar
        def _(act):
            for t in range(NT + 1):
                if t < NT:
                    act.wait_ge(s["stats_done"], t + 1)
                    ln_std(act, K, st[:, t, :]).then_inc(s["std_done"], 1)
                if t > 0:
                    act.wait_ge(s["back_turned"], t)
                    act.activation(xo[:, :, (t - 1) * P:t * P], K.bank[6 + (t - 1) % 2][:, 0:D].rearrange("p (c k) -> p c k", c=2),
                                   ACT.Copy).then_inc(s["copied"], 1)
    K.cur = 1 - K.cur


def project(nc, K, es, n_m, n_k, wt, src, evac_act, evac_dve, n_blk=NB, loads=(), width=lambda j: BLK):
    with phase(nc, K.sems, "loaded done act_out dve_out") as (block, s):
        steps = [(m, j) for m in range(n_m) for j in range(n_blk)]

        @block.sync
        def _(sp):
            for dst, srcd in loads:
                sp.dma_start(dst, srcd).then_inc(s["loaded"], 16)

        @block.tensor
        def _(pe):
            pe.wait_ge(s["loaded"], 16 * len(loads)) if loads else None
            for n, (m, j) in enumerate(steps):
                if n >= 8:
                    pe.wait_ge(s["act_out"] if n % 2 == 0 else s["dve_out"], (n - 8) // 2 + 1)
                for k in range(n_k):
                    last = pe.matmul(K.bank[n % 8][:, 0:width(j)], wt(k, m), src(k, j), start=(k == 0), stop=(k == n_k - 1))
                last.then_inc(s["done"], 1)

        @block.scalar
        def _(act):
            act.wait_ge(s["loaded"], 16 * len(loads)) if loads else None
            for n, (m, j) in enumerate(steps):
                if n % 2 == 0:
                    act.wait_ge(s["done"], n + 1)
                    evac_act(act, m, j, K.bank[n % 8][:, 0:width(j)]).then_inc(s["act_out"], 1)

        @block.vector
        def _(dve):
            dve.wait_ge(s["loaded"], 16 * len(loads)) if loads else None
            for n, (m, j) in enumerate(steps):
                if n % 2 == 1:
                    dve.wait_ge(s["done"], n + 1)
                    evac_dve(dve, m, j, K.bank[n % 8][:, 0:width(j)]).then_inc(s["dve_out"], 1)


def load(nc, K, *pairs):
    with phase(nc, K.sems, "loaded") as (block, s):
        @block.sync
        def _(sp):
            for dst, src in pairs[0::2]:
                sp.dma_start(dst, src).then_inc(s["loaded"], 16)
            sp.wait_ge(s["loaded"], 16 * len(pairs))

        @block.scalar
        def _(act):
            for dst, src in pairs[1::2]:
                act.dma_start(dst, src).then_inc(s["loaded"], 16)


def copy_to(dst, bias=None, relu=False):
    def by_act(act, m, j, src):
        if bias is None:
            return act.activation(dst(m, j), src, ACT.Copy)
        return act.activation(dst(m, j), src, ACT.Relu if relu else ACT.Identity, bias=bias(m))

    def by_dve(dve, m, j, src):
        if bias is None:
            return dve.tensor_copy(dst(m, j), src)
        if relu:
            return dve.tensor_scalar(dst(m, j), src, bias(m), 0.0, ALU.add, ALU.max)
        return dve.tensor_scalar(dst(m, j), src, bias(m), None, ALU.add)
    return by_act, by_dve


def block_of(xT):
    return lambda k, j: xT[:, k, j * BLK:(j + 1) * BLK]


def ctx_values(nc, K, V, Wv, bias_row, relu, live=True):
    with phase(nc, K.sems, "done summed") as (block, s):
        @block.tensor
        def _(pe):
            for n in range(2 * B):
                b, kt = divmod(n, 2)
                for k in range(DC):
                    last = pe.matmul(K.bank[n][:, 0:D], K.ctxT[:, k, b, kt * P:(kt + 1) * P], Wv[:, k, :], start=(k == 0), stop=(k == DC - 1))
                last.then_inc(s["done"], 1)

        @block.vector
        def _(dve):
            for n in range(2 * B):
                b, kt = divmod(n, 2)
                v = V[:, b, kt, :]
                dve.wait_ge(s["done"], n + 1)
                dve.tensor_tensor(v, K.bank[n][:, 0:D], bias_row, ALU.add)
                dve.drain()
                if relu:
                    dve.tensor_scalar(v, v, 0.0, None, ALU.max)
                    dve.drain()
                if kt == 1:
                    dve.tensor_scalar(v, v, K.live_keys[:, 0:1], None, ALU.mult)
                    dve.drain()


def L1_xattn_layout(i):
    maskT = np.ascontiguousarray(pad(np.asarray(i["mask_1xSxS2_ff0"])[0].T, 0, 2 * P))
    return {"L1x_Wq": rows(i["L1_xattn_kernel_q"][0, 0]), "L1x_Wk": rows(i["L1_xattn_kernel_k"][0, 0]),
            "L1x_Wv": rows(i["L1_xattn_kernel_v"][0, 0]), "L1x_bq": cols(i["L1_xattn_bias_q"]),
            "L1x_bk": cols(i["L1_xattn_bias_k"]), "L1x_bv": np.asarray(i["L1_xattn_bias_v"]), "L1x_maskT": rows(maskT)}


def L1_xattn(nc, K, w):
    with ExitStack() as es:
        Wq, Wk, Wv = (sbuf(es, nc, n, [P, DC, D]) for n in ("Wq", "Wk", "Wv"))
        bq, bk = (sbuf(es, nc, n, [P, DC]) for n in ("bq", "bk"))
        bv = sbuf(es, nc, "bv", [P, D])
        maskT = sbuf(es, nc, "maskT", [P, 2, S])
        QT = sbuf(es, nc, "QT", [P, DC, TOK])
        KT = sbuf(es, nc, "KT", [P, DC, B * 256])
        V = sbuf(es, nc, "V", [P, B, 2, D])
        ST = sbuf(es, nc, "ST", [P, 2, TOK])
        load(nc, K, (Wq[:], w["L1x_Wq"]), (Wk[:], w["L1x_Wk"]), (Wv[:], w["L1x_Wv"]), (bq[:], w["L1x_bq"]),
             (bk[:], w["L1x_bk"]), (bv[:], spread(w["L1x_bv"])), (maskT[:], w["L1x_maskT"]))
        a, v = copy_to(lambda m, j: QT[:, m, j * BLK:(j + 1) * BLK], lambda m: bq[:, m:m + 1], True)
        project(nc, K, es, DC, DC, lambda k, m: Wq[:, k, m * P:(m + 1) * P], block_of(K.XT[K.cur]), a, v)
        a, v = copy_to(lambda m, j: KT[:, m, :], lambda m: bk[:, m:m + 1], True)
        project(nc, K, es, DC, DC, lambda k, m: Wk[:, k, m * P:(m + 1) * P],
                lambda k, j: K.ctxT[:, k].rearrange("p b n -> p (b n)"), a, v, n_blk=1)
        ctx_values(nc, K, V, Wv, bv[:], True)
        with phase(nc, K.sems, "done relued masked") as (block, s):
            @block.tensor
            def _(pe):
                for n in range(2 * NB):
                    j, kt = divmod(n, 2)
                    for k in range(DC):
                        last = pe.matmul(K.bank[n][:], KT[:, k, (j // 2) * 256 + kt * P:(j // 2) * 256 + (kt + 1) * P],
                                         QT[:, k, j * BLK:(j + 1) * BLK], start=(k == 0), stop=(k == DC - 1))
                    last.then_inc(s["done"], 1)

            @block.scalar
            def _(act):
                for n in range(2 * NB):
                    act.wait_ge(s["done"], n + 1)
                    j, kt = divmod(n, 2)
                    act.activation(ST[:, kt, j * BLK:(j + 1) * BLK], K.bank[n][:], ACT.Relu, scale=float(D) ** -0.5).then_inc(s["relued"], 1)

            @block.vector
            def _(dve):
                for n in range(2 * NB):
                    dve.wait_ge(s["relued"], n + 1)
                    j, kt = divmod(n, 2)
                    st = ST[:, kt, j * BLK:(j + 1) * BLK]
                    dve.tensor_tensor(st, st, maskT[:, kt, (j % 2) * BLK:(j % 2 + 1) * BLK], ALU.add)
        finish(nc, K, lambda k, h, j: V[:, j // 2, k, h * P:(h + 1) * P], block_of(ST), 2, relu=True)


HEADS = 16
HD = D // HEADS
HPC = P // HD
HK = HPC * CTX
HKT = -(-HK // P)
GROUPS = [(0, 3), (3, 3), (6, 2)]
ALIBI_OFF = S - CTX


def middle(ap, n):
    return ap.unsqueeze(1).broadcast_to((ap.shape[0], n, ap.shape[1]))


def inner(ap, n):
    return ap.unsqueeze(2).broadcast_to((ap.shape[0], ap.shape[1], n))


def cross_attention(nc, K, w, pre, scale, slopes=None):
    with ExitStack() as es:
        Wo = sbuf(es, nc, "Wo", [P, DC, D])
        bo = sbuf(es, nc, "bo", [P, DC])
        OT = sbuf(es, nc, "OT", [P, DC, TOK])
        with ExitStack() as inside:
            Vb = sbuf(inside, nc, "Vblocks", [P, DC, B, HKT, P])
            Kb = sbuf(inside, nc, "Kblocks", [P, DC, B, HK])
            QT = sbuf(inside, nc, "QT", [P, DC, TOK])
            Pr = sbuf(inside, nc, "probs", [P, 2 * 2 * HK])
            with ExitStack() as temp:
                Wq, Wk, Wv = (sbuf(temp, nc, n, [P, DC, D]) for n in ("Wq", "Wk", "Wv"))
                bq, bk, bv = (sbuf(temp, nc, n, [P, DC]) for n in ("bq", "bk", "bv"))
                KT, VT = (sbuf(temp, nc, n, [P, DC, B * 256]) for n in ("KT", "VT"))
                load(nc, K, (Wq[:], w[pre + "Wq"]), (Wk[:], w[pre + "Wk"]), (Wv[:], w[pre + "Wv"]), (Wo[:], w[pre + "Wo"]),
                     (bq[:], w[pre + "bq"]), (bk[:], w[pre + "bk"]), (bv[:], w[pre + "bv"]), (bo[:], w[pre + "bo"]))
                a, v = copy_to(lambda m, j: QT[:, m, j * BLK:(j + 1) * BLK], lambda m: bq[:, m:m + 1])
                project(nc, K, es, DC, DC, lambda k, m: Wq[:, k, m * P:(m + 1) * P], block_of(K.XT[K.cur]), a, v)
                ctx = lambda k, j: K.ctxT[:, k].rearrange("p b n -> p (b n)")
                a, v = copy_to(lambda m, j: KT[:, m, :], lambda m: bk[:, m:m + 1])
                project(nc, K, es, DC, DC, lambda k, m: Wk[:, k, m * P:(m + 1) * P], ctx, a, v, n_blk=1)
                a, v = copy_to(lambda m, j: VT[:, m, :], lambda m: bv[:, m:m + 1])
                project(nc, K, es, DC, DC, lambda k, m: Wv[:, k, m * P:(m + 1) * P], ctx, a, v, n_blk=1)
                with phase(nc, K.sems, "spread turned out") as (block, s):
                    VbT = Pr[:].rearrange("p (n hk) -> p n hk", hk=HK)

                    @block.vector
                    def _(dve):
                        for n in range(DC * B):
                            c, b = divmod(n, B)
                            dve.tensor_tensor(VbT[:, n, :].rearrange("p (h k) -> p h k", h=HPC), middle(VT[:, c, b * 256:b * 256 + CTX], HPC),
                                              inner(K.head_rows[:], CTX), ALU.mult).then_inc(s["spread"], 1)
                        for n in range(DC * B):
                            c, b = divmod(n, B)
                            dve.tensor_tensor(Kb[:, c, b, :].rearrange("p (h k) -> p h k", h=HPC), middle(KT[:, c, b * 256:b * 256 + CTX], HPC),
                                              inner(K.head_rows[:], CTX), ALU.mult)

                    @block.tensor
                    def _(pe):
                        for n in range(DC * B):
                            pe.wait_ge(s["spread"], n + 1)
                            for g in range(3):
                                if 3 * n + g >= 8:
                                    pe.wait_ge(s["out"], 3 * n + g - 7)
                                for i in range(4 * g, min(4 * g + 4, HKT)):
                                    r = min(P, HK - i * P)
                                    last = pe.transpose(K.bank[(3 * n + g) % 8][0:r, (i % 4) * P:(i % 4 + 1) * P],
                                                        VbT[:, n, i * P:i * P + r], K.ident[:])
                                last.then_inc(s["turned"], 1)

                    @block.scalar
                    def _(act):
                        for n in range(DC * B):
                            c, b = divmod(n, B)
                            for g in range(3):
                                act.wait_ge(s["turned"], 3 * n + g + 1)
                                src = K.bank[(3 * n + g) % 8]
                                if g < 2:
                                    act.activation(Vb[:, c, b, 4 * g:4 * g + 4, :], src[:].rearrange("p (i k) -> p i k", i=4), ACT.Copy).then_inc(s["out"], 1)
                                else:
                                    act.activation(Vb[:, c, b, 8, :], src[:, 0:P], ACT.Copy)
                                    act.activation(Vb[0:HK - 9 * P, c, b, 9, :], src[0:HK - 9 * P, P:2 * P], ACT.Copy).then_inc(s["out"], 1)

            PT = sbuf(inside, nc, "probsT", [P, HKT, P])
            stat = sbuf(inside, nc, "stat", [P, 2, 3, HPC])
            Rx = sbuf(inside, nc, "recip_spread", [P, 2, P])
            RT = sbuf(inside, nc, "recipT", [P, 2, P])
            names = "recip_spread recip_turned scored max_done exp_done recip_done turned probs_out recip_out pv_done out"
            with phase(nc, K.sems, names) as (block, s):
                steps = NT * DC
                sc = lambda n, g: K.bank[3 * (n % 2) + g]
                probs = lambda n: Pr[:].rearrange("p (n hk) -> p n hk", hk=HK)[:, n % 2, :]
                st = lambda n, i: stat[:, n % 2, i, :]

                @block.gpsimd
                def _(pool):
                    for n in range(steps):
                        pool.wait_ge(s["recip_done"], n + 1)
                        pool.tensor_copy(Rx[:, n % 2, :].rearrange("p (h d) -> p h d", h=HPC), inner(st(n, 2), HD)).then_inc(s["recip_spread"], 1)

                @block.tensor
                def _(pe):
                    def score(n, g):
                        t, c = divmod(n, DC)
                        if g == 0 and n >= 2:
                            pe.wait_ge(s["probs_out"], 3 * (n - 1))
                            pe.wait_ge(s["recip_out"], n - 1)
                        h0, nh = GROUPS[g]
                        pe.matmul(sc(n, g)[:, 0:nh * CTX], QT[:, c, t * P:(t + 1) * P],
                                  Kb[:, c, t // 8, h0 * CTX:(h0 + nh) * CTX], start=True, stop=True).then_inc(s["scored"], 1)

                    def turn(n, g):
                        pe.wait_ge(s["exp_done"], 3 * n + g + 1)
                        for i in range(4 * g, min(4 * g + 4, HKT)):
                            r = min(P, HK - i * P)
                            last = pe.transpose(sc(n, g)[0:r, (i % 4) * P:(i % 4 + 1) * P], probs(n)[:, i * P:i * P + r], K.ident[:])
                        last.then_inc(s["turned"], 1)

                    for g in range(3):
                        score(0, g)
                    for n in range(steps):
                        t, c = divmod(n, DC)
                        turn(n, 0)
                        if n + 1 < steps:
                            score(n + 1, 0)
                            score(n + 1, 1)
                        turn(n, 1)
                        if n + 1 < steps:
                            score(n + 1, 2)
                        turn(n, 2)
                        if n >= 2:
                            pe.wait_ge(s["out"], n - 1)
                        for i in range(HKT):
                            r = min(P, HK - i * P)
                            if i % 4 == 0:
                                pe.wait_ge(s["probs_out"], 3 * n + i // 4 + 1)
                            last = pe.matmul(K.bank[6 + n % 2][:, 0:P], Vb[0:r, c, t // 8, i, :], PT[0:r, i, :], start=(i == 0), stop=(i == HKT - 1))
                        last.then_inc(s["pv_done"], 1)
                        pe.wait_ge(s["recip_spread"], n + 1)
                        pe.transpose(sc(n, 2)[:, 2 * P:3 * P], Rx[:, n % 2, :], K.ident[:]).then_inc(s["recip_turned"], 1)

                @block.vector
                def _(dve):
                    def bias(n, g):
                        t, c = divmod(n, DC)
                        h0, nh = GROUPS[g]
                        dve.wait_ge(s["scored"], 3 * n + g + 1)
                        for h in range(h0, h0 + nh) if slopes else ():
                            dve.scalar_tensor_tensor(out=probs(n)[:, h * CTX:(h + 1) * CTX], in0=K.rel[:, t % 8, :],
                                                     scalar=-slopes[c * HPC + h] / scale,
                                                     in1=sc(n, g)[:, (h - h0) * CTX:(h - h0 + 1) * CTX], op0=ALU.mult, op1=ALU.add)

                    def reduce(n, g):
                        h0, nh = GROUPS[g]
                        src = probs(n)[:, h0 * CTX:(h0 + nh) * CTX] if slopes else sc(n, g)[:, 0:nh * CTX]
                        dve.reduce_max(st(n, 0)[:, h0:h0 + nh], src.rearrange("p (h k) -> p h k", h=nh), AX)

                    def negate(n, h0, h1):
                        dve.tensor_scalar(st(n, 0)[:, h0:h1], st(n, 0)[:, h0:h1], -scale, None, ALU.mult).then_inc(s["max_done"], 1)

                    def maxima(n, groups):
                        if slopes and n >= 2 and groups[0] == 0:
                            dve.wait_ge(s["turned"], 3 * (n - 1))
                        for g in groups:
                            bias(n, g)
                        if slopes:
                            dve.drain()
                        for g in groups:
                            reduce(n, g)
                        dve.drain()
                        negate(n, GROUPS[groups[0]][0], GROUPS[groups[-1]][0] + GROUPS[groups[-1]][1])

                    def probs_out(n, g):
                        dve.wait_ge(s["turned"], 3 * n + g + 1)
                        if g < 2:
                            dve.tensor_copy(PT[:, 4 * g:4 * g + 4, :], sc(n, g)[:].rearrange("p (i k) -> p i k", i=4)).then_inc(s["probs_out"], 1)
                        else:
                            dve.tensor_copy(PT[:, 8, :], sc(n, g)[:, 0:P])
                            dve.tensor_copy(PT[0:HK - 9 * P, 9, :], sc(n, g)[0:HK - 9 * P, P:2 * P]).then_inc(s["probs_out"], 1)

                    def output(n):
                        t, c = divmod(n, DC)
                        dve.wait_ge(s["pv_done"], n + 1)
                        dve.wait_ge(s["recip_out"], n + 1)
                        dve.tensor_tensor(OT[:, c, t * P:(t + 1) * P], K.bank[6 + n % 2][:, 0:P], RT[:, n % 2, :], ALU.mult).then_inc(s["out"], 1)

                    maxima(0, (0, 1))
                    maxima(0, (2,))
                    for n in range(steps):
                        if n >= 1:
                            dve.wait_ge(s["pv_done"], n)
                        probs_out(n, 0)
                        if n + 1 < steps:
                            maxima(n + 1, (0, 1))
                        probs_out(n, 1)
                        if n + 1 < steps:
                            maxima(n + 1, (2,))
                        probs_out(n, 2)
                        dve.wait_ge(s["exp_done"], 3 * n + 3)
                        if n >= 2:
                            dve.wait_ge(s["recip_spread"], n - 1)
                        dve.reciprocal(st(n, 2), st(n, 1)).then_inc(s["recip_done"], 1)
                        if n >= 1:
                            output(n - 1)
                    output(steps - 1)

                @block.scalar
                def _(act):
                    def recip_out(n):
                        act.wait_ge(s["recip_turned"], n + 1)
                        if n >= 2:
                            act.wait_ge(s["out"], n - 1)
                        act.activation(RT[:, n % 2, :], sc(n, 2)[:, 2 * P:3 * P], ACT.Copy).then_inc(s["recip_out"], 1)

                    for n in range(steps):
                        act.wait_ge(s["max_done"], 2 * n + 1)
                        if n >= 2:
                            act.wait_ge(s["turned"], 3 * (n - 1))
                            act.wait_ge(s["recip_done"], n - 1)
                        for g, (h0, nh) in enumerate(GROUPS):
                            if g == 2:
                                act.wait_ge(s["max_done"], 2 * n + 2)
                            for h in range(h0, h0 + nh):
                                p = probs(n)[:, h * CTX:(h + 1) * CTX]
                                src = p if slopes else sc(n, g)[:, (h - h0) * CTX:(h - h0 + 1) * CTX]
                                last = act.activation(p, src, ACT.Exp, bias=st(n, 0)[:, h:h + 1], scale=scale, accum_out=st(n, 1)[:, h:h + 1])
                                if h in (3, 6, 7):
                                    last.then_inc(s["exp_done"], 1)
                                if h == 3 and n >= 1:
                                    recip_out(n - 1)
                    recip_out(steps - 1)
        finish(nc, K, lambda k, h, j: Wo[:, k, h * P:(h + 1) * P], block_of(OT), DC, bias=bo)


def L0_xattn_layout(i):
    return {"L0x_Wq": rows(i["L0_xattn_Wq"]), "L0x_Wk": rows(np.tile(i["L0_xattn_Wk"], (1, HEADS))),
            "L0x_Wv": rows(np.tile(i["L0_xattn_Wv"], (1, HEADS))), "L0x_Wo": rows(i["L0_xattn_Wo"]),
            "L0x_bq": cols(i["L0_xattn_bq"]), "L0x_bk": cols(np.tile(i["L0_xattn_bk"], HEADS)),
            "L0x_bv": cols(np.tile(i["L0_xattn_bv"], HEADS)), "L0x_bo": cols(i["L0_xattn_bo"])}


def L0_xattn(nc, K, w):
    cross_attention(nc, K, w, "L0x_", float(HD) ** -0.5)


def L3_xattn_layout(i):
    Wkv, bkv = np.asarray(i["L3_xattn_Wkv"]), np.asarray(i["L3_xattn_bkv"])
    rel = np.abs(np.arange(CTX)[None, :] - np.arange(S)[:, None] - (CTX - S)).astype(np.float32)
    return {"L3x_Wq": rows(i["L3_xattn_Wq"]), "L3x_Wk": rows(Wkv[:, :D]), "L3x_Wv": rows(Wkv[:, D:]), "L3x_Wo": rows(i["L3_xattn_Wo"]),
            "L3x_bq": cols(i["L3_xattn_bq"]), "L3x_bk": cols(bkv[:D]), "L3x_bv": cols(bkv[D:]), "L3x_bo": cols(i["L3_xattn_bo"]),
            "L3x_rel": rows(rel)}


def L3_xattn(nc, K, w):
    with ExitStack() as es:
        K.rel = sbuf(es, nc, "rel", [P, S // P, CTX])
        load(nc, K, (K.rel[:], w["L3x_rel"]))
        cross_attention(nc, K, w, "L3x_", float(HD) ** -0.5, [2.0 ** (-8.0 * (h + 1) / HEADS) for h in range(HEADS)])


def L2_xattn_layout(i):
    g = lambda n: i["L2_xattn_" + n]
    return {"L2x_Wq": rows(g("Wq")), "L2x_Wk": rows(g("Wk")), "L2x_Wv": rows(g("Wv")), "L2x_Wo": rows(g("Wo")),
            "L2x_bq": cols(g("bq")), "L2x_bk": cols(g("bk")), "L2x_bv": np.asarray(g("bv")), "L2x_bo": cols(g("bo"))}


def L2_xattn(nc, K, w):
    with ExitStack() as es:
        Wq, Wk, Wv, Wo = (sbuf(es, nc, n, [P, DC, D]) for n in ("Wq", "Wk", "Wv", "Wo"))
        bq, bk, bo = (sbuf(es, nc, n, [P, DC]) for n in ("bq", "bk", "bo"))
        bv = sbuf(es, nc, "bv", [P, D])
        QT, OT = (sbuf(es, nc, n, [P, DC, TOK]) for n in ("QT", "OT"))
        KT = sbuf(es, nc, "KT", [P, DC, B * 256])
        V = sbuf(es, nc, "V", [P, B, 2, D])
        load(nc, K, *[(dst[:], w["L2x_" + n]) for n, dst in (("Wq", Wq), ("Wk", Wk), ("Wv", Wv), ("Wo", Wo), ("bq", bq), ("bk", bk), ("bo", bo))],
             (bv[:], spread(w["L2x_bv"])))
        a, v = copy_to(lambda m, j: QT[:, m, j * BLK:(j + 1) * BLK], lambda m: bq[:, m:m + 1])
        project(nc, K, es, DC, DC, lambda k, m: Wq[:, k, m * P:(m + 1) * P], block_of(K.XT[K.cur]), a, v)
        a, v = copy_to(lambda m, j: KT[:, m, :], lambda m: bk[:, m:m + 1])
        project(nc, K, es, DC, DC, lambda k, m: Wk[:, k, m * P:(m + 1) * P],
                lambda k, j: K.ctxT[:, k].rearrange("p b n -> p (b n)"), a, v, n_blk=1)
        ctx_values(nc, K, V, Wv, bv[:], False)
        scale = float(D) ** -0.5
        Pr = sbuf(es, nc, "probs", [P, 2, CTX])
        PT = sbuf(es, nc, "probsT", [P, 2, BLK])
        stat = sbuf(es, nc, "stat", [P, 2, 3])
        with phase(nc, K.sems, "zeroed scored max_done exp_done normed turned probs_out pv_done out") as (block, s):
            @block.gpsimd
            def _(pool):
                pool.memset(PT[:, 1, :], 0.0).then_inc(s["zeroed"], 1)

            @block.tensor
            def _(pe):
                def score(t):
                    if t >= 2:
                        pe.wait_ge(s["exp_done"], t - 1)
                    for k in range(DC):
                        last = pe.matmul(K.bank[t % 2][:, 0:CTX], QT[:, k, t * P:(t + 1) * P], KT[:, k, (t // 8) * 256:(t // 8) * 256 + CTX],
                                         start=(k == 0), stop=(k == DC - 1))
                    last.then_inc(s["scored"], 1)

                score(0)
                for t in range(NT):
                    if t + 1 < NT:
                        score(t + 1)
                    pe.wait_ge(s["normed"], t + 1)
                    if t >= 2:
                        pe.wait_ge(s["probs_out"], t - 1)
                    pe.transpose(K.bank[2 + t % 2][:, 0:P], Pr[:, t % 2, 0:P], K.ident[:])
                    pe.transpose(K.bank[2 + t % 2][0:CTX - P, P:2 * P], Pr[:, t % 2, P:CTX], K.ident[:]).then_inc(s["turned"], 1)
                    if t % TPB == TPB - 1:
                        j = t // TPB
                        pe.wait_ge(s["probs_out"], t + 1)
                        if j >= 2:
                            pe.wait_ge(s["out"], 2 * (j - 1))
                        for h in range(DC):
                            for kt in range(2):
                                last = pe.matmul(K.bank[4 + 2 * (j % 2) + h][:], V[:, j // 2, kt, h * P:(h + 1) * P], PT[:, kt, :],
                                                 start=(kt == 0), stop=(kt == 1))
                        last.then_inc(s["pv_done"], 1)

            @block.vector
            def _(dve):
                def maximum(t):
                    dve.wait_ge(s["scored"], t + 1)
                    if t >= 2:
                        dve.wait_ge(s["exp_done"], t - 1)
                    dve.reduce_max(stat[:, t % 2, 0:1], K.bank[t % 2][:, 0:CTX], AX)
                    dve.drain()
                    dve.tensor_scalar(stat[:, t % 2, 0:1], stat[:, t % 2, 0:1], -scale, None, ALU.mult).then_inc(s["max_done"], 1)

                maximum(0)
                for t in range(NT):
                    if t + 1 < NT:
                        maximum(t + 1)
                    dve.wait_ge(s["exp_done"], t + 1)
                    dve.reciprocal(stat[:, t % 2, 2:3], stat[:, t % 2, 1:2])
                    dve.drain()
                    dve.tensor_scalar(Pr[:, t % 2, :], Pr[:, t % 2, :], stat[:, t % 2, 2:3], None, ALU.mult).then_inc(s["normed"], 1)

            @block.scalar
            def _(act):
                def exp(t):
                    act.wait_ge(s["max_done"], t + 1)
                    if t >= 2:
                        act.wait_ge(s["turned"], t - 1)
                    act.activation(Pr[:, t % 2, :], K.bank[t % 2][:, 0:CTX], ACT.Exp, bias=stat[:, t % 2, 0:1], scale=scale,
                                   accum_out=stat[:, t % 2, 1:2]).then_inc(s["exp_done"], 1)

                act.wait_ge(s["zeroed"], 1)
                exp(0)
                for t in range(NT):
                    if t + 1 < NT:
                        exp(t + 1)
                    act.wait_ge(s["turned"], t + 1)
                    if t % TPB == 0 and t:
                        act.wait_ge(s["pv_done"], t // TPB)
                    cols_ = slice((t % TPB) * P, (t % TPB + 1) * P)
                    act.activation(PT[:, 0, cols_], K.bank[2 + t % 2][:, 0:P], ACT.Copy)
                    act.activation(PT[0:CTX - P, 1, cols_], K.bank[2 + t % 2][0:CTX - P, P:2 * P], ACT.Copy).then_inc(s["probs_out"], 1)
                    if t % TPB == TPB - 1:
                        j = t // TPB
                        act.wait_ge(s["pv_done"], j + 1)
                        for h in range(DC):
                            act.activation(OT[:, h, j * BLK:(j + 1) * BLK], K.bank[4 + 2 * (j % 2) + h][:], ACT.Copy).then_inc(s["out"], 1)
        finish(nc, K, lambda k, h, j: Wo[:, k, h * P:(h + 1) * P], block_of(OT), DC, bias=bo)


def finish_tokens(nc, K, r, last=False):
    xo = K.XT[1 - K.cur]
    with ExitStack() as es, phase(nc, K.sems, "stats_done std_done tok_done turned") as (block, s):
        st = sbuf(es, nc, "ln_stats", [P, NT, 9])

        @block.vector
        def _(dve):
            for t in range(NT):
                dve.bn_stats(st[:, t, 2:8], r[:, t, :])
            dve.drain()
            for t in range(NT):
                ins = dve.bn_aggr(st[:, t, 0:2], st[:, t, 2:8])
            ins.then_inc(s["stats_done"], 1)
            dve.wait_ge(s["std_done"], 1)
            dve.reciprocal(st[:, :, 8:9], st[:, :, 8:9])
            dve.drain()
            for t in range(NT):
                dve.tensor_scalar(K.Xtok[:, t, :], r[:, t, :], st[:, t, 0:1], st[:, t, 8:9], ALU.subtract, ALU.mult).then_inc(s["tok_done"], 1)

        @block.scalar
        def _(act):
            act.wait_ge(s["stats_done"], 1)
            act.activation(st[:, :, 8:9], st[:, :, 1:2], ACT.Sqrt, bias=K.eps[:, 0:1]).then_inc(s["std_done"], 1)
            for t in range(0 if last else NT):
                act.wait_ge(s["turned"], t + 1)
                act.activation(xo[:, :, t * P:(t + 1) * P], K.bank[t % 4][:, 0:D].rearrange("p (c k) -> p c k", c=2), ACT.Copy).then_inc(s["std_done"], 1)

        @block.tensor
        def _(pe):
            for t in range(0 if last else NT):
                pe.wait_ge(s["tok_done"], t + 1)
                if t >= 4:
                    pe.wait_ge(s["std_done"], 1 + t - 3)
                for h in range(DC):
                    ins = pe.transpose(K.bank[t % 4][:, h * P:(h + 1) * P], K.Xtok[:, t, h * P:(h + 1) * P], K.ident[:])
                ins.then_inc(s["turned"], 1)
    K.cur = 1 - K.cur


TAPS = 4
L3A_M = 4


def L3_attn_layout(i):
    cw = np.asarray(i["L3_attn_conv_w"]).reshape(4, P, TAPS).transpose(1, 0, 2)
    return {"L3a_Win": rows(i["L3_attn_W_in"]), "L3a_cw": np.ascontiguousarray(cw), "L3a_cb": cols(i["L3_attn_conv_b"]),
            "L3a_Wout": rows(i["L3_attn_W_out"])}


def L3_attn(nc, K, w):
    with ExitStack() as es:
        Wout = sbuf(es, nc, "Wout", [P, L3A_M, D])
        Y = sbuf(es, nc, "Y", [P, L3A_M, TOK])
        with ExitStack() as inside:
            Win = sbuf(inside, nc, "Win", [P, DC, 2 * L3A_M * P])
            cw = sbuf(inside, nc, "cw", [P, L3A_M, TAPS])
            cb = sbuf(inside, nc, "cb", [P, L3A_M])
            H = sbuf(inside, nc, "H", [P, L3A_M, B, TAPS - 1 + S])
            sg = sbuf(inside, nc, "sigmoid", [P, 2, BLK])
            acc = sbuf(inside, nc, "conv", [P, 2, BLK])
            load(nc, K, (Win[:], w["L3a_Win"]), (cw[:], w["L3a_cw"]), (cb[:], w["L3a_cb"]), (Wout[:], w["L3a_Wout"]))
            steps = [(m, j) for m in range(L3A_M) for j in range(NB)]
            with phase(nc, K.sems, "padded done gated h_done conv_done silu_done") as (block, s):
                @block.gpsimd
                def _(pool):
                    pool.memset(H[:, :, :, 0:TAPS - 1], 0.0).then_inc(s["padded"], 1)

                @block.tensor
                def _(pe):
                    for n, (m, j) in enumerate(steps):
                        if n >= 4:
                            pe.wait_ge(s["h_done"], n - 3)
                        for part in range(2):
                            for k in range(DC):
                                col = (part * L3A_M + m) * P
                                last = pe.matmul(K.bank[2 * (n % 4) + part][:], Win[:, k, col:col + P], K.XT[K.cur][:, k, j * BLK:(j + 1) * BLK],
                                                 start=(k == 0), stop=(k == DC - 1))
                        last.then_inc(s["done"], 1)

                @block.scalar
                def _(act):
                    for n in range(len(steps)):
                        act.wait_ge(s["done"], n + 1)
                        if n >= 2:
                            act.wait_ge(s["h_done"], n - 1)
                        act.activation(sg[:, n % 2, :], K.bank[2 * (n % 4) + 1][:], ACT.Sigmoid).then_inc(s["gated"], 1)
                    for n, (m, j) in enumerate(steps):
                        act.wait_ge(s["conv_done"], n + 1)
                        act.activation(Y[:, m, j * BLK:(j + 1) * BLK], acc[:, n % 2, :], ACT.Silu).then_inc(s["silu_done"], 1)

                @block.vector
                def _(dve):
                    for n, (m, j) in enumerate(steps):
                        dve.wait_ge(s["gated"], n + 1)
                        b, o = divmod(j * BLK, S)
                        dve.tensor_tensor(H[:, m, b, TAPS - 1 + o:TAPS - 1 + o + BLK], K.bank[2 * (n % 4)][:], sg[:, n % 2, :],
                                          ALU.mult).then_inc(s["h_done"], 1)
                    dve.wait_ge(s["padded"], 1)
                    dve.drain()
                    for n, (m, j) in enumerate(steps):
                        b, o = divmod(j * BLK, S)
                        if n >= 2:
                            dve.wait_ge(s["silu_done"], n - 1)
                        dve.tensor_scalar(acc[:, n % 2, :], H[:, m, b, o:o + BLK], cw[:, m, 0:1], cb[:, m:m + 1], ALU.mult, ALU.add)
                        for tap in range(1, TAPS):
                            dve.drain()
                            ins = dve.scalar_tensor_tensor(out=acc[:, n % 2, :], in0=H[:, m, b, o + tap:o + tap + BLK], scalar=cw[:, m, tap:tap + 1],
                                                           in1=acc[:, n % 2, :], op0=ALU.mult, op1=ALU.add)
                        ins.then_inc(s["conv_done"], 1)
        finish(nc, K, lambda k, h, j: Wout[:, k, h * P:(h + 1) * P], block_of(Y), L3A_M)


EXPERTS = 8
INTER = 1024
IC = INTER // P
EW = DC * INTER
SLOT_TILES = (2 * TOK + EXPERTS * (P - 1)) // P
ROUND = 1.5 * 2.0 ** 23


def L3_ffn_layout(i):
    W1, W2 = np.asarray(i["L3_ffn_W1"]), np.asarray(i["L3_ffn_W2"])
    b1 = np.asarray(i["L3_ffn_b1"]).reshape(EXPERTS * IC, P).T
    return {"L3f_Wg": rows(np.asarray(i["L3_ffn_Wg"]).T), "L3f_W1": np.stack([rows(a) for a in W1]), "L3f_W2": np.stack([rows(a) for a in W2]),
            "L3f_b1": np.ascontiguousarray(b1), "L3f_b2": np.asarray(i["L3_ffn_b2"])}


def number_experts(nc, K, es, dst, n):
    ints = sbuf(es, nc, "ints", [P, n], I32)
    with phase(nc, K.sems, "counted") as (block, s):
        @block.gpsimd
        def _(pool):
            pool.iota(ints[:], pattern=[[1, n]], base=0, channel_multiplier=0).then_inc(s["counted"], 1)

        @block.vector
        def _(dve):
            dve.wait_ge(s["counted"], 1)
            dve.tensor_copy(dst, ints[:])


def L3_ffn(nc, K, w):
    xT = K.XT[K.cur]
    x_rows = nc.dram_tensor("L3f_x_rows", [TOK, D], F32, kind="Internal").ap()
    y_rows = nc.dram_tensor("L3f_y_rows", [SLOT_TILES * P, D], F32, kind="Internal").ap()
    weights_in = nc.alloc_semaphore("L3f_weights_in")
    with ExitStack() as es:
        slot = sbuf(es, nc, "slot_of_token", [P, 2, NT], U32)
        ew = sbuf(es, nc, "weights", [P, 4, NT])
        with ExitStack() as kept:
            W1 = sbuf(kept, nc, "W1", [P, EXPERTS * DC * INTER])
            W2 = sbuf(kept, nc, "W2", [P, EXPERTS * IC * D])
            b1 = sbuf(kept, nc, "b1", [P, EXPERTS * IC])
            token_at = sbuf(kept, nc, "token_at_slot", [P, SLOT_TILES], U32)
            w_at = sbuf(kept, nc, "weights_at", [P, 2, SLOT_TILES], I32)
            route_tokens(nc, K, w, xT, x_rows, W1, W2, b1, weights_in, slot, ew, token_at, w_at)
            run_experts(nc, K, x_rows, y_rows, W1, W2, b1, weights_in, token_at, w_at)

        with ExitStack() as inside, phase(nc, K.sems, "gathered added") as (block, s):
            Y = sbuf(inside, nc, "y_of_token", [P, NT, 2, D])
            n_in = NT * 2

            @block.gpsimd
            def _(pool):
                for n in range(n_in):
                    t, i = divmod(n, 2)
                    pool.indirect_dma_start(out=Y[:, t, i, :], out_offset=None, in_=y_rows[:, :],
                                            in_offset=bass.IndirectOffsetOnAxis(ap=slot[:, i, t:t + 1], axis=0)).then_inc(s["gathered"], 16)
                pool.wait_ge(s["gathered"], 16 * n_in)

            @block.vector
            def _(dve):
                dve.wait_ge(s["gathered"], 16 * n_in)
                for i in range(2):
                    for t in range(NT):
                        ins = dve.scalar_tensor_tensor(out=K.Xtok[:, t, :], in0=Y[:, t, i, :], scalar=ew[:, 2 + i, t:t + 1], in1=K.Xtok[:, t, :],
                                                       op0=ALU.mult, op1=ALU.add)
                    dve.drain()
        finish_tokens(nc, K, K.Xtok, last=True)


def route_tokens(nc, K, w, xT, x_rows, W1, W2, b1, weights_in, slot, ew, token_at, w_at):
    PAIRS = 2 * NT
    with ExitStack() as es:
        Wg = sbuf(es, nc, "Wg", [P, DC, EXPERTS])
        b2 = sbuf(es, nc, "b2", [EXPERTS, D])
        ints = sbuf(es, nc, "integers", [P, P], I32)
        token_ints = sbuf(es, nc, "token_integers", [P, 2, NT], I32)
        num = sbuf(es, nc, "numbers", [P, P])
        place = sbuf(es, nc, "token_place", [P, 2, NT])
        L = sbuf(es, nc, "logits", [P, NT, EXPERTS])
        top = sbuf(es, nc, "top", [P, NT, 8])
        at = sbuf(es, nc, "top_index", [P, NT, 8], U32)
        atf = sbuf(es, nc, "top_index_f", [P, NT, 8])
        one = sbuf(es, nc, "one_hot", [P, 2, NT, EXPERTS])
        gates = sbuf(es, nc, "gates", [P, 2, NT, EXPERTS])
        chosen = sbuf(es, nc, "chosen", [P, NT, EXPERTS])
        upto = sbuf(es, nc, "chosen_up_to_tile", [P, 3, NT, EXPERTS])
        tiles = sbuf(es, nc, "tiles_of_expert", [P, 4, EXPERTS])
        sl = sbuf(es, nc, "slots", [P, 3, 2, NT])
        lo_hot = K.XT[1 - K.cur].rearrange("p c t -> p (c t)")[:, 0:PAIRS * P // 2].bitcast(BF16).rearrange("p (n j) -> p n j", j=P)
        hi_hot = sbuf(es, nc, "slot_tile_hot", [P, PAIRS, 2, SLOT_TILES], BF16)
        passed = sbuf(es, nc, "experts_passed", [P, SLOT_TILES, EXPERTS])
        found = sbuf(es, nc, "found", [P, 3, SLOT_TILES])
        gT = sbuf(es, nc, "gatesT", [EXPERTS, 2, P])
        names = "loaded x_stored counted scored ready exp_done gates_done mask_done ranked hot_done found turned turned_out bias_done bias_out"
        with phase(nc, K.sems, names) as (block, s):
            @block.sync
            def _(sp):
                sp.dma_start(Wg[:], w["L3f_Wg"]).then_inc(s["loaded"], 16)
                sp.dma_start(b2[:], w["L3f_b2"]).then_inc(s["loaded"], 16)
                sp.dma_start(x_rows.rearrange("(t p) d -> p t d", p=P), K.Xtok[:]).then_inc(s["x_stored"], 16)
                for e in range(EXPERTS):
                    sp.dma_start(W1[:, e * EW:(e + 1) * EW].rearrange("p (k n) -> p k n", k=DC), w["L3f_W1"][e]).then_inc(weights_in, 16)
                    sp.dma_start(W2[:, e * EW:(e + 1) * EW].rearrange("p (m n) -> p m n", m=IC), w["L3f_W2"][e]).then_inc(weights_in, 16)
                sp.dma_start(b1[:], w["L3f_b1"]).then_inc(weights_in, 16)

            @block.gpsimd
            def _(pool):
                pool.iota(ints[:], pattern=[[1, P]], base=0, channel_multiplier=0).then_inc(s["counted"], 1)
                pool.iota(token_ints[:, 0], pattern=[[1, NT]], base=0, channel_multiplier=0).then_inc(s["counted"], 1)
                pool.iota(token_ints[:, 1], pattern=[[0, NT]], base=0, channel_multiplier=1).then_inc(s["counted"], 1)

            @block.tensor
            def _(pe):
                pe.wait_ge(s["loaded"], 32)
                for t in range(NT):
                    for k in range(DC):
                        ins = pe.matmul(K.bank[0][:, t * EXPERTS:(t + 1) * EXPERTS], xT[:, k, t * P:(t + 1) * P], Wg[:, k, :], start=(k == 0), stop=(k == DC - 1))
                ins.then_inc(s["scored"], 1)
                pe.wait_ge(s["mask_done"], 1)
                m = chosen[:].rearrange("p t e -> p (t e)")
                pe.matmul(K.bank[5][:, 0:NT * EXPERTS], K.causal_T[:], m, start=True, stop=True)
                pe.matmul(K.bank[6][:, 0:NT * EXPERTS], K.ones[:, 0:P], m, start=True, stop=True).then_inc(s["ranked"], 1)
                pe.wait_ge(s["gates_done"], 1)
                for t in range(NT):
                    if t >= 2:
                        pe.wait_ge(s["turned_out"], t - 1)
                    pe.transpose(K.bank[1 + t % 2][0:EXPERTS, 0:P], gates[:, 0, t, :], K.ident[:]).then_inc(s["turned"], 1)
                    if t >= 2:
                        pe.wait_ge(s["bias_out"], t - 1)
                    pe.wait_ge(s["turned_out"], t + 1)
                    pe.matmul(K.bank[3 + t % 2][:, 0:D], gT[:, t % 2, :], b2[:], start=True, stop=True).then_inc(s["bias_done"], 1)
                pe.wait_ge(s["hot_done"], 1)
                for n in range(PAIRS):
                    ins = pe.matmul(K.bank[7][:, 0:2 * SLOT_TILES], lo_hot[:, n, :], hi_hot[:, n].rearrange("p a g -> p (a g)"),
                                    start=(n == 0), stop=(n == PAIRS - 1))
                ins.then_inc(s["found"], 1)

            @block.scalar
            def _(act):
                act.wait_ge(s["ready"], 1)
                act.activation(ew[:, 1, :], ew[:, 0, :], ACT.Exp).then_inc(s["exp_done"], 1)
                for t in range(NT):
                    act.wait_ge(s["turned"], t + 1)
                    if t >= 2:
                        act.wait_ge(s["bias_done"], t - 1)
                    act.activation(gT[:, t % 2, :], K.bank[1 + t % 2][0:EXPERTS, 0:P], ACT.Copy).then_inc(s["turned_out"], 1)

            @block.vector
            def _(dve):
                def step(f, *args):
                    f(*args)
                    dve.drain()

                dve.wait_ge(s["counted"], 3)
                dve.tensor_copy(num[:], ints[:])
                dve.tensor_copy(place[:], token_ints[:])
                dve.wait_ge(s["scored"], 1)
                step(dve.tensor_copy, L[:], K.bank[0][:, 0:NT * EXPERTS].rearrange("p (t e) -> p t e", e=EXPERTS))
                for t in range(NT):
                    dve.max(top[:, t, :], L[:, t, :])
                dve.drain()
                for t in range(NT):
                    dve.max_index(at[:, t, :], top[:, t, :], L[:, t, :])
                dve.tensor_tensor(ew[:, 0, :], top[:, :, 1], top[:, :, 0], ALU.subtract).then_inc(s["ready"], 1)
                dve.drain()
                step(dve.tensor_copy, atf[:], at[:])
                for i in range(2):
                    dve.tensor_tensor(one[:, i], middle(num[:, 0:EXPERTS], NT), inner(atf[:, :, i], EXPERTS), ALU.is_equal)
                dve.drain()
                dve.tensor_tensor(chosen[:], one[:, 0], one[:, 1], ALU.add).then_inc(s["mask_done"], 1)
                dve.wait_ge(s["exp_done"], 1)
                step(dve.tensor_scalar, ew[:, 2, :], ew[:, 1, :], 1.0, None, ALU.add)
                step(dve.reciprocal, ew[:, 2, :], ew[:, 2, :])
                step(dve.tensor_tensor, ew[:, 3, :], ew[:, 1, :], ew[:, 2, :], ALU.mult)
                for i in range(2):
                    dve.tensor_tensor(gates[:, i], one[:, i], inner(ew[:, 2 + i, :], EXPERTS), ALU.mult)
                dve.drain()
                dve.tensor_tensor(gates[:, 0], gates[:, 0], gates[:, 1], ALU.add).then_inc(s["gates_done"], 1)

                dve.wait_ge(s["ranked"], 1)
                total = upto[:, 2]
                dve.tensor_copy(total, K.bank[6][:, 0:NT * EXPERTS].rearrange("p (t e) -> p t e", e=EXPERTS))
                step(dve.tensor_copy, upto[:, 0], K.bank[6][:, 0:NT * EXPERTS].rearrange("p (t e) -> p t e", e=EXPERTS))
                a, d = 0, 1
                while d < NT:
                    dve.tensor_copy(upto[:, 1 - a, 0:d], upto[:, a, 0:d])
                    step(dve.tensor_tensor, upto[:, 1 - a, d:], upto[:, a, d:], upto[:, a, 0:NT - d], ALU.add)
                    a, d = 1 - a, 2 * d
                T, end = tiles[:, 3], upto[:, a]
                step(dve.tensor_scalar, T, end[:, NT - 1], P / 2 - 0.5, 1.0 / P, ALU.add, ALU.mult)
                step(dve.tensor_scalar, T, T, ROUND, None, ALU.add)
                step(dve.tensor_scalar, T, T, ROUND, None, ALU.subtract)
                step(dve.tensor_copy, tiles[:, 0], T)
                c, d = 0, 1
                while d < EXPERTS:
                    dve.tensor_copy(tiles[:, 1 - c, 0:d], tiles[:, c, 0:d])
                    step(dve.tensor_tensor, tiles[:, 1 - c, d:], tiles[:, c, d:], tiles[:, c, 0:EXPERTS - d], ALU.add)
                    c, d = 1 - c, 2 * d
                past, first = tiles[:, c], tiles[:, 2]
                step(dve.tensor_tensor, first, past, T, ALU.subtract)
                step(dve.tensor_scalar, first, first, float(P), -1.0, ALU.mult, ALU.add)
                step(dve.tensor_tensor, end, end, total, ALU.subtract)
                step(dve.tensor_tensor, end, end, middle(first, NT), ALU.add)
                step(dve.tensor_tensor, end, end, K.bank[5][:, 0:NT * EXPERTS].rearrange("p (t e) -> p t e", e=EXPERTS), ALU.add)
                for i in range(2):
                    dve.tensor_tensor(one[:, i], one[:, i], end, ALU.mult)
                dve.drain()
                for i in range(2):
                    dve.reduce_sum(sl[:, 0, i], one[:, i], AX)
                dve.drain()
                dve.tensor_copy(slot[:], sl[:, 0])
                hi, lo = sl[:, 1], sl[:, 2]
                step(dve.tensor_scalar, hi, sl[:, 0], -(P / 2 - 0.5), 1.0 / P, ALU.add, ALU.mult)
                step(dve.tensor_scalar, hi, hi, ROUND, None, ALU.add)
                step(dve.tensor_scalar, hi, hi, ROUND, None, ALU.subtract)
                step(dve.scalar_tensor_tensor, lo, hi, -float(P), sl[:, 0], ALU.mult, ALU.add)
                flat = lambda v: v.rearrange("p i t -> p (i t)")
                dve.tensor_tensor(lo_hot, middle(num[:], PAIRS), inner(flat(lo), P), ALU.is_equal)
                step(dve.tensor_tensor, hi_hot[:, :, 0], middle(num[:, 0:SLOT_TILES], PAIRS), inner(flat(hi), SLOT_TILES), ALU.is_equal)
                for i in range(2):
                    v = hi_hot[:, i * NT:(i + 1) * NT]
                    dve.tensor_tensor(v[:, :, 1], v[:, :, 0], inner(place[:, 1], SLOT_TILES), ALU.mult)
                dve.drain()
                for i in range(2):
                    v = hi_hot[:, i * NT:(i + 1) * NT]
                    ins = dve.tensor_tensor(v[:, :, 0], v[:, :, 0], inner(place[:, 0], SLOT_TILES), ALU.mult)
                ins.then_inc(s["hot_done"], 1)
                step(dve.tensor_tensor, passed[:], middle(past, SLOT_TILES), inner(num[:, 0:SLOT_TILES], EXPERTS), ALU.is_le)
                step(dve.reduce_sum, found[:, 2], passed[:, :, 0:EXPERTS - 1], AX)
                for i, width in enumerate((EW, IC)):
                    step(dve.tensor_scalar, found[:, i], found[:, 2], float(width), None, ALU.mult)
                dve.tensor_copy(w_at[:], found[:, 0:2])
                dve.wait_ge(s["x_stored"], 16)
                for t in range(NT):
                    dve.wait_ge(s["bias_done"], t + 1)
                    dve.tensor_tensor(K.Xtok[:, t, :], K.bank[3 + t % 2][:, 0:D], K.Xtok[:, t, :], ALU.add).then_inc(s["bias_out"], 1)
                dve.wait_ge(s["found"], 1)
                step(dve.tensor_copy, found[:, 0:2], K.bank[7][:, 0:2 * SLOT_TILES].rearrange("p (a g) -> p a g", a=2))
                step(dve.scalar_tensor_tensor, found[:, 0], found[:, 0], float(P), found[:, 1], ALU.mult, ALU.add)
                dve.tensor_copy(token_at[:], found[:, 0])


def run_experts(nc, K, x_rows, y_rows, W1, W2, b1, weights_in, token_at, w_at):
    HALF = IC // 2
    TURNS = SLOT_TILES // 3
    with ExitStack() as es:
        Xg = sbuf(es, nc, "x_gathered", [P, 3, D])
        XgT = sbuf(es, nc, "x_gatheredT", [P, 3, DC, P])
        H = K.XT[0][:, 0, 0:INTER]
        HT = K.XT[1][:, 0, 0:INTER].rearrange("p (m t) -> p m t", m=IC)
        Yt = sbuf(es, nc, "y", [P, 3, D])
        bt = sbuf(es, nc, "b1_of_tile", [P, 3, IC])
        names = "gathered0 gathered1 gathered2 stored0 stored1 stored2 x_turned x_out b_set h_done h_out turned gelu_done down_done y_out"
        with phase(nc, K.sems, names) as (block, s):
            gathered = [s["gathered0"], s["gathered1"], s["gathered2"]]
            stored = [s["stored0"], s["stored1"], s["stored2"]]

            @block.gpsimd
            def _(pool):
                for g in range(SLOT_TILES):
                    if g >= 3:
                        pool.wait_ge(s["x_turned"], g - 2)
                    pool.indirect_dma_start(out=Xg[:, g % 3, :], out_offset=None, in_=x_rows[:, :],
                                            in_offset=bass.IndirectOffsetOnAxis(ap=token_at[:, g:g + 1], axis=0)).then_inc(gathered[g % 3], 16)

            @block.sync
            def _(sp):
                for q in range(3):
                    sp.sem_inc(stored[q], 16)
                with sp.Fori(0, TURNS) as i:
                    for q in range(3):
                        sp.wait_ge(s["y_out"], i * 3 + q + 4)
                        sp.dma_start(y_rows[bass.ds(i * (3 * P) + q * P, P), :], Yt[:, q, :]).then_inc(stored[q], 16)
                for q in range(3):
                    sp.wait_ge(stored[q], 16 * (TURNS + 1))

            @block.tensor
            def _(pe):
                def expert(i, q):
                    return pe.value_load(w_at[0:1, 0, bass.ds(i * 3 + q, 1)], min_val=0, max_val=(EXPERTS - 1) * EW)

                def turn_x(i, q):
                    pe.wait_ge(gathered[q], i * 16 + 16)
                    pe.wait_ge(s["x_out"], i * 3 + q + 1)
                    for k in range(DC):
                        ins = pe.transpose(K.bank[7][:, k * P:(k + 1) * P], Xg[:, q, k * P:(k + 1) * P], K.ident[:])
                    ins.then_inc(s["x_turned"], 1)

                def up(i, q, part, at):
                    pe.wait_ge(s["x_out"], i * 3 + q + 2)
                    pe.wait_ge(s["h_out"], i * 6 + 2 * q + part + 1)
                    for k in range(DC):
                        ins = pe.matmul(K.bank[part][:], XgT[:, q, k, :], W1[:, bass.ds(at + (k * INTER + part * BLK), BLK)], start=(k == 0), stop=(k == DC - 1))
                    ins.then_inc(s["h_done"], 1)

                def turn_h(i, q, part):
                    pe.wait_ge(s["h_out"], i * 6 + 2 * q + part + 3)
                    pe.wait_ge(s["gelu_done"], i * 6 + 2 * q + part + 1)
                    for m in range(HALF):
                        c = part * HALF + m
                        ins = pe.transpose(K.bank[2 + part][:, m * P:(m + 1) * P], H[:, c * P:(c + 1) * P], K.ident[:])
                    ins.then_inc(s["turned"], 1)

                def down(i, q, at):
                    pe.wait_ge(s["y_out"], i * 3 + q + 1)
                    for c in range(IC):
                        if c % HALF == 0:
                            pe.wait_ge(s["gelu_done"], i * 6 + 2 * q + c // HALF + 3)
                        ins = pe.matmul(K.bank[4 + q][:, 0:D], HT[:, c, :], W2[:, bass.ds(at + c * D, D)], start=(c == 0), stop=(c == IC - 1))
                    ins.then_inc(s["down_done"], 1)

                def tile(i, q, ahead):
                    nq, ni = (q + 1) % 3, (i if q < 2 else i + 1)
                    at_next = expert(ni, nq) if ahead >= 1 else None
                    if ahead >= 1:
                        up(ni, nq, 0, at_next)
                    turn_h(i, q, 0)
                    if ahead >= 1:
                        up(ni, nq, 1, at_next)
                    turn_h(i, q, 1)
                    if ahead >= 2:
                        turn_x(i if q < 1 else i + 1, (q + 2) % 3)
                    down(i, q, expert(i, q))

                pe.sem_inc(s["turned"], 2)
                pe.sem_inc(s["down_done"], 1)
                turn_x(0, 0)
                pe.wait_ge(weights_in, 16 * (2 * EXPERTS + 1))
                at = expert(0, 0)
                for part in range(2):
                    up(0, 0, part, at)
                turn_x(0, 1)
                with pe.Fori(0, TURNS - 1) as i:
                    for q in range(3):
                        tile(i, q, 2)
                for q in range(3):
                    tile(TURNS - 1, q, 2 - q)

            @block.vector
            def _(dve):
                dve.sem_inc(s["x_out"], 1)
                dve.sem_inc(s["h_out"], 2)
                dve.sem_inc(s["y_out"], 3)

                def x_out(i, q):
                    dve.wait_ge(s["x_turned"], i * 3 + q + 1)
                    dve.tensor_copy(XgT[:, q], K.bank[7][:, 0:D].rearrange("p (k t) -> p k t", k=DC)).then_inc(s["x_out"], 1)

                def h_out(i, q, part):
                    dve.wait_ge(s["turned"], i * 6 + 2 * q + part + 1)
                    dve.wait_ge(s["h_done"], i * 6 + 2 * q + part + 1)
                    dve.tensor_copy(H[:, part * BLK:(part + 1) * BLK], K.bank[part][:]).then_inc(s["h_out"], 1)

                def hidden_out(i, q):
                    h_out(i, q, 0)
                    at = dve.value_load(w_at[0:1, 1, bass.ds(i * 3 + q, 1)], min_val=0, max_val=(EXPERTS - 1) * IC)
                    dve.tensor_scalar(bt[:, q], b1[:, bass.ds(at, IC)], 0.0, None, ALU.add).then_inc(s["b_set"], 1)
                    h_out(i, q, 1)

                def tile(i, q, ahead):
                    if ahead >= 1:
                        hidden_out(i if q < 2 else i + 1, (q + 1) % 3)
                    if ahead >= 2:
                        x_out(i if q < 1 else i + 1, (q + 2) % 3)
                    dve.wait_ge(s["down_done"], i * 3 + q + 2)
                    dve.wait_ge(stored[q], i * 16 + 16)
                    dve.tensor_copy(Yt[:, q], K.bank[4 + q][:, 0:D]).then_inc(s["y_out"], 1)

                x_out(0, 0)
                dve.wait_ge(weights_in, 16 * (2 * EXPERTS + 1))
                hidden_out(0, 0)
                x_out(0, 1)
                with dve.Fori(0, TURNS - 1) as i:
                    for q in range(3):
                        tile(i, q, 2)
                for q in range(3):
                    tile(TURNS - 1, q, 2 - q)

            @block.scalar
            def _(act):
                act.sem_inc(s["gelu_done"], 2)
                with act.Fori(0, TURNS) as i:
                    for q in range(3):
                        for part in range(2):
                            act.wait_ge(s["down_done"], i * 3 + q + 1)
                            act.wait_ge(s["b_set"], i * 3 + q + 1)
                            act.wait_ge(s["turned"], i * 6 + 2 * q + part + 3)
                            for m in range(HALF):
                                c = part * HALF + m
                                ins = act.activation(HT[:, c, :], K.bank[2 + part][:, m * P:(m + 1) * P], ACT.Gelu, bias=bt[:, q, c:c + 1])
                            ins.then_inc(s["gelu_done"], 1)


INNER = 1024
QCLIP = 1e-5


def L1_ffn_layout(i):
    return {"L1f_Wg": rows(np.asarray(i["L1_ffn_w_gate"]).T), "L1f_Wu": rows(np.asarray(i["L1_ffn_w_up"]).T),
            "L1f_Wd": rows(np.asarray(i["L1_ffn_w_down"]).T)}


def L1_ffn(nc, K, w):
    xT = K.XT[K.cur]
    n_w = INNER * D
    with ExitStack() as es:
        r = sbuf(es, nc, "sum", [P, NT, D])
        Wq = [sbuf(es, nc, f"W{n}_int", [P, n_w // P], BF16) for n in "gud"]
        wsc = sbuf(es, nc, "w_scale", [P, 3, 3])
        xsc = sbuf(es, nc, "x_scale", [P, NT, 4])
        with ExitStack() as inside:
            W = [sbuf(inside, nc, f"W{n}", [P, n_w // P]) for n in "gud"]
            junk = sbuf(inside, nc, "junk", [P, n_w // P])
            with phase(nc, K.sems, "loaded summed total clipped recip stepped") as (block, s):
                @block.sync
                def _(sp):
                    for i, n in enumerate(("L1f_Wg", "L1f_Wu", "L1f_Wd")):
                        sp.dma_start(W[i][:], w[n].rearrange("p c n -> p (c n)")).then_inc(s["loaded"], 16)

                @block.scalar
                def _(act):
                    act.wait_ge(s["loaded"], 48)
                    for i in range(3):
                        act.activation(junk[:], W[i][:], ACT.Abs, accum_out=wsc[:, i, 0:1]).then_inc(s["summed"], 1)
                        act.drain()

                @block.tensor
                def _(pe):
                    pe.wait_ge(s["summed"], 3)
                    pe.matmul(K.bank[0][:, 0:3], K.ones[:, 0:P], wsc[:, :, 0], start=True, stop=True).then_inc(s["total"], 1)

                @block.vector
                def _(dve):
                    dve.wait_ge(s["total"], 1)
                    dve.tensor_scalar(wsc[:, :, 1], K.bank[0][:, 0:3], 1.0 / n_w, QCLIP, ALU.mult, ALU.max)
                    dve.drain()
                    dve.reciprocal(wsc[:, :, 2], wsc[:, :, 1])
                    dve.drain()
                    for i in range(3):
                        dve.tensor_scalar(W[i][:], W[i][:], wsc[:, i, 2:3], 1.0, ALU.mult, ALU.min)
                        dve.drain()
                        dve.tensor_scalar(W[i][:], W[i][:], -1.0, ROUND, ALU.max, ALU.add).then_inc(s["stepped"], 1)

                @block.gpsimd
                def _(pool):
                    for i in range(3):
                        pool.wait_ge(s["stepped"], i + 1)
                        pool.tensor_scalar(Wq[i][:], W[i][:], ROUND, None, ALU.subtract)
        Wg, Wu = (Wq[i][:].rearrange("p (c n) -> p c n", c=DC) for i in range(2))
        Wd = Wq[2][:].rearrange("p (c n) -> p c n", n=D)
        XqT = sbuf(es, nc, "XqT", [P, DC, TOK], BF16)

        def quantise(dve, src, tmp, out, sc):
            dve.tensor_reduce(sc[:, 0:1], src, AX, ALU.max, apply_absolute_value=True)
            dve.drain()
            dve.tensor_scalar(sc[:, 0:1], sc[:, 0:1], QCLIP, None, ALU.max)
            dve.drain()
            dve.reciprocal(sc[:, 1:2], sc[:, 0:1])
            dve.tensor_scalar(sc[:, 2:3], sc[:, 0:1], 1.0 / 127.0, None, ALU.mult)
            dve.drain()
            dve.tensor_scalar(sc[:, 1:2], sc[:, 1:2], 127.0, None, ALU.mult)
            dve.drain()
            dve.tensor_scalar(tmp, src, sc[:, 1:2], ROUND, ALU.mult, ALU.add)
            dve.drain()
            return dve.tensor_scalar(out, tmp, ROUND, 127.0, ALU.subtract, ALU.min)

        with ExitStack() as inside, phase(nc, K.sems, "quantised turned out") as (block, s):
            tmp = sbuf(inside, nc, "tmp", [P, D])
            xq = sbuf(inside, nc, "xq", [P, 2, D], BF16)

            @block.vector
            def _(dve):
                for t in range(NT):
                    if t >= 2:
                        dve.wait_ge(s["turned"], t - 1)
                    quantise(dve, K.Xtok[:, t, :], tmp[:], xq[:, t % 2, :], xsc[:, t, :]).then_inc(s["quantised"], 1)
                    dve.drain()

            @block.tensor
            def _(pe):
                for t in range(NT):
                    pe.wait_ge(s["quantised"], t + 1)
                    if t >= 4:
                        pe.wait_ge(s["out"], t - 3)
                    for h in range(DC):
                        ins = pe.transpose(K.bank[t % 4][:].bitcast(BF16)[:, h * P:(h + 1) * P], xq[:, t % 2, h * P:(h + 1) * P], K.identb[:])
                    ins.then_inc(s["turned"], 1)

            @block.scalar
            def _(act):
                for t in range(NT):
                    act.wait_ge(s["turned"], t + 1)
                    act.activation(XqT[:, :, t * P:(t + 1) * P], K.bank[t % 4][:].bitcast(BF16)[:, 0:D].rearrange("p (c k) -> p c k", c=2),
                                   ACT.Copy).then_inc(s["out"], 1)
        names = "scaled inner_done silu_done h_done hq_done turned turned_out down_done sum_done"
        with phase(nc, K.sems, names) as (block, s):
            hsc = sbuf(es, nc, "h_scale", [P, 2, 4])
            G = sbuf(es, nc, "gate", [P, 2, INNER])
            H = sbuf(es, nc, "h", [P, INNER])
            Hq = sbuf(es, nc, "hq", [P, 2, INNER], BF16)
            HqT = sbuf(es, nc, "hqT", [P, 2, INNER // P, P], BF16)
            wscale = sbuf(es, nc, "both_scales", [P, NT, 2])

            @block.tensor
            def _(pe):
                def inner_product(t):
                    if t >= 1:
                        pe.wait_ge(s["h_done"], t)
                    for part, W_ in enumerate((Wg, Wu)):
                        for c in range(2):
                            for k in range(DC):
                                ins = pe.matmul(K.bank[2 * part + c][:], XqT[:, k, t * P:(t + 1) * P], W_[:, k, c * BLK:(c + 1) * BLK],
                                                start=(k == 0), stop=(k == DC - 1))
                    ins.then_inc(s["inner_done"], 1)

                inner_product(0)
                for t in range(NT):
                    if t + 1 < NT:
                        inner_product(t + 1)
                    pe.wait_ge(s["hq_done"], t + 1)
                    if t >= 2:
                        pe.wait_ge(s["turned_out"], t - 1)
                    for m in range(INNER // P):
                        ins = pe.transpose(K.bank[4 + t % 2][:].bitcast(BF16)[:, m * P:(m + 1) * P], Hq[:, t % 2, m * P:(m + 1) * P], K.identb[:])
                    ins.then_inc(s["turned"], 1)
                    pe.wait_ge(s["turned_out"], t + 1)
                    if t >= 2:
                        pe.wait_ge(s["sum_done"], t - 1)
                    for m in range(INNER // P):
                        ins = pe.matmul(K.bank[6 + t % 2][:, 0:D], HqT[:, t % 2, m, :], Wd[:, m, :], start=(m == 0), stop=(m == INNER // P - 1))
                    ins.then_inc(s["down_done"], 1)

            @block.scalar
            def _(act):
                act.wait_ge(s["scaled"], 1)
                for t in range(NT + 1):
                    if t < NT:
                        act.wait_ge(s["inner_done"], t + 1)
                        if t >= 2:
                            act.wait_ge(s["h_done"], t - 1)
                        for c in range(2):
                            ins = act.activation(G[:, t % 2, c * BLK:(c + 1) * BLK], K.bank[c][:], ACT.Silu, scale=wscale[:, t, 0:1])
                        ins.then_inc(s["silu_done"], 1)
                    if t > 0:
                        act.wait_ge(s["turned"], t)
                        if t >= 3:
                            act.wait_ge(s["down_done"], t - 2)
                        act.activation(HqT[:, (t - 1) % 2].rearrange("p m k -> p (m k)"), K.bank[4 + (t - 1) % 2][:].bitcast(BF16)[:, 0:INNER],
                                       ACT.Copy).then_inc(s["turned_out"], 1)

            @block.vector
            def _(dve):
                for i in range(2):
                    dve.tensor_scalar(wscale[:, :, i], xsc[:, :, 2], wsc[:, i, 1:2], None, ALU.mult)
                dve.drain()
                dve.sem_inc(s["scaled"], 1)

                def total(t):
                    dve.wait_ge(s["down_done"], t + 1)
                    dve.scalar_tensor_tensor(out=r[:, t, :], in0=K.bank[6 + t % 2][:, 0:D], scalar=hsc[:, t % 2, 3:4], in1=K.Xtok[:, t, :],
                                             op0=ALU.mult, op1=ALU.add).then_inc(s["sum_done"], 1)

                for t in range(NT):
                    dve.wait_ge(s["silu_done"], t + 1)
                    for c in range(2):
                        ins = dve.scalar_tensor_tensor(out=H[:, c * BLK:(c + 1) * BLK], in0=K.bank[2 + c][:], scalar=wscale[:, t, 1:2],
                                                       in1=G[:, t % 2, c * BLK:(c + 1) * BLK], op0=ALU.mult, op1=ALU.mult)
                    ins.then_inc(s["h_done"], 1)
                    dve.drain()
                    if t >= 2:
                        dve.wait_ge(s["turned"], t - 1)
                    quantise(dve, H[:], H[:], Hq[:, t % 2, :], hsc[:, t % 2, :]).then_inc(s["hq_done"], 1)
                    dve.tensor_scalar(hsc[:, t % 2, 3:4], hsc[:, t % 2, 2:3], wsc[:, 2, 1:2], None, ALU.mult)
                    dve.drain()
                    if t >= 1:
                        total(t - 1)
                total(NT - 1)
        finish_tokens(nc, K, r)


def L2_attn_layout(i):
    W = np.asarray(i["L2_attn_W_qkv"]).T
    return {"L2a_W": rows(W), "L2a_Wo": rows(np.asarray(i["L2_attn_W_out"]).T)}


def L2_attn(nc, K, w):
    xT = K.XT[K.cur]
    NQ = 2 * DC
    with ExitStack() as es:
        Wo = sbuf(es, nc, "Wo", [P, DC, D])
        OT = sbuf(es, nc, "OT", [P, DC, TOK])
        with ExitStack() as inside:
            W = sbuf(inside, nc, "Wqkv", [P, DC, 3 * D])
            QT, KT, RT = (sbuf(inside, nc, n, [P, DC, TOK]) for n in ("QT", "KT", "recip_den"))
            same = sbuf(inside, nc, "same_head", [P, P])
            load(nc, K, (W[:], w["L2a_W"]), (Wo[:], w["L2a_Wo"]))
            with ExitStack() as inn, phase(nc, K.sems, "done min_done exp_done out") as (block, s):
                low = sbuf(inn, nc, "low", [P, 2, BLK])
                steps = [(m, j) for m in range(NQ) for j in range(NB)]

                @block.tensor
                def _(pe):
                    for n, (m, j) in enumerate(steps):
                        if n >= 8:
                            pe.wait_ge(s["out"], n - 7)
                        for k in range(DC):
                            ins = pe.matmul(K.bank[n % 8][:], W[:, k, m * P:(m + 1) * P], xT[:, k, j * BLK:(j + 1) * BLK], start=(k == 0), stop=(k == DC - 1))
                        ins.then_inc(s["done"], 1)

                @block.vector
                def _(dve):
                    dve.tensor_copy(same[:].rearrange("p (h d) -> p h d", d=HD), inner(K.head_rows[:], HD))
                    for n in range(len(steps) + 1):
                        if n < len(steps):
                            dve.wait_ge(s["done"], n + 1)
                            if n >= 2:
                                dve.drain()
                            dve.tensor_scalar(low[:, n % 2, :], K.bank[n % 8][:], 0.0, None, ALU.min).then_inc(s["min_done"], 1)
                        if n > 0:
                            m, j = steps[n - 1]
                            dve.wait_ge(s["exp_done"], n)
                            dst = (QT if m < DC else KT)[:, m % DC, j * BLK:(j + 1) * BLK]
                            dve.scalar_tensor_tensor(out=dst, in0=K.bank[(n - 1) % 8][:], scalar=0.0, in1=low[:, (n - 1) % 2, :],
                                                     op0=ALU.max, op1=ALU.add)
                            dve.drain()
                            if m < DC:
                                dve.tensor_scalar(dst, dst, float(HD) ** -0.5, None, ALU.mult).then_inc(s["out"], 1)
                            else:
                                dve.sem_inc(s["out"], 1)

                @block.scalar
                def _(act):
                    for n in range(len(steps)):
                        act.wait_ge(s["min_done"], n + 1)
                        act.activation(low[:, n % 2, :], low[:, n % 2, :], ACT.Exp).then_inc(s["exp_done"], 1)

            with ExitStack() as inn, phase(nc, K.sems, "prod_done den_done recip_done") as (block, s):
                run = sbuf(inn, nc, "running", [P, DC, TOK])
                none = sbuf(inn, nc, "zeros", [P, S])

                @block.vector
                def _(dve):
                    dve.memset(none[:], 0.0)
                    dve.drain()
                    for c in range(DC):
                        for b in range(B):
                            dve.tensor_tensor_scan(run[:, c, b * S:(b + 1) * S], KT[:, c, b * S:(b + 1) * S], none[:], 0.0, ALU.add, ALU.add)
                    dve.drain()
                    for c in range(DC):
                        for j in range(NB):
                            z = run[:, c, j * BLK:(j + 1) * BLK]
                            dve.tensor_tensor(z, z, QT[:, c, j * BLK:(j + 1) * BLK], ALU.mult).then_inc(s["prod_done"], 1)
                    for n in range(DC * NB):
                        c, j = divmod(n, NB)
                        z = RT[:, c, j * BLK:(j + 1) * BLK]
                        dve.wait_ge(s["den_done"], n + 1)
                        dve.tensor_scalar(z, K.bank[n][:], 1e-6, None, ALU.max)
                        dve.drain()
                        dve.reciprocal(z, z)

                @block.tensor
                def _(pe):
                    for n in range(DC * NB):
                        c, j = divmod(n, NB)
                        pe.wait_ge(s["prod_done"], n + 1)
                        pe.matmul(K.bank[n][:], same[:], run[:, c, j * BLK:(j + 1) * BLK], start=True, stop=True).then_inc(s["den_done"], 1)

            Qh = sbuf(inside, nc, "Q_heads", [P, HPC, P])
            Vh = sbuf(inside, nc, "V_heads", [P, 2, HPC, P])
            AT = sbuf(inside, nc, "attnT", [P, HPC, P])
            kv = sbuf(inside, nc, "k_v_tokens", [P, 2, 2 * P])
            St = sbuf(inside, nc, "state", [P, P])
            with phase(nc, K.sems, "q_spread kv_done kv_out v_spread attn_done attn_out state_out o_done out") as (block, s):
                steps = NT * DC

                @block.tensor
                def _(pe):
                    for n in range(steps):
                        t, c = divmod(n, DC)
                        ts = slice(t * P, (t + 1) * P)
                        if n >= 1:
                            pe.wait_ge(s["kv_out"], n)
                        for k in range(DC):
                            pe.matmul(K.bank[2][:, 0:P], xT[:, k, ts], W[:, k, 2 * D + c * P:2 * D + (c + 1) * P], start=(k == 0), stop=(k == DC - 1))
                        pe.transpose(K.bank[2][:, P:2 * P], KT[:, c, ts], K.ident[:]).then_inc(s["kv_done"], 1)
                        pe.wait_ge(s["q_spread"], n + 1)
                        if n >= 1:
                            pe.wait_ge(s["attn_out"], n)
                        for g in range(2):
                            ins = pe.matmul(K.bank[g][:], KT[:, c, ts], Qh[:, 4 * g:4 * g + 4, :], start=True, stop=True)
                        ins.then_inc(s["attn_done"], 1)
                        if n >= 1:
                            pe.wait_ge(s["out"], n)
                        first = t % 8 == 0
                        if not first:
                            pe.wait_ge(s["state_out"], n + 1)
                            pe.matmul(K.bank[3][:, 0:P], St[:], QT[:, c, ts], start=True, stop=False)
                        pe.wait_ge(s["v_spread"], n + 1)
                        pe.wait_ge(s["attn_out"], n + 1)
                        for h in range(HPC):
                            ins = pe.matmul(K.bank[3][:, 0:P], Vh[:, n % 2, h, :], AT[:, h, :], start=(first and h == 0), stop=(h == HPC - 1))
                        ins.then_inc(s["o_done"], 1)
                        pe.wait_ge(s["kv_out"], n + 1)
                        pe.wait_ge(s["state_out"], n + 1)
                        pe.matmul(K.bank[4 + 2 * (t // 8) + c][:, 0:P], kv[:, n % 2, P:2 * P], kv[:, n % 2, 0:P], start=first, stop=True,
                                  skip_group_check=True)

                @block.scalar
                def _(act):
                    for n in range(steps):
                        act.wait_ge(s["kv_done"], n + 1)
                        if n >= 2:
                            act.wait_ge(s["o_done"], n)
                        act.activation(kv[:, n % 2, :], K.bank[2][:, 0:2 * P], ACT.Copy).then_inc(s["kv_out"], 1)

                @block.gpsimd
                def _(pool):
                    for n in range(steps):
                        pool.wait_ge(s["kv_out"], n + 1)
                        if n >= 2:
                            pool.wait_ge(s["o_done"], n - 1)
                        pool.tensor_tensor(Vh[:, n % 2], middle(kv[:, n % 2, 0:P], HPC), K.head_cols[:], ALU.mult).then_inc(s["v_spread"], 1)

                @block.vector
                def _(dve):
                    for n in range(steps):
                        t, c = divmod(n, DC)
                        ts = slice(t * P, (t + 1) * P)
                        if n >= 1:
                            dve.wait_ge(s["attn_done"], n)
                        dve.tensor_tensor(Qh[:], middle(QT[:, c, ts], HPC), inner(K.head_rows[:], P), ALU.mult).then_inc(s["q_spread"], 1)
                        if n >= 1:
                            dve.wait_ge(s["o_done"], n)
                            tp, cp = divmod(n - 1, DC)
                            dve.tensor_tensor(OT[:, cp, tp * P:(tp + 1) * P], K.bank[3][:, 0:P], RT[:, cp, tp * P:(tp + 1) * P], ALU.mult).then_inc(s["out"], 1)
                        if t % 8 == 0:
                            dve.sem_inc(s["state_out"], 1)
                        else:
                            dve.wait_ge(s["kv_done"], n + 1)
                            dve.tensor_tensor(St[:], K.bank[4 + 2 * (t // 8) + c][:, 0:P], same[:], ALU.mult).then_inc(s["state_out"], 1)
                        dve.wait_ge(s["attn_done"], n + 1)
                        for g in range(2):
                            ins = dve.tensor_tensor(AT[:, 4 * g:4 * g + 4, :], K.bank[g][:].rearrange("p (h l) -> p h l", h=4), middle(K.causal_T[:], 4), ALU.mult)
                        ins.then_inc(s["attn_out"], 1)
                    dve.wait_ge(s["o_done"], steps)
                    dve.tensor_tensor(OT[:, DC - 1, TOK - P:TOK], K.bank[3][:, 0:P], RT[:, DC - 1, TOK - P:TOK], ALU.mult).then_inc(s["out"], 1)
        finish(nc, K, lambda k, h, j: Wo[:, k, h * P:(h + 1) * P], block_of(OT), DC)


def block_mean(nc, K, out, size):
    with phase(nc, K.sems, "step") as (block, s):
        @block.gpsimd
        def _(pool):
            n = P // size
            pool.memset(out, 1.0 / size).then_inc(s["step"], 1)
            v = out.rearrange("p (n j) -> p n j", n=n)
            pool.wait_ge(s["step"], 1)
            pool.affine_select(out=v, in_=v, compare_op=ALU.is_ge, fill=0.0, base=0, pattern=[[-size, n], [0, size]], channel_multiplier=1).then_inc(s["step"], 1)
            pool.wait_ge(s["step"], 2)
            pool.affine_select(out=v, in_=v, compare_op=ALU.is_ge, fill=0.0, base=size - 1, pattern=[[size, n], [0, size]], channel_multiplier=-1)


def feature_ln(nc, K, J, n, halves_, src, dst, g, b):
    with ExitStack() as es, phase(nc, K.sems, "mean_done centred squared var_done std_done normed out") as (block, s):
        sq = sbuf(es, nc, "squares", [P, 2, halves_, BLK])
        std = sbuf(es, nc, "std", [P, 2, BLK])
        xc = sbuf(es, nc, "centred", [P, 2, halves_, BLK])

        @block.tensor
        def _(pe):
            def mean(j):
                if j >= 2:
                    pe.wait_ge(s["centred"], j - 1)
                for h in range(halves_):
                    ins = pe.matmul(K.bank[j % 2][:], J, src(j, h), start=(h == 0), stop=(h == halves_ - 1))
                ins.then_inc(s["mean_done"], 1)
            mean(0)
            for j in range(n):
                if j + 1 < n:
                    mean(j + 1)
                pe.wait_ge(s["squared"], j + 1)
                if j >= 2:
                    pe.wait_ge(s["std_done"], j - 1)
                for h in range(halves_):
                    ins = pe.matmul(K.bank[2 + j % 2][:], J, sq[:, j % 2, h, :], start=(h == 0), stop=(h == halves_ - 1))
                ins.then_inc(s["var_done"], 1)

        @block.vector
        def _(dve):
            def centre(j):
                dve.wait_ge(s["mean_done"], j + 1)
                if j >= 2:
                    dve.wait_ge(s["out"], j - 1)
                for h in range(halves_):
                    ins = dve.tensor_tensor(xc[:, j % 2, h, :], src(j, h), K.bank[j % 2][:], ALU.subtract)
                ins.then_inc(s["centred"], 1)
            centre(0)
            for j in range(n):
                if j + 1 < n:
                    centre(j + 1)
                dve.wait_ge(s["std_done"], j + 1)
                dve.reciprocal(std[:, j % 2, :], std[:, j % 2, :])
                dve.drain()
                for h in range(halves_):
                    ins = dve.tensor_tensor(xc[:, j % 2, h, :], xc[:, j % 2, h, :], std[:, j % 2, :], ALU.mult)
                ins.then_inc(s["normed"], 1)

        @block.scalar
        def _(act):
            def square(j):
                act.wait_ge(s["centred"], j + 1)
                if j >= 2:
                    act.wait_ge(s["var_done"], j - 1)
                for h in range(halves_):
                    ins = act.activation(sq[:, j % 2, h, :], xc[:, j % 2, h, :], ACT.Square)
                ins.then_inc(s["squared"], 1)
            square(0)
            for j in range(n):
                if j + 1 < n:
                    square(j + 1)
                act.wait_ge(s["var_done"], j + 1)
                if j >= 2:
                    act.wait_ge(s["normed"], j - 1)
                act.activation(std[:, j % 2, :], K.bank[2 + j % 2][:], ACT.Sqrt, bias=K.eps[:, 0:1]).then_inc(s["std_done"], 1)
                act.wait_ge(s["normed"], j + 1)
                for h in range(halves_):
                    ins = act.activation(dst(j, h), xc[:, j % 2, h, :], ACT.Identity, scale=g(j)[:, h:h + 1], bias=b(j)[:, h:h + 1])
                ins.then_inc(s["out"], 1)


LAT = D // 4


def L1_attn_layout(i):
    g = lambda n: np.asarray(i["L1_attn_" + n])
    uq = pad(g("W_uq"), 0, P)
    ukv = np.concatenate([np.zeros((LAT, 2 * D), np.float32), g("W_ukv")])
    return {"L1a_Wd": rows(np.concatenate([g("W_dq"), g("W_dkv")], axis=1)), "L1a_uq": uq, "L1a_ukv": ukv,
            "L1a_g": np.concatenate([g("q_ln_g"), g("kv_ln_g")]).reshape(P, 1), "L1a_b": np.concatenate([g("q_ln_b"), g("kv_ln_b")]).reshape(P, 1),
            "L1a_Wo": rows(g("W_o").T)}


def L1_attn(nc, K, w):
    xT = K.XT[K.cur]
    QT_ = S // P
    with ExitStack() as es:
        Wo = sbuf(es, nc, "Wo", [P, DC, D])
        OT = sbuf(es, nc, "OT", [P, DC * TOK])
        with ExitStack() as inside:
            QT, KT = (sbuf(inside, nc, n, [P, DC * TOK]) for n in ("QT", "KT"))
            V = sbuf(inside, nc, "V", [P, DC, NT, P])
            with ExitStack() as inn:
                Wd = sbuf(inn, nc, "Wd", [P, DC, P])
                uq = sbuf(inn, nc, "uq", [P, D])
                ukv = sbuf(inn, nc, "ukv", [P, 2 * D])
                g, b = (sbuf(inn, nc, n, [P, 1]) for n in ("g", "b"))
                cT = sbuf(inn, nc, "latents", [P, TOK])
                J = sbuf(inn, nc, "J", [P, P])
                load(nc, K, (Wd[:], w["L1a_Wd"]), (uq[:], w["L1a_uq"]), (ukv[:], w["L1a_ukv"]), (g[:], w["L1a_g"]), (b[:], w["L1a_b"]), (Wo[:], w["L1a_Wo"]))
                block_mean(nc, K, J[:], LAT)
                cb = lambda j: cT[:, j * BLK:(j + 1) * BLK]
                project(nc, K, inn, 1, DC, lambda k, m: Wd[:, k, :], block_of(xT), *copy_to(lambda m, j: cb(j)))
                feature_ln(nc, K, J[:], NB, 1, lambda j, h: cb(j), lambda j, h: cb(j), lambda j: g[:], lambda j: b[:])
                for dst, W in ((QT, uq), (KT, ukv)):
                    project(nc, K, inn, DC, 1, lambda k, m: W[:, m * P:(m + 1) * P], lambda k, j: cb(j),
                            *copy_to(lambda m, j: dst[:, m * TOK + j * BLK:m * TOK + (j + 1) * BLK]))
                with phase(nc, K.sems, "done out") as (block, s):
                    @block.tensor
                    def _(pe):
                        for t in range(NT):
                            if t >= 8:
                                pe.wait_ge(s["out"], t - 7)
                            pe.matmul(K.bank[t % 8][:, 0:D], cT[:, t * P:(t + 1) * P], ukv[:, D:2 * D], start=True, stop=True).then_inc(s["done"], 1)

                    @block.vector
                    def _(dve):
                        for t in range(NT):
                            dve.wait_ge(s["done"], t + 1)
                            dve.tensor_copy(V[:, :, t, :], K.bank[t % 8][:, 0:D].rearrange("p (c k) -> p c k", c=DC)).then_inc(s["out"], 1)

            Vh = sbuf(inside, nc, "V_heads", [P, QT_, HPC, P])
            Qh = sbuf(inside, nc, "Q_heads", [P, 2, HPC, P])
            Sc = sbuf(inside, nc, "scores", [P, 2, S])
            zero = sbuf(inside, nc, "zero_marks", [P, S])
            PT = sbuf(inside, nc, "probsT", [P, 2, S])
            mx = sbuf(inside, nc, "max", [P, 2])
            sums = sbuf(inside, nc, "sums", [P, 2, HPC])
            rec = sbuf(inside, nc, "recip", [P, HPC])
            Rx, RT = (sbuf(inside, nc, n, [P, 2, P]) for n in ("recip_spread", "recipT"))
            scale = float(HD) ** -0.5
            N = QT_ * HPC
            names = "q_spread scored max_done exp_done turned pt_out v_spread r_spread pv_done o_done rt_out out"
            with phase(nc, K.sems, names) as (block, s):
                sc = lambda i: K.psum[:, 2 * (i % 2):2 * (i % 2) + 2, :].rearrange("p b k -> p (b k)")
                ob = lambda q: K.bank[6 + q % 2]

                def slot_free(eng, sem, u, per, i):
                    if i >= 2:
                        eng.wait_ge(sem, u * per + i - 1)

                def turn_over(eng, u, *pairs):
                    for sem, per in pairs:
                        eng.wait_ge(sem, u * per + per)

                @block.gpsimd
                def _(pool):
                    with pool.Fori(0, DC * B) as u:
                        for kt in range(QT_):
                            src = V[:].rearrange("p c t k -> p (c t k)")[:, bass.ds(u * (QT_ * P) + kt * P, P)]
                            pool.tensor_tensor(Vh[:, kt], middle(src, HPC), K.head_cols[:], ALU.mult).then_inc(s["v_spread"], 1)
                        turn_over(pool, u, (s["pv_done"], N))

                @block.tensor
                def _(pe):
                    with pe.Fori(0, DC * B) as u:
                        def score(i):
                            q, h = divmod(i, HPC)
                            if h == 0:
                                pe.wait_ge(s["q_spread"], u * QT_ + q + 1)
                            slot_free(pe, s["max_done"], u, N, i)
                            n = (q + 1) * P
                            for o in range(0, n, BLK):
                                e = min(n, o + BLK)
                                pe.matmul(sc(i)[:, o:e], Qh[:, q % 2, h, :], KT[:, bass.ds(u * S + o, e - o)], start=True, stop=(e < n),
                                          skip_group_check=True)
                            pe.matmul(sc(i)[:, n - P:n], K.identb[:], K.above[:], start=False, stop=True, skip_group_check=True).then_inc(s["scored"], 1)

                        def values(i):
                            q, h = divmod(i, HPC)
                            pe.wait_ge(s["pt_out"], u * N + i + 1)
                            if h == 0:
                                pe.wait_ge(s["v_spread"], u * QT_ + q + 1)
                                slot_free(pe, s["out"], u, QT_, q)
                            for kt in range(q + 1):
                                ins = pe.matmul(ob(q)[:, 0:P], Vh[:, kt, h, :], PT[:, i % 2, kt * P:(kt + 1) * P], start=(h == 0 and kt == 0),
                                                stop=(h == HPC - 1 and kt == q))
                            ins.then_inc(s["pv_done"], 1)
                            if h == HPC - 1:
                                pe.wait_ge(s["r_spread"], u * QT_ + q + 1)
                                pe.transpose(ob(q)[:, P:2 * P], Rx[:, q % 2, :], K.ident[:]).then_inc(s["o_done"], 1)

                        score(0)
                        for i in range(N):
                            if i + 1 < N:
                                score(i + 1)
                            pe.wait_ge(s["exp_done"], u * N + i + 1)
                            if i > 0:
                                pe.wait_ge(s["pt_out"], u * N + i)
                            for kt in range(i // HPC + 1):
                                ins = pe.transpose(K.bank[4 + kt // 4][:, (kt % 4) * P:(kt % 4 + 1) * P], Sc[:, i % 2, kt * P:(kt + 1) * P], K.ident[:])
                            ins.then_inc(s["turned"], 1)
                            if i > 0:
                                values(i - 1)
                        values(N - 1)
                        turn_over(pe, u, (s["max_done"], N), (s["out"], QT_))

                @block.vector
                def _(dve):
                    with dve.Fori(0, DC * B) as u:
                        def spread(q):
                            if q >= 2:
                                dve.wait_ge(s["scored"], u * N + (q - 1) * HPC)
                            dve.tensor_tensor(Qh[:, q % 2], middle(QT[:, bass.ds(u * S + q * P, P)], HPC), inner(K.head_rows[:], P), ALU.mult).then_inc(s["q_spread"], 1)

                        def output(q):
                            dve.wait_ge(s["rt_out"], u * QT_ + q + 1)
                            dve.tensor_tensor(OT[:, bass.ds(u * S + q * P, P)], ob(q)[:, 0:P], RT[:, q % 2, :], ALU.mult).then_inc(s["out"], 1)

                        def recip(q):
                            dve.wait_ge(s["exp_done"], u * N + (q + 1) * HPC)
                            slot_free(dve, s["o_done"], u, QT_, q)
                            dve.reciprocal(rec[:], sums[:, q % 2, :])
                            dve.drain()
                            dve.tensor_copy(Rx[:, q % 2, :].rearrange("p (h d) -> p h d", h=HPC), inner(rec[:], HD)).then_inc(s["r_spread"], 1)

                        spread(0)
                        for i in range(N):
                            q, h = divmod(i, HPC)
                            n = (q + 1) * P
                            if h == 2 and q + 1 < QT_:
                                spread(q + 1)
                            slot_free(dve, s["turned"], u, N, i)
                            dve.wait_ge(s["scored"], u * N + i + 1)
                            dve.tensor_scalar(zero[:, 0:n], sc(i)[:, 0:n], 0.0, NEG, ALU.is_equal, ALU.mult)
                            dve.drain()
                            dve.tensor_tensor_reduce(Sc[:, i % 2, 0:n], sc(i)[:, 0:n], zero[:, 0:n], 1.0, NEG, ALU.add, ALU.max, mx[:, i % 2:i % 2 + 1])
                            dve.drain()
                            dve.tensor_scalar(mx[:, i % 2:i % 2 + 1], mx[:, i % 2:i % 2 + 1], -scale, None, ALU.mult).then_inc(s["max_done"], 1)
                            if q > 0 and h == 0:
                                recip(q - 1)
                            if q > 0 and h == 2:
                                output(q - 1)
                        recip(QT_ - 1)
                        output(QT_ - 1)
                        turn_over(dve, u, (s["turned"], N), (s["o_done"], QT_))

                @block.scalar
                def _(act):
                    with act.Fori(0, DC * B) as u:
                        def exp(i):
                            q, h = divmod(i, HPC)
                            act.wait_ge(s["max_done"], u * N + i + 1)
                            if h == 0:
                                slot_free(act, s["r_spread"], u, QT_, q)
                            p = Sc[:, i % 2, 0:(q + 1) * P]
                            act.activation(p, p, ACT.Exp, bias=mx[:, i % 2:i % 2 + 1], scale=scale, accum_out=sums[:, q % 2, h:h + 1]).then_inc(s["exp_done"], 1)

                        def turn_recip(q):
                            act.wait_ge(s["o_done"], u * QT_ + q + 1)
                            act.activation(RT[:, q % 2, :], ob(q)[:, P:2 * P], ACT.Copy).then_inc(s["rt_out"], 1)

                        exp(0)
                        for i in range(N):
                            q, h = divmod(i, HPC)
                            if i + 1 < N:
                                exp(i + 1)
                            n = (q + 1) * P
                            act.wait_ge(s["turned"], u * N + i + 1)
                            slot_free(act, s["pv_done"], u, N, i)
                            act.activation(PT[:, i % 2, 0:n], K.psum[:, 4:6, :].rearrange("p b k -> p (b k)")[:, 0:n], ACT.Copy).then_inc(s["pt_out"], 1)
                            if q > 0 and h == 0:
                                turn_recip(q - 1)
                        turn_recip(QT_ - 1)
                        turn_over(act, u, (s["r_spread"], QT_), (s["pv_done"], N))
        OTv = OT[:].rearrange("p (c t) -> p c t", c=DC)
        finish(nc, K, lambda k, h, j: Wo[:, k, h * P:(h + 1) * P], block_of(OTv), DC)


L0E = 8
PICKED = 512
PT4 = PICKED // P


def L0_ffn_layout(i):
    g = lambda n: np.asarray(i["L0_ffn_" + n])
    up = lambda a, sh: np.concatenate([rows(g(a)[e].T) for e in range(L0E)] + [rows(g(sh).T)], axis=2)
    vec = lambda a, sh: np.ascontiguousarray(np.concatenate([g(a), g(sh)[None]]).T)
    ln = lambda a, sh: np.stack([g(a), g(sh)], axis=1)
    return {"L0f_W1": up("ew1", "sw1"), "L0f_W2": up("ew2", "sw2"), "L0f_b1": vec("eb1", "sb1"), "L0f_b2": vec("eb2", "sb2"),
            "L0f_W3": np.concatenate([g("ew3").transpose(2, 0, 1).reshape(P, L0E * D), g("sw3").T], axis=1),
            "L0f_b3": np.concatenate([g("eb3"), g("sb3")[None]]), "L0f_sb3": cols(g("sb3")),
            "L0f_g": ln("sel_ln_g", "s_ln_g"), "L0f_b": ln("sel_ln_b", "s_ln_b"),
            "L0f_Wgate": rows(np.concatenate([g("eg_w"), g("sg_w")]).T), "L0f_bgate": np.concatenate([g("eg_b"), g("sg_b")]),
            "L0f_ebias": g("exp_bias"), "L0f_ib": cols(g("index_b")), "L0f_it": cols(g("index_t")),
            "L0f_ibr": g("index_b"), "L0f_itr": g("index_t")}


def turn_tokens(nc, K):
    xo = K.XT[K.cur]
    with phase(nc, K.sems, "turned act_out dve_out") as (block, s):
        @block.tensor
        def _(pe):
            for t in range(NT):
                if t >= 8:
                    pe.wait_ge(s["act_out"] if t % 2 == 0 else s["dve_out"], (t - 8) // 2 + 1)
                for h in range(DC):
                    ins = pe.transpose(K.bank[t % 8][:, h * P:(h + 1) * P], K.Xtok[:, t, h * P:(h + 1) * P], K.ident[:])
                ins.then_inc(s["turned"], 1)

        @block.scalar
        def _(act):
            for t in range(0, NT, 2):
                act.wait_ge(s["turned"], t + 1)
                act.activation(xo[:, :, t * P:(t + 1) * P], K.bank[t % 8][:, 0:D].rearrange("p (c k) -> p c k", c=2), ACT.Copy).then_inc(s["act_out"], 1)

        @block.vector
        def _(dve):
            for t in range(1, NT, 2):
                dve.wait_ge(s["turned"], t + 1)
                dve.tensor_copy(xo[:, :, t * P:(t + 1) * P], K.bank[t % 8][:, 0:D].rearrange("p (c k) -> p c k", c=2)).then_inc(s["dve_out"], 1)


def L0_ffn(nc, K, w):
    xT = K.XT[K.cur]
    NJ = L0E + 1 + NB
    expert = lambda n: min(n, L0E)
    pool_of_rows = nc.dram_tensor("L0f_rows", [TOK + PICKED, D], F32, kind="Internal").ap()
    with ExitStack() as es:
        num = sbuf(es, nc, "expert_number", [P, L0E])
        W3 = sbuf(es, nc, "W3", [P, (L0E + 1) * D])
        b3 = sbuf(es, nc, "b3", [L0E + 1, D])
        sb3 = sbuf(es, nc, "sb3", [P, DC])
        Z = sbuf(es, nc, "Z", [P, NJ, BLK])
        Xm = sbuf(es, nc, "picked", [P, PT4, D])
        XmT = sbuf(es, nc, "pickedT", [P, DC, PICKED])
        G = sbuf(es, nc, "gates", [P, PT4, L0E + 1])
        home = sbuf(es, nc, "home_row", [P, NT], U32)
        number_experts(nc, K, es, num[:], L0E)
        with ExitStack() as inn:
            W1, W2 = (sbuf(inn, nc, n, [P, DC, (L0E + 1) * P]) for n in ("W1", "W2"))
            b1, b2 = (sbuf(inn, nc, n, [P, L0E + 1]) for n in ("b1", "b2"))
            lng, lnb = (sbuf(inn, nc, n, [P, 2]) for n in ("lng", "lnb"))
            Wg = sbuf(inn, nc, "Wgate", [P, DC, L0E + 1])
            bg = sbuf(inn, nc, "bgate", [P, L0E + 1])
            eb = sbuf(inn, nc, "ebias", [P, L0E])
            J = sbuf(inn, nc, "J", [P, P])
            load(nc, K, (W1[:], w["L0f_W1"]), (W2[:], w["L0f_W2"]), (W3[:], w["L0f_W3"]), (b3[:], w["L0f_b3"]), (sb3[:], w["L0f_sb3"]), (b1[:], w["L0f_b1"]),
                 (b2[:], w["L0f_b2"]), (lng[:], w["L0f_g"]), (lnb[:], w["L0f_b"]), (Wg[:], w["L0f_Wgate"]), (bg[:], spread(w["L0f_bgate"])),
                 (eb[:], spread(w["L0f_ebias"])))
            block_mean(nc, K, J[:], P)
            with ExitStack() as ix, phase(nc, K.sems, "loaded rows_out counted index_done picked turned out") as (block, s):
                ints = sbuf(ix, nc, "index_cols", [P, 2, PT4], I32)
                intr = sbuf(ix, nc, "index_rows", [P, 2, PICKED], I32)
                fc = sbuf(ix, nc, "index_cols_f", [P, 2, PT4])
                fr = sbuf(ix, nc, "index_rows_f", [P, 2, PICKED])
                at = sbuf(ix, nc, "flat_index", [P, PT4], U32)
                ordi = sbuf(ix, nc, "order_int", [P, PICKED], I32)
                order = sbuf(ix, nc, "order", [P, PICKED])
                toki = sbuf(ix, nc, "token_int", [P, NT], I32)
                tok = sbuf(ix, nc, "token", [P, NT])
                hit = sbuf(ix, nc, "hit", [P, PICKED])
                last = sbuf(ix, nc, "last_hit", [P, NT, 3])

                @block.sync
                def _(sp):
                    sp.dma_start(pool_of_rows[0:TOK].rearrange("(t p) d -> p t d", p=P), K.Xtok[:]).then_inc(s["rows_out"], 16)
                    sp.dma_start(ints[:, 0], w["L0f_ib"]).then_inc(s["loaded"], 16)
                    sp.dma_start(ints[:, 1], w["L0f_it"]).then_inc(s["loaded"], 16)
                    sp.dma_start(intr[:, 0], spread(w["L0f_ibr"])).then_inc(s["loaded"], 16)
                    sp.dma_start(intr[:, 1], spread(w["L0f_itr"])).then_inc(s["loaded"], 16)

                @block.gpsimd
                def _(pool):
                    pool.iota(ordi[:], pattern=[[1, PICKED]], base=1, channel_multiplier=0).then_inc(s["counted"], 1)
                    pool.iota(toki[:], pattern=[[P, NT]], base=0, channel_multiplier=1).then_inc(s["counted"], 1)
                    pool.wait_ge(s["index_done"], 1)
                    pool.wait_ge(s["rows_out"], 16)
                    for q in range(PT4):
                        pool.indirect_dma_start(out=Xm[:, q, :], out_offset=None, in_=pool_of_rows[0:TOK, :],
                                                in_offset=bass.IndirectOffsetOnAxis(ap=at[:, q:q + 1], axis=0)).then_inc(s["picked"], 16)

                @block.vector
                def _(dve):
                    dve.wait_ge(s["loaded"], 64)
                    dve.wait_ge(s["counted"], 2)
                    dve.tensor_copy(fc[:], ints[:])
                    dve.tensor_copy(fr[:], intr[:])
                    dve.tensor_copy(order[:], ordi[:])
                    dve.tensor_copy(tok[:], toki[:])
                    dve.drain()
                    dve.scalar_tensor_tensor(out=at[:], in0=fc[:, 0], scalar=float(S), in1=fc[:, 1], op0=ALU.mult, op1=ALU.add).then_inc(s["index_done"], 1)
                    dve.scalar_tensor_tensor(out=fr[:, 0], in0=fr[:, 0], scalar=float(S), in1=fr[:, 1], op0=ALU.mult, op1=ALU.add)
                    dve.drain()
                    for t in range(NT):
                        dve.scalar_tensor_tensor(out=hit[:], in0=fr[:, 0], scalar=tok[:, t:t + 1], in1=order[:], op0=ALU.is_equal, op1=ALU.mult)
                        dve.drain()
                        dve.reduce_max(last[:, t, 0:1], hit[:], AX)
                        dve.drain()
                    dve.tensor_scalar(last[:, :, 1], last[:, :, 0], 0.0, None, ALU.is_gt)
                    dve.scalar_tensor_tensor(out=last[:, :, 2], in0=last[:, :, 0], scalar=float(TOK - 1), in1=tok[:], op0=ALU.add, op1=ALU.subtract)
                    dve.drain()
                    dve.tensor_tensor(last[:, :, 2], last[:, :, 2], last[:, :, 1], ALU.mult)
                    dve.drain()
                    dve.tensor_tensor(home[:], last[:, :, 2], tok[:], ALU.add)

                @block.tensor
                def _(pe):
                    pe.wait_ge(s["picked"], 16 * PT4)
                    for q in range(PT4):
                        for h in range(DC):
                            ins = pe.transpose(K.bank[q][:, h * P:(h + 1) * P], Xm[:, q, h * P:(h + 1) * P], K.ident[:])
                        ins.then_inc(s["turned"], 1)

                @block.scalar
                def _(act):
                    for q in range(PT4):
                        act.wait_ge(s["turned"], q + 1)
                        act.activation(XmT[:, :, q * P:(q + 1) * P], K.bank[q][:, 0:D].rearrange("p (c k) -> p c k", c=2), ACT.Copy).then_inc(s["out"], 1)

            with ExitStack() as up, phase(nc, K.sems, "done silu_done z_done") as (block, s):
                sl = sbuf(up, nc, "silu", [P, 2, BLK])

                @block.tensor
                def _(pe):
                    for n in range(NJ):
                        e = expert(n)
                        src = XmT if n <= L0E else xT
                        o = 0 if n <= L0E else (n - L0E - 1) * BLK
                        if n >= 4:
                            pe.wait_ge(s["z_done"], n - 3)
                        for part, W in enumerate((W1, W2)):
                            for k in range(DC):
                                ins = pe.matmul(K.bank[2 * (n % 4) + part][:], W[:, k, e * P:(e + 1) * P], src[:, k, o:o + BLK], start=(k == 0), stop=(k == DC - 1))
                        ins.then_inc(s["done"], 1)

                @block.scalar
                def _(act):
                    for n in range(NJ):
                        act.wait_ge(s["done"], n + 1)
                        if n >= 2:
                            act.wait_ge(s["z_done"], n - 1)
                        act.activation(sl[:, n % 2, :], K.bank[2 * (n % 4)][:], ACT.Silu, bias=b1[:, expert(n):expert(n) + 1]).then_inc(s["silu_done"], 1)

                @block.vector
                def _(dve):
                    for n in range(NJ):
                        dve.wait_ge(s["silu_done"], n + 1)
                        dve.scalar_tensor_tensor(out=Z[:, n, :], in0=K.bank[2 * (n % 4) + 1][:], scalar=b2[:, expert(n):expert(n) + 1], in1=sl[:, n % 2, :],
                                                 op0=ALU.add, op1=ALU.mult).then_inc(s["z_done"], 1)

            ln = lambda v: lambda n: v[:, 0:1] if n < L0E else v[:, 1:2]
            feature_ln(nc, K, J[:], NJ, 1, lambda n, h: Z[:, n, :], lambda n, h: Z[:, n, :], ln(lng), ln(lnb))

            with ExitStack() as gt, phase(nc, K.sems, "scored biased sigma_done ready weights_done") as (block, s):
                sc = sbuf(gt, nc, "scores", [P, PT4, L0E + 1])
                v = sbuf(gt, nc, "biased", [P, PT4, L0E])
                top = sbuf(gt, nc, "top", [P, PT4, 8])
                at = sbuf(gt, nc, "top_index", [P, PT4, 8], U32)
                atf = sbuf(gt, nc, "top_index_f", [P, PT4, 8])
                d = sbuf(gt, nc, "difference", [P, 3, PT4])

                @block.tensor
                def _(pe):
                    for q in range(PT4):
                        for k in range(DC):
                            ins = pe.matmul(K.bank[0][:, q * 16:q * 16 + L0E + 1], XmT[:, k, q * P:(q + 1) * P], Wg[:, k, :], start=(k == 0), stop=(k == DC - 1))
                    ins.then_inc(s["scored"], 1)

                @block.vector
                def _(dve):
                    dve.wait_ge(s["scored"], 1)
                    dve.tensor_tensor(sc[:], K.bank[0][:, 0:16 * PT4].rearrange("p (q e) -> p q e", e=16)[:, :, 0:L0E + 1], middle(bg[:], PT4), ALU.add).then_inc(s["biased"], 1)
                    dve.wait_ge(s["sigma_done"], 1)
                    dve.tensor_tensor(v[:], sc[:, :, 0:L0E], middle(eb[:], PT4), ALU.add)
                    dve.drain()
                    for q in range(PT4):
                        dve.max(top[:, q, :], v[:, q, :])
                    dve.drain()
                    for q in range(PT4):
                        dve.max_index(at[:, q, :], top[:, q, :], v[:, q, :])
                    dve.drain()
                    dve.tensor_copy(atf[:], at[:])
                    dve.drain()
                    dve.tensor_tensor(G[:, :, 0:L0E], middle(num[:], PT4), inner(atf[:, :, 0], L0E), ALU.is_equal)
                    dve.drain()
                    dve.tensor_tensor(v[:], G[:, :, 0:L0E], sc[:, :, 0:L0E], ALU.mult)
                    dve.drain()
                    dve.reduce_sum(d[:, 0, :], v[:], AX)
                    dve.drain()
                    dve.tensor_tensor(d[:, 1, :], d[:, 0, :], sc[:, :, L0E], ALU.subtract)
                    dve.drain()
                    dve.tensor_scalar(d[:, 2, :], d[:, 1, :], -1.0, None, ALU.mult).then_inc(s["ready"], 1)
                    dve.wait_ge(s["weights_done"], 1)
                    dve.tensor_tensor(G[:, :, 0:L0E], G[:, :, 0:L0E], inner(d[:, 1, :], L0E), ALU.mult)
                    dve.tensor_copy(G[:, :, L0E], d[:, 2, :])

                @block.scalar
                def _(act):
                    act.wait_ge(s["biased"], 1)
                    act.activation(sc[:], sc[:], ACT.Sigmoid).then_inc(s["sigma_done"], 1)
                    act.wait_ge(s["ready"], 1)
                    act.activation(d[:, 1:3, :], d[:, 1:3, :], ACT.Sigmoid).then_inc(s["weights_done"], 1)

        acc = sbuf(es, nc, "acc", [P, PT4, D])
        st = sbuf(es, nc, "ln_stats", [P, PT4, 9])
        with ExitStack() as gt, phase(nc, K.sems, "turned turned_out bias_done bias_out done added stats_done std_done stored") as (block, s):
            gT = sbuf(gt, nc, "gatesT", [L0E + 1, PICKED])

            @block.tensor
            def _(pe):
                for q in range(PT4):
                    ins = pe.transpose(K.bank[0][0:L0E + 1, q * P:(q + 1) * P], G[:, q, :], K.ident[:])
                ins.then_inc(s["turned"], 1)
                pe.wait_ge(s["turned_out"], 1)
                for q in range(PT4):
                    if q:
                        pe.wait_ge(s["bias_out"], q)
                    pe.matmul(K.bank[1][:, 0:D], gT[:, q * P:(q + 1) * P], b3[:], start=True, stop=True).then_inc(s["bias_done"], 1)
                for n in range(PT4 * (L0E + 1)):
                    q, e = divmod(n, L0E + 1)
                    if n >= 6:
                        pe.wait_ge(s["added"], n - 5)
                    pe.matmul(K.bank[2 + n % 6][:, 0:D], Z[:, e, q * P:(q + 1) * P], W3[:, e * D:(e + 1) * D], start=True, stop=True).then_inc(s["done"], 1)

            @block.scalar
            def _(act):
                act.wait_ge(s["turned"], 1)
                act.activation(gT[:], K.bank[0][0:L0E + 1, :], ACT.Copy).then_inc(s["turned_out"], 1)
                act.wait_ge(s["stats_done"], 1)
                act.activation(st[:, :, 8:9], st[:, :, 1:2], ACT.Sqrt, bias=K.eps[:, 0:1]).then_inc(s["std_done"], 1)

            @block.vector
            def _(dve):
                for q in range(PT4):
                    dve.wait_ge(s["bias_done"], q + 1)
                    dve.tensor_tensor(acc[:, q, :], K.bank[1][:, 0:D], Xm[:, q, :], ALU.add).then_inc(s["bias_out"], 1)
                dve.drain()
                for n in range(PT4 * (L0E + 1)):
                    q, e = divmod(n, L0E + 1)
                    dve.wait_ge(s["done"], n + 1)
                    dve.scalar_tensor_tensor(out=acc[:, q, :], in0=K.bank[2 + n % 6][:, 0:D], scalar=G[:, q, e:e + 1], in1=acc[:, q, :],
                                             op0=ALU.mult, op1=ALU.add).then_inc(s["added"], 1)
                    dve.drain()
                for q in range(PT4):
                    dve.bn_stats(st[:, q, 2:8], acc[:, q, :])
                dve.drain()
                for q in range(PT4):
                    ins = dve.bn_aggr(st[:, q, 0:2], st[:, q, 2:8])
                ins.then_inc(s["stats_done"], 1)
                dve.wait_ge(s["std_done"], 1)
                dve.reciprocal(st[:, :, 8:9], st[:, :, 8:9])
                dve.drain()
                for q in range(PT4):
                    ins = dve.tensor_scalar(acc[:, q, :], acc[:, q, :], st[:, q, 0:1], st[:, q, 8:9], ALU.subtract, ALU.mult)
                ins.then_inc(s["added"], 1)

            @block.sync
            def _(sp):
                sp.wait_ge(s["added"], PT4 * (L0E + 1) + 1)
                sp.dma_start(pool_of_rows[TOK:TOK + PICKED].rearrange("(q p) d -> p q d", p=P), acc[:]).then_inc(s["stored"], 16)
                sp.wait_ge(s["stored"], 16)

        finish(nc, K, lambda k, h, j: W3[:, L0E * D + h * P:L0E * D + (h + 1) * P], lambda k, j: Z[:, L0E + 1 + j, :], 1, bias=sb3)
        with phase(nc, K.sems, "stored gathered") as (block, s):
            @block.sync
            def _(sp):
                sp.dma_start(pool_of_rows[0:TOK].rearrange("(t p) d -> p t d", p=P), K.Xtok[:]).then_inc(s["stored"], 16)

            @block.gpsimd
            def _(pool):
                pool.wait_ge(s["stored"], 16)
                for t in range(NT):
                    pool.indirect_dma_start(out=K.Xtok[:, t, :], out_offset=None, in_=pool_of_rows[:, :],
                                            in_offset=bass.IndirectOffsetOnAxis(ap=home[:, t:t + 1], axis=0)).then_inc(s["gathered"], 16)
                pool.wait_ge(s["gathered"], 16 * NT)
        turn_tokens(nc, K)


L0H = 4
CH = 64
NCH = TOK // CH


def L0_attn_layout(i):
    g = lambda n: np.asarray(i["L0_attn_" + n])
    cw = np.stack([g(n).reshape(DC, P, 4).transpose(1, 0, 2) for n in ("conv_q", "conv_k", "conv_v")], axis=1)
    return {"L0a_W": rows(np.concatenate([g("Wq"), g("Wk"), g("Wv")], axis=1)), "L0a_Wb": rows(g("Wb")), "L0a_cw": np.ascontiguousarray(cw),
            "L0a_g": np.tile(g("g"), L0H), "L0a_Wo": rows(g("Wo"))}


def L0_attn(nc, K, w):
    xT = K.XT[K.cur]
    with ExitStack() as es:
        Wo = sbuf(es, nc, "Wo", [P, DC, D])
        OT = sbuf(es, nc, "OT", [P, DC, TOK])
        g4 = sbuf(es, nc, "g", [P, D])
        with ExitStack() as q_life:
            QK = sbuf(q_life, nc, "q_k_tokens", [P, NT, 2 * D])
            KV = sbuf(q_life, nc, "beta_k_v", [P, NT, 2 * D])
            beta = sbuf(q_life, nc, "beta", [P, NT, L0H])
            with ExitStack() as inn:
                W = sbuf(inn, nc, "W", [P, DC, 3 * D])
                Wb = sbuf(inn, nc, "Wb", [P, DC, L0H])
                cw = sbuf(inn, nc, "cw", [P, 3, DC, TAPS])
                raw = sbuf(inn, nc, "raw", [P, 2, TAPS - 1 + S])
                act_T = sbuf(inn, nc, "act_T", [P, 4, BLK])
                acc = sbuf(inn, nc, "conv", [P, 2, BLK])
                sq = sbuf(inn, nc, "squares", [P, 2, 2 * P])
                nrm = sbuf(inn, nc, "norm", [P, 2, L0H])
                load(nc, K, (W[:], w["L0a_W"]), (Wb[:], w["L0a_Wb"]), (cw[:], w["L0a_cw"]), (g4[:], spread(w["L0a_g"])), (Wo[:], w["L0a_Wo"]))
                names = "padded done raw_out conv_done silu_done turned tok_out"
                with phase(nc, K.sems, names) as (block, s):
                    runs = [(x, c, b) for x in range(3) for c in range(DC) for b in range(B)]
                    NR = len(runs)

                    @block.gpsimd
                    def _(pool):
                        pool.memset(raw[:, :, 0:TAPS - 1], 0.0).then_inc(s["padded"], 1)

                    @block.tensor
                    def _(pe):
                        def projection(r):
                            x, c, b = runs[r]
                            for i in range(2):
                                n = 2 * r + i
                                if n >= 4:
                                    pe.wait_ge(s["raw_out"], n - 3)
                                for k in range(DC):
                                    ins = pe.matmul(K.bank[n % 4][:], W[:, k, x * D + c * P:x * D + (c + 1) * P],
                                                    xT[:, k, b * S + i * BLK:b * S + (i + 1) * BLK], start=(k == 0), stop=(k == DC - 1))
                                ins.then_inc(s["done"], 1)
                        projection(0)
                        for r in range(NR):
                            if r + 1 < NR:
                                projection(r + 1)
                            for i in range(2):
                                n = 2 * r + i
                                pe.wait_ge(s["silu_done"], n + 1)
                                if n >= 4:
                                    pe.wait_ge(s["tok_out"], n - 3)
                                for t in range(TPB):
                                    ins = pe.transpose(K.bank[4 + n % 4][:, t * P:(t + 1) * P], act_T[:, n % 4, t * P:(t + 1) * P], K.ident[:])
                                ins.then_inc(s["turned"], 1)

                    @block.scalar
                    def _(act):
                        act.wait_ge(s["padded"], 1)
                        for n in range(2 * NR + 2):
                            if n < 2 * NR:
                                r, i = divmod(n, 2)
                                act.wait_ge(s["done"], n + 1)
                                if r >= 2:
                                    act.wait_ge(s["conv_done"], 2 * (r - 1))
                                act.activation(raw[:, r % 2, TAPS - 1 + i * BLK:TAPS - 1 + (i + 1) * BLK], K.bank[n % 4][:], ACT.Copy).then_inc(s["raw_out"], 1)
                            if n >= 2:
                                m = n - 2
                                act.wait_ge(s["conv_done"], m + 1)
                                if m >= 4:
                                    act.wait_ge(s["turned"], m - 3)
                                act.activation(act_T[:, m % 4, :], acc[:, m % 2, :], ACT.Silu).then_inc(s["silu_done"], 1)

                    @block.vector
                    def _(dve):
                        def take(m):
                            x, c, b = runs[m // 2]
                            t0 = b * (S // P) + (m % 2) * TPB
                            dve.wait_ge(s["turned"], m + 1)
                            dst = (QK, QK, KV)[x]
                            col = (0, D, D)[x] + c * P
                            dve.tensor_copy(dst[:, t0:t0 + TPB, col:col + P], K.bank[4 + m % 4][:].rearrange("p (t k) -> p t k", t=TPB)).then_inc(s["tok_out"], 1)

                        for n in range(2 * NR):
                            r, i = divmod(n, 2)
                            x, c, b = runs[r]
                            dve.wait_ge(s["raw_out"], n + 1)
                            if n >= 2:
                                dve.wait_ge(s["silu_done"], n - 1)
                            a = acc[:, n % 2, :]
                            dve.tensor_scalar(a, raw[:, r % 2, i * BLK:(i + 1) * BLK], cw[:, x, c, 0:1], None, ALU.mult)
                            for tap in range(1, TAPS):
                                dve.drain()
                                ins = dve.scalar_tensor_tensor(out=a, in0=raw[:, r % 2, i * BLK + tap:(i + 1) * BLK + tap], scalar=cw[:, x, c, tap:tap + 1],
                                                               in1=a, op0=ALU.mult, op1=ALU.add)
                            ins.then_inc(s["conv_done"], 1)
                            if n >= 3:
                                take(n - 3)
                        for m in range(2 * NR - 3, 2 * NR):
                            take(m)

                with phase(nc, K.sems, "done") as (block, s):
                    @block.tensor
                    def _(pe):
                        for t in range(NT):
                            for k in range(DC):
                                ins = pe.matmul(K.bank[0][:, t * L0H:(t + 1) * L0H], xT[:, k, t * P:(t + 1) * P], Wb[:, k, :], start=(k == 0), stop=(k == DC - 1))
                        ins.then_inc(s["done"], 1)

                    @block.scalar
                    def _(act):
                        act.wait_ge(s["done"], 1)
                        act.activation(beta[:], K.bank[0][:, 0:NT * L0H].rearrange("p (t h) -> p t h", h=L0H), ACT.Sigmoid)

                with ExitStack() as nn, phase(nc, K.sems, "squared summed root") as (block, s):
                    sq2 = sbuf(nn, nc, "squares", [P, 2, 2 * D])
                    nr = sbuf(nn, nc, "norms", [P, NT, 2 * L0H])

                    @block.scalar
                    def _(act):
                        for t in range(NT):
                            if t >= 2:
                                act.wait_ge(s["summed"], t - 1)
                            act.activation(sq2[:, t % 2, :], QK[:, t, :], ACT.Square).then_inc(s["squared"], 1)
                        act.wait_ge(s["summed"], NT)
                        act.activation(nr[:], nr[:], ACT.Sqrt).then_inc(s["root"], 1)

                    @block.vector
                    def _(dve):
                        for t in range(NT):
                            dve.wait_ge(s["squared"], t + 1)
                            dve.reduce_sum(nr[:, t, :], sq2[:, t % 2, :].rearrange("p (h d) -> p h d", h=2 * L0H), AX).then_inc(s["summed"], 1)
                        dve.wait_ge(s["root"], 1)
                        dve.reciprocal(nr[:], nr[:])
                        dve.drain()
                        for t in range(NT):
                            v = QK[:, t, :].rearrange("p (h d) -> p h d", h=2 * L0H)
                            dve.tensor_tensor(v, v, inner(nr[:, t, :], D // L0H), ALU.mult)
                        dve.drain()
                        for t in range(NT):
                            b_ = inner(beta[:, t, :], D // L0H)
                            kb, vb = (KV[:, t, o:o + D].rearrange("p (h d) -> p h d", h=L0H) for o in (0, D))
                            dve.tensor_tensor(kb, QK[:, t, D:2 * D].rearrange("p (h d) -> p h d", h=L0H), b_, ALU.mult)
                            dve.tensor_tensor(vb, vb, b_, ALU.mult)

            TT = sbuf(q_life, nc, "T_transposed", [P, NT, P])
            LEVELS = 6
            with ExitStack() as inn:
                masks = sbuf(inn, nc, "masks", [P, LEVELS + 1, P])
                with phase(nc, K.sems, "step") as (block, s):
                    @block.gpsimd
                    def _(pool):
                        n = 0
                        pool.memset(masks[:], 1.0).then_inc(s["step"], 1)
                        for lv in range(LEVELS + 1):
                            z = 1 << lv if lv < LEVELS else 1
                            m = masks[:, lv, :]
                            v = m.rearrange("p (n a j) -> p n a j", a=2, j=z)
                            blocks = P // (2 * z)
                            first, second = (0, 1) if lv < LEVELS else (1, 0)
                            for cmp_base, pat, mul in (
                                    (-z * first, [[-2 * z, blocks], [0, 2], [0, z]], 1),
                                    (z * first + z - 1, [[2 * z, blocks], [0, 2], [0, z]], -1),
                                    (-second if second else 0, [[0, blocks], [1 if second else -1, 2], [0, z]], 0)):
                                n += 1
                                pool.wait_ge(s["step"], n)
                                pool.affine_select(out=v, in_=v, compare_op=ALU.is_ge, fill=0.0, base=cmp_base, pattern=pat,
                                                   channel_multiplier=mul).then_inc(s["step"], 1)

                GT = 4
                kT = sbuf(inn, nc, "kT", [P, 2, 2 * DC * P])
                E = sbuf(inn, nc, "E_T", [P, LEVELS - 1, GT, P])
                M, MT, X = (sbuf(inn, nc, n, [P, GT, P]) for n in ("M", "M_T", "X"))
                four = lambda ap: middle(ap, GT)
                bank4 = lambda i: K.bank[i][:].rearrange("p (t k) -> p t k", t=GT)
                with phase(nc, K.sems, "k_turned k_out a_done m_ready x_done x_out y_done") as (block, s):
                    @block.tensor
                    def _(pe):
                        for gr in range(NT // GT):
                            for i in range(GT):
                                t = gr * GT + i
                                if t >= 2:
                                    pe.wait_ge(s["k_out"], t - 1)
                                for c in range(DC):
                                    pe.transpose(K.bank[t % 2][:, c * P:(c + 1) * P], QK[:, t, D + c * P:D + (c + 1) * P], K.ident[:])
                                    ins = pe.transpose(K.bank[t % 2][:, (2 + c) * P:(3 + c) * P], KV[:, t, c * P:(c + 1) * P], K.ident[:])
                                ins.then_inc(s["k_turned"], 1)
                                if i == 0 and gr:
                                    pe.wait_ge(s["m_ready"], gr * (LEVELS + 1))
                                pe.wait_ge(s["k_out"], t + 1)
                                k_, kb = (lambda c: kT[:, t % 2, c * P:(c + 1) * P]), (lambda c: kT[:, t % 2, (2 + c) * P:(3 + c) * P])
                                for c in range(DC):
                                    pe.matmul(K.bank[2][:, i * P:(i + 1) * P], k_(c), kb(c), start=(c == 0), stop=(c == DC - 1))
                                for c in range(DC):
                                    ins = pe.matmul(K.bank[3][:, i * P:(i + 1) * P], kb(c), k_(c), start=(c == 0), stop=(c == DC - 1))
                                ins.then_inc(s["a_done"], 1)
                            for lv in range(1, LEVELS):
                                pe.wait_ge(s["m_ready"], gr * (LEVELS + 1) + lv)
                                for i in range(GT):
                                    ins = pe.matmul(K.bank[4][:, i * P:(i + 1) * P], E[:, lv - 1, i, :], M[:, i, :], start=True, stop=True)
                                ins.then_inc(s["x_done"], 1)
                                pe.wait_ge(s["x_out"], gr * (LEVELS - 1) + lv)
                                for i in range(GT):
                                    pe.matmul(K.bank[5][:, i * P:(i + 1) * P], MT[:, i, :], X[:, i, :], start=True, stop=True)
                                for i in range(GT):
                                    ins = pe.matmul(K.bank[6][:, i * P:(i + 1) * P], X[:, i, :], MT[:, i, :], start=True, stop=True)
                                ins.then_inc(s["y_done"], 1)

                    @block.scalar
                    def _(act):
                        for gr in range(NT // GT):
                            for i in range(GT):
                                t = gr * GT + i
                                act.wait_ge(s["k_turned"], t + 1)
                                if t >= 2:
                                    act.wait_ge(s["a_done"], t - 1)
                                act.activation(kT[:, t % 2, :], K.bank[t % 2][:], ACT.Copy).then_inc(s["k_out"], 1)
                            for lv in range(1, LEVELS):
                                act.wait_ge(s["x_done"], gr * (LEVELS - 1) + lv)
                                act.activation(X[:], bank4(4), ACT.Copy).then_inc(s["x_out"], 1)

                    @block.vector
                    def _(dve):
                        for gr in range(NT // GT):
                            dve.wait_ge(s["a_done"], GT * (gr + 1))
                            for lv in range(1, LEVELS):
                                dve.tensor_tensor(E[:, lv - 1], bank4(2), four(masks[:, lv, :]), ALU.mult)
                            dve.tensor_tensor(MT[:], bank4(2), four(masks[:, 0, :]), ALU.mult)
                            dve.tensor_tensor(M[:], bank4(3), four(masks[:, LEVELS, :]), ALU.mult)
                            dve.drain()
                            dve.tensor_tensor(MT[:], four(K.ident[:]), MT[:], ALU.subtract)
                            dve.tensor_tensor(M[:], four(K.ident[:]), M[:], ALU.subtract).then_inc(s["m_ready"], 1)
                            dve.drain()
                            for lv in range(1, LEVELS):
                                dve.wait_ge(s["y_done"], gr * (LEVELS - 1) + lv)
                                dve.tensor_tensor(M[:], M[:], bank4(5), ALU.subtract)
                                dve.tensor_tensor(MT[:], MT[:], bank4(6), ALU.subtract).then_inc(s["m_ready"], 1)
                                dve.drain()
                            dve.tensor_scalar(X[:], four(K.ident[:]), -2.0, None, ALU.mult)
                            dve.drain()
                            dve.scalar_tensor_tensor(out=TT[:, gr * GT:(gr + 1) * GT, :], in0=MT[:], scalar=3.0, in1=X[:], op0=ALU.mult, op1=ALU.add).then_inc(s["m_ready"], 1)

            sums = sbuf(q_life, nc, "chunk_sums", [P, 2 * DC, NCH])
            pick = sbuf(q_life, nc, "chunk_of", [P, 2])
            with ExitStack() as inn, phase(nc, K.sems, "step wu_done wu_out prod_done summed") as (block, s):
                prod = sbuf(inn, nc, "k_products", [P, 2, 2 * D])

                @block.gpsimd
                def _(pool):
                    pool.memset(pick[:], 1.0).then_inc(s["step"], 1)
                    pool.wait_ge(s["step"], 1)
                    pool.affine_select(out=pick[:], in_=pick[:], compare_op=ALU.is_ge, fill=0.0, base=0, pattern=[[-CH, 2]], channel_multiplier=1).then_inc(s["step"], 1)
                    pool.wait_ge(s["step"], 2)
                    pool.affine_select(out=pick[:], in_=pick[:], compare_op=ALU.is_ge, fill=0.0, base=CH - 1, pattern=[[CH, 2]], channel_multiplier=-1).then_inc(s["step"], 1)

                @block.tensor
                def _(pe):
                    def products(t):
                        if t >= 2:
                            pe.wait_ge(s["wu_out"], t - 1)
                        pe.matmul(K.bank[t % 2][:], TT[:, t, :], KV[:, t, :], start=True, stop=True).then_inc(s["wu_done"], 1)
                    products(0)
                    pe.wait_ge(s["step"], 3)
                    for t in range(NT):
                        if t + 1 < NT:
                            products(t + 1)
                        pe.wait_ge(s["prod_done"], t + 1)
                        for c in range(2 * DC):
                            ins = pe.matmul(K.bank[2][:, c * NCH + 2 * t:c * NCH + 2 * t + 2], prod[:, t % 2, c * P:(c + 1) * P], pick[:], start=True, stop=True)
                        ins.then_inc(s["summed"], 1)

                @block.scalar
                def _(act):
                    for t in range(NT):
                        act.wait_ge(s["wu_done"], t + 1)
                        act.activation(KV[:, t, :], K.bank[t % 2][:], ACT.Copy).then_inc(s["wu_out"], 1)

                @block.vector
                def _(dve):
                    for t in range(NT):
                        dve.wait_ge(s["wu_out"], t + 1)
                        if t >= 2:
                            dve.wait_ge(s["summed"], t - 1)
                        dve.tensor_tensor(prod[:, t % 2, :].rearrange("p (a d) -> p a d", a=2), middle(QK[:, t, D:2 * D], 2),
                                          KV[:, t, :].rearrange("p (a d) -> p a d", a=2), ALU.mult).then_inc(s["prod_done"], 1)
                    dve.wait_ge(s["summed"], NT)
                    v = K.bank[2][:, 0:2 * DC * NCH].rearrange("p (c n) -> p c n", n=NCH)
                    dve.tensor_scalar(sums[:, 0:DC], v[:, 0:DC], -1.0, 1.0, ALU.mult, ALU.add)
                    dve.tensor_copy(sums[:, DC:2 * DC], v[:, DC:2 * DC])

            diag = sbuf(q_life, nc, "diagonal", [NCH, D])
            sel = sbuf(q_life, nc, "chunk_select", [NCH, TOK])
            rowm = sbuf(q_life, nc, "first_rows", [P, B])
            with ExitStack() as inn, phase(nc, K.sems, "step scanned turned") as (block, s):
                dT = sbuf(inn, nc, "diagonalT", [P, DC, B, NCH // B + 1])
                dC = sbuf(inn, nc, "diagonal_before", [P, DC, NCH])

                @block.gpsimd
                def _(pool):
                    v = sel[:].rearrange("p (n j) -> p n j", j=CH)
                    pool.memset(sel[:], 1.0).then_inc(s["step"], 1)
                    pool.memset(rowm[:], 1.0).then_inc(s["step"], 1)
                    pool.wait_ge(s["step"], 2)
                    pool.affine_select(out=v, in_=v, compare_op=ALU.is_equal, fill=0.0, base=0, pattern=[[-1, NCH], [0, CH]], channel_multiplier=1)
                    pool.affine_select(out=rowm[0:CH], in_=rowm[0:CH], compare_op=ALU.is_ge, fill=0.0, base=0, pattern=[[1, B]], channel_multiplier=-1)
                    pool.affine_select(out=rowm[CH:P], in_=rowm[CH:P], compare_op=ALU.is_ge, fill=0.0, base=0, pattern=[[1, B]], channel_multiplier=-1)

                @block.vector
                def _(dve):
                    dve.memset(dT[:, :, :, 0:1], 0.0)
                    n = NCH // B
                    for c in range(DC):
                        for b in range(B):
                            dve.tensor_tensor_scan(dT[:, c, b, 1:n + 1], sums[:, c, b * n:(b + 1) * n], sums[:, DC + c, b * n:(b + 1) * n], 0.0, ALU.mult, ALU.add)
                    dve.drain()
                    dve.tensor_copy(dC[:].rearrange("p c (b n) -> p (c b) n", b=B), dT[:].rearrange("p c b n -> p (c b) n")[:, :, 0:n]).then_inc(s["scanned"], 1)
                    dve.wait_ge(s["turned"], 1)
                    dve.tensor_copy(diag[:], K.bank[0][0:NCH, 0:D])

                @block.tensor
                def _(pe):
                    pe.wait_ge(s["scanned"], 1)
                    for c in range(DC):
                        ins = pe.transpose(K.bank[0][0:NCH, c * P:(c + 1) * P], dC[:, c, :], K.ident[:])
                    ins.then_inc(s["turned"], 1)

            with ExitStack() as inn, phase(nc, K.sems, "d_done o_done squared summed root o_normed turned out") as (block, s):
                tmp = sbuf(inn, nc, "tmp", [P, 2, D])
                dot = sbuf(inn, nc, "dot", [P, NT])
                sq = sbuf(inn, nc, "squares", [P, 2, D])
                ms = sbuf(inn, nc, "mean_square", [P, NT, L0H])
                O = sbuf(inn, nc, "O", [P, NT, D])

                @block.tensor
                def _(pe):
                    for t in range(NT):
                        if t >= 4:
                            pe.wait_ge(s["o_done"], t - 3)
                        pe.matmul(K.bank[t % 4][:, 0:D], sel[:, t * P:(t + 1) * P], diag[:], start=True, stop=True).then_inc(s["d_done"], 1)
                    for t in range(NT):
                        pe.wait_ge(s["o_normed"], t + 1)
                        if t >= 4:
                            pe.wait_ge(s["out"], t - 3)
                        for c in range(DC):
                            ins = pe.transpose(K.bank[4 + t % 4][:, c * P:(c + 1) * P], O[:, t, c * P:(c + 1) * P], K.ident[:])
                        ins.then_inc(s["turned"], 1)

                @block.vector
                def _(dve):
                    for t in range(NT):
                        q_, k_ = QK[:, t, 0:D], QK[:, t, D:2 * D]
                        a, b_ = tmp[:, 0, :], tmp[:, 1, :]
                        dve.wait_ge(s["d_done"], t + 1)
                        d_ = K.bank[t % 4][:, 0:D]
                        dve.tensor_tensor_reduce(a, q_, k_, 1.0, 0.0, ALU.mult, ALU.add, dot[:, t:t + 1])
                        dve.tensor_tensor(b_, KV[:, t, 0:D], d_, ALU.mult)
                        dve.drain()
                        dve.tensor_tensor(dot[:, t:t + 1], dot[:, t:t + 1], rowm[:, t // 8:t // 8 + 1], ALU.mult)
                        dve.tensor_tensor(b_, KV[:, t, D:2 * D], b_, ALU.subtract)
                        dve.tensor_tensor(a, q_, d_, ALU.mult)
                        dve.drain()
                        dve.scalar_tensor_tensor(out=O[:, t, :], in0=b_, scalar=dot[:, t:t + 1], in1=a, op0=ALU.mult, op1=ALU.add).then_inc(s["o_done"], 1)
                        dve.drain()
                    for t in range(NT):
                        dve.wait_ge(s["squared"], t + 1)
                        dve.reduce_sum(ms[:, t, :], sq[:, t % 2, :].rearrange("p (h d) -> p h d", h=L0H), AX).then_inc(s["summed"], 1)
                    dve.wait_ge(s["root"], 1)
                    dve.reciprocal(ms[:], ms[:])
                    dve.drain()
                    for t in range(NT):
                        v = O[:, t, :].rearrange("p (h d) -> p h d", h=L0H)
                        dve.tensor_tensor(v, v, inner(ms[:, t, :], D // L0H), ALU.mult)
                        dve.drain()
                        dve.tensor_tensor(O[:, t, :], O[:, t, :], g4[:], ALU.mult).then_inc(s["o_normed"], 1)

                @block.scalar
                def _(act):
                    for t in range(NT):
                        act.wait_ge(s["o_done"], t + 1)
                        if t >= 2:
                            act.wait_ge(s["summed"], t - 1)
                        act.activation(sq[:, t % 2, :], O[:, t, :], ACT.Square).then_inc(s["squared"], 1)
                    act.wait_ge(s["summed"], NT)
                    act.activation(ms[:], ms[:], ACT.Sqrt, scale=1.0 / (D // L0H), bias=K.eps[:, 0:1]).then_inc(s["root"], 1)
                    for t in range(NT):
                        act.wait_ge(s["turned"], t + 1)
                        act.activation(OT[:, :, t * P:(t + 1) * P], K.bank[4 + t % 4][:, 0:D].rearrange("p (c k) -> p c k", c=2), ACT.Copy).then_inc(s["out"], 1)
        finish(nc, K, lambda k, h, j: Wo[:, k, h * P:(h + 1) * P], block_of(OT), DC)


L2D = 2
LH, LHD = 8, 64
LM = LH * LHD // P
HIDP = 6 * P
L2HID = 682
WINDOW = 128


def xpos_tables():
    f = np.float32
    half = np.arange(0, LHD, 2, dtype=f)
    inv = f(1.0) / np.power(f(10000.0), half / f(LHD), dtype=f)
    t = np.arange(S, dtype=f)
    ang = t[:, None] * inv[None, :]
    ang = np.concatenate([ang, ang], axis=1)
    base = (half + f(0.4 * LHD)) / f(1.4 * LHD)
    power = (t - f(S // 2)) / f(WINDOW // 2)
    scale = np.power(base[None, :], power[:, None], dtype=f)
    scale = np.concatenate([scale, scale], axis=1)
    cos, sin = np.cos(ang, dtype=f), np.sin(ang, dtype=f)
    sin[:, :LHD // 2] *= -1
    tab = np.stack([cos * scale, sin * scale, cos / scale, sin / scale])
    return np.ascontiguousarray(tab.reshape(4, S // P, P, LHD).transpose(2, 0, 1, 3))


def L2_ffn_layout(i):
    g = lambda n, l: np.asarray(i["L2_ffn_" + n])[l]
    out = {"L2f_tab": xpos_tables()}
    halves_swapped = lambda v: np.concatenate([v[LHD // 2:], v[:LHD // 2]])
    for l in range(L2D):
        two = lambda a, axis: np.concatenate([pad(a[..., :L2HID], axis, HIDP), pad(a[..., L2HID:], axis, HIDP)], axis=axis)
        qs, ks = g("q_scale", l), g("k_scale", l)
        out.update({f"L2f{l}_Wqkv": rows(g("wqkv", l)), f"L2f{l}_s": np.concatenate([qs, halves_swapped(qs), ks, halves_swapped(ks)]),
                    f"L2f{l}_Wo": rows(g("wo", l)),
                    f"L2f{l}_g": cols(g("ln_g", l)), f"L2f{l}_b": cols(g("ln_b", l)), f"L2f{l}_W1": rows(two(g("w1", l), 1)),
                    f"L2f{l}_b1": cols(two(g("b1", l), 0)), f"L2f{l}_W2": rows(pad(g("w2", l), 0, HIDP)), f"L2f{l}_b2": cols(g("b2", l))})
    return out


def shift_half(nc, K, X, sh):
    with phase(nc, K.sems, "copied") as (block, s):
        v = X[:, 1, :].rearrange("p (b t) -> p b t", b=B)

        @block.scalar
        def _(act):
            act.activation(sh[:, 0, 1:], v[:, 0], ACT.Copy)

        @block.vector
        def _(dve):
            dve.tensor_copy(sh[:, 1, 1:], v[:, 1])


def local_qkv(nc, K, tile_of, W, tab, QT, KT, V):
    NTB = S // P
    N = 2 * NTB
    HF = LHD // 2
    with ExitStack() as es, phase(nc, K.sems, "done squared ss_done root_done r_ready crossed added normed turned t_out v_done v_out") as (block, s):
        sq = sbuf(es, nc, "squares", [P, 2, LH, LHD])
        t1, t2 = (sbuf(es, nc, n, [P, 2, LH, LHD]) for n in ("straight", "crossed"))
        r = sbuf(es, nc, "norm", [P, 2, LH])
        heads = lambda v: v.rearrange("p (h d) -> p h d", h=LH)

        @block.tensor
        def _(pe):
            def projection(n):
                if n >= 3:
                    pe.wait_ge(s["crossed"], n - 2)
                for k in range(DC):
                    ins = pe.matmul(K.bank[n % 3][:], tile_of(k, n // 2), W[:, k, (n % 2) * BLK:(n % 2 + 1) * BLK], start=(k == 0), stop=(k == DC - 1))
                ins.then_inc(s["done"], 1)

            def value(t):
                if t >= 2:
                    pe.wait_ge(s["v_out"], t - 1)
                for k in range(DC):
                    ins = pe.matmul(K.bank[5 + t % 2][:], tile_of(k, t), W[:, k, 2 * BLK:3 * BLK], start=(k == 0), stop=(k == DC - 1))
                ins.then_inc(s["v_done"], 1)

            projection(0)
            projection(1)
            for n in range(N):
                if n + 2 < N:
                    projection(n + 2)
                if n % 2 == 0:
                    value(n // 2)
                pe.wait_ge(s["normed"], n + 1)
                if n >= 2:
                    pe.wait_ge(s["t_out"], n - 1)
                for m in range(LM):
                    ins = pe.transpose(K.bank[3 + n % 2][:, m * P:(m + 1) * P], t1[:, n % 2].rearrange("p h d -> p (h d)")[:, m * P:(m + 1) * P], K.ident[:])
                ins.then_inc(s["turned"], 1)

        @block.scalar
        def _(act):
            def square(n):
                act.wait_ge(s["done"], n + 1)
                if n >= 2:
                    act.wait_ge(s["ss_done"], n - 1)
                act.activation(sq[:, n % 2], heads(K.bank[n % 3][:]), ACT.Square).then_inc(s["squared"], 1)

            def turned_out(n):
                act.wait_ge(s["turned"], n + 1)
                dst = (QT, KT)[n % 2]
                act.activation(dst[:, :, (n // 2) * P:(n // 2 + 1) * P], K.bank[3 + n % 2][:].rearrange("p (m t) -> p m t", m=LM), ACT.Copy).then_inc(s["t_out"], 1)

            square(0)
            for n in range(N):
                if n + 1 < N:
                    square(n + 1)
                act.wait_ge(s["ss_done"], n + 1)
                act.activation(r[:, n % 2], r[:, n % 2], ACT.Sqrt).then_inc(s["root_done"], 1)
                if n % 2 == 0:
                    act.wait_ge(s["v_done"], n // 2 + 1)
                    act.activation(V[:, n // 2, :], K.bank[5 + (n // 2) % 2][:], ACT.Copy).then_inc(s["v_out"], 1)
                if n > 0:
                    turned_out(n - 1)
            turned_out(N - 1)

        @block.vector
        def _(dve):
            for n in range(N):
                raw = heads(K.bank[n % 3][:])
                t, part = divmod(n, 2)
                cos, sin = (middle(tab[:, 2 * part + i, t, :], LH) for i in range(2))
                dve.wait_ge(s["squared"], n + 1)
                if n >= 2:
                    dve.wait_ge(s["normed"], n - 1)
                dve.reduce_sum(r[:, n % 2], sq[:, n % 2], AX).then_inc(s["ss_done"], 1)
                if n >= 2:
                    dve.wait_ge(s["turned"], n - 1)
                dve.tensor_tensor(t1[:, n % 2], raw, cos, ALU.mult)
                dve.tensor_tensor(t2[:, n % 2, :, 0:HF], raw[:, :, HF:], sin[:, :, 0:HF], ALU.mult)
                dve.tensor_tensor(t2[:, n % 2, :, HF:], raw[:, :, 0:HF], sin[:, :, HF:], ALU.mult).then_inc(s["crossed"], 1)
                dve.wait_ge(s["root_done"], n + 1)
                dve.tensor_scalar(r[:, n % 2], r[:, n % 2], 1e-12, None, ALU.max)
                dve.drain()
                dve.reciprocal(r[:, n % 2], r[:, n % 2]).then_inc(s["r_ready"], 1)

        @block.gpsimd
        def _(pool):
            for n in range(N):
                pool.wait_ge(s["crossed"], n + 1)
                pool.tensor_tensor(t1[:, n % 2], t1[:, n % 2], t2[:, n % 2], ALU.add).then_inc(s["added"], 1)
                pool.wait_ge(s["added"], n + 1)
                pool.wait_ge(s["r_ready"], n + 1)
                pool.tensor_tensor(t1[:, n % 2], t1[:, n % 2], inner(r[:, n % 2], LHD), ALU.mult).then_inc(s["normed"], 1)


def local_attention(nc, K, b, QT, KT, V, half, window_mask, OT):
    NTB = S // P
    QK_SCALE = 8.0
    with ExitStack() as es, phase(nc, K.sems, "q_spread scored max_done exp_done recip_done normed turned pt_out pv_done out") as (block, s):
        Qh = sbuf(es, nc, "Q_heads", [P, 2, LM, 2, P])
        Pr = sbuf(es, nc, "probs", [P, 2, LH, 2 * P])
        PT = sbuf(es, nc, "probsT", [P, LM, 4 * P])
        stat = sbuf(es, nc, "stat", [P, 2, 3, LH])
        keys = lambda t: slice(0 if t else P, 2 * P)

        @block.tensor
        def _(pe):
            def score(t):
                pe.wait_ge(s["q_spread"], 2 * (t + 1))
                for g in range(LM):
                    if t:
                        pe.wait_ge(s["exp_done"], LH * (t - 1) + 2 * (g + 1))
                    for hh in range(2):
                        ks = keys(t)
                        o = K.bank[g][:, hh * 2 * P + ks.start:(hh + 1) * 2 * P]
                        pe.matmul(o, Qh[:, t % 2, g, hh, :], KT[:, g, t * P - P + ks.start:(t + 1) * P], start=True, stop=False, skip_group_check=True)
                        ins = pe.matmul(o, K.identb[:], window_mask[:, ks], start=False, stop=True, skip_group_check=True)
                    ins.then_inc(s["scored"], 1)

            score(0)
            for t in range(NTB):
                if t + 1 < NTB:
                    score(t + 1)
                kts = (0, 1) if t else (1,)
                for g in range(LM):
                    n = LM * t + g
                    pe.wait_ge(s["normed"], n + 1)
                    if n >= 2:
                        pe.wait_ge(s["pt_out"], n - 1)
                    for hh in range(2):
                        for kt in kts:
                            ins = pe.transpose(K.bank[4 + n % 2][:, (2 * hh + kt) * P:(2 * hh + kt + 1) * P], Pr[:, t % 2, 2 * g + hh, kt * P:(kt + 1) * P], K.ident[:])
                    ins.then_inc(s["turned"], 1)
                for g in range(LM):
                    pe.wait_ge(s["pt_out"], LM * t + g + 1)
                    if g == 0 and t >= 2:
                        pe.wait_ge(s["out"], t - 1)
                    for hh in range(2):
                        for kt in kts:
                            h = 2 * g + hh
                            ins = pe.matmul(K.bank[6 + t % 2][hh * LHD:(hh + 1) * LHD, g * P:(g + 1) * P], V[:, t - 1 + kt, h * LHD:(h + 1) * LHD],
                                            PT[:, g, (2 * hh + kt) * P:(2 * hh + kt + 1) * P], start=(kt == kts[0]), stop=(kt == 1))
                    ins.then_inc(s["pv_done"], 1)

        @block.vector
        def _(dve):
            def spread(t):
                if t >= 2:
                    dve.wait_ge(s["scored"], LM * (t - 1))
                for hh in range(2):
                    dve.tensor_scalar(Qh[:, t % 2, :, hh, :], QT[:, :, t * P:(t + 1) * P], half[:, hh:hh + 1], None, ALU.mult).then_inc(s["q_spread"], 1)

            spread(0)
            for t in range(NTB):
                if t + 1 < NTB:
                    spread(t + 1)
                ks = keys(t)
                if t >= 2:
                    dve.wait_ge(s["exp_done"], LH * (t - 1))
                for g in range(LM):
                    dve.wait_ge(s["scored"], LM * t + g + 1)
                    mx = stat[:, t % 2, 0, 2 * g:2 * g + 2]
                    dve.reduce_max(mx, K.bank[g][:].rearrange("p (h k) -> p h k", h=2)[:, :, ks], AX)
                    dve.drain()
                    dve.tensor_scalar(mx, mx, -QK_SCALE, None, ALU.mult).then_inc(s["max_done"], 1)
                for g in range(LM):
                    dve.wait_ge(s["exp_done"], LH * t + 2 * (g + 1))
                    if g == 0 and t >= 2:
                        dve.wait_ge(s["normed"], LM * (t - 1))
                    dve.reciprocal(stat[:, t % 2, 2, 2 * g:2 * g + 2], stat[:, t % 2, 1, 2 * g:2 * g + 2]).then_inc(s["recip_done"], 1)
                if t:
                    dve.wait_ge(s["pv_done"], LM * t)
                    dve.tensor_copy(OT[:, :, b * S + (t - 1) * P:b * S + t * P], K.bank[6 + (t - 1) % 2][:].rearrange("p (g k) -> p g k", g=LM)).then_inc(s["out"], 1)
            dve.wait_ge(s["pv_done"], LM * NTB)
            t = NTB
            dve.tensor_copy(OT[:, :, b * S + (t - 1) * P:b * S + t * P], K.bank[6 + (t - 1) % 2][:].rearrange("p (g k) -> p g k", g=LM)).then_inc(s["out"], 1)

        @block.gpsimd
        def _(pool):
            for t in range(NTB):
                ks = keys(t)
                for g in range(LM):
                    pool.wait_ge(s["recip_done"], LM * t + g + 1)
                    v = Pr[:, t % 2, 2 * g:2 * g + 2, ks]
                    pool.tensor_tensor(v, v, inner(stat[:, t % 2, 2, 2 * g:2 * g + 2], ks.stop - ks.start), ALU.mult).then_inc(s["normed"], 1)

        @block.scalar
        def _(act):
            def exps(t):
                ks = keys(t)
                for g in range(LM):
                    act.wait_ge(s["max_done"], LM * t + g + 1)
                    if t >= 2:
                        act.wait_ge(s["turned"], LM * (t - 2) + g + 1)
                        act.wait_ge(s["recip_done"], LM * (t - 2) + g + 1)
                    for hh in range(2):
                        h = 2 * g + hh
                        act.activation(Pr[:, t % 2, h, ks], K.bank[g][:, hh * 2 * P + ks.start:hh * 2 * P + ks.stop], ACT.Exp, bias=stat[:, t % 2, 0, h:h + 1],
                                       scale=QK_SCALE, accum_out=stat[:, t % 2, 1, h:h + 1]).then_inc(s["exp_done"], 1)
            exps(0)
            for t in range(NTB):
                if t + 1 < NTB:
                    exps(t + 1)
                for g in range(LM):
                    n = LM * t + g
                    act.wait_ge(s["turned"], n + 1)
                    if t:
                        act.wait_ge(s["pv_done"], n - LM + 1)
                    src, dst = (v.rearrange("p (h k) -> p h k", h=2)[:, :, keys(t)] for v in (K.bank[4 + n % 2][:], PT[:, g, :]))
                    act.activation(dst, src, ACT.Copy).then_inc(s["pt_out"], 1)


def add_residual(nc, K, n_k, wt, src, bias, old, new):
    with phase(nc, K.sems, "done out") as (block, s):
        steps = [(h, j) for j in range(NB) for h in range(DC)]

        @block.tensor
        def _(pe):
            for n, (h, j) in enumerate(steps):
                for k in range(n_k):
                    ins = pe.matmul(K.bank[n][:], wt(k, h), src(k, j), start=(k == 0), stop=(k == n_k - 1))
                ins.then_inc(s["done"], 1)

        @block.vector
        def _(dve):
            for n, (h, j) in enumerate(steps):
                dve.wait_ge(s["done"], n + 1)
                o, d = (v[:, h, j * BLK:(j + 1) * BLK] for v in (old, new))
                if bias is None:
                    dve.tensor_tensor(d, K.bank[n][:], o, ALU.add)
                else:
                    dve.scalar_tensor_tensor(out=d, in0=K.bank[n][:], scalar=bias[:, h:h + 1], in1=o, op0=ALU.add, op1=ALU.add)


def L2_ffn(nc, K, w):
    x0, x1 = K.XT[K.cur], K.XT[1 - K.cur]
    with ExitStack() as es:
        sh = sbuf(es, nc, "shifted", [P, B, 1 + S])
        half = sbuf(es, nc, "head_half", [P, 2])
        ones64 = sbuf(es, nc, "ones64", [P, P])
        J = sbuf(es, nc, "J", [P, P])
        wm = sbuf(es, nc, "window_mask", [P, 2 * P], BF16)
        block_mean(nc, K, ones64[:], LHD)
        block_mean(nc, K, J[:], P)
        with phase(nc, K.sems, "step") as (block, s):
            @block.vector
            def _(dve):
                dve.tensor_scalar(ones64[:], ones64[:], float(LHD), None, ALU.mult)
                dve.tensor_scalar(J[:], J[:], 0.5, None, ALU.mult)
                dve.tensor_copy(wm[:, 0:P], K.below[:])
                dve.tensor_copy(wm[:, P:2 * P], K.above[:])
                dve.drain()
                for hh in range(2):
                    dve.tensor_copy(half[:, hh:hh + 1], ones64[:, hh * LHD:hh * LHD + 1])
                dve.memset(sh[:, :, 0:1], 0.0)
        h_of = lambda X: lambda k, j: X[:, 0, j * BLK:(j + 1) * BLK] if k == 0 else sh[:, j // 2, (j % 2) * BLK:(j % 2) * BLK + BLK]
        for l in range(L2D):
            X = x0 if l == 0 else x1
            pre = f"L2f{l}_"
            shift_half(nc, K, X, sh)
            with ExitStack() as att:
                OT = sbuf(att, nc, "OT", [P, LM, TOK])
                with ExitStack() as inn:
                    W = sbuf(inn, nc, "Wqkv", [P, DC, 3 * LM * P])
                    tab = sbuf(inn, nc, "tables", [P, 4, S // P, LHD])
                    sc = sbuf(inn, nc, "scales", [P, 4, LHD])
                    QT, KT = (sbuf(inn, nc, n, [P, LM, S]) for n in ("QT", "KT"))
                    V = K.Xtok[:].rearrange("p (t c) d -> p t (c d)", c=2)
                    load(nc, K, (W[:], w[pre + "Wqkv"]), (tab[:], w["L2f_tab"]), (sc[:].rearrange("p i d -> p (i d)"), spread(w[pre + "s"])))
                    with phase(nc, K.sems, "step") as (block, s):
                        @block.vector
                        def _(dve):
                            for i in range(4):
                                dve.tensor_tensor(tab[:, i], tab[:, i], middle(sc[:, i, :], S // P), ALU.mult)
                    for b in range(B):
                        tile_of = lambda k, t: X[:, 0, b * S + t * P:b * S + (t + 1) * P] if k == 0 else sh[:, b, t * P:(t + 1) * P]
                        local_qkv(nc, K, tile_of, W, tab, QT, KT, V)
                        local_attention(nc, K, b, QT, KT, V, half, wm, OT)
                with ExitStack() as inn:
                    Wo = sbuf(inn, nc, "Wo", [P, LM, D])
                    load(nc, K, (Wo[:], w[pre + "Wo"]))
                    add_residual(nc, K, LM, lambda k, h: Wo[:, k, h * P:(h + 1) * P], block_of(OT), None, X, x1)
            shift_half(nc, K, x1, sh)
            with ExitStack() as ff:
                W2 = sbuf(ff, nc, "W2", [P, HIDP // P, D])
                b2 = sbuf(ff, nc, "b2", [P, DC])
                GT = sbuf(ff, nc, "GT", [P, HIDP // P, TOK])
                with ExitStack() as inn:
                    W1 = sbuf(inn, nc, "W1", [P, DC, 2 * HIDP])
                    b1 = sbuf(inn, nc, "b1", [P, 2 * HIDP // P])
                    g, b_ = (sbuf(inn, nc, n, [P, DC]) for n in ("g", "b"))
                    Hn = sbuf(inn, nc, "Hn", [P, DC, TOK])
                    ge = sbuf(inn, nc, "gelu", [P, 2, BLK])
                    load(nc, K, (W1[:], w[pre + "W1"]), (b1[:], w[pre + "b1"]), (g[:], w[pre + "g"]), (b_[:], w[pre + "b"]), (W2[:], w[pre + "W2"]), (b2[:], w[pre + "b2"]))
                    feature_ln(nc, K, J[:], NB, DC, lambda j, h: h_of(x1)(h, j), lambda j, h: Hn[:, h, j * BLK:(j + 1) * BLK], lambda j: g[:], lambda j: b_[:])
                    HC = HIDP // P
                    steps = [(m, j) for m in range(HC) for j in range(NB)]
                    with phase(nc, K.sems, "done gelu_done out") as (block, s):
                        @block.tensor
                        def _(pe):
                            for n, (m, j) in enumerate(steps):
                                if n >= 4:
                                    pe.wait_ge(s["out"], n - 3)
                                for part in range(2):
                                    for k in range(DC):
                                        ins = pe.matmul(K.bank[2 * (n % 4) + part][:], W1[:, k, (part * HC + m) * P:(part * HC + m + 1) * P],
                                                        Hn[:, k, j * BLK:(j + 1) * BLK], start=(k == 0), stop=(k == DC - 1))
                                ins.then_inc(s["done"], 1)

                        @block.scalar
                        def _(act):
                            for n, (m, j) in enumerate(steps):
                                act.wait_ge(s["done"], n + 1)
                                if n >= 2:
                                    act.wait_ge(s["out"], n - 1)
                                act.activation(ge[:, n % 2, :], K.bank[2 * (n % 4) + 1][:], ACT.Gelu, bias=b1[:, HC + m:HC + m + 1]).then_inc(s["gelu_done"], 1)

                        @block.vector
                        def _(dve):
                            for n, (m, j) in enumerate(steps):
                                dve.wait_ge(s["gelu_done"], n + 1)
                                dve.scalar_tensor_tensor(out=GT[:, m, j * BLK:(j + 1) * BLK], in0=K.bank[2 * (n % 4)][:], scalar=b1[:, m:m + 1],
                                                         in1=ge[:, n % 2, :], op0=ALU.add, op1=ALU.mult).then_inc(s["out"], 1)
                if l < L2D - 1:
                    add_residual(nc, K, HIDP // P, lambda k, h: W2[:, k, h * P:(h + 1) * P], block_of(GT), b2, x1, x1)
                else:
                    with phase(nc, K.sems, "step") as (block, s):
                        @block.vector
                        def _(dve):
                            dve.tensor_tensor(x1[:, 0, :], x1[:, 0, :], x0[:, 0, :], ALU.add)

                        @block.gpsimd
                        def _(pool):
                            pool.tensor_tensor(x1[:, 1, :], x1[:, 1, :], x0[:, 1, :], ALU.add)
                    finish(nc, K, lambda k, h, j: W2[:, k, h * P:(h + 1) * P], block_of(GT), HIDP // P, bias=b2, res=x1)


def program(nc, w, out, first=0, last=12):
    stored = nc.alloc_semaphore("stored")
    with ExitStack() as es:
        K = Fixed()
        K.sems, K.cur = [], 0
        K.XT = [sbuf(es, nc, f"XT{i}", [P, DC, TOK])[:] for i in range(2)]
        K.Xtok = sbuf(es, nc, "Xtok", [P, NT, D])
        K.ctxT = sbuf(es, nc, "ctxT", [P, DC, B, 256])
        K.ones = sbuf(es, nc, "ones", [P, 8 * P])
        K.ident = sbuf(es, nc, "ident", [P, P])
        K.identb = sbuf(es, nc, "identb", [P, P], BF16)
        K.causal_T = sbuf(es, nc, "causal_T", [P, P])
        K.head_cols = sbuf(es, nc, "head_cols", [P, 8, P])
        K.head_rows = sbuf(es, nc, "head_rows", [P, 8])
        K.above = sbuf(es, nc, "above", [P, P], BF16)
        K.below = sbuf(es, nc, "below", [P, P], BF16)
        K.live_keys = sbuf(es, nc, "live_keys", [P, 1])
        K.eps = sbuf(es, nc, "eps", [P, 1])
        K.psum = es.enter_context(nc.psum_tensor("psum", [P, 8, BLK], F32))
        K.bank = [K.psum[:, i, :] for i in range(8)]
        setup(nc, K, w)
        for sublayer in SUBLAYERS[first:last]:
            sublayer(nc, K, w)
        with nc.Block() as block:
            @block.sync
            def _(sp):
                sp.dma_start(out.rearrange("b (t p) d -> p (b t) d", p=P), K.Xtok[:]).then_inc(stored, 16)
                sp.wait_ge(stored, 16)


def layouts(i):
    x = np.asarray(i["x"]).reshape(TOK, D)
    out = {"xT": rows(x.T), "xtok": rows(x)}
    ctx = np.concatenate([pad(np.asarray(i["ctx_1024"])[b].T, 1, 2 * P) for b in range(B)], axis=1)
    out["ctxT"] = rows(ctx).reshape(P, DC, B, 2 * P)
    for f in LAYOUTS:
        out.update(f(i))
    return out


LAYOUTS = (L0_attn_layout, L0_xattn_layout, L0_ffn_layout, L1_attn_layout, L1_xattn_layout, L1_ffn_layout,
           L2_attn_layout, L2_xattn_layout, L2_ffn_layout, L3_attn_layout, L3_xattn_layout, L3_ffn_layout)
SUBLAYERS = (L0_attn, L0_xattn, L0_ffn, L1_attn, L1_xattn, L1_ffn, L2_attn, L2_xattn, L2_ffn, L3_attn, L3_xattn, L3_ffn)


def kernel(**inputs):
    import concourse.bacc as _bacc
    from concourse import mybir as _mybir
    from concourse.bass_utils import run_bass_kernel_spmd as _run

    nc = _bacc.Bacc("TRN2", target_bir_lowering=False, num_devices=1)
    arrays, w = {}, {}
    for name, a in layouts(inputs).items():
        a = np.ascontiguousarray(a)
        arrays[f"in_{name}"] = a
        w[name] = nc.dram_tensor(f"in_{name}", a.shape, _mybir.dt.from_np(a.dtype), kind="ExternalInput").ap()
    out = nc.dram_tensor("out", (B, S, D), _mybir.dt.float32, kind="ExternalOutput").ap()
    program(nc, w, out)
    return _run(nc, [arrays], core_ids=[0]).results[0]["out"]
```

```python
from contextlib import ExitStack, contextmanager

import numpy as np

import concourse.bass as bass
from concourse import mybir

F32 = mybir.dt.float32
BF16 = mybir.dt.bfloat16
I32 = mybir.dt.int32
U32 = mybir.dt.uint32
ALU = mybir.AluOpType
ACT = mybir.ActivationFunctionType
AX = mybir.AxisListType.X

P = 128
B = 2
S = 1024
D = 256
DC = D // P
TOK = B * S
NT = TOK // P
BLK = 512
NB = TOK // BLK
TPB = BLK // P
CTX = 154
LN_EPS = 1e-5
NEG = -1e30
SEM_LIMIT = 100


class Fixed:
    pass


@contextmanager
def phase(nc, pool, names):
    names = names.split()
    if len(pool) + len(names) > SEM_LIMIT:
        nc.clear_and_free_semaphores(list(pool))
        nc.all_engine_barrier()
        pool.clear()
    sems = {n: nc.alloc_semaphore(f"{n}_{nc.next_id()}") for n in names}
    pool.extend(sems.values())
    with nc.Block() as block:
        yield block, sems


def sbuf(es, nc, name, shape, dt=F32):
    return es.enter_context(nc.sbuf_tensor(f"{name}_{nc.next_id()}", shape, dt))


def spread(v, parts=P):
    return v.rearrange("(o n) -> o n", o=1).broadcast_to((parts, v.shape[0]))



def rows(a):
    a = np.asarray(a)
    return np.ascontiguousarray(a.reshape(a.shape[0] // P, P, -1).transpose(1, 0, 2))


def cols(v):
    return np.ascontiguousarray(np.asarray(v).reshape(-1, P).T)


def pad(a, axis, n):
    width = [(0, 0)] * a.ndim
    width[axis] = (0, n - a.shape[axis])
    return np.pad(np.asarray(a), width)


def setup(nc, K, w):
    with phase(nc, K.sems, "loaded ones_set masks_set") as (block, s):
        @block.sync
        def _(sp):
            sp.dma_start(K.XT[0][:], w["xT"]).then_inc(s["loaded"], 16)
            sp.dma_start(K.ctxT[:], w["ctxT"]).then_inc(s["loaded"], 16)
            sp.dma_start(K.Xtok[:], w["xtok"]).then_inc(s["loaded"], 16)
            sp.wait_ge(s["loaded"], 16 * 3)

        @block.gpsimd
        def _(pool):
            pool.memset(K.eps[:], LN_EPS)
            pool.memset(K.ones[:], 1.0).then_inc(s["ones_set"], 1)
            pool.wait_ge(s["ones_set"], 1)

            def select(out, op, base, pattern, mult, fill=0.0, src=None):
                return pool.affine_select(out=out, in_=out if src is None else src, compare_op=op, fill=fill,
                                          base=base, pattern=pattern, channel_multiplier=mult)
            ones = K.ones[:, 0:P]
            select(K.ident[:], ALU.is_equal, 0, [[-1, P]], 1, src=ones).then_inc(s["masks_set"], 1)
            select(K.identb[:], ALU.is_equal, 0, [[-1, P]], 1, src=ones).then_inc(s["masks_set"], 1)
            select(K.causal_T[:], ALU.is_ge, 0, [[1, P]], -1, src=ones).then_inc(s["masks_set"], 1)
            o8 = K.ones[:, 0:8 * P].rearrange("p (h j) -> p h j", h=8)
            select(K.head_cols[:], ALU.is_ge, 0, [[-16, 8], [1, P]], 0, src=o8).then_inc(s["masks_set"], 1)
            pool.wait_ge(s["masks_set"], 4)
            select(K.head_cols[:], ALU.is_ge, 15, [[16, 8], [-1, P]], 0).then_inc(s["masks_set"], 1)
            select(K.head_rows[:], ALU.is_ge, 0, [[-16, 8]], 1, src=K.ones[:, 0:8]).then_inc(s["masks_set"], 1)
            pool.wait_ge(s["masks_set"], 6)
            select(K.head_rows[:], ALU.is_ge, 15, [[16, 8]], -1).then_inc(s["masks_set"], 1)
            pool.memset(K.above[:], 0.0).then_inc(s["masks_set"], 1)
            pool.memset(K.below[:], 0.0).then_inc(s["masks_set"], 1)
            pool.wait_ge(s["masks_set"], 9)
            select(K.above[:], ALU.is_ge, 0, [[-1, P]], 1, fill=NEG).then_inc(s["masks_set"], 1)
            select(K.below[:], ALU.is_ge, 0, [[1, P]], -1, fill=NEG).then_inc(s["masks_set"], 1)
            select(K.live_keys[:], ALU.is_ge, CTX - P - 1, [[0, 1]], -1, src=K.ones[:, 0:1]).then_inc(s["masks_set"], 1)


def finish(nc, K, wt, src, n_k, bias=None, relu=False, res=None):
    xi, xo = K.XT[K.cur], K.XT[1 - K.cur]
    res = xi if res is None else res
    with ExitStack() as es, phase(nc, K.sems, "y_done sum_done turned stats_done std_done tok_done back_turned copied") as (block, s):
        rT = sbuf(es, nc, "rT", [P, 2, DC, BLK])
        st = sbuf(es, nc, "ln_stats", [P, NT, 9])
        pair = lambda p: range(2 * p, 2 * p + 2)
        summed = lambda t: K.bank[2 + t % 4][:, 0:D]

        @block.tensor
        def _(pe):
            def product(j, h):
                if j >= 1:
                    pe.wait_ge(s["sum_done"], DC * (j - 1) + h + 1)
                for k in range(n_k):
                    last = pe.matmul(K.bank[h][:], wt(k, h, j), src(k, j), start=(k == 0), stop=(k == n_k - 1))
                last.then_inc(s["y_done"], 1)

            def turn(p):
                if p >= 2:
                    pe.wait_ge(s["tok_done"], 2 * (p - 1))
                for t in pair(p):
                    for h in range(DC):
                        last = pe.transpose(K.bank[2 + t % 4][:, h * P:(h + 1) * P],
                                            rT[:, (t // TPB) % 2, h, (t % TPB) * P:(t % TPB + 1) * P], K.ident[:])
                last.then_inc(s["turned"], 1)

            def turn_back(p):
                for t in pair(p):
                    pe.wait_ge(s["tok_done"], t + 1)
                    if t >= 2:
                        pe.wait_ge(s["copied"], t - 1)
                    for h in range(DC):
                        last = pe.transpose(K.bank[6 + t % 2][:, h * P:(h + 1) * P], K.Xtok[:, t, h * P:(h + 1) * P], K.ident[:])
                    last.then_inc(s["back_turned"], 1)

            for h in range(DC):
                product(0, h)
            for j in range(NB):
                pe.wait_ge(s["sum_done"], DC * (j + 1))
                for i in range(2):
                    turn(2 * j + i)
                    if j + 1 < NB:
                        product(j + 1, i)
                    if 2 * j + i > 0:
                        turn_back(2 * j + i - 1)
            turn_back(NT // 2 - 1)

        @block.vector
        def _(dve):
            def add(j, h):
                dve.wait_ge(s["y_done"], DC * j + h + 1)
                y, old, out = K.bank[h][:], res[:, h, j * BLK:(j + 1) * BLK], rT[:, j % 2, h, :]
                if relu:
                    last = dve.scalar_tensor_tensor(out=out, in0=y, scalar=0.0, in1=old, op0=ALU.max, op1=ALU.add)
                elif bias is not None:
                    last = dve.scalar_tensor_tensor(out=out, in0=y, scalar=bias[:, h:h + 1], in1=old, op0=ALU.add, op1=ALU.add)
                else:
                    last = dve.tensor_tensor(out, y, old, ALU.add)
                last.then_inc(s["sum_done"], 1)

            def stats(p):
                dve.wait_ge(s["turned"], p + 1)
                for t in pair(p):
                    dve.bn_stats(st[:, t, 2:8], summed(t))
                dve.drain()
                for t in pair(p):
                    last = dve.bn_aggr(st[:, t, 0:2], st[:, t, 2:8])
                last.then_inc(s["stats_done"], 1)

            def normalise(p):
                dve.wait_ge(s["std_done"], p + 1)
                std = st[:, 2 * p:2 * p + 2, 8:9]
                dve.reciprocal(std, std)
                dve.drain()
                for t in pair(p):
                    dve.tensor_scalar(K.Xtok[:, t, :], summed(t), st[:, t, 0:1], st[:, t, 8:9], ALU.subtract, ALU.mult).then_inc(s["tok_done"], 1)

            for h in range(DC):
                add(0, h)
            for j in range(NB):
                for i in range(2):
                    stats(2 * j + i)
                    if 2 * j + i > 0:
                        normalise(2 * j + i - 1)
                if j + 1 < NB:
                    for h in range(DC):
                        add(j + 1, h)
            normalise(NT // 2 - 1)

        @block.scalar
        def _(act):
            for p in range(NT // 2 + 1):
                if p < NT // 2:
                    act.wait_ge(s["stats_done"], p + 1)
                    act.activation(st[:, 2 * p:2 * p + 2, 8:9], st[:, 2 * p:2 * p + 2, 1:2], ACT.Sqrt, bias=K.eps[:, 0:1]).then_inc(s["std_done"], 1)
                for t in pair(p - 1) if p > 0 else ():
                    act.wait_ge(s["back_turned"], t + 1)
                    act.activation(xo[:, :, t * P:(t + 1) * P], K.bank[6 + t % 2][:, 0:D].rearrange("p (c k) -> p c k", c=2),
                                   ACT.Copy).then_inc(s["copied"], 1)
    K.cur = 1 - K.cur


def project(nc, K, es, n_m, n_k, wt, src, evac_act, evac_dve, n_blk=NB, loads=(), width=lambda j: BLK):
    with phase(nc, K.sems, "loaded done act_out dve_out") as (block, s):
        steps = [(m, j) for m in range(n_m) for j in range(n_blk)]

        @block.sync
        def _(sp):
            for dst, srcd in loads:
                sp.dma_start(dst, srcd).then_inc(s["loaded"], 16)

        @block.tensor
        def _(pe):
            pe.wait_ge(s["loaded"], 16 * len(loads)) if loads else None
            for n, (m, j) in enumerate(steps):
                if n >= 8:
                    pe.wait_ge(s["act_out"] if n % 2 == 0 else s["dve_out"], (n - 8) // 2 + 1)
                for k in range(n_k):
                    last = pe.matmul(K.bank[n % 8][:, 0:width(j)], wt(k, m), src(k, j), start=(k == 0), stop=(k == n_k - 1))
                last.then_inc(s["done"], 1)

        @block.scalar
        def _(act):
            act.wait_ge(s["loaded"], 16 * len(loads)) if loads else None
            for n, (m, j) in enumerate(steps):
                if n % 2 == 0:
                    act.wait_ge(s["done"], n + 1)
                    evac_act(act, m, j, K.bank[n % 8][:, 0:width(j)]).then_inc(s["act_out"], 1)

        @block.vector
        def _(dve):
            dve.wait_ge(s["loaded"], 16 * len(loads)) if loads else None
            for n, (m, j) in enumerate(steps):
                if n % 2 == 1:
                    dve.wait_ge(s["done"], n + 1)
                    evac_dve(dve, m, j, K.bank[n % 8][:, 0:width(j)]).then_inc(s["dve_out"], 1)


def load(nc, K, *pairs, later=()):
    K.late_count += 16 * len(later)
    with phase(nc, K.sems, "loaded") as (block, s):
        @block.sync
        def _(sp):
            for dst, src in pairs[0::2]:
                sp.dma_start(dst, src).then_inc(s["loaded"], 16)
            for dst, src in later:
                sp.dma_start(dst, src).then_inc(K.late, 16)
            if pairs:
                sp.wait_ge(s["loaded"], 16 * len(pairs))

        @block.scalar
        def _(act):
            for dst, src in pairs[1::2]:
                act.dma_start(dst, src).then_inc(s["loaded"], 16)


def arrive(nc, K):
    with nc.Block() as block:
        @block.sync
        def _(sp):
            sp.wait_ge(K.late, K.late_count)


def copy_to(dst, bias=None, relu=False):
    def by_act(act, m, j, src):
        if bias is None:
            return act.activation(dst(m, j), src, ACT.Copy)
        return act.activation(dst(m, j), src, ACT.Relu if relu else ACT.Identity, bias=bias(m))

    def by_dve(dve, m, j, src):
        if bias is None:
            return dve.tensor_copy(dst(m, j), src)
        if relu:
            return dve.tensor_scalar(dst(m, j), src, bias(m), 0.0, ALU.add, ALU.max)
        return dve.tensor_scalar(dst(m, j), src, bias(m), None, ALU.add)
    return by_act, by_dve


def block_of(xT):
    return lambda k, j: xT[:, k, j * BLK:(j + 1) * BLK]


def ctx_values(nc, K, V, Wv, bias_row, relu, live=True):
    with phase(nc, K.sems, "done summed") as (block, s):
        @block.tensor
        def _(pe):
            for n in range(2 * B):
                b, kt = divmod(n, 2)
                for k in range(DC):
                    last = pe.matmul(K.bank[n][:, 0:D], K.ctxT[:, k, b, kt * P:(kt + 1) * P], Wv[:, k, :], start=(k == 0), stop=(k == DC - 1))
                last.then_inc(s["done"], 1)

        @block.vector
        def _(dve):
            for n in range(2 * B):
                b, kt = divmod(n, 2)
                v = V[:, b, kt, :]
                dve.wait_ge(s["done"], n + 1)
                dve.tensor_tensor(v, K.bank[n][:, 0:D], bias_row, ALU.add)
                dve.drain()
                if relu:
                    dve.tensor_scalar(v, v, 0.0, None, ALU.max)
                    dve.drain()
                if kt == 1:
                    dve.tensor_scalar(v, v, K.live_keys[:, 0:1], None, ALU.mult)
                    dve.drain()


def L1_xattn_layout(i):
    maskT = np.ascontiguousarray(pad(np.asarray(i["mask_1xSxS2_ff0"])[0].T, 0, 2 * P))
    return {"L1x_Wq": rows(i["L1_xattn_kernel_q"][0, 0]), "L1x_Wk": rows(i["L1_xattn_kernel_k"][0, 0]),
            "L1x_Wv": rows(i["L1_xattn_kernel_v"][0, 0]), "L1x_bq": cols(i["L1_xattn_bias_q"]),
            "L1x_bk": cols(i["L1_xattn_bias_k"]), "L1x_bv": np.asarray(i["L1_xattn_bias_v"]), "L1x_maskT": rows(maskT)}


def L1_xattn(nc, K, w):
    with ExitStack() as es:
        Wq, Wk, Wv = (sbuf(es, nc, n, [P, DC, D]) for n in ("Wq", "Wk", "Wv"))
        bq, bk = (sbuf(es, nc, n, [P, DC]) for n in ("bq", "bk"))
        bv = sbuf(es, nc, "bv", [P, D])
        maskT = sbuf(es, nc, "maskT", [P, 2, S])
        QT = sbuf(es, nc, "QT", [P, DC, TOK])
        KT = sbuf(es, nc, "KT", [P, DC, B * 256])
        V = sbuf(es, nc, "V", [P, B, 2, D])
        ST = sbuf(es, nc, "ST", [P, 2, TOK])
        load(nc, K, (Wq[:], w["L1x_Wq"]), (bq[:], w["L1x_bq"]),
             later=((Wk[:], w["L1x_Wk"]), (bk[:], w["L1x_bk"]), (Wv[:], w["L1x_Wv"]), (bv[:], spread(w["L1x_bv"])), (maskT[:], w["L1x_maskT"])))
        a, v = copy_to(lambda m, j: QT[:, m, j * BLK:(j + 1) * BLK], lambda m: bq[:, m:m + 1], True)
        project(nc, K, es, DC, DC, lambda k, m: Wq[:, k, m * P:(m + 1) * P], block_of(K.XT[K.cur]), a, v)
        arrive(nc, K)
        a, v = copy_to(lambda m, j: KT[:, m, :], lambda m: bk[:, m:m + 1], True)
        project(nc, K, es, DC, DC, lambda k, m: Wk[:, k, m * P:(m + 1) * P],
                lambda k, j: K.ctxT[:, k].rearrange("p b n -> p (b n)"), a, v, n_blk=1)
        ctx_values(nc, K, V, Wv, bv[:], True)
        with phase(nc, K.sems, "done relued masked") as (block, s):
            @block.tensor
            def _(pe):
                for n in range(2 * NB):
                    j, kt = divmod(n, 2)
                    for k in range(DC):
                        last = pe.matmul(K.bank[n][:], KT[:, k, (j // 2) * 256 + kt * P:(j // 2) * 256 + (kt + 1) * P],
                                         QT[:, k, j * BLK:(j + 1) * BLK], start=(k == 0), stop=(k == DC - 1))
                    last.then_inc(s["done"], 1)

            @block.scalar
            def _(act):
                for n in range(2 * NB):
                    act.wait_ge(s["done"], n + 1)
                    j, kt = divmod(n, 2)
                    act.activation(ST[:, kt, j * BLK:(j + 1) * BLK], K.bank[n][:], ACT.Relu, scale=float(D) ** -0.5).then_inc(s["relued"], 1)

            @block.vector
            def _(dve):
                for n in range(2 * NB):
                    dve.wait_ge(s["relued"], n + 1)
                    j, kt = divmod(n, 2)
                    st = ST[:, kt, j * BLK:(j + 1) * BLK]
                    dve.tensor_tensor(st, st, maskT[:, kt, (j % 2) * BLK:(j % 2 + 1) * BLK], ALU.add)
        finish(nc, K, lambda k, h, j: V[:, j // 2, k, h * P:(h + 1) * P], block_of(ST), 2, relu=True)


HEADS = 16
HD = D // HEADS
HPC = P // HD
HK = HPC * CTX
HKT = -(-HK // P)
GROUPS = [(0, 3), (3, 3), (6, 2)]
ALIBI_OFF = S - CTX


def middle(ap, n):
    return ap.unsqueeze(1).broadcast_to((ap.shape[0], n, ap.shape[1]))


def inner(ap, n):
    return ap.unsqueeze(2).broadcast_to((ap.shape[0], ap.shape[1], n))


def cross_attention(nc, K, w, pre, scale, slopes=None):
    with ExitStack() as es:
        Wo = sbuf(es, nc, "Wo", [P, DC, D])
        bo = sbuf(es, nc, "bo", [P, DC])
        OT = sbuf(es, nc, "OT", [P, DC, TOK])
        with ExitStack() as inside:
            Vb = sbuf(inside, nc, "Vblocks", [P, DC, B, HKT, P])
            Kb = sbuf(inside, nc, "Kblocks", [P, DC, B, HK])
            QT = sbuf(inside, nc, "QT", [P, DC, TOK])
            Pr = sbuf(inside, nc, "probs", [P, 2 * 2 * HK])
            with ExitStack() as temp:
                Wq, Wk, Wv = (sbuf(temp, nc, n, [P, DC, D]) for n in ("Wq", "Wk", "Wv"))
                bq, bk, bv = (sbuf(temp, nc, n, [P, DC]) for n in ("bq", "bk", "bv"))
                KT, VT = (sbuf(temp, nc, n, [P, DC, B * 256]) for n in ("KT", "VT"))
                load(nc, K, (Wq[:], w[pre + "Wq"]), (bq[:], w[pre + "bq"]),
                     later=((Wk[:], w[pre + "Wk"]), (bk[:], w[pre + "bk"]), (Wv[:], w[pre + "Wv"]), (bv[:], w[pre + "bv"]),
                            (Wo[:], w[pre + "Wo"]), (bo[:], w[pre + "bo"])))
                a, v = copy_to(lambda m, j: QT[:, m, j * BLK:(j + 1) * BLK], lambda m: bq[:, m:m + 1])
                project(nc, K, es, DC, DC, lambda k, m: Wq[:, k, m * P:(m + 1) * P], block_of(K.XT[K.cur]), a, v)
                arrive(nc, K)
                ctx = lambda k, j: K.ctxT[:, k].rearrange("p b n -> p (b n)")
                a, v = copy_to(lambda m, j: KT[:, m, :], lambda m: bk[:, m:m + 1])
                project(nc, K, es, DC, DC, lambda k, m: Wk[:, k, m * P:(m + 1) * P], ctx, a, v, n_blk=1)
                a, v = copy_to(lambda m, j: VT[:, m, :], lambda m: bv[:, m:m + 1])
                project(nc, K, es, DC, DC, lambda k, m: Wv[:, k, m * P:(m + 1) * P], ctx, a, v, n_blk=1)
                with phase(nc, K.sems, "spread turned out") as (block, s):
                    VbT = Pr[:].rearrange("p (n hk) -> p n hk", hk=HK)

                    @block.vector
                    def _(dve):
                        for n in range(DC * B):
                            c, b = divmod(n, B)
                            dve.tensor_tensor(VbT[:, n, :].rearrange("p (h k) -> p h k", h=HPC), middle(VT[:, c, b * 256:b * 256 + CTX], HPC),
                                              inner(K.head_rows[:], CTX), ALU.mult).then_inc(s["spread"], 1)
                        for n in range(DC * B):
                            c, b = divmod(n, B)
                            dve.tensor_tensor(Kb[:, c, b, :].rearrange("p (h k) -> p h k", h=HPC), middle(KT[:, c, b * 256:b * 256 + CTX], HPC),
                                              inner(K.head_rows[:], CTX), ALU.mult)

                    @block.tensor
                    def _(pe):
                        for n in range(DC * B):
                            pe.wait_ge(s["spread"], n + 1)
                            for g in range(3):
                                if 3 * n + g >= 8:
                                    pe.wait_ge(s["out"], 3 * n + g - 7)
                                for i in range(4 * g, min(4 * g + 4, HKT)):
                                    r = min(P, HK - i * P)
                                    last = pe.transpose(K.bank[(3 * n + g) % 8][0:r, (i % 4) * P:(i % 4 + 1) * P],
                                                        VbT[:, n, i * P:i * P + r], K.ident[:])
                                last.then_inc(s["turned"], 1)

                    @block.scalar
                    def _(act):
                        for n in range(DC * B):
                            c, b = divmod(n, B)
                            for g in range(3):
                                act.wait_ge(s["turned"], 3 * n + g + 1)
                                src = K.bank[(3 * n + g) % 8]
                                if g < 2:
                                    act.activation(Vb[:, c, b, 4 * g:4 * g + 4, :], src[:].rearrange("p (i k) -> p i k", i=4), ACT.Copy).then_inc(s["out"], 1)
                                else:
                                    act.activation(Vb[:, c, b, 8, :], src[:, 0:P], ACT.Copy)
                                    act.activation(Vb[0:HK - 9 * P, c, b, 9, :], src[0:HK - 9 * P, P:2 * P], ACT.Copy).then_inc(s["out"], 1)

            PT = sbuf(inside, nc, "probsT", [P, HKT, P])
            stat = sbuf(inside, nc, "stat", [P, 2, 3, HPC])
            Rx = sbuf(inside, nc, "recip_spread", [P, 2, P])
            RT = sbuf(inside, nc, "recipT", [P, 2, P])
            names = "recip_spread recip_turned scored max_done exp_done recip_done turned probs_out probs_out_act recip_out pv_done out"
            with phase(nc, K.sems, names) as (block, s):
                steps = NT * DC
                sc = lambda n, g: K.bank[3 * (n % 2) + g]
                probs = lambda n: Pr[:].rearrange("p (n hk) -> p n hk", hk=HK)[:, n % 2, :]
                st = lambda n, i: stat[:, n % 2, i, :]

                @block.gpsimd
                def _(pool):
                    for n in range(steps):
                        pool.wait_ge(s["recip_done"], n + 1)
                        pool.tensor_copy(Rx[:, n % 2, :].rearrange("p (h d) -> p h d", h=HPC), inner(st(n, 2), HD)).then_inc(s["recip_spread"], 1)

                @block.tensor
                def _(pe):
                    def score(n, g):
                        t, c = divmod(n, DC)
                        if g == 0 and n >= 2:
                            pe.wait_ge(s["probs_out"], 2 * (n - 1))
                            pe.wait_ge(s["probs_out_act"], n - 1)
                            pe.wait_ge(s["recip_out"], n - 1)
                        h0, nh = GROUPS[g]
                        pe.matmul(sc(n, g)[:, 0:nh * CTX], QT[:, c, t * P:(t + 1) * P],
                                  Kb[:, c, t // 8, h0 * CTX:(h0 + nh) * CTX], start=True, stop=True).then_inc(s["scored"], 1)

                    def turn(n, g):
                        pe.wait_ge(s["exp_done"], 3 * n + g + 1)
                        for i in range(4 * g, min(4 * g + 4, HKT)):
                            r = min(P, HK - i * P)
                            last = pe.transpose(sc(n, g)[0:r, (i % 4) * P:(i % 4 + 1) * P], probs(n)[:, i * P:i * P + r], K.ident[:])
                        last.then_inc(s["turned"], 1)

                    for g in range(3):
                        score(0, g)
                    for n in range(steps):
                        t, c = divmod(n, DC)
                        turn(n, 0)
                        if n + 1 < steps:
                            score(n + 1, 0)
                            score(n + 1, 1)
                        turn(n, 1)
                        if n + 1 < steps:
                            score(n + 1, 2)
                        turn(n, 2)
                        if n >= 2:
                            pe.wait_ge(s["out"], n - 1)
                        for i in range(HKT):
                            r = min(P, HK - i * P)
                            if i in (0, 8):
                                pe.wait_ge(s["probs_out"], 2 * n + i // 8 + 1)
                            if i == 4:
                                pe.wait_ge(s["probs_out_act"], n + 1)
                            last = pe.matmul(K.bank[6 + n % 2][:, 0:P], Vb[0:r, c, t // 8, i, :], PT[0:r, i, :], start=(i == 0), stop=(i == HKT - 1))
                        last.then_inc(s["pv_done"], 1)
                        pe.wait_ge(s["recip_spread"], n + 1)
                        pe.transpose(sc(n, 2)[:, 2 * P:3 * P], Rx[:, n % 2, :], K.ident[:]).then_inc(s["recip_turned"], 1)

                @block.vector
                def _(dve):
                    def bias(n, g):
                        t, c = divmod(n, DC)
                        h0, nh = GROUPS[g]
                        dve.wait_ge(s["scored"], 3 * n + g + 1)
                        for h in range(h0, h0 + nh) if slopes else ():
                            dve.scalar_tensor_tensor(out=probs(n)[:, h * CTX:(h + 1) * CTX], in0=K.rel[:, t % 8, :],
                                                     scalar=-slopes[c * HPC + h] / scale,
                                                     in1=sc(n, g)[:, (h - h0) * CTX:(h - h0 + 1) * CTX], op0=ALU.mult, op1=ALU.add)

                    def reduce(n, g):
                        h0, nh = GROUPS[g]
                        src = probs(n)[:, h0 * CTX:(h0 + nh) * CTX] if slopes else sc(n, g)[:, 0:nh * CTX]
                        dve.reduce_max(st(n, 0)[:, h0:h0 + nh], src.rearrange("p (h k) -> p h k", h=nh), AX)

                    def negate(n, h0, h1):
                        dve.tensor_scalar(st(n, 0)[:, h0:h1], st(n, 0)[:, h0:h1], -scale, None, ALU.mult).then_inc(s["max_done"], 1)

                    def maxima(n, groups):
                        if slopes and n >= 2 and groups[0] == 0:
                            dve.wait_ge(s["turned"], 3 * (n - 1))
                        for g in groups:
                            bias(n, g)
                        if slopes:
                            dve.drain()
                        for g in groups:
                            reduce(n, g)
                        dve.drain()
                        negate(n, GROUPS[groups[0]][0], GROUPS[groups[-1]][0] + GROUPS[groups[-1]][1])

                    def probs_out(n, g):
                        dve.wait_ge(s["turned"], 3 * n + g + 1)
                        if g == 0:
                            dve.tensor_copy(PT[:, 0:4, :], sc(n, g)[:].rearrange("p (i k) -> p i k", i=4)).then_inc(s["probs_out"], 1)
                        else:
                            dve.tensor_copy(PT[:, 8, :], sc(n, g)[:, 0:P])
                            dve.tensor_copy(PT[0:HK - 9 * P, 9, :], sc(n, g)[0:HK - 9 * P, P:2 * P]).then_inc(s["probs_out"], 1)

                    def output(n):
                        t, c = divmod(n, DC)
                        dve.wait_ge(s["pv_done"], n + 1)
                        dve.wait_ge(s["recip_out"], n + 1)
                        dve.tensor_tensor(OT[:, c, t * P:(t + 1) * P], K.bank[6 + n % 2][:, 0:P], RT[:, n % 2, :], ALU.mult).then_inc(s["out"], 1)

                    maxima(0, (0, 1))
                    maxima(0, (2,))
                    for n in range(steps):
                        if n >= 1:
                            dve.wait_ge(s["pv_done"], n)
                        probs_out(n, 0)
                        if n + 1 < steps:
                            maxima(n + 1, (0, 1))
                        if n + 1 < steps:
                            maxima(n + 1, (2,))
                        probs_out(n, 2)
                        dve.wait_ge(s["exp_done"], 3 * n + 3)
                        if n >= 2:
                            dve.wait_ge(s["recip_spread"], n - 1)
                        dve.reciprocal(st(n, 2), st(n, 1)).then_inc(s["recip_done"], 1)
                        if n >= 1:
                            output(n - 1)
                    output(steps - 1)

                @block.scalar
                def _(act):
                    def recip_out(n):
                        act.wait_ge(s["recip_turned"], n + 1)
                        if n >= 2:
                            act.wait_ge(s["out"], n - 1)
                        act.activation(RT[:, n % 2, :], sc(n, 2)[:, 2 * P:3 * P], ACT.Copy).then_inc(s["recip_out"], 1)

                    def probs_out(n):
                        act.wait_ge(s["turned"], 3 * n + 2)
                        if n >= 1:
                            act.wait_ge(s["pv_done"], n)
                        act.activation(PT[:, 4:8, :], sc(n, 1)[:].rearrange("p (i k) -> p i k", i=4), ACT.Copy).then_inc(s["probs_out_act"], 1)

                    for n in range(steps):
                        if n >= 1:
                            probs_out(n - 1)
                        act.wait_ge(s["max_done"], 2 * n + 1)
                        if n >= 2:
                            act.wait_ge(s["turned"], 3 * (n - 1))
                            act.wait_ge(s["recip_done"], n - 1)
                        for g, (h0, nh) in enumerate(GROUPS):
                            if g == 2:
                                act.wait_ge(s["max_done"], 2 * n + 2)
                            for h in range(h0, h0 + nh):
                                p = probs(n)[:, h * CTX:(h + 1) * CTX]
                                src = p if slopes else sc(n, g)[:, (h - h0) * CTX:(h - h0 + 1) * CTX]
                                last = act.activation(p, src, ACT.Exp, bias=st(n, 0)[:, h:h + 1], scale=scale, accum_out=st(n, 1)[:, h:h + 1])
                                if h in (3, 6, 7):
                                    last.then_inc(s["exp_done"], 1)
                                if h == 3 and n >= 1:
                                    recip_out(n - 1)
                    probs_out(steps - 1)
                    recip_out(steps - 1)
        finish(nc, K, lambda k, h, j: Wo[:, k, h * P:(h + 1) * P], block_of(OT), DC, bias=bo)


def L0_xattn_layout(i):
    return {"L0x_Wq": rows(i["L0_xattn_Wq"]), "L0x_Wk": rows(np.tile(i["L0_xattn_Wk"], (1, HEADS))),
            "L0x_Wv": rows(np.tile(i["L0_xattn_Wv"], (1, HEADS))), "L0x_Wo": rows(i["L0_xattn_Wo"]),
            "L0x_bq": cols(i["L0_xattn_bq"]), "L0x_bk": cols(np.tile(i["L0_xattn_bk"], HEADS)),
            "L0x_bv": cols(np.tile(i["L0_xattn_bv"], HEADS)), "L0x_bo": cols(i["L0_xattn_bo"])}


def L0_xattn(nc, K, w):
    cross_attention(nc, K, w, "L0x_", float(HD) ** -0.5)


def L3_xattn_layout(i):
    Wkv, bkv = np.asarray(i["L3_xattn_Wkv"]), np.asarray(i["L3_xattn_bkv"])
    rel = np.abs(np.arange(CTX)[None, :] - np.arange(S)[:, None] - (CTX - S)).astype(np.float32)
    return {"L3x_Wq": rows(i["L3_xattn_Wq"]), "L3x_Wk": rows(Wkv[:, :D]), "L3x_Wv": rows(Wkv[:, D:]), "L3x_Wo": rows(i["L3_xattn_Wo"]),
            "L3x_bq": cols(i["L3_xattn_bq"]), "L3x_bk": cols(bkv[:D]), "L3x_bv": cols(bkv[D:]), "L3x_bo": cols(i["L3_xattn_bo"]),
            "L3x_rel": rows(rel)}


def L3_xattn(nc, K, w):
    with ExitStack() as es:
        K.rel = sbuf(es, nc, "rel", [P, S // P, CTX])
        load(nc, K, (K.rel[:], w["L3x_rel"]))
        cross_attention(nc, K, w, "L3x_", float(HD) ** -0.5, [2.0 ** (-8.0 * (h + 1) / HEADS) for h in range(HEADS)])


def L2_xattn_layout(i):
    g = lambda n: i["L2_xattn_" + n]
    return {"L2x_Wq": rows(g("Wq")), "L2x_Wk": rows(g("Wk")), "L2x_Wv": rows(g("Wv")), "L2x_Wo": rows(g("Wo")),
            "L2x_bq": cols(g("bq")), "L2x_bk": cols(g("bk")), "L2x_bv": np.asarray(g("bv")), "L2x_bo": cols(g("bo"))}


def L2_xattn(nc, K, w):
    with ExitStack() as es:
        Wq, Wk, Wv, Wo = (sbuf(es, nc, n, [P, DC, D]) for n in ("Wq", "Wk", "Wv", "Wo"))
        bq, bk, bo = (sbuf(es, nc, n, [P, DC]) for n in ("bq", "bk", "bo"))
        bv = sbuf(es, nc, "bv", [P, D])
        QT, OT = (sbuf(es, nc, n, [P, DC, TOK]) for n in ("QT", "OT"))
        KT = sbuf(es, nc, "KT", [P, DC, B * 256])
        V = sbuf(es, nc, "V", [P, B, 2, D])
        load(nc, K, (Wq[:], w["L2x_Wq"]), (bq[:], w["L2x_bq"]),
             later=((Wk[:], w["L2x_Wk"]), (bk[:], w["L2x_bk"]), (Wv[:], w["L2x_Wv"]), (bv[:], spread(w["L2x_bv"])),
                    (Wo[:], w["L2x_Wo"]), (bo[:], w["L2x_bo"])))
        a, v = copy_to(lambda m, j: QT[:, m, j * BLK:(j + 1) * BLK], lambda m: bq[:, m:m + 1])
        project(nc, K, es, DC, DC, lambda k, m: Wq[:, k, m * P:(m + 1) * P], block_of(K.XT[K.cur]), a, v)
        arrive(nc, K)
        a, v = copy_to(lambda m, j: KT[:, m, :], lambda m: bk[:, m:m + 1])
        project(nc, K, es, DC, DC, lambda k, m: Wk[:, k, m * P:(m + 1) * P],
                lambda k, j: K.ctxT[:, k].rearrange("p b n -> p (b n)"), a, v, n_blk=1)
        ctx_values(nc, K, V, Wv, bv[:], False)
        scale = float(D) ** -0.5
        Pr = sbuf(es, nc, "probs", [P, 2, CTX])
        PT = sbuf(es, nc, "probsT", [P, 2, 2, BLK])
        stat = sbuf(es, nc, "stat", [P, 2, 3])
        with phase(nc, K.sems, "zeroed scored max_done exp_done normed turned probs_out pv_done out") as (block, s):
            @block.gpsimd
            def _(pool):
                pool.memset(PT[:, :, 1, :], 0.0).then_inc(s["zeroed"], 1)

            @block.tensor
            def _(pe):
                def score(t):
                    if t >= 2:
                        pe.wait_ge(s["exp_done"], t - 1)
                    for k in range(DC):
                        last = pe.matmul(K.bank[t % 2][:, 0:CTX], QT[:, k, t * P:(t + 1) * P], KT[:, k, (t // 8) * 256:(t // 8) * 256 + CTX],
                                         start=(k == 0), stop=(k == DC - 1))
                    last.then_inc(s["scored"], 1)

                def values(j):
                    pe.wait_ge(s["probs_out"], TPB * (j + 1))
                    if j >= 2:
                        pe.wait_ge(s["out"], DC * (j - 1))
                    for h in range(DC):
                        for kt in range(2):
                            last = pe.matmul(K.bank[4 + 2 * (j % 2) + h][:], V[:, j // 2, kt, h * P:(h + 1) * P], PT[:, j % 2, kt, :],
                                             start=(kt == 0), stop=(kt == 1))
                    last.then_inc(s["pv_done"], 1)

                score(0)
                for t in range(NT):
                    if t + 1 < NT:
                        score(t + 1)
                    pe.wait_ge(s["normed"], t + 1)
                    if t >= 2:
                        pe.wait_ge(s["probs_out"], t - 1)
                    pe.transpose(K.bank[2 + t % 2][:, 0:P], Pr[:, t % 2, 0:P], K.ident[:])
                    pe.transpose(K.bank[2 + t % 2][0:CTX - P, P:2 * P], Pr[:, t % 2, P:CTX], K.ident[:]).then_inc(s["turned"], 1)
                    if t % TPB == 0 and t:
                        values(t // TPB - 1)
                values(NB - 1)

            @block.vector
            def _(dve):
                def maximum(t):
                    dve.wait_ge(s["scored"], t + 1)
                    if t >= 2:
                        dve.wait_ge(s["exp_done"], t - 1)
                    dve.reduce_max(stat[:, t % 2, 0:1], K.bank[t % 2][:, 0:CTX], AX)
                    dve.drain()
                    dve.tensor_scalar(stat[:, t % 2, 0:1], stat[:, t % 2, 0:1], -scale, None, ALU.mult).then_inc(s["max_done"], 1)

                def output(j):
                    dve.wait_ge(s["pv_done"], j + 1)
                    for h in range(DC):
                        dve.tensor_copy(OT[:, h, j * BLK:(j + 1) * BLK], K.bank[4 + 2 * (j % 2) + h][:]).then_inc(s["out"], 1)

                maximum(0)
                for t in range(NT):
                    if t + 1 < NT:
                        maximum(t + 1)
                    dve.wait_ge(s["exp_done"], t + 1)
                    dve.reciprocal(stat[:, t % 2, 2:3], stat[:, t % 2, 1:2])
                    dve.drain()
                    dve.tensor_scalar(Pr[:, t % 2, :], Pr[:, t % 2, :], stat[:, t % 2, 2:3], None, ALU.mult).then_inc(s["normed"], 1)
                    if t % TPB == 2 and t > TPB:
                        output(t // TPB - 1)
                output(NB - 1)

            @block.scalar
            def _(act):
                def exp(t):
                    act.wait_ge(s["max_done"], t + 1)
                    if t >= 2:
                        act.wait_ge(s["turned"], t - 1)
                    act.activation(Pr[:, t % 2, :], K.bank[t % 2][:, 0:CTX], ACT.Exp, bias=stat[:, t % 2, 0:1], scale=scale,
                                   accum_out=stat[:, t % 2, 1:2]).then_inc(s["exp_done"], 1)

                act.wait_ge(s["zeroed"], 1)
                exp(0)
                for t in range(NT):
                    if t + 1 < NT:
                        exp(t + 1)
                    act.wait_ge(s["turned"], t + 1)
                    j = t // TPB
                    if t % TPB == 0 and j >= 2:
                        act.wait_ge(s["pv_done"], j - 1)
                    cols_ = slice((t % TPB) * P, (t % TPB + 1) * P)
                    act.activation(PT[:, j % 2, 0, cols_], K.bank[2 + t % 2][:, 0:P], ACT.Copy)
                    act.activation(PT[0:CTX - P, j % 2, 1, cols_], K.bank[2 + t % 2][0:CTX - P, P:2 * P], ACT.Copy).then_inc(s["probs_out"], 1)
        finish(nc, K, lambda k, h, j: Wo[:, k, h * P:(h + 1) * P], block_of(OT), DC, bias=bo)


def finish_tokens(nc, K, r):
    xo = K.XT[1 - K.cur]
    with ExitStack() as es, phase(nc, K.sems, "stats_done std_done tok_done turned") as (block, s):
        st = sbuf(es, nc, "ln_stats", [P, NT, 9])

        @block.vector
        def _(dve):
            for t in range(NT):
                dve.bn_stats(st[:, t, 2:8], r[:, t, :])
            dve.drain()
            for t in range(NT):
                ins = dve.bn_aggr(st[:, t, 0:2], st[:, t, 2:8])
            ins.then_inc(s["stats_done"], 1)
            dve.wait_ge(s["std_done"], 1)
            dve.reciprocal(st[:, :, 8:9], st[:, :, 8:9])
            dve.drain()
            for t in range(NT):
                dve.tensor_scalar(K.Xtok[:, t, :], r[:, t, :], st[:, t, 0:1], st[:, t, 8:9], ALU.subtract, ALU.mult).then_inc(s["tok_done"], 1)

        @block.scalar
        def _(act):
            act.wait_ge(s["stats_done"], 1)
            act.activation(st[:, :, 8:9], st[:, :, 1:2], ACT.Sqrt, bias=K.eps[:, 0:1]).then_inc(s["std_done"], 1)
            for t in range(NT):
                act.wait_ge(s["turned"], t + 1)
                act.activation(xo[:, :, t * P:(t + 1) * P], K.bank[t % 4][:, 0:D].rearrange("p (c k) -> p c k", c=2), ACT.Copy).then_inc(s["std_done"], 1)

        @block.tensor
        def _(pe):
            for t in range(NT):
                pe.wait_ge(s["tok_done"], t + 1)
                if t >= 4:
                    pe.wait_ge(s["std_done"], 1 + t - 3)
                for h in range(DC):
                    ins = pe.transpose(K.bank[t % 4][:, h * P:(h + 1) * P], K.Xtok[:, t, h * P:(h + 1) * P], K.ident[:])
                ins.then_inc(s["turned"], 1)
    K.cur = 1 - K.cur


TAPS = 4
L3A_M = 4


def L3_attn_layout(i):
    cw = np.asarray(i["L3_attn_conv_w"]).reshape(4, P, TAPS).transpose(1, 0, 2)
    return {"L3a_Win": rows(i["L3_attn_W_in"]), "L3a_cw": np.ascontiguousarray(cw), "L3a_cb": cols(i["L3_attn_conv_b"]),
            "L3a_Wout": rows(i["L3_attn_W_out"])}


def L3_attn(nc, K, w):
    with ExitStack() as es:
        Wout = sbuf(es, nc, "Wout", [P, L3A_M, D])
        Y = sbuf(es, nc, "Y", [P, L3A_M, TOK])
        with ExitStack() as inside:
            Win = sbuf(inside, nc, "Win", [P, DC, 2 * L3A_M * P])
            cw = sbuf(inside, nc, "cw", [P, L3A_M, TAPS])
            cb = sbuf(inside, nc, "cb", [P, L3A_M])
            H = sbuf(inside, nc, "H", [P, L3A_M, B, TAPS - 1 + S])
            sg, ss = (sbuf(inside, nc, n, [P, 2, BLK]) for n in ("sigmoid", "sigmoid_of_conv"))
            acc = sbuf(inside, nc, "conv", [P, 2, BLK])
            load(nc, K, (Win[:], w["L3a_Win"]), (cw[:], w["L3a_cw"]), (cb[:], w["L3a_cb"]), later=((Wout[:], w["L3a_Wout"]),))
            steps = [(m, j) for m in range(L3A_M) for j in range(NB)]
            with phase(nc, K.sems, "padded done gated h_done conv_done silu_gated silu_done") as (block, s):
                N = len(steps)

                @block.tensor
                def _(pe):
                    for n, (m, j) in enumerate(steps):
                        if n >= 4:
                            pe.wait_ge(s["h_done"], n - 3)
                        for part in range(2):
                            for k in range(DC):
                                col = (part * L3A_M + m) * P
                                last = pe.matmul(K.bank[2 * (n % 4) + part][:], Win[:, k, col:col + P], K.XT[K.cur][:, k, j * BLK:(j + 1) * BLK],
                                                 start=(k == 0), stop=(k == DC - 1))
                        last.then_inc(s["done"], 1)

                @block.scalar
                def _(act):
                    for n in range(N + 2):
                        if n < N:
                            act.wait_ge(s["done"], n + 1)
                            if n >= 2:
                                act.wait_ge(s["h_done"], n - 1)
                            act.activation(sg[:, n % 2, :], K.bank[2 * (n % 4) + 1][:], ACT.Sigmoid).then_inc(s["gated"], 1)
                        if n >= 2:
                            act.wait_ge(s["conv_done"], n - 1)
                            if n >= 4:
                                act.wait_ge(s["silu_done"], n - 3)
                            act.activation(ss[:, n % 2, :], acc[:, n % 2, :], ACT.Sigmoid).then_inc(s["silu_gated"], 1)

                @block.gpsimd
                def _(pool):
                    pool.memset(H[:, :, :, 0:TAPS - 1], 0.0).then_inc(s["padded"], 1)
                    for n, (m, j) in enumerate(steps):
                        pool.wait_ge(s["silu_gated"], n + 1)
                        pool.tensor_tensor(Y[:, m, j * BLK:(j + 1) * BLK], acc[:, n % 2, :], ss[:, n % 2, :], ALU.mult).then_inc(s["silu_done"], 1)

                @block.vector
                def _(dve):
                    def gate(n):
                        m, j = steps[n]
                        b, o = divmod(j * BLK, S)
                        dve.wait_ge(s["gated"], n + 1)
                        dve.tensor_tensor(H[:, m, b, TAPS - 1 + o:TAPS - 1 + o + BLK], K.bank[2 * (n % 4)][:], sg[:, n % 2, :],
                                          ALU.mult).then_inc(s["h_done"], 1)

                    dve.wait_ge(s["padded"], 1)
                    gate(0)
                    for n, (m, j) in enumerate(steps):
                        b, o = divmod(j * BLK, S)
                        if n + 1 < N:
                            gate(n + 1)
                        dve.wait_ge(s["h_done"], n + 1)
                        if n >= 2:
                            dve.wait_ge(s["silu_done"], n - 1)
                        dve.tensor_scalar(acc[:, n % 2, :], H[:, m, b, o:o + BLK], cw[:, m, 0:1], cb[:, m:m + 1], ALU.mult, ALU.add)
                        for tap in range(1, TAPS):
                            dve.drain()
                            ins = dve.scalar_tensor_tensor(out=acc[:, n % 2, :], in0=H[:, m, b, o + tap:o + tap + BLK], scalar=cw[:, m, tap:tap + 1],
                                                           in1=acc[:, n % 2, :], op0=ALU.mult, op1=ALU.add)
                        ins.then_inc(s["conv_done"], 1)
        arrive(nc, K)
        finish(nc, K, lambda k, h, j: Wout[:, k, h * P:(h + 1) * P], block_of(Y), L3A_M)


EXPERTS = 8
INTER = 1024
IC = INTER // P
EW = DC * INTER
SLOT_TILES = (2 * TOK + EXPERTS * (P - 1)) // P
ROUND = 1.5 * 2.0 ** 23


def L3_ffn_layout(i):
    W1, W2 = np.asarray(i["L3_ffn_W1"]), np.asarray(i["L3_ffn_W2"])
    b1 = np.asarray(i["L3_ffn_b1"]).reshape(EXPERTS * IC, P).T
    return {"L3f_Wg": rows(np.asarray(i["L3_ffn_Wg"]).T), "L3f_W1": np.stack([rows(a) for a in W1]), "L3f_W2": np.stack([rows(a) for a in W2]),
            "L3f_b1": np.ascontiguousarray(b1), "L3f_b2": np.asarray(i["L3_ffn_b2"])}


def number_experts(nc, K, es, dst, n):
    ints = sbuf(es, nc, "ints", [P, n], I32)
    with phase(nc, K.sems, "counted") as (block, s):
        @block.gpsimd
        def _(pool):
            pool.iota(ints[:], pattern=[[1, n]], base=0, channel_multiplier=0).then_inc(s["counted"], 1)

        @block.vector
        def _(dve):
            dve.wait_ge(s["counted"], 1)
            dve.tensor_copy(dst, ints[:])


def L3_ffn(nc, K, w):
    xT = K.XT[K.cur]
    x_rows = nc.dram_tensor("L3f_x_rows", [TOK, D], F32, kind="Internal").ap()
    y_rows = nc.dram_tensor("L3f_y_rows", [SLOT_TILES * P, D], F32, kind="Internal").ap()
    weights_in = nc.alloc_semaphore("L3f_weights_in")
    with ExitStack() as es:
        slot = sbuf(es, nc, "slot_of_token", [P, 2, NT], U32)
        ew = sbuf(es, nc, "weights", [P, 4, NT])
        with ExitStack() as kept:
            W1 = sbuf(kept, nc, "W1", [P, EXPERTS * DC * INTER])
            W2 = sbuf(kept, nc, "W2", [P, EXPERTS * IC * D])
            b1 = sbuf(kept, nc, "b1", [P, EXPERTS * IC])
            token_at = sbuf(kept, nc, "token_at_slot", [P, SLOT_TILES], U32)
            w_at = sbuf(kept, nc, "weights_at", [P, 2, SLOT_TILES], I32)
            route_tokens(nc, K, w, xT, x_rows, W1, W2, b1, weights_in, slot, ew, token_at, w_at)
            run_experts(nc, K, x_rows, y_rows, W1, W2, b1, weights_in, token_at, w_at)

        GT = 4
        names = "gathered0 gathered1 gathered2 gathered3 stats_done std_done normed"
        with ExitStack() as inside, phase(nc, K.sems, names) as (block, s):
            gathered = [s["gathered0"], s["gathered1"], s["gathered2"], s["gathered3"]]
            Y = sbuf(inside, nc, "y_of_token", [P, NT, 2, D])
            st = sbuf(inside, nc, "ln_stats", [P, NT, 9])
            groups = [range(k, k + GT) for k in range(0, NT, GT)]

            @block.gpsimd
            def _(pool):
                for k, tiles in enumerate(groups):
                    for t in tiles:
                        for i in range(2):
                            pool.indirect_dma_start(out=Y[:, t, i, :], out_offset=None, in_=y_rows[:, :],
                                                    in_offset=bass.IndirectOffsetOnAxis(ap=slot[:, i, t:t + 1], axis=0)).then_inc(gathered[k], 16)

            @block.vector
            def _(dve):
                def normalise(k):
                    dve.wait_ge(s["std_done"], k + 1)
                    std = st[:, k * GT:(k + 1) * GT, 8:9]
                    dve.reciprocal(std, std)
                    dve.drain()
                    for t in groups[k]:
                        last = dve.tensor_scalar(K.Xtok[:, t, :], K.Xtok[:, t, :], st[:, t, 0:1], st[:, t, 8:9], ALU.subtract, ALU.mult)
                    last.then_inc(s["normed"], 1)

                for k, tiles in enumerate(groups):
                    dve.wait_ge(gathered[k], 16 * 2 * GT)
                    for i in range(2):
                        for t in tiles:
                            dve.scalar_tensor_tensor(out=K.Xtok[:, t, :], in0=Y[:, t, i, :], scalar=ew[:, 2 + i, t:t + 1], in1=K.Xtok[:, t, :],
                                                     op0=ALU.mult, op1=ALU.add)
                        dve.drain()
                    for t in tiles:
                        dve.bn_stats(st[:, t, 2:8], K.Xtok[:, t, :])
                    dve.drain()
                    for t in tiles:
                        last = dve.bn_aggr(st[:, t, 0:2], st[:, t, 2:8])
                    last.then_inc(s["stats_done"], 1)
                    normalise(k)

            @block.scalar
            def _(act):
                for k in range(len(groups)):
                    act.wait_ge(s["stats_done"], k + 1)
                    v = st[:, k * GT:(k + 1) * GT]
                    act.activation(v[:, :, 8:9], v[:, :, 1:2], ACT.Sqrt, bias=K.eps[:, 0:1]).then_inc(s["std_done"], 1)

            @block.sync
            def _(sp):
                rows_of = K.out.rearrange("b (t p) d -> p (b t) d", p=P)
                for k in range(len(groups)):
                    sp.wait_ge(s["normed"], k + 1)
                    sp.dma_start(rows_of[:, k * GT:(k + 1) * GT, :], K.Xtok[:, k * GT:(k + 1) * GT, :]).then_inc(K.stored, 16)
                sp.wait_ge(K.stored, 16 * len(groups))


def route_tokens(nc, K, w, xT, x_rows, W1, W2, b1, weights_in, slot, ew, token_at, w_at):
    PAIRS = 2 * NT
    with ExitStack() as es:
        Wg = sbuf(es, nc, "Wg", [P, DC, EXPERTS])
        b2 = sbuf(es, nc, "b2", [EXPERTS, D])
        ints = sbuf(es, nc, "integers", [P, P], I32)
        token_ints = sbuf(es, nc, "token_integers", [P, 2, NT], I32)
        num = sbuf(es, nc, "numbers", [P, P])
        place = sbuf(es, nc, "token_place", [P, 2, NT])
        L = sbuf(es, nc, "logits", [P, NT, EXPERTS])
        top = sbuf(es, nc, "top", [P, NT, 8])
        at = sbuf(es, nc, "top_index", [P, NT, 8], U32)
        atf = sbuf(es, nc, "top_index_f", [P, NT, 8])
        one = sbuf(es, nc, "one_hot", [P, 2, NT, EXPERTS])
        gates = sbuf(es, nc, "gates", [P, 2, NT, EXPERTS])
        chosen = sbuf(es, nc, "chosen", [P, NT, EXPERTS])
        upto = sbuf(es, nc, "chosen_up_to_tile", [P, 3, NT, EXPERTS])
        tiles = sbuf(es, nc, "tiles_of_expert", [P, 4, EXPERTS])
        sl = sbuf(es, nc, "slots", [P, 3, 2, NT])
        lo_hot = K.XT[1 - K.cur].rearrange("p c t -> p (c t)")[:, 0:PAIRS * P // 2].bitcast(BF16).rearrange("p (n j) -> p n j", j=P)
        hi_hot = sbuf(es, nc, "slot_tile_hot", [P, PAIRS, 2, SLOT_TILES], BF16)
        passed = sbuf(es, nc, "experts_passed", [P, SLOT_TILES, EXPERTS])
        found = sbuf(es, nc, "found", [P, 3, SLOT_TILES])
        gT = sbuf(es, nc, "gatesT", [EXPERTS, 2, P])
        names = "loaded x_stored counted scored ready exp_done gates_done mask_done ranked hot_done found turned turned_out bias_done bias_out"
        with phase(nc, K.sems, names) as (block, s):
            @block.sync
            def _(sp):
                sp.dma_start(Wg[:], w["L3f_Wg"]).then_inc(s["loaded"], 16)
                sp.dma_start(b2[:], w["L3f_b2"]).then_inc(s["loaded"], 16)
                sp.dma_start(x_rows.rearrange("(t p) d -> p t d", p=P), K.Xtok[:]).then_inc(s["x_stored"], 16)
                for e in range(EXPERTS):
                    sp.dma_start(W1[:, e * EW:(e + 1) * EW].rearrange("p (k n) -> p k n", k=DC), w["L3f_W1"][e]).then_inc(weights_in, 16)
                    sp.dma_start(W2[:, e * EW:(e + 1) * EW].rearrange("p (m n) -> p m n", m=IC), w["L3f_W2"][e]).then_inc(weights_in, 16)
                sp.dma_start(b1[:], w["L3f_b1"]).then_inc(weights_in, 16)

            @block.gpsimd
            def _(pool):
                pool.iota(ints[:], pattern=[[1, P]], base=0, channel_multiplier=0).then_inc(s["counted"], 1)
                pool.iota(token_ints[:, 0], pattern=[[1, NT]], base=0, channel_multiplier=0).then_inc(s["counted"], 1)
                pool.iota(token_ints[:, 1], pattern=[[0, NT]], base=0, channel_multiplier=1).then_inc(s["counted"], 1)

            @block.tensor
            def _(pe):
                pe.wait_ge(s["loaded"], 32)
                for t in range(NT):
                    for k in range(DC):
                        ins = pe.matmul(K.bank[0][:, t * EXPERTS:(t + 1) * EXPERTS], xT[:, k, t * P:(t + 1) * P], Wg[:, k, :], start=(k == 0), stop=(k == DC - 1))
                ins.then_inc(s["scored"], 1)
                pe.wait_ge(s["mask_done"], 1)
                m = chosen[:].rearrange("p t e -> p (t e)")
                pe.matmul(K.bank[5][:, 0:NT * EXPERTS], K.causal_T[:], m, start=True, stop=True)
                pe.matmul(K.bank[6][:, 0:NT * EXPERTS], K.ones[:, 0:P], m, start=True, stop=True).then_inc(s["ranked"], 1)
                pe.wait_ge(s["gates_done"], 1)
                for t in range(NT):
                    if t >= 2:
                        pe.wait_ge(s["turned_out"], t - 1)
                    pe.transpose(K.bank[1 + t % 2][0:EXPERTS, 0:P], gates[:, 0, t, :], K.ident[:]).then_inc(s["turned"], 1)
                    if t >= 2:
                        pe.wait_ge(s["bias_out"], t - 1)
                    pe.wait_ge(s["turned_out"], t + 1)
                    pe.matmul(K.bank[3 + t % 2][:, 0:D], gT[:, t % 2, :], b2[:], start=True, stop=True).then_inc(s["bias_done"], 1)
                pe.wait_ge(s["hot_done"], 1)
                for n in range(PAIRS):
                    ins = pe.matmul(K.bank[7][:, 0:2 * SLOT_TILES], lo_hot[:, n, :], hi_hot[:, n].rearrange("p a g -> p (a g)"),
                                    start=(n == 0), stop=(n == PAIRS - 1))
                ins.then_inc(s["found"], 1)

            @block.scalar
            def _(act):
                act.wait_ge(s["ready"], 1)
                act.activation(ew[:, 1, :], ew[:, 0, :], ACT.Exp).then_inc(s["exp_done"], 1)
                for t in range(NT):
                    act.wait_ge(s["turned"], t + 1)
                    if t >= 2:
                        act.wait_ge(s["bias_done"], t - 1)
                    act.activation(gT[:, t % 2, :], K.bank[1 + t % 2][0:EXPERTS, 0:P], ACT.Copy).then_inc(s["turned_out"], 1)

            @block.vector
            def _(dve):
                def step(f, *args):
                    f(*args)
                    dve.drain()

                dve.wait_ge(s["counted"], 3)
                dve.tensor_copy(num[:], ints[:])
                dve.tensor_copy(place[:], token_ints[:])
                dve.wait_ge(s["scored"], 1)
                step(dve.tensor_copy, L[:], K.bank[0][:, 0:NT * EXPERTS].rearrange("p (t e) -> p t e", e=EXPERTS))
                for t in range(NT):
                    dve.max(top[:, t, :], L[:, t, :])
                dve.drain()
                for t in range(NT):
                    dve.max_index(at[:, t, :], top[:, t, :], L[:, t, :])
                dve.tensor_tensor(ew[:, 0, :], top[:, :, 1], top[:, :, 0], ALU.subtract).then_inc(s["ready"], 1)
                dve.drain()
                step(dve.tensor_copy, atf[:], at[:])
                for i in range(2):
                    dve.tensor_tensor(one[:, i], middle(num[:, 0:EXPERTS], NT), inner(atf[:, :, i], EXPERTS), ALU.is_equal)
                dve.drain()
                dve.tensor_tensor(chosen[:], one[:, 0], one[:, 1], ALU.add).then_inc(s["mask_done"], 1)
                dve.wait_ge(s["exp_done"], 1)
                step(dve.tensor_scalar, ew[:, 2, :], ew[:, 1, :], 1.0, None, ALU.add)
                step(dve.reciprocal, ew[:, 2, :], ew[:, 2, :])
                step(dve.tensor_tensor, ew[:, 3, :], ew[:, 1, :], ew[:, 2, :], ALU.mult)
                for i in range(2):
                    dve.tensor_tensor(gates[:, i], one[:, i], inner(ew[:, 2 + i, :], EXPERTS), ALU.mult)
                dve.drain()
                dve.tensor_tensor(gates[:, 0], gates[:, 0], gates[:, 1], ALU.add).then_inc(s["gates_done"], 1)

                dve.wait_ge(s["ranked"], 1)
                total = upto[:, 2]
                dve.tensor_copy(total, K.bank[6][:, 0:NT * EXPERTS].rearrange("p (t e) -> p t e", e=EXPERTS))
                step(dve.tensor_copy, upto[:, 0], K.bank[6][:, 0:NT * EXPERTS].rearrange("p (t e) -> p t e", e=EXPERTS))
                a, d = 0, 1
                while d < NT:
                    dve.tensor_copy(upto[:, 1 - a, 0:d], upto[:, a, 0:d])
                    step(dve.tensor_tensor, upto[:, 1 - a, d:], upto[:, a, d:], upto[:, a, 0:NT - d], ALU.add)
                    a, d = 1 - a, 2 * d
                T, end = tiles[:, 3], upto[:, a]
                step(dve.tensor_scalar, T, end[:, NT - 1], P / 2 - 0.5, 1.0 / P, ALU.add, ALU.mult)
                step(dve.tensor_scalar, T, T, ROUND, None, ALU.add)
                step(dve.tensor_scalar, T, T, ROUND, None, ALU.subtract)
                step(dve.tensor_copy, tiles[:, 0], T)
                c, d = 0, 1
                while d < EXPERTS:
                    dve.tensor_copy(tiles[:, 1 - c, 0:d], tiles[:, c, 0:d])
                    step(dve.tensor_tensor, tiles[:, 1 - c, d:], tiles[:, c, d:], tiles[:, c, 0:EXPERTS - d], ALU.add)
                    c, d = 1 - c, 2 * d
                past, first = tiles[:, c], tiles[:, 2]
                step(dve.tensor_tensor, first, past, T, ALU.subtract)
                step(dve.tensor_scalar, first, first, float(P), -1.0, ALU.mult, ALU.add)
                step(dve.tensor_tensor, end, end, total, ALU.subtract)
                step(dve.tensor_tensor, end, end, middle(first, NT), ALU.add)
                step(dve.tensor_tensor, end, end, K.bank[5][:, 0:NT * EXPERTS].rearrange("p (t e) -> p t e", e=EXPERTS), ALU.add)
                for i in range(2):
                    dve.tensor_tensor(one[:, i], one[:, i], end, ALU.mult)
                dve.drain()
                for i in range(2):
                    dve.reduce_sum(sl[:, 0, i], one[:, i], AX)
                dve.drain()
                dve.tensor_copy(slot[:], sl[:, 0])
                hi, lo = sl[:, 1], sl[:, 2]
                step(dve.tensor_scalar, hi, sl[:, 0], -(P / 2 - 0.5), 1.0 / P, ALU.add, ALU.mult)
                step(dve.tensor_scalar, hi, hi, ROUND, None, ALU.add)
                step(dve.tensor_scalar, hi, hi, ROUND, None, ALU.subtract)
                step(dve.scalar_tensor_tensor, lo, hi, -float(P), sl[:, 0], ALU.mult, ALU.add)
                flat = lambda v: v.rearrange("p i t -> p (i t)")
                dve.tensor_tensor(lo_hot, middle(num[:], PAIRS), inner(flat(lo), P), ALU.is_equal)
                step(dve.tensor_tensor, hi_hot[:, :, 0], middle(num[:, 0:SLOT_TILES], PAIRS), inner(flat(hi), SLOT_TILES), ALU.is_equal)
                for i in range(2):
                    v = hi_hot[:, i * NT:(i + 1) * NT]
                    dve.tensor_tensor(v[:, :, 1], v[:, :, 0], inner(place[:, 1], SLOT_TILES), ALU.mult)
                dve.drain()
                for i in range(2):
                    v = hi_hot[:, i * NT:(i + 1) * NT]
                    ins = dve.tensor_tensor(v[:, :, 0], v[:, :, 0], inner(place[:, 0], SLOT_TILES), ALU.mult)
                ins.then_inc(s["hot_done"], 1)
                step(dve.tensor_tensor, passed[:], middle(past, SLOT_TILES), inner(num[:, 0:SLOT_TILES], EXPERTS), ALU.is_le)
                step(dve.reduce_sum, found[:, 2], passed[:, :, 0:EXPERTS - 1], AX)
                for i, width in enumerate((EW, IC)):
                    step(dve.tensor_scalar, found[:, i], found[:, 2], float(width), None, ALU.mult)
                dve.tensor_copy(w_at[:], found[:, 0:2])
                dve.wait_ge(s["x_stored"], 16)
                for t in range(NT):
                    dve.wait_ge(s["bias_done"], t + 1)
                    dve.tensor_tensor(K.Xtok[:, t, :], K.bank[3 + t % 2][:, 0:D], K.Xtok[:, t, :], ALU.add).then_inc(s["bias_out"], 1)
                dve.wait_ge(s["found"], 1)
                step(dve.tensor_copy, found[:, 0:2], K.bank[7][:, 0:2 * SLOT_TILES].rearrange("p (a g) -> p a g", a=2))
                step(dve.scalar_tensor_tensor, found[:, 0], found[:, 0], float(P), found[:, 1], ALU.mult, ALU.add)
                dve.tensor_copy(token_at[:], found[:, 0])


def run_experts(nc, K, x_rows, y_rows, W1, W2, b1, weights_in, token_at, w_at):
    HALF = IC // 2
    TURNS = SLOT_TILES // 3
    with ExitStack() as es:
        Xg = sbuf(es, nc, "x_gathered", [P, 3, D])
        XgT = sbuf(es, nc, "x_gatheredT", [P, 3, DC, P])
        H = K.XT[0][:, 0, 0:INTER]
        HT = K.XT[1][:, 0, 0:INTER].rearrange("p (m t) -> p m t", m=IC)
        Yt = sbuf(es, nc, "y", [P, 3, D])
        bt = sbuf(es, nc, "b1_of_tile", [P, 3, IC])
        names = "gathered0 gathered1 gathered2 stored0 stored1 stored2 x_turned x_out b_set h_done h_out turned gelu_done down_done y_out"
        with phase(nc, K.sems, names) as (block, s):
            gathered = [s["gathered0"], s["gathered1"], s["gathered2"]]
            stored = [s["stored0"], s["stored1"], s["stored2"]]

            @block.gpsimd
            def _(pool):
                for g in range(SLOT_TILES):
                    if g >= 3:
                        pool.wait_ge(s["x_turned"], g - 2)
                    pool.indirect_dma_start(out=Xg[:, g % 3, :], out_offset=None, in_=x_rows[:, :],
                                            in_offset=bass.IndirectOffsetOnAxis(ap=token_at[:, g:g + 1], axis=0)).then_inc(gathered[g % 3], 16)

            @block.sync
            def _(sp):
                for q in range(3):
                    sp.sem_inc(stored[q], 16)
                with sp.Fori(0, TURNS) as i:
                    for q in range(3):
                        sp.wait_ge(s["y_out"], i * 3 + q + 4)
                        sp.dma_start(y_rows[bass.ds(i * (3 * P) + q * P, P), :], Yt[:, q, :]).then_inc(stored[q], 16)
                for q in range(3):
                    sp.wait_ge(stored[q], 16 * (TURNS + 1))

            @block.tensor
            def _(pe):
                def expert(i, q):
                    return pe.value_load(w_at[0:1, 0, bass.ds(i * 3 + q, 1)], min_val=0, max_val=(EXPERTS - 1) * EW)

                def turn_x(i, q):
                    pe.wait_ge(gathered[q], i * 16 + 16)
                    pe.wait_ge(s["x_out"], i * 3 + q + 1)
                    for k in range(DC):
                        ins = pe.transpose(K.bank[7][:, k * P:(k + 1) * P], Xg[:, q, k * P:(k + 1) * P], K.ident[:])
                    ins.then_inc(s["x_turned"], 1)

                def up(i, q, part, at):
                    pe.wait_ge(s["x_out"], i * 3 + q + 2)
                    pe.wait_ge(s["h_out"], i * 6 + 2 * q + part + 1)
                    for k in range(DC):
                        ins = pe.matmul(K.bank[part][:], XgT[:, q, k, :], W1[:, bass.ds(at + (k * INTER + part * BLK), BLK)], start=(k == 0), stop=(k == DC - 1))
                    ins.then_inc(s["h_done"], 1)

                def turn_h(i, q, part):
                    pe.wait_ge(s["h_out"], i * 6 + 2 * q + part + 3)
                    pe.wait_ge(s["gelu_done"], i * 6 + 2 * q + part + 1)
                    for m in range(HALF):
                        c = part * HALF + m
                        ins = pe.transpose(K.bank[2 + part][:, m * P:(m + 1) * P], H[:, c * P:(c + 1) * P], K.ident[:])
                    ins.then_inc(s["turned"], 1)

                def down(i, q, at):
                    pe.wait_ge(s["y_out"], i * 3 + q + 1)
                    for c in range(IC):
                        if c % HALF == 0:
                            pe.wait_ge(s["gelu_done"], i * 6 + 2 * q + c // HALF + 3)
                        ins = pe.matmul(K.bank[4 + q][:, 0:D], HT[:, c, :], W2[:, bass.ds(at + c * D, D)], start=(c == 0), stop=(c == IC - 1))
                    ins.then_inc(s["down_done"], 1)

                def tile(i, q, ahead):
                    nq, ni = (q + 1) % 3, (i if q < 2 else i + 1)
                    at_next = expert(ni, nq) if ahead >= 1 else None
                    if ahead >= 1:
                        up(ni, nq, 0, at_next)
                    turn_h(i, q, 0)
                    if ahead >= 1:
                        up(ni, nq, 1, at_next)
                    turn_h(i, q, 1)
                    if ahead >= 2:
                        turn_x(i if q < 1 else i + 1, (q + 2) % 3)
                    down(i, q, expert(i, q))

                pe.sem_inc(s["turned"], 2)
                pe.sem_inc(s["down_done"], 1)
                turn_x(0, 0)
                pe.wait_ge(weights_in, 16 * (2 * EXPERTS + 1))
                at = expert(0, 0)
                for part in range(2):
                    up(0, 0, part, at)
                turn_x(0, 1)
                with pe.Fori(0, TURNS - 1) as i:
                    for q in range(3):
                        tile(i, q, 2)
                for q in range(3):
                    tile(TURNS - 1, q, 2 - q)

            @block.vector
            def _(dve):
                dve.sem_inc(s["x_out"], 1)
                dve.sem_inc(s["h_out"], 2)
                dve.sem_inc(s["y_out"], 3)

                def x_out(i, q):
                    dve.wait_ge(s["x_turned"], i * 3 + q + 1)
                    dve.tensor_copy(XgT[:, q], K.bank[7][:, 0:D].rearrange("p (k t) -> p k t", k=DC)).then_inc(s["x_out"], 1)

                def h_out(i, q, part):
                    dve.wait_ge(s["turned"], i * 6 + 2 * q + part + 1)
                    dve.wait_ge(s["h_done"], i * 6 + 2 * q + part + 1)
                    dve.tensor_copy(H[:, part * BLK:(part + 1) * BLK], K.bank[part][:]).then_inc(s["h_out"], 1)

                def hidden_out(i, q):
                    h_out(i, q, 0)
                    at = dve.value_load(w_at[0:1, 1, bass.ds(i * 3 + q, 1)], min_val=0, max_val=(EXPERTS - 1) * IC)
                    dve.tensor_scalar(bt[:, q], b1[:, bass.ds(at, IC)], 0.0, None, ALU.add).then_inc(s["b_set"], 1)
                    h_out(i, q, 1)

                def tile(i, q, ahead):
                    if ahead >= 1:
                        hidden_out(i if q < 2 else i + 1, (q + 1) % 3)
                    if ahead >= 2:
                        x_out(i if q < 1 else i + 1, (q + 2) % 3)
                    dve.wait_ge(s["down_done"], i * 3 + q + 2)
                    dve.wait_ge(stored[q], i * 16 + 16)
                    dve.tensor_copy(Yt[:, q], K.bank[4 + q][:, 0:D]).then_inc(s["y_out"], 1)

                x_out(0, 0)
                dve.wait_ge(weights_in, 16 * (2 * EXPERTS + 1))
                hidden_out(0, 0)
                x_out(0, 1)
                with dve.Fori(0, TURNS - 1) as i:
                    for q in range(3):
                        tile(i, q, 2)
                for q in range(3):
                    tile(TURNS - 1, q, 2 - q)

            @block.scalar
            def _(act):
                act.sem_inc(s["gelu_done"], 2)
                with act.Fori(0, TURNS) as i:
                    for q in range(3):
                        for part in range(2):
                            act.wait_ge(s["down_done"], i * 3 + q + 1)
                            act.wait_ge(s["b_set"], i * 3 + q + 1)
                            act.wait_ge(s["turned"], i * 6 + 2 * q + part + 3)
                            for m in range(HALF):
                                c = part * HALF + m
                                ins = act.activation(HT[:, c, :], K.bank[2 + part][:, m * P:(m + 1) * P], ACT.Gelu, bias=bt[:, q, c:c + 1])
                            ins.then_inc(s["gelu_done"], 1)


INNER = 1024
QCLIP = 1e-5


def L1_ffn_layout(i):
    return {"L1f_Wg": rows(np.asarray(i["L1_ffn_w_gate"]).T), "L1f_Wu": rows(np.asarray(i["L1_ffn_w_up"]).T),
            "L1f_Wd": rows(np.asarray(i["L1_ffn_w_down"]).T)}


def L1_ffn(nc, K, w):
    xT = K.XT[K.cur]
    n_w = INNER * D
    with ExitStack() as es:
        r = sbuf(es, nc, "sum", [P, NT, D])
        Wq = [sbuf(es, nc, f"W{n}_int", [P, n_w // P], BF16) for n in "gud"]
        wsc = sbuf(es, nc, "w_scale", [P, 3, 3])
        xsc = sbuf(es, nc, "x_scale", [P, NT, 3])
        XqT = sbuf(es, nc, "XqT", [P, DC, TOK], BF16)
        with ExitStack() as inside:
            W = [sbuf(inside, nc, f"W{n}", [P, n_w // P]) for n in "gud"]
            junk = sbuf(inside, nc, "junk", [P, n_w // P])
            tmp = sbuf(inside, nc, "x_scaled", [P, NT, D])
            xq = sbuf(inside, nc, "xq", [P, 2, D], BF16)
            minus_round = sbuf(inside, nc, "minus_round", [P, 1])
            with phase(nc, K.sems, "loaded summed total stepped constant quantised turned out") as (block, s):
                @block.sync
                def _(sp):
                    for i, n in enumerate(("L1f_Wg", "L1f_Wu", "L1f_Wd")):
                        sp.dma_start(W[i][:], w[n].rearrange("p c n -> p (c n)")).then_inc(s["loaded"], 16)

                @block.scalar
                def _(act):
                    act.wait_ge(s["loaded"], 48)
                    for i in range(3):
                        act.activation(junk[:], W[i][:], ACT.Abs, accum_out=wsc[:, i, 0:1]).then_inc(s["summed"], 1)
                        act.drain()
                    for t in range(NT):
                        act.wait_ge(s["turned"], t + 1)
                        act.activation(XqT[:, :, t * P:(t + 1) * P], K.bank[1 + t % 4][:].bitcast(BF16)[:, 0:D].rearrange("p (c k) -> p c k", c=2),
                                       ACT.Copy).then_inc(s["out"], 1)
                    act.wait_ge(s["constant"], 1)
                    for i in range(3):
                        act.wait_ge(s["stepped"], i + 1)
                        act.activation(Wq[i][:], W[i][:], ACT.Identity, bias=minus_round[:, 0:1])

                @block.tensor
                def _(pe):
                    for t in range(NT):
                        pe.wait_ge(s["quantised"], t + 1)
                        if t >= 4:
                            pe.wait_ge(s["out"], t - 3)
                        for h in range(DC):
                            ins = pe.transpose(K.bank[1 + t % 4][:].bitcast(BF16)[:, h * P:(h + 1) * P], xq[:, t % 2, h * P:(h + 1) * P], K.identb[:])
                        ins.then_inc(s["turned"], 1)
                    pe.wait_ge(s["summed"], 3)
                    pe.matmul(K.bank[0][:, 0:3], K.ones[:, 0:P], wsc[:, :, 0], start=True, stop=True).then_inc(s["total"], 1)

                @block.vector
                def _(dve):
                    big, inv, unit = (xsc[:, :, i] for i in range(3))
                    dve.tensor_reduce(big, K.Xtok[:], AX, ALU.max, apply_absolute_value=True)
                    dve.drain()
                    dve.tensor_scalar(big, big, QCLIP, None, ALU.max)
                    dve.drain()
                    dve.reciprocal(inv, big)
                    dve.tensor_scalar(unit, big, 1.0 / 127.0, None, ALU.mult)
                    dve.drain()
                    dve.tensor_scalar(inv, inv, 127.0, None, ALU.mult)
                    dve.drain()
                    for t in range(NT + 1):
                        if t < NT:
                            dve.tensor_scalar(tmp[:, t, :], K.Xtok[:, t, :], xsc[:, t, 1:2], ROUND, ALU.mult, ALU.add)
                        if t >= 1:
                            if t >= 3:
                                dve.wait_ge(s["turned"], t - 2)
                            dve.drain()
                            dve.tensor_scalar(xq[:, (t - 1) % 2, :], tmp[:, t - 1, :], ROUND, 127.0, ALU.subtract, ALU.min).then_inc(s["quantised"], 1)
                    dve.wait_ge(s["total"], 1)
                    dve.tensor_scalar(wsc[:, :, 1], K.bank[0][:, 0:3], 1.0 / n_w, QCLIP, ALU.mult, ALU.max)
                    dve.drain()
                    dve.reciprocal(wsc[:, :, 2], wsc[:, :, 1])
                    dve.drain()
                    for i in range(3):
                        dve.tensor_scalar(W[i][:], W[i][:], wsc[:, i, 2:3], 1.0, ALU.mult, ALU.min)
                        dve.drain()
                        dve.tensor_scalar(W[i][:], W[i][:], -1.0, ROUND, ALU.max, ALU.add).then_inc(s["stepped"], 1)

                @block.gpsimd
                def _(pool):
                    pool.memset(minus_round[:], -ROUND).then_inc(s["constant"], 1)
        Wg, Wu = (Wq[i][:].rearrange("p (c n) -> p c n", c=DC) for i in range(2))
        Wd = Wq[2][:].rearrange("p (c n) -> p c n", n=D)

        def quantise(dve, src, tmp, out, sc):
            dve.tensor_reduce(sc[:, 0:1], src, AX, ALU.max, apply_absolute_value=True)
            dve.drain()
            dve.tensor_scalar(sc[:, 0:1], sc[:, 0:1], QCLIP, None, ALU.max)
            dve.drain()
            dve.reciprocal(sc[:, 1:2], sc[:, 0:1])
            dve.tensor_scalar(sc[:, 2:3], sc[:, 0:1], 1.0 / 127.0, None, ALU.mult)
            dve.drain()
            dve.tensor_scalar(sc[:, 1:2], sc[:, 1:2], 127.0, None, ALU.mult)
            dve.drain()
            dve.tensor_scalar(tmp, src, sc[:, 1:2], ROUND, ALU.mult, ALU.add)
            dve.drain()
            return dve.tensor_scalar(out, tmp, ROUND, 127.0, ALU.subtract, ALU.min)

        gate = lambda t, c: K.bank[6 * (t % 2) + c]
        names = "scaled gate_done up_done silu_done h_done hq_done turned turned_out down_done sum_done"
        with phase(nc, K.sems, names) as (block, s):
            hsc = sbuf(es, nc, "h_scale", [P, 2, 4])
            G = sbuf(es, nc, "gate", [P, 2, INNER])
            H = sbuf(es, nc, "h", [P, INNER])
            Hq = sbuf(es, nc, "hq", [P, 2, INNER], BF16)
            HqT = sbuf(es, nc, "hqT", [P, 2, INNER // P, P], BF16)
            wscale = sbuf(es, nc, "both_scales", [P, NT, 2])

            @block.tensor
            def _(pe):
                def inner_product(t, part):
                    if part == 0 and t >= 2:
                        pe.wait_ge(s["silu_done"], t - 1)
                    if part == 1 and t >= 1:
                        pe.wait_ge(s["h_done"], t)
                    for c in range(2):
                        for k in range(DC):
                            ins = pe.matmul((gate(t, c), K.bank[2 + c])[part][:], XqT[:, k, t * P:(t + 1) * P], (Wg, Wu)[part][:, k, c * BLK:(c + 1) * BLK],
                                            start=(k == 0), stop=(k == DC - 1))
                    ins.then_inc((s["gate_done"], s["up_done"])[part], 1)

                for part in range(2):
                    inner_product(0, part)
                for t in range(NT):
                    if t + 1 < NT:
                        for part in range(2):
                            inner_product(t + 1, part)
                    pe.wait_ge(s["hq_done"], t + 1)
                    if t >= 1:
                        pe.wait_ge(s["turned_out"], t)
                    for m in range(INNER // P):
                        ins = pe.transpose(K.bank[4][:].bitcast(BF16)[:, m * P:(m + 1) * P], Hq[:, t % 2, m * P:(m + 1) * P], K.identb[:])
                    ins.then_inc(s["turned"], 1)
                    pe.wait_ge(s["turned_out"], t + 1)
                    if t >= 1:
                        pe.wait_ge(s["sum_done"], t)
                    for m in range(INNER // P):
                        ins = pe.matmul(K.bank[5][:, 0:D], HqT[:, t % 2, m, :], Wd[:, m, :], start=(m == 0), stop=(m == INNER // P - 1))
                    ins.then_inc(s["down_done"], 1)

            @block.scalar
            def _(act):
                act.wait_ge(s["scaled"], 1)
                for t in range(NT + 1):
                    if t < NT:
                        act.wait_ge(s["gate_done"], t + 1)
                        if t >= 2:
                            act.wait_ge(s["h_done"], t - 1)
                        for c in range(2):
                            ins = act.activation(G[:, t % 2, c * BLK:(c + 1) * BLK], gate(t, c)[:], ACT.Silu, scale=wscale[:, t, 0:1])
                        ins.then_inc(s["silu_done"], 1)
                    if t > 0:
                        act.wait_ge(s["turned"], t)
                        if t >= 3:
                            act.wait_ge(s["down_done"], t - 2)
                        act.activation(HqT[:, (t - 1) % 2].rearrange("p m k -> p (m k)"), K.bank[4][:].bitcast(BF16)[:, 0:INNER],
                                       ACT.Copy).then_inc(s["turned_out"], 1)

            @block.vector
            def _(dve):
                for i in range(2):
                    dve.tensor_scalar(wscale[:, :, i], xsc[:, :, 2], wsc[:, i, 1:2], None, ALU.mult)
                dve.drain()
                dve.sem_inc(s["scaled"], 1)

                def total(t):
                    dve.wait_ge(s["down_done"], t + 1)
                    dve.scalar_tensor_tensor(out=r[:, t, :], in0=K.bank[5][:, 0:D], scalar=hsc[:, t % 2, 3:4], in1=K.Xtok[:, t, :],
                                             op0=ALU.mult, op1=ALU.add).then_inc(s["sum_done"], 1)

                for t in range(NT):
                    dve.wait_ge(s["silu_done"], t + 1)
                    dve.wait_ge(s["up_done"], t + 1)
                    for c in range(2):
                        ins = dve.scalar_tensor_tensor(out=H[:, c * BLK:(c + 1) * BLK], in0=K.bank[2 + c][:], scalar=wscale[:, t, 1:2],
                                                       in1=G[:, t % 2, c * BLK:(c + 1) * BLK], op0=ALU.mult, op1=ALU.mult)
                    ins.then_inc(s["h_done"], 1)
                    dve.drain()
                    if t >= 2:
                        dve.wait_ge(s["turned"], t - 1)
                    quantise(dve, H[:], H[:], Hq[:, t % 2, :], hsc[:, t % 2, :]).then_inc(s["hq_done"], 1)
                    dve.tensor_scalar(hsc[:, t % 2, 3:4], hsc[:, t % 2, 2:3], wsc[:, 2, 1:2], None, ALU.mult)
                    dve.drain()
                    if t >= 1:
                        total(t - 1)
                total(NT - 1)
        finish_tokens(nc, K, r)


def L2_attn_layout(i):
    W = np.asarray(i["L2_attn_W_qkv"]).T
    return {"L2a_W": rows(W), "L2a_Wo": rows(np.asarray(i["L2_attn_W_out"]).T)}


def L2_attn(nc, K, w):
    xT = K.XT[K.cur]
    NQ = 2 * DC
    with ExitStack() as es:
        Wo = sbuf(es, nc, "Wo", [P, DC, D])
        OT = sbuf(es, nc, "OT", [P, DC, TOK])
        with ExitStack() as inside:
            W = sbuf(inside, nc, "Wqkv", [P, DC, 3 * D])
            QT, KT, RT = (sbuf(inside, nc, n, [P, DC, TOK]) for n in ("QT", "KT", "recip_den"))
            same = sbuf(inside, nc, "same_head", [P, P])
            load(nc, K, (W[:], w["L2a_W"]), later=((Wo[:], w["L2a_Wo"]),))
            with ExitStack() as inn, phase(nc, K.sems, "done min_done exp_done out") as (block, s):
                low = sbuf(inn, nc, "low", [P, 2, BLK])
                steps = [(m, j) for m in range(NQ) for j in range(NB)]

                @block.tensor
                def _(pe):
                    for n, (m, j) in enumerate(steps):
                        if n >= 8:
                            pe.wait_ge(s["out"], n - 7)
                        for k in range(DC):
                            ins = pe.matmul(K.bank[n % 8][:], W[:, k, m * P:(m + 1) * P], xT[:, k, j * BLK:(j + 1) * BLK], start=(k == 0), stop=(k == DC - 1))
                        ins.then_inc(s["done"], 1)

                @block.vector
                def _(dve):
                    dve.tensor_copy(same[:].rearrange("p (h d) -> p h d", d=HD), inner(K.head_rows[:], HD))
                    for n in range(len(steps) + 1):
                        if n < len(steps):
                            dve.wait_ge(s["done"], n + 1)
                            if n >= 2:
                                dve.drain()
                            dve.tensor_scalar(low[:, n % 2, :], K.bank[n % 8][:], 0.0, None, ALU.min).then_inc(s["min_done"], 1)
                        if n > 0:
                            m, j = steps[n - 1]
                            dve.wait_ge(s["exp_done"], n)
                            dst = (QT if m < DC else KT)[:, m % DC, j * BLK:(j + 1) * BLK]
                            dve.scalar_tensor_tensor(out=dst, in0=K.bank[(n - 1) % 8][:], scalar=0.0, in1=low[:, (n - 1) % 2, :],
                                                     op0=ALU.max, op1=ALU.add)
                            dve.drain()
                            if m < DC:
                                dve.tensor_scalar(dst, dst, float(HD) ** -0.5, None, ALU.mult).then_inc(s["out"], 1)
                            else:
                                dve.sem_inc(s["out"], 1)

                @block.scalar
                def _(act):
                    for n in range(len(steps)):
                        act.wait_ge(s["min_done"], n + 1)
                        act.activation(low[:, n % 2, :], low[:, n % 2, :], ACT.Exp).then_inc(s["exp_done"], 1)

            with ExitStack() as inn, phase(nc, K.sems, "prod_done den_done recip_done") as (block, s):
                run = sbuf(inn, nc, "running", [P, DC, TOK])
                none = sbuf(inn, nc, "zeros", [P, S])

                @block.vector
                def _(dve):
                    dve.memset(none[:], 0.0)
                    dve.drain()
                    for c in range(DC):
                        for b in range(B):
                            dve.tensor_tensor_scan(run[:, c, b * S:(b + 1) * S], KT[:, c, b * S:(b + 1) * S], none[:], 0.0, ALU.add, ALU.add)
                    dve.drain()
                    for c in range(DC):
                        for j in range(NB):
                            z = run[:, c, j * BLK:(j + 1) * BLK]
                            dve.tensor_tensor(z, z, QT[:, c, j * BLK:(j + 1) * BLK], ALU.mult).then_inc(s["prod_done"], 1)
                    for n in range(DC * NB):
                        c, j = divmod(n, NB)
                        z = RT[:, c, j * BLK:(j + 1) * BLK]
                        dve.wait_ge(s["den_done"], n + 1)
                        dve.tensor_scalar(z, K.bank[n][:], 1e-6, None, ALU.max)
                        dve.drain()
                        dve.reciprocal(z, z)

                @block.tensor
                def _(pe):
                    for n in range(DC * NB):
                        c, j = divmod(n, NB)
                        pe.wait_ge(s["prod_done"], n + 1)
                        pe.matmul(K.bank[n][:], same[:], run[:, c, j * BLK:(j + 1) * BLK], start=True, stop=True).then_inc(s["den_done"], 1)

            Qh = sbuf(inside, nc, "Q_heads", [P, 2, HPC, P])
            Vh = sbuf(inside, nc, "V_heads", [P, 2, HPC, P])
            AT = sbuf(inside, nc, "attnT", [P, 2, HPC, P])
            kv = sbuf(inside, nc, "k_v_tokens", [P, 2, 2 * P])
            St = sbuf(inside, nc, "state", [P, P])
            with phase(nc, K.sems, "q_spread kv_done kv_out v_spread attn_done attn_out state_out o_done out") as (block, s):
                steps = NT * DC
                attn = lambda n, g: K.bank[6 * (n % 2) + g][:]

                @block.tensor
                def _(pe):
                    def prepare(n):
                        t, c = divmod(n, DC)
                        ts = slice(t * P, (t + 1) * P)
                        if n >= 1:
                            pe.wait_ge(s["kv_out"], n)
                        for k in range(DC):
                            pe.matmul(K.bank[2][:, 0:P], xT[:, k, ts], W[:, k, 2 * D + c * P:2 * D + (c + 1) * P], start=(k == 0), stop=(k == DC - 1))
                        pe.transpose(K.bank[2][:, P:2 * P], KT[:, c, ts], K.ident[:]).then_inc(s["kv_done"], 1)
                        pe.wait_ge(s["q_spread"], n + 1)
                        if n >= 2:
                            pe.wait_ge(s["attn_out"], n - 1)
                        for g in range(2):
                            ins = pe.matmul(attn(n, g), KT[:, c, ts], Qh[:, n % 2, 4 * g:4 * g + 4, :], start=True, stop=True)
                        ins.then_inc(s["attn_done"], 1)

                    prepare(0)
                    for n in range(steps):
                        t, c = divmod(n, DC)
                        ts = slice(t * P, (t + 1) * P)
                        if n + 1 < steps:
                            prepare(n + 1)
                        if n >= 1:
                            pe.wait_ge(s["out"], n)
                        first = t % 8 == 0
                        pe.wait_ge(s["state_out"], n + 1)
                        if not first:
                            pe.matmul(K.bank[3][:, 0:P], St[:], QT[:, c, ts], start=True, stop=False)
                        pe.wait_ge(s["v_spread"], n + 1)
                        pe.wait_ge(s["attn_out"], n + 1)
                        for h in range(HPC):
                            ins = pe.matmul(K.bank[3][:, 0:P], Vh[:, n % 2, h, :], AT[:, n % 2, h, :], start=(first and h == 0), stop=(h == HPC - 1))
                        ins.then_inc(s["o_done"], 1)
                        pe.matmul(K.bank[4 + c][:, 0:P], kv[:, n % 2, P:2 * P], kv[:, n % 2, 0:P], start=first, stop=True, skip_group_check=True)

                @block.scalar
                def _(act):
                    for n in range(steps):
                        act.wait_ge(s["kv_done"], n + 1)
                        act.activation(kv[:, n % 2, :], K.bank[2][:, 0:2 * P], ACT.Copy).then_inc(s["kv_out"], 1)

                @block.gpsimd
                def _(pool):
                    for n in range(steps):
                        pool.wait_ge(s["kv_out"], n + 1)
                        if n >= 2:
                            pool.wait_ge(s["o_done"], n - 1)
                        pool.tensor_tensor(Vh[:, n % 2], middle(kv[:, n % 2, 0:P], HPC), K.head_cols[:], ALU.mult).then_inc(s["v_spread"], 1)

                @block.vector
                def _(dve):
                    def spread_q(n):
                        t, c = divmod(n, DC)
                        if n >= 2:
                            dve.wait_ge(s["attn_done"], n - 1)
                        dve.tensor_tensor(Qh[:, n % 2], middle(QT[:, c, t * P:(t + 1) * P], HPC), inner(K.head_rows[:], P), ALU.mult).then_inc(s["q_spread"], 1)

                    def output(n):
                        t, c = divmod(n, DC)
                        dve.wait_ge(s["o_done"], n + 1)
                        dve.tensor_tensor(OT[:, c, t * P:(t + 1) * P], K.bank[3][:, 0:P], RT[:, c, t * P:(t + 1) * P], ALU.mult).then_inc(s["out"], 1)

                    spread_q(0)
                    for n in range(steps):
                        t, c = divmod(n, DC)
                        if n + 1 < steps:
                            spread_q(n + 1)
                        dve.wait_ge(s["attn_done"], n + 1)
                        if n >= 2:
                            dve.wait_ge(s["o_done"], n - 1)
                        for g in range(2):
                            ins = dve.tensor_tensor(AT[:, n % 2, 4 * g:4 * g + 4, :], attn(n, g).rearrange("p (h l) -> p h l", h=4), middle(K.causal_T[:], 4), ALU.mult)
                        ins.then_inc(s["attn_out"], 1)
                        if n >= 1:
                            output(n - 1)
                        if t % 8 == 0:
                            dve.sem_inc(s["state_out"], 1)
                        else:
                            dve.tensor_tensor(St[:], K.bank[4 + c][:, 0:P], same[:], ALU.mult).then_inc(s["state_out"], 1)
                    output(steps - 1)
        arrive(nc, K)
        finish(nc, K, lambda k, h, j: Wo[:, k, h * P:(h + 1) * P], block_of(OT), DC)


def block_mean(nc, K, out, size):
    with phase(nc, K.sems, "step") as (block, s):
        @block.gpsimd
        def _(pool):
            n = P // size
            pool.memset(out, 1.0 / size).then_inc(s["step"], 1)
            v = out.rearrange("p (n j) -> p n j", n=n)
            pool.wait_ge(s["step"], 1)
            pool.affine_select(out=v, in_=v, compare_op=ALU.is_ge, fill=0.0, base=0, pattern=[[-size, n], [0, size]], channel_multiplier=1).then_inc(s["step"], 1)
            pool.wait_ge(s["step"], 2)
            pool.affine_select(out=v, in_=v, compare_op=ALU.is_ge, fill=0.0, base=size - 1, pattern=[[size, n], [0, size]], channel_multiplier=-1)


def feature_ln(nc, K, J, n, halves_, src, dst, g, b):
    with ExitStack() as es, phase(nc, K.sems, "mean_done centred squared var_done std_done normed out") as (block, s):
        sq = sbuf(es, nc, "squares", [P, 2, halves_, BLK])
        std = sbuf(es, nc, "std", [P, 2, BLK])
        xc = sbuf(es, nc, "centred", [P, 2, halves_, BLK])

        @block.tensor
        def _(pe):
            def mean(j):
                if j >= 2:
                    pe.wait_ge(s["centred"], j - 1)
                for h in range(halves_):
                    ins = pe.matmul(K.bank[j % 2][:], J, src(j, h), start=(h == 0), stop=(h == halves_ - 1))
                ins.then_inc(s["mean_done"], 1)
            mean(0)
            for j in range(n):
                if j + 1 < n:
                    mean(j + 1)
                pe.wait_ge(s["squared"], j + 1)
                if j >= 2:
                    pe.wait_ge(s["std_done"], j - 1)
                for h in range(halves_):
                    ins = pe.matmul(K.bank[2 + j % 2][:], J, sq[:, j % 2, h, :], start=(h == 0), stop=(h == halves_ - 1))
                ins.then_inc(s["var_done"], 1)

        @block.vector
        def _(dve):
            def centre(j):
                dve.wait_ge(s["mean_done"], j + 1)
                if j >= 2:
                    dve.wait_ge(s["out"], j - 1)
                for h in range(halves_):
                    ins = dve.tensor_tensor(xc[:, j % 2, h, :], src(j, h), K.bank[j % 2][:], ALU.subtract)
                ins.then_inc(s["centred"], 1)
            centre(0)
            for j in range(n):
                if j + 1 < n:
                    centre(j + 1)
                dve.wait_ge(s["std_done"], j + 1)
                dve.reciprocal(std[:, j % 2, :], std[:, j % 2, :])
                dve.drain()
                for h in range(halves_):
                    ins = dve.tensor_tensor(xc[:, j % 2, h, :], xc[:, j % 2, h, :], std[:, j % 2, :], ALU.mult)
                ins.then_inc(s["normed"], 1)

        @block.scalar
        def _(act):
            def square(j):
                act.wait_ge(s["centred"], j + 1)
                if j >= 2:
                    act.wait_ge(s["var_done"], j - 1)
                for h in range(halves_):
                    ins = act.activation(sq[:, j % 2, h, :], xc[:, j % 2, h, :], ACT.Square)
                ins.then_inc(s["squared"], 1)
            square(0)
            for j in range(n):
                if j + 1 < n:
                    square(j + 1)
                act.wait_ge(s["var_done"], j + 1)
                if j >= 2:
                    act.wait_ge(s["normed"], j - 1)
                act.activation(std[:, j % 2, :], K.bank[2 + j % 2][:], ACT.Sqrt, bias=K.eps[:, 0:1]).then_inc(s["std_done"], 1)
                act.wait_ge(s["normed"], j + 1)
                for h in range(halves_):
                    ins = act.activation(dst(j, h), xc[:, j % 2, h, :], ACT.Identity, scale=g(j)[:, h:h + 1], bias=b(j)[:, h:h + 1])
                ins.then_inc(s["out"], 1)


def feature_ln_rows(nc, K, J, n, halves_, src, dst, g, b):
    with ExitStack() as es, phase(nc, K.sems, "prepared mean_done centred squared var_done std_done recip_done spread normed out") as (block, s):
        sq = sbuf(es, nc, "squares", [P, 2, halves_, BLK])
        std = sbuf(es, nc, "std", [P, BLK])
        wide = sbuf(es, nc, "averaging_column", [P, 2 * n - 1])

        @block.gpsimd
        def _(pool):
            pool.memset(std[:], 0.0).then_inc(s["prepared"], 1)
            pool.memset(wide[:], 0.0).then_inc(s["prepared"], 1)
            pool.wait_ge(s["prepared"], 2)
            pool.tensor_copy(wide[:, n - 1:n], J[:, 0:1]).then_inc(s["prepared"], 1)

        @block.tensor
        def _(pe):
            def mean(j):
                if j >= 2:
                    pe.wait_ge(s["centred"], j - 1)
                for h in range(halves_):
                    ins = pe.matmul(K.bank[j % 2][:], J, src(j, h), start=(h == 0), stop=(h == halves_ - 1))
                ins.then_inc(s["mean_done"], 1)
            mean(0)
            mean(1)
            pe.wait_ge(s["prepared"], 3)
            for j in range(n):
                if j + 2 < n:
                    mean(j + 2)
                pe.wait_ge(s["squared"], j + 1)
                for h in range(halves_):
                    ins = pe.matmul(K.bank[2][0:n, :], wide[:, n - 1 - j:2 * n - 1 - j], sq[:, j % 2, h, :], start=(j == 0 and h == 0),
                                    stop=(j == n - 1 and h == halves_ - 1))
                ins.then_inc(s["var_done"], 1)
            pe.wait_ge(s["recip_done"], 1)
            for j in range(n):
                if j >= 4:
                    pe.wait_ge(s["normed"], j - 3)
                pe.matmul(K.bank[4 + j % 4][:], K.ident[:, j:j + 1].broadcast_to((P, P)), std[:], start=True, stop=True).then_inc(s["spread"], 1)

        @block.vector
        def _(dve):
            for j in range(n):
                dve.wait_ge(s["mean_done"], j + 1)
                for h in range(halves_):
                    ins = dve.tensor_tensor(dst(j, h), src(j, h), K.bank[j % 2][:], ALU.subtract)
                ins.then_inc(s["centred"], 1)
            dve.wait_ge(s["std_done"], 1)
            dve.reciprocal(std[0:n, :], std[0:n, :]).then_inc(s["recip_done"], 1)
            for j in range(n):
                dve.wait_ge(s["spread"], j + 1)
                for h in range(halves_):
                    ins = dve.tensor_tensor(dst(j, h), dst(j, h), K.bank[4 + j % 4][:], ALU.mult)
                ins.then_inc(s["normed"], 1)

        @block.scalar
        def _(act):
            for j in range(n):
                act.wait_ge(s["centred"], j + 1)
                if j >= 2:
                    act.wait_ge(s["var_done"], j - 1)
                for h in range(halves_):
                    ins = act.activation(sq[:, j % 2, h, :], dst(j, h), ACT.Square)
                ins.then_inc(s["squared"], 1)
            act.wait_ge(s["var_done"], n)
            act.wait_ge(s["prepared"], 1)
            act.activation(std[0:n, :], K.bank[2][0:n, :], ACT.Sqrt, bias=K.eps[0:n, 0:1]).then_inc(s["std_done"], 1)
            for j in range(n):
                act.wait_ge(s["normed"], j + 1)
                for h in range(halves_):
                    act.activation(dst(j, h), dst(j, h), ACT.Identity, scale=g(j)[:, h:h + 1], bias=b(j)[:, h:h + 1])


LAT = D // 4


def L1_attn_layout(i):
    g = lambda n: np.asarray(i["L1_attn_" + n])
    uq = pad(g("W_uq"), 0, P)
    ukv = np.concatenate([np.zeros((LAT, 2 * D), np.float32), g("W_ukv")])
    return {"L1a_Wd": rows(np.concatenate([g("W_dq"), g("W_dkv")], axis=1)), "L1a_uq": uq, "L1a_ukv": ukv,
            "L1a_g": np.concatenate([g("q_ln_g"), g("kv_ln_g")]).reshape(P, 1), "L1a_b": np.concatenate([g("q_ln_b"), g("kv_ln_b")]).reshape(P, 1),
            "L1a_Wo": rows(g("W_o").T)}


def L1_attn(nc, K, w):
    xT = K.XT[K.cur]
    QT_ = S // P
    with ExitStack() as es:
        Wo = sbuf(es, nc, "Wo", [P, DC, D])
        OT = sbuf(es, nc, "OT", [P, DC * TOK])
        with ExitStack() as inside:
            QT, KT = (sbuf(inside, nc, n, [P, DC * TOK]) for n in ("QT", "KT"))
            V = sbuf(inside, nc, "V", [P, DC, NT, P])
            with ExitStack() as inn:
                Wd = sbuf(inn, nc, "Wd", [P, DC, P])
                uq = sbuf(inn, nc, "uq", [P, D])
                ukv = sbuf(inn, nc, "ukv", [P, 2 * D])
                g, b = (sbuf(inn, nc, n, [P, 1]) for n in ("g", "b"))
                cT = sbuf(inn, nc, "latents", [P, TOK])
                J = sbuf(inn, nc, "J", [P, P])
                load(nc, K, (Wd[:], w["L1a_Wd"]),
                     later=((uq[:], w["L1a_uq"]), (ukv[:], w["L1a_ukv"]), (g[:], w["L1a_g"]), (b[:], w["L1a_b"]), (Wo[:], w["L1a_Wo"])))
                block_mean(nc, K, J[:], LAT)
                cb = lambda j: cT[:, j * BLK:(j + 1) * BLK]
                project(nc, K, inn, 1, DC, lambda k, m: Wd[:, k, :], block_of(xT), *copy_to(lambda m, j: cb(j)))
                arrive(nc, K)
                feature_ln(nc, K, J[:], NB, 1, lambda j, h: cb(j), lambda j, h: cb(j), lambda j: g[:], lambda j: b[:])
                for dst, W in ((QT, uq), (KT, ukv)):
                    project(nc, K, inn, DC, 1, lambda k, m: W[:, m * P:(m + 1) * P], lambda k, j: cb(j),
                            *copy_to(lambda m, j: dst[:, m * TOK + j * BLK:m * TOK + (j + 1) * BLK]))
                with phase(nc, K.sems, "done out") as (block, s):
                    @block.tensor
                    def _(pe):
                        for t in range(NT):
                            if t >= 8:
                                pe.wait_ge(s["out"], t - 7)
                            pe.matmul(K.bank[t % 8][:, 0:D], cT[:, t * P:(t + 1) * P], ukv[:, D:2 * D], start=True, stop=True).then_inc(s["done"], 1)

                    @block.vector
                    def _(dve):
                        for t in range(NT):
                            dve.wait_ge(s["done"], t + 1)
                            dve.tensor_copy(V[:, :, t, :], K.bank[t % 8][:, 0:D].rearrange("p (c k) -> p c k", c=DC)).then_inc(s["out"], 1)

            Vh = sbuf(inside, nc, "V_heads", [P, QT_, HPC, P])
            Qh = sbuf(inside, nc, "Q_heads", [P, 2, HPC, P])
            Sc = sbuf(inside, nc, "scores", [P, 2, S])
            zero = sbuf(inside, nc, "zero_marks", [P, S])
            PT = sbuf(inside, nc, "probsT", [P, 2, S])
            mx = sbuf(inside, nc, "max", [P, 2])
            sums = sbuf(inside, nc, "sums", [P, 2, HPC])
            rec = sbuf(inside, nc, "recip", [P, HPC])
            Rx, RT = (sbuf(inside, nc, n, [P, 2, P]) for n in ("recip_spread", "recipT"))
            scale = float(HD) ** -0.5
            N = QT_ * HPC
            names = "q_spread scored max_done exp_done turned pt_out v_spread r_spread pv_done o_done rt_out out"
            with phase(nc, K.sems, names) as (block, s):
                sc = lambda i: K.psum[:, 2 * (i % 2):2 * (i % 2) + 2, :].rearrange("p b k -> p (b k)")
                ob = lambda q: K.bank[6 + q % 2]

                def slot_free(eng, sem, u, per, i):
                    if i >= 2:
                        eng.wait_ge(sem, u * per + i - 1)

                def turn_over(eng, u, *pairs):
                    for sem, per in pairs:
                        eng.wait_ge(sem, u * per + per)

                @block.gpsimd
                def _(pool):
                    with pool.Fori(0, DC * B) as u:
                        for kt in range(QT_):
                            src = V[:].rearrange("p c t k -> p (c t k)")[:, bass.ds(u * (QT_ * P) + kt * P, P)]
                            pool.tensor_tensor(Vh[:, kt], middle(src, HPC), K.head_cols[:], ALU.mult).then_inc(s["v_spread"], 1)
                        turn_over(pool, u, (s["pv_done"], N))

                @block.tensor
                def _(pe):
                    with pe.Fori(0, DC * B) as u:
                        def score(i):
                            q, h = divmod(i, HPC)
                            if h == 0:
                                pe.wait_ge(s["q_spread"], u * QT_ + q + 1)
                            slot_free(pe, s["max_done"], u, N, i)
                            n = (q + 1) * P
                            for o in range(0, n, BLK):
                                e = min(n, o + BLK)
                                pe.matmul(sc(i)[:, o:e], Qh[:, q % 2, h, :], KT[:, bass.ds(u * S + o, e - o)], start=True, stop=(e < n),
                                          skip_group_check=True)
                            pe.matmul(sc(i)[:, n - P:n], K.identb[:], K.above[:], start=False, stop=True, skip_group_check=True).then_inc(s["scored"], 1)

                        def values(i):
                            q, h = divmod(i, HPC)
                            pe.wait_ge(s["pt_out"], u * N + i + 1)
                            if h == 0:
                                pe.wait_ge(s["v_spread"], u * QT_ + q + 1)
                                slot_free(pe, s["out"], u, QT_, q)
                            for kt in range(q + 1):
                                ins = pe.matmul(ob(q)[:, 0:P], Vh[:, kt, h, :], PT[:, i % 2, kt * P:(kt + 1) * P], start=(h == 0 and kt == 0),
                                                stop=(h == HPC - 1 and kt == q))
                            ins.then_inc(s["pv_done"], 1)
                            if h == HPC - 1:
                                pe.wait_ge(s["r_spread"], u * QT_ + q + 1)
                                pe.transpose(ob(q)[:, P:2 * P], Rx[:, q % 2, :], K.ident[:]).then_inc(s["o_done"], 1)

                        score(0)
                        for i in range(N):
                            if i + 1 < N:
                                score(i + 1)
                            pe.wait_ge(s["exp_done"], u * N + i + 1)
                            if i > 0:
                                pe.wait_ge(s["pt_out"], u * N + i)
                            for kt in range(i // HPC + 1):
                                ins = pe.transpose(K.bank[4 + kt // 4][:, (kt % 4) * P:(kt % 4 + 1) * P], Sc[:, i % 2, kt * P:(kt + 1) * P], K.ident[:])
                            ins.then_inc(s["turned"], 1)
                            if i > 0:
                                values(i - 1)
                        values(N - 1)
                        turn_over(pe, u, (s["max_done"], N), (s["out"], QT_))

                @block.vector
                def _(dve):
                    with dve.Fori(0, DC * B) as u:
                        def spread(q):
                            if q >= 2:
                                dve.wait_ge(s["scored"], u * N + (q - 1) * HPC)
                            dve.tensor_tensor(Qh[:, q % 2], middle(QT[:, bass.ds(u * S + q * P, P)], HPC), inner(K.head_rows[:], P), ALU.mult).then_inc(s["q_spread"], 1)

                        def output(q):
                            dve.wait_ge(s["rt_out"], u * QT_ + q + 1)
                            dve.tensor_tensor(OT[:, bass.ds(u * S + q * P, P)], ob(q)[:, 0:P], RT[:, q % 2, :], ALU.mult).then_inc(s["out"], 1)

                        def recip(q):
                            dve.wait_ge(s["exp_done"], u * N + (q + 1) * HPC)
                            slot_free(dve, s["o_done"], u, QT_, q)
                            dve.reciprocal(rec[:], sums[:, q % 2, :])
                            dve.drain()
                            dve.tensor_copy(Rx[:, q % 2, :].rearrange("p (h d) -> p h d", h=HPC), inner(rec[:], HD)).then_inc(s["r_spread"], 1)

                        spread(0)
                        for i in range(N):
                            q, h = divmod(i, HPC)
                            n = (q + 1) * P
                            if h == 2 and q + 1 < QT_:
                                spread(q + 1)
                            slot_free(dve, s["turned"], u, N, i)
                            dve.wait_ge(s["scored"], u * N + i + 1)
                            dve.tensor_scalar(zero[:, 0:n], sc(i)[:, 0:n], 0.0, NEG, ALU.is_equal, ALU.mult)
                            dve.drain()
                            dve.tensor_tensor_reduce(Sc[:, i % 2, 0:n], sc(i)[:, 0:n], zero[:, 0:n], 1.0, NEG, ALU.add, ALU.max, mx[:, i % 2:i % 2 + 1])
                            dve.drain()
                            dve.tensor_scalar(mx[:, i % 2:i % 2 + 1], mx[:, i % 2:i % 2 + 1], -scale, None, ALU.mult).then_inc(s["max_done"], 1)
                            if q > 0 and h == 0:
                                recip(q - 1)
                            if q > 0 and h == 2:
                                output(q - 1)
                        recip(QT_ - 1)
                        output(QT_ - 1)
                        turn_over(dve, u, (s["turned"], N), (s["o_done"], QT_))

                @block.scalar
                def _(act):
                    with act.Fori(0, DC * B) as u:
                        def exp(i):
                            q, h = divmod(i, HPC)
                            act.wait_ge(s["max_done"], u * N + i + 1)
                            if h == 0:
                                slot_free(act, s["r_spread"], u, QT_, q)
                            p = Sc[:, i % 2, 0:(q + 1) * P]
                            act.activation(p, p, ACT.Exp, bias=mx[:, i % 2:i % 2 + 1], scale=scale, accum_out=sums[:, q % 2, h:h + 1]).then_inc(s["exp_done"], 1)

                        def turn_recip(q):
                            act.wait_ge(s["o_done"], u * QT_ + q + 1)
                            act.activation(RT[:, q % 2, :], ob(q)[:, P:2 * P], ACT.Copy).then_inc(s["rt_out"], 1)

                        exp(0)
                        for i in range(N):
                            q, h = divmod(i, HPC)
                            n = (q + 1) * P
                            act.wait_ge(s["turned"], u * N + i + 1)
                            slot_free(act, s["pv_done"], u, N, i)
                            act.activation(PT[:, i % 2, 0:n], K.psum[:, 4:6, :].rearrange("p b k -> p (b k)")[:, 0:n], ACT.Copy).then_inc(s["pt_out"], 1)
                            if i + 1 < N:
                                exp(i + 1)
                            if q > 0 and h == 0:
                                turn_recip(q - 1)
                        turn_recip(QT_ - 1)
                        turn_over(act, u, (s["r_spread"], QT_), (s["pv_done"], N))
        OTv = OT[:].rearrange("p (c t) -> p c t", c=DC)
        finish(nc, K, lambda k, h, j: Wo[:, k, h * P:(h + 1) * P], block_of(OTv), DC)


L0E = 8
PICKED = 512
PT4 = PICKED // P


def L0_ffn_layout(i):
    g = lambda n: np.asarray(i["L0_ffn_" + n])
    up = lambda a, sh: np.concatenate([rows(g(a)[e].T) for e in range(L0E)] + [rows(g(sh).T)], axis=2)
    vec = lambda a, sh: np.ascontiguousarray(np.concatenate([g(a), g(sh)[None]]).T)
    ln = lambda a, sh: np.stack([g(a), g(sh)], axis=1)
    return {"L0f_W1": up("ew1", "sw1"), "L0f_W2": up("ew2", "sw2"), "L0f_b1": vec("eb1", "sb1"), "L0f_b2": vec("eb2", "sb2"),
            "L0f_W3": np.concatenate([g("ew3").transpose(2, 0, 1).reshape(P, L0E * D), g("sw3").T], axis=1),
            "L0f_b3": np.concatenate([g("eb3"), g("sb3")[None]]), "L0f_sb3": cols(g("sb3")),
            "L0f_g": ln("sel_ln_g", "s_ln_g"), "L0f_b": ln("sel_ln_b", "s_ln_b"),
            "L0f_Wgate": rows(np.concatenate([g("eg_w"), g("sg_w")]).T), "L0f_bgate": np.concatenate([g("eg_b"), g("sg_b")]),
            "L0f_ebias": g("exp_bias"), "L0f_ib": cols(g("index_b")), "L0f_it": cols(g("index_t")),
            "L0f_ibr": g("index_b"), "L0f_itr": g("index_t")}


def turn_tokens(nc, K):
    xo = K.XT[K.cur]
    with phase(nc, K.sems, "turned act_out dve_out") as (block, s):
        @block.tensor
        def _(pe):
            for t in range(NT):
                if t >= 8:
                    pe.wait_ge(s["act_out"] if t % 2 == 0 else s["dve_out"], (t - 8) // 2 + 1)
                for h in range(DC):
                    ins = pe.transpose(K.bank[t % 8][:, h * P:(h + 1) * P], K.Xtok[:, t, h * P:(h + 1) * P], K.ident[:])
                ins.then_inc(s["turned"], 1)

        @block.scalar
        def _(act):
            for t in range(0, NT, 2):
                act.wait_ge(s["turned"], t + 1)
                act.activation(xo[:, :, t * P:(t + 1) * P], K.bank[t % 8][:, 0:D].rearrange("p (c k) -> p c k", c=2), ACT.Copy).then_inc(s["act_out"], 1)

        @block.vector
        def _(dve):
            for t in range(1, NT, 2):
                dve.wait_ge(s["turned"], t + 1)
                dve.tensor_copy(xo[:, :, t * P:(t + 1) * P], K.bank[t % 8][:, 0:D].rearrange("p (c k) -> p c k", c=2)).then_inc(s["dve_out"], 1)


def L0_ffn(nc, K, w):
    xT = K.XT[K.cur]
    NJ = L0E + 1 + NB
    expert = lambda n: min(n, L0E)
    pool_of_rows = nc.dram_tensor("L0f_rows", [TOK + PICKED, D], F32, kind="Internal").ap()
    with ExitStack() as es:
        num = sbuf(es, nc, "expert_number", [P, L0E])
        W3 = sbuf(es, nc, "W3", [P, (L0E + 1) * D])
        b3 = sbuf(es, nc, "b3", [L0E + 1, D])
        sb3 = sbuf(es, nc, "sb3", [P, DC])
        Z = sbuf(es, nc, "Z", [P, NJ, BLK])
        Xm = sbuf(es, nc, "picked", [P, PT4, D])
        XmT = sbuf(es, nc, "pickedT", [P, DC, PICKED])
        G = sbuf(es, nc, "gates", [P, PT4, L0E + 1])
        home = sbuf(es, nc, "home_row", [P, NT], U32)
        number_experts(nc, K, es, num[:], L0E)
        with ExitStack() as inn:
            W1, W2 = (sbuf(inn, nc, n, [P, DC, (L0E + 1) * P]) for n in ("W1", "W2"))
            b1, b2 = (sbuf(inn, nc, n, [P, L0E + 1]) for n in ("b1", "b2"))
            lng, lnb = (sbuf(inn, nc, n, [P, 2]) for n in ("lng", "lnb"))
            Wg = sbuf(inn, nc, "Wgate", [P, DC, L0E + 1])
            bg = sbuf(inn, nc, "bgate", [P, L0E + 1])
            eb = sbuf(inn, nc, "ebias", [P, L0E])
            J = sbuf(inn, nc, "J", [P, P])
            load(nc, K, later=((W1[:], w["L0f_W1"]), (W2[:], w["L0f_W2"]), (W3[:], w["L0f_W3"]), (b3[:], w["L0f_b3"]), (sb3[:], w["L0f_sb3"]),
                               (b1[:], w["L0f_b1"]), (b2[:], w["L0f_b2"]), (lng[:], w["L0f_g"]), (lnb[:], w["L0f_b"]), (Wg[:], w["L0f_Wgate"]),
                               (bg[:], spread(w["L0f_bgate"])), (eb[:], spread(w["L0f_ebias"]))))
            block_mean(nc, K, J[:], P)
            with ExitStack() as ix, phase(nc, K.sems, "loaded rows_out counted index_done picked turned out") as (block, s):
                ints = sbuf(ix, nc, "index_cols", [P, 2, PT4], I32)
                intr = sbuf(ix, nc, "index_rows", [P, 2, PICKED], I32)
                fc = sbuf(ix, nc, "index_cols_f", [P, 2, PT4])
                fr = sbuf(ix, nc, "index_rows_f", [P, 2, PICKED])
                at = sbuf(ix, nc, "flat_index", [P, PT4], U32)
                ordi = sbuf(ix, nc, "order_int", [P, PICKED], I32)
                order = sbuf(ix, nc, "order", [P, PICKED])
                toki = sbuf(ix, nc, "token_int", [P, NT], I32)
                tok = sbuf(ix, nc, "token", [P, NT])
                hit = sbuf(ix, nc, "hit", [P, PICKED])
                last = sbuf(ix, nc, "last_hit", [P, NT, 3])

                @block.sync
                def _(sp):
                    sp.dma_start(pool_of_rows[0:TOK].rearrange("(t p) d -> p t d", p=P), K.Xtok[:]).then_inc(s["rows_out"], 16)
                    sp.dma_start(ints[:, 0], w["L0f_ib"]).then_inc(s["loaded"], 16)
                    sp.dma_start(ints[:, 1], w["L0f_it"]).then_inc(s["loaded"], 16)
                    sp.dma_start(intr[:, 0], spread(w["L0f_ibr"])).then_inc(s["loaded"], 16)
                    sp.dma_start(intr[:, 1], spread(w["L0f_itr"])).then_inc(s["loaded"], 16)

                @block.gpsimd
                def _(pool):
                    pool.iota(ordi[:], pattern=[[1, PICKED]], base=1, channel_multiplier=0).then_inc(s["counted"], 1)
                    pool.iota(toki[:], pattern=[[P, NT]], base=0, channel_multiplier=1).then_inc(s["counted"], 1)
                    pool.wait_ge(s["index_done"], 1)
                    pool.wait_ge(s["rows_out"], 16)
                    for q in range(PT4):
                        pool.indirect_dma_start(out=Xm[:, q, :], out_offset=None, in_=pool_of_rows[0:TOK, :],
                                                in_offset=bass.IndirectOffsetOnAxis(ap=at[:, q:q + 1], axis=0)).then_inc(s["picked"], 16)

                @block.vector
                def _(dve):
                    dve.wait_ge(s["loaded"], 64)
                    dve.wait_ge(s["counted"], 2)
                    dve.tensor_copy(fc[:], ints[:])
                    dve.tensor_copy(fr[:], intr[:])
                    dve.tensor_copy(order[:], ordi[:])
                    dve.tensor_copy(tok[:], toki[:])
                    dve.drain()
                    dve.scalar_tensor_tensor(out=at[:], in0=fc[:, 0], scalar=float(S), in1=fc[:, 1], op0=ALU.mult, op1=ALU.add).then_inc(s["index_done"], 1)
                    dve.scalar_tensor_tensor(out=fr[:, 0], in0=fr[:, 0], scalar=float(S), in1=fr[:, 1], op0=ALU.mult, op1=ALU.add)
                    dve.drain()
                    for t in range(NT):
                        dve.scalar_tensor_tensor(out=hit[:], in0=fr[:, 0], scalar=tok[:, t:t + 1], in1=order[:], op0=ALU.is_equal, op1=ALU.mult)
                        dve.drain()
                        dve.reduce_max(last[:, t, 0:1], hit[:], AX)
                        dve.drain()
                    dve.tensor_scalar(last[:, :, 1], last[:, :, 0], 0.0, None, ALU.is_gt)
                    dve.scalar_tensor_tensor(out=last[:, :, 2], in0=last[:, :, 0], scalar=float(TOK - 1), in1=tok[:], op0=ALU.add, op1=ALU.subtract)
                    dve.drain()
                    dve.tensor_tensor(last[:, :, 2], last[:, :, 2], last[:, :, 1], ALU.mult)
                    dve.drain()
                    dve.tensor_tensor(home[:], last[:, :, 2], tok[:], ALU.add)

                @block.tensor
                def _(pe):
                    pe.wait_ge(s["picked"], 16 * PT4)
                    for q in range(PT4):
                        for h in range(DC):
                            ins = pe.transpose(K.bank[q][:, h * P:(h + 1) * P], Xm[:, q, h * P:(h + 1) * P], K.ident[:])
                        ins.then_inc(s["turned"], 1)

                @block.scalar
                def _(act):
                    for q in range(PT4):
                        act.wait_ge(s["turned"], q + 1)
                        act.activation(XmT[:, :, q * P:(q + 1) * P], K.bank[q][:, 0:D].rearrange("p (c k) -> p c k", c=2), ACT.Copy).then_inc(s["out"], 1)

            arrive(nc, K)
            with ExitStack() as up, phase(nc, K.sems, "done silu_done z_done") as (block, s):
                sl = sbuf(up, nc, "silu", [P, 2, BLK])

                @block.tensor
                def _(pe):
                    for n in range(NJ):
                        e = expert(n)
                        src = XmT if n <= L0E else xT
                        o = 0 if n <= L0E else (n - L0E - 1) * BLK
                        if n >= 4:
                            pe.wait_ge(s["z_done"], n - 3)
                        for part, W in enumerate((W1, W2)):
                            for k in range(DC):
                                ins = pe.matmul(K.bank[2 * (n % 4) + part][:], W[:, k, e * P:(e + 1) * P], src[:, k, o:o + BLK], start=(k == 0), stop=(k == DC - 1))
                        ins.then_inc(s["done"], 1)

                @block.scalar
                def _(act):
                    for n in range(NJ):
                        act.wait_ge(s["done"], n + 1)
                        if n >= 2:
                            act.wait_ge(s["z_done"], n - 1)
                        act.activation(sl[:, n % 2, :], K.bank[2 * (n % 4)][:], ACT.Silu, bias=b1[:, expert(n):expert(n) + 1]).then_inc(s["silu_done"], 1)

                @block.vector
                def _(dve):
                    for n in range(NJ):
                        dve.wait_ge(s["silu_done"], n + 1)
                        dve.scalar_tensor_tensor(out=Z[:, n, :], in0=K.bank[2 * (n % 4) + 1][:], scalar=b2[:, expert(n):expert(n) + 1], in1=sl[:, n % 2, :],
                                                 op0=ALU.add, op1=ALU.mult).then_inc(s["z_done"], 1)

            ln = lambda v: lambda n: v[:, 0:1] if n < L0E else v[:, 1:2]
            feature_ln_rows(nc, K, J[:], NJ, 1, lambda n, h: Z[:, n, :], lambda n, h: Z[:, n, :], ln(lng), ln(lnb))

            with ExitStack() as gt, phase(nc, K.sems, "scored biased sigma_done ready weights_done") as (block, s):
                sc = sbuf(gt, nc, "scores", [P, PT4, L0E + 1])
                v = sbuf(gt, nc, "biased", [P, PT4, L0E])
                top = sbuf(gt, nc, "top", [P, PT4, 8])
                at = sbuf(gt, nc, "top_index", [P, PT4, 8], U32)
                atf = sbuf(gt, nc, "top_index_f", [P, PT4, 8])
                d = sbuf(gt, nc, "difference", [P, 3, PT4])

                @block.tensor
                def _(pe):
                    for q in range(PT4):
                        for k in range(DC):
                            ins = pe.matmul(K.bank[0][:, q * 16:q * 16 + L0E + 1], XmT[:, k, q * P:(q + 1) * P], Wg[:, k, :], start=(k == 0), stop=(k == DC - 1))
                    ins.then_inc(s["scored"], 1)

                @block.vector
                def _(dve):
                    dve.wait_ge(s["scored"], 1)
                    dve.tensor_tensor(sc[:], K.bank[0][:, 0:16 * PT4].rearrange("p (q e) -> p q e", e=16)[:, :, 0:L0E + 1], middle(bg[:], PT4), ALU.add).then_inc(s["biased"], 1)
                    dve.wait_ge(s["sigma_done"], 1)
                    dve.tensor_tensor(v[:], sc[:, :, 0:L0E], middle(eb[:], PT4), ALU.add)
                    dve.drain()
                    for q in range(PT4):
                        dve.max(top[:, q, :], v[:, q, :])
                    dve.drain()
                    for q in range(PT4):
                        dve.max_index(at[:, q, :], top[:, q, :], v[:, q, :])
                    dve.drain()
                    dve.tensor_copy(atf[:], at[:])
                    dve.drain()
                    dve.tensor_tensor(G[:, :, 0:L0E], middle(num[:], PT4), inner(atf[:, :, 0], L0E), ALU.is_equal)
                    dve.drain()
                    dve.tensor_tensor(v[:], G[:, :, 0:L0E], sc[:, :, 0:L0E], ALU.mult)
                    dve.drain()
                    dve.reduce_sum(d[:, 0, :], v[:], AX)
                    dve.drain()
                    dve.tensor_tensor(d[:, 1, :], d[:, 0, :], sc[:, :, L0E], ALU.subtract)
                    dve.drain()
                    dve.tensor_scalar(d[:, 2, :], d[:, 1, :], -1.0, None, ALU.mult).then_inc(s["ready"], 1)
                    dve.wait_ge(s["weights_done"], 1)
                    dve.tensor_tensor(G[:, :, 0:L0E], G[:, :, 0:L0E], inner(d[:, 1, :], L0E), ALU.mult)
                    dve.tensor_copy(G[:, :, L0E], d[:, 2, :])

                @block.scalar
                def _(act):
                    act.wait_ge(s["biased"], 1)
                    act.activation(sc[:], sc[:], ACT.Sigmoid).then_inc(s["sigma_done"], 1)
                    act.wait_ge(s["ready"], 1)
                    act.activation(d[:, 1:3, :], d[:, 1:3, :], ACT.Sigmoid).then_inc(s["weights_done"], 1)

        acc = sbuf(es, nc, "acc", [P, PT4, D])
        st = sbuf(es, nc, "ln_stats", [P, PT4, 9])
        with ExitStack() as gt, phase(nc, K.sems, "turned turned_out bias_done bias_out done added stats_done std_done stored") as (block, s):
            gT = sbuf(gt, nc, "gatesT", [L0E + 1, PICKED])

            @block.tensor
            def _(pe):
                for q in range(PT4):
                    ins = pe.transpose(K.bank[0][0:L0E + 1, q * P:(q + 1) * P], G[:, q, :], K.ident[:])
                ins.then_inc(s["turned"], 1)
                pe.wait_ge(s["turned_out"], 1)
                for q in range(PT4):
                    if q:
                        pe.wait_ge(s["bias_out"], q)
                    pe.matmul(K.bank[1][:, 0:D], gT[:, q * P:(q + 1) * P], b3[:], start=True, stop=True).then_inc(s["bias_done"], 1)
                for n in range(PT4 * (L0E + 1)):
                    q, e = divmod(n, L0E + 1)
                    if n >= 6:
                        pe.wait_ge(s["added"], n - 5)
                    pe.matmul(K.bank[2 + n % 6][:, 0:D], Z[:, e, q * P:(q + 1) * P], W3[:, e * D:(e + 1) * D], start=True, stop=True).then_inc(s["done"], 1)

            @block.scalar
            def _(act):
                act.wait_ge(s["turned"], 1)
                act.activation(gT[:], K.bank[0][0:L0E + 1, :], ACT.Copy).then_inc(s["turned_out"], 1)
                act.wait_ge(s["stats_done"], 1)
                act.activation(st[:, :, 8:9], st[:, :, 1:2], ACT.Sqrt, bias=K.eps[:, 0:1]).then_inc(s["std_done"], 1)

            @block.vector
            def _(dve):
                for q in range(PT4):
                    dve.wait_ge(s["bias_done"], q + 1)
                    dve.tensor_tensor(acc[:, q, :], K.bank[1][:, 0:D], Xm[:, q, :], ALU.add).then_inc(s["bias_out"], 1)
                dve.drain()
                for n in range(PT4 * (L0E + 1)):
                    q, e = divmod(n, L0E + 1)
                    dve.wait_ge(s["done"], n + 1)
                    dve.scalar_tensor_tensor(out=acc[:, q, :], in0=K.bank[2 + n % 6][:, 0:D], scalar=G[:, q, e:e + 1], in1=acc[:, q, :],
                                             op0=ALU.mult, op1=ALU.add).then_inc(s["added"], 1)
                    dve.drain()
                for q in range(PT4):
                    dve.bn_stats(st[:, q, 2:8], acc[:, q, :])
                dve.drain()
                for q in range(PT4):
                    ins = dve.bn_aggr(st[:, q, 0:2], st[:, q, 2:8])
                ins.then_inc(s["stats_done"], 1)
                dve.wait_ge(s["std_done"], 1)
                dve.reciprocal(st[:, :, 8:9], st[:, :, 8:9])
                dve.drain()
                for q in range(PT4):
                    ins = dve.tensor_scalar(acc[:, q, :], acc[:, q, :], st[:, q, 0:1], st[:, q, 8:9], ALU.subtract, ALU.mult)
                ins.then_inc(s["added"], 1)

            @block.sync
            def _(sp):
                sp.wait_ge(s["added"], PT4 * (L0E + 1) + 1)
                sp.dma_start(pool_of_rows[TOK:TOK + PICKED].rearrange("(q p) d -> p q d", p=P), acc[:]).then_inc(s["stored"], 16)
                sp.wait_ge(s["stored"], 16)

        finish(nc, K, lambda k, h, j: W3[:, L0E * D + h * P:L0E * D + (h + 1) * P], lambda k, j: Z[:, L0E + 1 + j, :], 1, bias=sb3)
        with phase(nc, K.sems, "stored gathered") as (block, s):
            @block.sync
            def _(sp):
                sp.dma_start(pool_of_rows[0:TOK].rearrange("(t p) d -> p t d", p=P), K.Xtok[:]).then_inc(s["stored"], 16)

            @block.gpsimd
            def _(pool):
                pool.wait_ge(s["stored"], 16)
                for t in range(NT):
                    pool.indirect_dma_start(out=K.Xtok[:, t, :], out_offset=None, in_=pool_of_rows[:, :],
                                            in_offset=bass.IndirectOffsetOnAxis(ap=home[:, t:t + 1], axis=0)).then_inc(s["gathered"], 16)
                pool.wait_ge(s["gathered"], 16 * NT)
        turn_tokens(nc, K)


L0H = 4
CH = 64
NCH = TOK // CH


def L0_attn_layout(i):
    g = lambda n: np.asarray(i["L0_attn_" + n])
    cw = np.stack([g(n).reshape(DC, P, 4).transpose(1, 0, 2) for n in ("conv_q", "conv_k", "conv_v")], axis=1)
    return {"L0a_W": rows(np.concatenate([g("Wq"), g("Wk"), g("Wv")], axis=1)), "L0a_Wb": rows(g("Wb")), "L0a_cw": np.ascontiguousarray(cw),
            "L0a_g": np.tile(g("g"), L0H), "L0a_Wo": rows(g("Wo"))}


def L0_attn(nc, K, w):
    xT = K.XT[K.cur]
    with ExitStack() as es:
        Wo = sbuf(es, nc, "Wo", [P, DC, D])
        OT = sbuf(es, nc, "OT", [P, DC, TOK])
        g4 = sbuf(es, nc, "g", [P, D])
        with ExitStack() as q_life:
            QK = sbuf(q_life, nc, "q_k_tokens", [P, NT, 2 * D])
            KV = sbuf(q_life, nc, "beta_k_v", [P, NT, 2 * D])
            beta = sbuf(q_life, nc, "beta", [P, NT, L0H])
            LEVELS = 6
            masks = sbuf(q_life, nc, "masks", [P, LEVELS + 1, P])
            with ExitStack() as inn:
                W = sbuf(inn, nc, "W", [P, DC, 3 * D])
                Wb = sbuf(inn, nc, "Wb", [P, DC, L0H])
                cw = sbuf(inn, nc, "cw", [P, 3, DC, TAPS])
                raw = sbuf(inn, nc, "raw", [P, 2, TAPS - 1 + S])
                act_T = sbuf(inn, nc, "act_T", [P, 4, BLK])
                acc = sbuf(inn, nc, "conv", [P, 2, BLK])
                sq = sbuf(inn, nc, "squares", [P, 2, 2 * P])
                nrm = sbuf(inn, nc, "norm", [P, 2, L0H])
                load(nc, K, (W[:], w["L0a_W"]), (Wb[:], w["L0a_Wb"]), (cw[:], w["L0a_cw"]), 
                     later=((g4[:], spread(w["L0a_g"])), (Wo[:], w["L0a_Wo"])))
                names = "padded done raw_out conv_done silu_done turned tok_out masked"
                with phase(nc, K.sems, names) as (block, s):
                    runs = [(x, c, b) for x in range(3) for c in range(DC) for b in range(B)]
                    NR = len(runs)

                    @block.gpsimd
                    def _(pool):
                        pool.memset(raw[:, :, 0:TAPS - 1], 0.0).then_inc(s["padded"], 1)
                        n = 0
                        pool.memset(masks[:], 1.0).then_inc(s["masked"], 1)
                        for lv in range(LEVELS + 1):
                            z = 1 << lv if lv < LEVELS else 1
                            m = masks[:, lv, :]
                            v = m.rearrange("p (n a j) -> p n a j", a=2, j=z)
                            blocks = P // (2 * z)
                            first, second = (0, 1) if lv < LEVELS else (1, 0)
                            for cmp_base, pat, mul in (
                                    (-z * first, [[-2 * z, blocks], [0, 2], [0, z]], 1),
                                    (z * first + z - 1, [[2 * z, blocks], [0, 2], [0, z]], -1),
                                    (-second if second else 0, [[0, blocks], [1 if second else -1, 2], [0, z]], 0)):
                                n += 1
                                pool.wait_ge(s["masked"], n)
                                pool.affine_select(out=v, in_=v, compare_op=ALU.is_ge, fill=0.0, base=cmp_base, pattern=pat,
                                                   channel_multiplier=mul).then_inc(s["masked"], 1)

                    @block.tensor
                    def _(pe):
                        def projection(r):
                            x, c, b = runs[r]
                            for i in range(2):
                                n = 2 * r + i
                                if n >= 4:
                                    pe.wait_ge(s["raw_out"], n - 3)
                                for k in range(DC):
                                    ins = pe.matmul(K.bank[n % 4][:], W[:, k, x * D + c * P:x * D + (c + 1) * P],
                                                    xT[:, k, b * S + i * BLK:b * S + (i + 1) * BLK], start=(k == 0), stop=(k == DC - 1))
                                ins.then_inc(s["done"], 1)
                        projection(0)
                        for r in range(NR):
                            if r + 1 < NR:
                                projection(r + 1)
                            for i in range(2):
                                n = 2 * r + i
                                pe.wait_ge(s["silu_done"], n + 1)
                                if n >= 4:
                                    pe.wait_ge(s["tok_out"], n - 3)
                                for t in range(TPB):
                                    ins = pe.transpose(K.bank[4 + n % 4][:, t * P:(t + 1) * P], act_T[:, n % 4, t * P:(t + 1) * P], K.ident[:])
                                ins.then_inc(s["turned"], 1)

                    @block.scalar
                    def _(act):
                        def take(m):
                            x, c, b = runs[m // 2]
                            t0 = b * (S // P) + (m % 2) * TPB
                            act.wait_ge(s["turned"], m + 1)
                            dst = (QK, QK, KV)[x]
                            col = (0, D, D)[x] + c * P
                            act.activation(dst[:, t0:t0 + TPB, col:col + P], K.bank[4 + m % 4][:].rearrange("p (t k) -> p t k", t=TPB), ACT.Copy).then_inc(s["tok_out"], 1)

                        act.wait_ge(s["padded"], 1)
                        for n in range(2 * NR + 2):
                            if n < 2 * NR:
                                r, i = divmod(n, 2)
                                act.wait_ge(s["done"], n + 1)
                                if r >= 2:
                                    act.wait_ge(s["conv_done"], 2 * (r - 1))
                                act.activation(raw[:, r % 2, TAPS - 1 + i * BLK:TAPS - 1 + (i + 1) * BLK], K.bank[n % 4][:], ACT.Copy).then_inc(s["raw_out"], 1)
                            if n >= 2:
                                m = n - 2
                                act.wait_ge(s["conv_done"], m + 1)
                                if m >= 4:
                                    act.wait_ge(s["turned"], m - 3)
                                act.activation(act_T[:, m % 4, :], acc[:, m % 2, :], ACT.Silu).then_inc(s["silu_done"], 1)
                                if m >= 1:
                                    take(m - 1)
                        take(2 * NR - 1)

                    @block.vector
                    def _(dve):
                        for n in range(2 * NR):
                            r, i = divmod(n, 2)
                            x, c, b = runs[r]
                            dve.wait_ge(s["raw_out"], n + 1)
                            if n >= 2:
                                dve.wait_ge(s["silu_done"], n - 1)
                            a = acc[:, n % 2, :]
                            dve.tensor_scalar(a, raw[:, r % 2, i * BLK:(i + 1) * BLK], cw[:, x, c, 0:1], None, ALU.mult)
                            for tap in range(1, TAPS):
                                dve.drain()
                                ins = dve.scalar_tensor_tensor(out=a, in0=raw[:, r % 2, i * BLK + tap:(i + 1) * BLK + tap], scalar=cw[:, x, c, tap:tap + 1],
                                                               in1=a, op0=ALU.mult, op1=ALU.add)
                            ins.then_inc(s["conv_done"], 1)

                with phase(nc, K.sems, "done") as (block, s):
                    @block.tensor
                    def _(pe):
                        for t in range(NT):
                            for k in range(DC):
                                ins = pe.matmul(K.bank[0][:, t * L0H:(t + 1) * L0H], xT[:, k, t * P:(t + 1) * P], Wb[:, k, :], start=(k == 0), stop=(k == DC - 1))
                        ins.then_inc(s["done"], 1)

                    @block.scalar
                    def _(act):
                        act.wait_ge(s["done"], 1)
                        act.activation(beta[:], K.bank[0][:, 0:NT * L0H].rearrange("p (t h) -> p t h", h=L0H), ACT.Sigmoid)

                with ExitStack() as nn, phase(nc, K.sems, "squared summed root recip") as (block, s):
                    heads = lambda v: v.rearrange("p (h d) -> p h d", h=L0H)
                    sq2 = sbuf(nn, nc, "squares", [P, 2, 2 * D])
                    nr = sbuf(nn, nc, "norms", [P, NT, 2 * L0H])

                    @block.scalar
                    def _(act):
                        for t in range(NT):
                            if t >= 2:
                                act.wait_ge(s["summed"], t - 1)
                            act.activation(sq2[:, t % 2, :], QK[:, t, :], ACT.Square).then_inc(s["squared"], 1)
                        act.wait_ge(s["summed"], NT)
                        act.activation(nr[:], nr[:], ACT.Sqrt).then_inc(s["root"], 1)

                    @block.vector
                    def _(dve):
                        for t in range(NT):
                            dve.wait_ge(s["squared"], t + 1)
                            dve.reduce_sum(nr[:, t, :], sq2[:, t % 2, :].rearrange("p (h d) -> p h d", h=2 * L0H), AX).then_inc(s["summed"], 1)
                        dve.wait_ge(s["root"], 1)
                        dve.reciprocal(nr[:], nr[:])
                        dve.drain()
                        dve.sem_inc(s["recip"], 1)
                        for t in range(NT):
                            v = heads(QK[:, t, D:2 * D])
                            dve.tensor_tensor(v, v, inner(nr[:, t, L0H:], D // L0H), ALU.mult)
                        dve.drain()
                        for t in range(NT):
                            dve.tensor_tensor(heads(KV[:, t, 0:D]), heads(QK[:, t, D:2 * D]), inner(beta[:, t, :], D // L0H), ALU.mult)

                    @block.gpsimd
                    def _(pool):
                        for t in range(NT):
                            v = heads(KV[:, t, D:2 * D])
                            pool.tensor_tensor(v, v, inner(beta[:, t, :], D // L0H), ALU.mult)
                        pool.wait_ge(s["recip"], 1)
                        for t in range(NT):
                            v = heads(QK[:, t, 0:D])
                            pool.tensor_tensor(v, v, inner(nr[:, t, 0:L0H], D // L0H), ALU.mult)

            TT = sbuf(q_life, nc, "T_transposed", [P, NT, P])
            with ExitStack() as inn:
                GT = 4
                kT = sbuf(inn, nc, "kT", [P, 2, 2 * DC * P])
                E = sbuf(inn, nc, "E_T", [P, 2, LEVELS - 1, GT, P])
                M, MT, X = (sbuf(inn, nc, n, [P, 2, GT, P]) for n in ("M", "M_T", "X"))
                four = lambda ap: middle(ap, GT)
                part = lambda u, i: K.bank[2 + 3 * u + i]
                bank4 = lambda u, i: part(u, i)[:].rearrange("p (t k) -> p t k", t=GT)
                names = "k_turned k_out a_done0 a_done1 m_ready0 m_ready1 x_done0 x_done1 x_out0 x_out1 y_done0 y_done1"
                with phase(nc, K.sems, names) as (block, s):
                    a_done, m_ready, x_done = (s["a_done0"], s["a_done1"]), (s["m_ready0"], s["m_ready1"]), (s["x_done0"], s["x_done1"])
                    x_out, y_done = (s["x_out0"], s["x_out1"]), (s["y_done0"], s["y_done1"])
                    ROUNDS = NT // (2 * GT)

                    @block.tensor
                    def _(pe):
                        def a_of(r, u):
                            for i in range(GT):
                                t = (2 * r + u) * GT + i
                                if t >= 2:
                                    pe.wait_ge(s["k_out"], t - 1)
                                for c in range(DC):
                                    pe.transpose(K.bank[t % 2][:, c * P:(c + 1) * P], QK[:, t, D + c * P:D + (c + 1) * P], K.ident[:])
                                    ins = pe.transpose(K.bank[t % 2][:, (2 + c) * P:(3 + c) * P], KV[:, t, c * P:(c + 1) * P], K.ident[:])
                                ins.then_inc(s["k_turned"], 1)
                                if i == 0 and r:
                                    pe.wait_ge(m_ready[u], r * (LEVELS + 1))
                                pe.wait_ge(s["k_out"], t + 1)
                                k_, kb = (lambda c: kT[:, t % 2, c * P:(c + 1) * P]), (lambda c: kT[:, t % 2, (2 + c) * P:(3 + c) * P])
                                for c in range(DC):
                                    pe.matmul(part(u, 1)[:, i * P:(i + 1) * P], k_(c), kb(c), start=(c == 0), stop=(c == DC - 1))
                                for c in range(DC):
                                    ins = pe.matmul(part(u, 2)[:, i * P:(i + 1) * P], kb(c), k_(c), start=(c == 0), stop=(c == DC - 1))
                                ins.then_inc(a_done[u], 1)

                        for r in range(ROUNDS):
                            for u in range(2):
                                a_of(r, u)
                            for lv in range(1, LEVELS):
                                for u in range(2):
                                    pe.wait_ge(m_ready[u], r * (LEVELS + 1) + lv)
                                    for i in range(GT):
                                        ins = pe.matmul(part(u, 0)[:, i * P:(i + 1) * P], E[:, u, lv - 1, i, :], M[:, u, i, :], start=True, stop=True)
                                    ins.then_inc(x_done[u], 1)
                                for u in range(2):
                                    pe.wait_ge(x_out[u], r * (LEVELS - 1) + lv)
                                    for i in range(GT):
                                        pe.matmul(part(u, 1)[:, i * P:(i + 1) * P], MT[:, u, i, :], X[:, u, i, :], start=True, stop=True)
                                    for i in range(GT):
                                        ins = pe.matmul(part(u, 2)[:, i * P:(i + 1) * P], X[:, u, i, :], MT[:, u, i, :], start=True, stop=True)
                                    ins.then_inc(y_done[u], 1)

                    @block.scalar
                    def _(act):
                        for r in range(ROUNDS):
                            for i in range(2 * GT):
                                t = 2 * r * GT + i
                                act.wait_ge(s["k_turned"], t + 1)
                                if t >= 2:
                                    act.wait_ge(a_done[(t - 2) // GT % 2], (t - 2) // (2 * GT) * GT + (t - 2) % GT + 1)
                                act.activation(kT[:, t % 2, :], K.bank[t % 2][:], ACT.Copy).then_inc(s["k_out"], 1)
                            for lv in range(1, LEVELS):
                                for u in range(2):
                                    act.wait_ge(x_done[u], r * (LEVELS - 1) + lv)
                                    act.activation(X[:, u], bank4(u, 0), ACT.Copy).then_inc(x_out[u], 1)

                    @block.vector
                    def _(dve):
                        for r in range(ROUNDS):
                            for u in range(2):
                                dve.wait_ge(a_done[u], GT * (r + 1))
                                dve.tensor_tensor(MT[:, u], bank4(u, 1), four(masks[:, 0, :]), ALU.mult)
                                dve.tensor_tensor(M[:, u], bank4(u, 2), four(masks[:, LEVELS, :]), ALU.mult)
                                for lv in range(1, LEVELS):
                                    dve.tensor_tensor(E[:, u, lv - 1], bank4(u, 1), four(masks[:, lv, :]), ALU.mult)
                                dve.drain()
                                dve.tensor_tensor(MT[:, u], four(K.ident[:]), MT[:, u], ALU.subtract)
                                dve.tensor_tensor(M[:, u], four(K.ident[:]), M[:, u], ALU.subtract).then_inc(m_ready[u], 1)
                            dve.drain()
                            for lv in range(1, LEVELS):
                                for u in range(2):
                                    dve.wait_ge(y_done[u], r * (LEVELS - 1) + lv)
                                    dve.tensor_tensor(M[:, u], M[:, u], bank4(u, 1), ALU.subtract)
                                    dve.tensor_tensor(MT[:, u], MT[:, u], bank4(u, 2), ALU.subtract).then_inc(m_ready[u], 1)
                                dve.drain()
                            for u in range(2):
                                dve.tensor_scalar(X[:, u], four(K.ident[:]), -2.0, None, ALU.mult)
                            dve.drain()
                            for u in range(2):
                                g = 2 * r + u
                                dve.scalar_tensor_tensor(out=TT[:, g * GT:(g + 1) * GT, :], in0=MT[:, u], scalar=3.0, in1=X[:, u], op0=ALU.mult, op1=ALU.add).then_inc(m_ready[u], 1)

            sums = sbuf(q_life, nc, "chunk_sums", [P, 2 * DC, NCH])
            with ExitStack() as inn, phase(nc, K.sems, "step wu_done wu_out prod_done summed rows_out turned") as (block, s):
                prod = sbuf(inn, nc, "k_products", [P, 2, 2 * D])
                pick = sbuf(inn, nc, "chunk_of", [P, 2])
                wide = sbuf(inn, nc, "chunk_of_wide", [P, 2 * NCH - 2])
                by_chunk = sbuf(inn, nc, "sums_by_chunk", [NCH, 2 * D])

                @block.gpsimd
                def _(pool):
                    pool.memset(pick[:], 1.0).then_inc(s["step"], 1)
                    pool.wait_ge(s["step"], 1)
                    pool.affine_select(out=pick[:], in_=pick[:], compare_op=ALU.is_ge, fill=0.0, base=0, pattern=[[-CH, 2]], channel_multiplier=1).then_inc(s["step"], 1)
                    pool.wait_ge(s["step"], 2)
                    pool.affine_select(out=pick[:], in_=pick[:], compare_op=ALU.is_ge, fill=0.0, base=CH - 1, pattern=[[CH, 2]], channel_multiplier=-1).then_inc(s["step"], 1)
                    pool.memset(wide[:], 0.0).then_inc(s["step"], 1)
                    pool.wait_ge(s["step"], 4)
                    pool.tensor_copy(wide[:, NCH - 2:NCH], pick[:]).then_inc(s["step"], 1)

                @block.tensor
                def _(pe):
                    def products(t):
                        if t >= 2:
                            pe.wait_ge(s["wu_out"], t - 1)
                        pe.matmul(K.bank[t % 2][:], TT[:, t, :], KV[:, t, :], start=True, stop=True).then_inc(s["wu_done"], 1)
                    products(0)
                    products(1)
                    pe.wait_ge(s["step"], 5)
                    for t in range(NT):
                        if t + 2 < NT:
                            products(t + 2)
                        pe.wait_ge(s["prod_done"], t + 1)
                        pe.matmul(K.bank[2][0:NCH, :], wide[:, NCH - 2 - 2 * t:2 * NCH - 2 - 2 * t], prod[:, t % 2, :], start=(t == 0), stop=(t == NT - 1)).then_inc(s["summed"], 1)
                    pe.wait_ge(s["rows_out"], 1)
                    for c in range(2 * DC):
                        ins = pe.transpose(K.bank[3][:, c * NCH:(c + 1) * NCH], by_chunk[:, c * P:(c + 1) * P], K.ident[0:NCH, 0:NCH])
                    ins.then_inc(s["turned"], 1)

                @block.scalar
                def _(act):
                    for t in range(NT):
                        act.wait_ge(s["wu_done"], t + 1)
                        act.activation(KV[:, t, :], K.bank[t % 2][:], ACT.Copy).then_inc(s["wu_out"], 1)

                @block.vector
                def _(dve):
                    for t in range(NT):
                        dve.wait_ge(s["wu_out"], t + 1)
                        if t >= 2:
                            dve.wait_ge(s["summed"], t - 1)
                        dve.tensor_tensor(prod[:, t % 2, :].rearrange("p (a d) -> p a d", a=2), middle(QK[:, t, D:2 * D], 2),
                                          KV[:, t, :].rearrange("p (a d) -> p a d", a=2), ALU.mult).then_inc(s["prod_done"], 1)
                    dve.wait_ge(s["summed"], NT)
                    dve.tensor_copy(by_chunk[:], K.bank[2][0:NCH, :]).then_inc(s["rows_out"], 1)
                    dve.wait_ge(s["turned"], 1)
                    v = K.bank[3][:, 0:2 * DC * NCH].rearrange("p (c n) -> p c n", n=NCH)
                    dve.tensor_scalar(sums[:, 0:DC], v[:, 0:DC], -1.0, 1.0, ALU.mult, ALU.add)
                    dve.tensor_copy(sums[:, DC:2 * DC], v[:, DC:2 * DC])

            diag = sbuf(q_life, nc, "diagonal", [NCH, D])
            sel = sbuf(q_life, nc, "chunk_select", [NCH, TOK])
            rowm = sbuf(q_life, nc, "first_rows", [P, B])
            with ExitStack() as inn, phase(nc, K.sems, "step scanned turned") as (block, s):
                dT = sbuf(inn, nc, "diagonalT", [P, DC, B, NCH // B + 1])
                dC = sbuf(inn, nc, "diagonal_before", [P, DC, NCH])

                @block.gpsimd
                def _(pool):
                    v = sel[:].rearrange("p (n j) -> p n j", j=CH)
                    pool.memset(sel[:], 1.0).then_inc(s["step"], 1)
                    pool.memset(rowm[:], 1.0).then_inc(s["step"], 1)
                    pool.wait_ge(s["step"], 2)
                    pool.affine_select(out=v, in_=v, compare_op=ALU.is_equal, fill=0.0, base=0, pattern=[[-1, NCH], [0, CH]], channel_multiplier=1)
                    pool.affine_select(out=rowm[0:CH], in_=rowm[0:CH], compare_op=ALU.is_ge, fill=0.0, base=0, pattern=[[1, B]], channel_multiplier=-1)
                    pool.affine_select(out=rowm[CH:P], in_=rowm[CH:P], compare_op=ALU.is_ge, fill=0.0, base=0, pattern=[[1, B]], channel_multiplier=-1)

                @block.vector
                def _(dve):
                    dve.memset(dT[:, :, :, 0:1], 0.0)
                    n = NCH // B
                    for c in range(DC):
                        for b in range(B):
                            dve.tensor_tensor_scan(dT[:, c, b, 1:n + 1], sums[:, c, b * n:(b + 1) * n], sums[:, DC + c, b * n:(b + 1) * n], 0.0, ALU.mult, ALU.add)
                    dve.drain()
                    dve.tensor_copy(dC[:].rearrange("p c (b n) -> p (c b) n", b=B), dT[:].rearrange("p c b n -> p (c b) n")[:, :, 0:n]).then_inc(s["scanned"], 1)
                    dve.wait_ge(s["turned"], 1)
                    dve.tensor_copy(diag[:], K.bank[0][0:NCH, 0:D])

                @block.tensor
                def _(pe):
                    pe.wait_ge(s["scanned"], 1)
                    for c in range(DC):
                        ins = pe.transpose(K.bank[0][0:NCH, c * P:(c + 1) * P], dC[:, c, :], K.ident[:])
                    ins.then_inc(s["turned"], 1)

            arrive(nc, K)
            with ExitStack() as inn, phase(nc, K.sems, "d_done o_done squared summed root scaled o_normed turned out") as (block, s):
                tmp = sbuf(inn, nc, "tmp", [P, 2, D])
                dot = sbuf(inn, nc, "dot", [P, NT])
                sq = sbuf(inn, nc, "squares", [P, 2, D])
                ms = sbuf(inn, nc, "mean_square", [P, NT, L0H])
                O = sbuf(inn, nc, "O", [P, NT, D])

                @block.tensor
                def _(pe):
                    for t in range(NT):
                        if t >= 4:
                            pe.wait_ge(s["o_done"], t - 3)
                        pe.matmul(K.bank[t % 4][:, 0:D], sel[:, t * P:(t + 1) * P], diag[:], start=True, stop=True).then_inc(s["d_done"], 1)
                    for t in range(NT):
                        pe.wait_ge(s["o_normed"], t + 1)
                        if t >= 4:
                            pe.wait_ge(s["out"], t - 3)
                        for c in range(DC):
                            ins = pe.transpose(K.bank[4 + t % 4][:, c * P:(c + 1) * P], O[:, t, c * P:(c + 1) * P], K.ident[:])
                        ins.then_inc(s["turned"], 1)

                @block.vector
                def _(dve):
                    for t in range(NT):
                        q_, k_ = QK[:, t, 0:D], QK[:, t, D:2 * D]
                        a, b_ = tmp[:, 0, :], tmp[:, 1, :]
                        dve.wait_ge(s["d_done"], t + 1)
                        d_ = K.bank[t % 4][:, 0:D]
                        dve.tensor_tensor_reduce(a, q_, k_, 1.0, 0.0, ALU.mult, ALU.add, dot[:, t:t + 1])
                        dve.tensor_tensor(b_, KV[:, t, 0:D], d_, ALU.mult)
                        dve.drain()
                        dve.tensor_tensor(dot[:, t:t + 1], dot[:, t:t + 1], rowm[:, t // 8:t // 8 + 1], ALU.mult)
                        dve.tensor_tensor(b_, KV[:, t, D:2 * D], b_, ALU.subtract)
                        dve.tensor_tensor(a, q_, d_, ALU.mult)
                        dve.drain()
                        dve.scalar_tensor_tensor(out=O[:, t, :], in0=b_, scalar=dot[:, t:t + 1], in1=a, op0=ALU.mult, op1=ALU.add).then_inc(s["o_done"], 1)
                        dve.drain()
                    for t in range(NT):
                        dve.wait_ge(s["squared"], t + 1)
                        dve.reduce_sum(ms[:, t, :], sq[:, t % 2, :].rearrange("p (h d) -> p h d", h=L0H), AX).then_inc(s["summed"], 1)
                    dve.wait_ge(s["root"], 1)
                    dve.reciprocal(ms[:], ms[:])
                    dve.drain()
                    for t in range(NT):
                        v = O[:, t, :].rearrange("p (h d) -> p h d", h=L0H)
                        dve.tensor_tensor(v, v, inner(ms[:, t, :], D // L0H), ALU.mult).then_inc(s["scaled"], 1)

                @block.gpsimd
                def _(pool):
                    for t in range(NT):
                        pool.wait_ge(s["scaled"], t + 1)
                        pool.tensor_tensor(O[:, t, :], O[:, t, :], g4[:], ALU.mult).then_inc(s["o_normed"], 1)

                @block.scalar
                def _(act):
                    for t in range(NT):
                        act.wait_ge(s["o_done"], t + 1)
                        if t >= 2:
                            act.wait_ge(s["summed"], t - 1)
                        act.activation(sq[:, t % 2, :], O[:, t, :], ACT.Square).then_inc(s["squared"], 1)
                    act.wait_ge(s["summed"], NT)
                    act.activation(ms[:], ms[:], ACT.Sqrt, scale=1.0 / (D // L0H), bias=K.eps[:, 0:1]).then_inc(s["root"], 1)
                    for t in range(NT):
                        act.wait_ge(s["turned"], t + 1)
                        act.activation(OT[:, :, t * P:(t + 1) * P], K.bank[4 + t % 4][:, 0:D].rearrange("p (c k) -> p c k", c=2), ACT.Copy).then_inc(s["out"], 1)
        finish(nc, K, lambda k, h, j: Wo[:, k, h * P:(h + 1) * P], block_of(OT), DC)


L2D = 2
LH, LHD = 8, 64
LM = LH * LHD // P
HIDP = 6 * P
L2HID = 682
WINDOW = 128


def xpos_tables():
    f = np.float32
    half = np.arange(0, LHD, 2, dtype=f)
    inv = f(1.0) / np.power(f(10000.0), half / f(LHD), dtype=f)
    t = np.arange(S, dtype=f)
    ang = t[:, None] * inv[None, :]
    ang = np.concatenate([ang, ang], axis=1)
    base = (half + f(0.4 * LHD)) / f(1.4 * LHD)
    power = (t - f(S // 2)) / f(WINDOW // 2)
    scale = np.power(base[None, :], power[:, None], dtype=f)
    scale = np.concatenate([scale, scale], axis=1)
    cos, sin = np.cos(ang, dtype=f), np.sin(ang, dtype=f)
    sin[:, :LHD // 2] *= -1
    tab = np.stack([cos * scale, sin * scale, cos / scale, sin / scale])
    return np.ascontiguousarray(tab.reshape(4, S // P, P, LHD).transpose(2, 0, 1, 3))


def L2_ffn_layout(i):
    g = lambda n, l: np.asarray(i["L2_ffn_" + n])[l]
    out = {"L2f_tab": xpos_tables()}
    halves_swapped = lambda v: np.concatenate([v[LHD // 2:], v[:LHD // 2]])
    for l in range(L2D):
        two = lambda a, axis: np.concatenate([pad(a[..., :L2HID], axis, HIDP), pad(a[..., L2HID:], axis, HIDP)], axis=axis)
        qs, ks = g("q_scale", l), g("k_scale", l)
        out.update({f"L2f{l}_Wqkv": rows(g("wqkv", l)), f"L2f{l}_s": np.concatenate([qs, halves_swapped(qs), ks, halves_swapped(ks)]),
                    f"L2f{l}_Wo": rows(g("wo", l)),
                    f"L2f{l}_g": cols(g("ln_g", l)), f"L2f{l}_b": cols(g("ln_b", l)), f"L2f{l}_W1": rows(two(g("w1", l), 1)),
                    f"L2f{l}_b1": cols(two(g("b1", l), 0)), f"L2f{l}_W2": rows(pad(g("w2", l), 0, HIDP)), f"L2f{l}_b2": cols(g("b2", l))})
    return out


def shift_half(nc, K, X, sh):
    with phase(nc, K.sems, "copied") as (block, s):
        v = X[:, 1, :].rearrange("p (b t) -> p b t", b=B)

        @block.scalar
        def _(act):
            act.activation(sh[:, 0, 1:], v[:, 0], ACT.Copy)

        @block.vector
        def _(dve):
            dve.tensor_copy(sh[:, 1, 1:], v[:, 1])


def local_qkv(nc, K, tile_of, W, tab, QT, KT, V):
    NTB = S // P
    N = 2 * NTB
    HF = LHD // 2
    with ExitStack() as es, phase(nc, K.sems, "done squared ss_done root_done r_ready crossed added normed turned t_out v_done v_out") as (block, s):
        sq = sbuf(es, nc, "squares", [P, 2, LH, LHD])
        t1, t2 = (sbuf(es, nc, n, [P, 2, LH, LHD]) for n in ("straight", "crossed"))
        r = sbuf(es, nc, "norm", [P, 2, LH])
        heads = lambda v: v.rearrange("p (h d) -> p h d", h=LH)

        @block.tensor
        def _(pe):
            def projection(n):
                if n >= 3:
                    pe.wait_ge(s["crossed"], n - 2)
                for k in range(DC):
                    ins = pe.matmul(K.bank[n % 3][:], tile_of(k, n // 2), W[:, k, (n % 2) * BLK:(n % 2 + 1) * BLK], start=(k == 0), stop=(k == DC - 1))
                ins.then_inc(s["done"], 1)

            def value(t):
                if t >= 2:
                    pe.wait_ge(s["v_out"], t - 1)
                for k in range(DC):
                    ins = pe.matmul(K.bank[5 + t % 2][:], tile_of(k, t), W[:, k, 2 * BLK:3 * BLK], start=(k == 0), stop=(k == DC - 1))
                ins.then_inc(s["v_done"], 1)

            projection(0)
            projection(1)
            for n in range(N):
                if n + 2 < N:
                    projection(n + 2)
                if n % 2 == 0:
                    value(n // 2)
                pe.wait_ge(s["normed"], n + 1)
                if n >= 2:
                    pe.wait_ge(s["t_out"], n - 1)
                for m in range(LM):
                    ins = pe.transpose(K.bank[3 + n % 2][:, m * P:(m + 1) * P], t1[:, n % 2].rearrange("p h d -> p (h d)")[:, m * P:(m + 1) * P], K.ident[:])
                ins.then_inc(s["turned"], 1)

        @block.scalar
        def _(act):
            def square(n):
                act.wait_ge(s["done"], n + 1)
                if n >= 2:
                    act.wait_ge(s["ss_done"], n - 1)
                act.activation(sq[:, n % 2], heads(K.bank[n % 3][:]), ACT.Square).then_inc(s["squared"], 1)

            def turned_out(n):
                act.wait_ge(s["turned"], n + 1)
                dst = (QT, KT)[n % 2]
                act.activation(dst[:, :, (n // 2) * P:(n // 2 + 1) * P], K.bank[3 + n % 2][:].rearrange("p (m t) -> p m t", m=LM), ACT.Copy).then_inc(s["t_out"], 1)

            square(0)
            for n in range(N):
                act.wait_ge(s["ss_done"], n + 1)
                act.activation(r[:, n % 2], r[:, n % 2], ACT.Sqrt).then_inc(s["root_done"], 1)
                if n + 1 < N:
                    square(n + 1)
                if n % 2 == 0:
                    act.wait_ge(s["v_done"], n // 2 + 1)
                    act.activation(V[:, n // 2, :], K.bank[5 + (n // 2) % 2][:], ACT.Copy).then_inc(s["v_out"], 1)
                if n > 0:
                    turned_out(n - 1)
            turned_out(N - 1)

        @block.vector
        def _(dve):
            for n in range(N):
                raw = heads(K.bank[n % 3][:])
                t, part = divmod(n, 2)
                cos, sin = (middle(tab[:, 2 * part + i, t, :], LH) for i in range(2))
                dve.wait_ge(s["squared"], n + 1)
                if n >= 2:
                    dve.wait_ge(s["normed"], n - 1)
                dve.reduce_sum(r[:, n % 2], sq[:, n % 2], AX).then_inc(s["ss_done"], 1)
                if n >= 2:
                    dve.wait_ge(s["turned"], n - 1)
                dve.tensor_tensor(t1[:, n % 2], raw, cos, ALU.mult)
                dve.tensor_tensor(t2[:, n % 2, :, 0:HF], raw[:, :, HF:], sin[:, :, 0:HF], ALU.mult)
                dve.tensor_tensor(t2[:, n % 2, :, HF:], raw[:, :, 0:HF], sin[:, :, HF:], ALU.mult).then_inc(s["crossed"], 1)
                dve.wait_ge(s["root_done"], n + 1)
                dve.tensor_scalar(r[:, n % 2], r[:, n % 2], 1e-12, None, ALU.max)
                dve.drain()
                dve.reciprocal(r[:, n % 2], r[:, n % 2]).then_inc(s["r_ready"], 1)

        @block.gpsimd
        def _(pool):
            for n in range(N):
                pool.wait_ge(s["crossed"], n + 1)
                pool.tensor_tensor(t1[:, n % 2], t1[:, n % 2], t2[:, n % 2], ALU.add).then_inc(s["added"], 1)
                pool.wait_ge(s["added"], n + 1)
                pool.wait_ge(s["r_ready"], n + 1)
                pool.tensor_tensor(t1[:, n % 2], t1[:, n % 2], inner(r[:, n % 2], LHD), ALU.mult).then_inc(s["normed"], 1)


def local_attention(nc, K, b, QT, KT, V, half, window_mask, OT):
    NTB = S // P
    QK_SCALE = 8.0
    with ExitStack() as es, phase(nc, K.sems, "q_spread scored max_done exp_done recip_done normed turned pt_out_even pt_out_odd pv_done out") as (block, s):
        Qh = sbuf(es, nc, "Q_heads", [P, 2, LM, 2, P])
        Pr = sbuf(es, nc, "probs", [P, 2, LH, 2 * P])
        PT = sbuf(es, nc, "probsT", [P, LM, 4 * P])
        stat = sbuf(es, nc, "stat", [P, 2, 3, LH])
        keys = lambda t: slice(0 if t else P, 2 * P)
        pt_out = (s["pt_out_even"], s["pt_out_odd"])

        def turned_probs(n):
            t, g = divmod(n, LM)
            return (v.rearrange("p (h k) -> p h k", h=2)[:, :, keys(t)] for v in (K.bank[4 + n % 2][:], PT[:, g, :]))

        @block.tensor
        def _(pe):
            def score(t, g):
                if g == 0:
                    pe.wait_ge(s["q_spread"], 2 * (t + 1))
                if t:
                    pe.wait_ge(s["exp_done"], LH * (t - 1) + 2 * (g + 1))
                for hh in range(2):
                    ks = keys(t)
                    o = K.bank[g][:, hh * 2 * P + ks.start:(hh + 1) * 2 * P]
                    pe.matmul(o, Qh[:, t % 2, g, hh, :], KT[:, g, t * P - P + ks.start:(t + 1) * P], start=True, stop=False, skip_group_check=True)
                    ins = pe.matmul(o, K.identb[:], window_mask[:, ks], start=False, stop=True, skip_group_check=True)
                ins.then_inc(s["scored"], 1)

            def turn(t, g):
                n = LM * t + g
                pe.wait_ge(s["normed"], n + 1)
                if n >= 2:
                    pe.wait_ge(pt_out[n % 2], n // 2)
                for hh in range(2):
                    for kt in ((0, 1) if t else (1,)):
                        ins = pe.transpose(K.bank[4 + n % 2][:, (2 * hh + kt) * P:(2 * hh + kt + 1) * P], Pr[:, t % 2, 2 * g + hh, kt * P:(kt + 1) * P], K.ident[:])
                ins.then_inc(s["turned"], 1)

            for g in range(LM):
                score(0, g)
            for t in range(NTB):
                for g in range(LM + 1):
                    if g < LM and t + 1 < NTB:
                        score(t + 1, g)
                    if g:
                        turn(t, g - 1)
                kts = (0, 1) if t else (1,)
                for g in range(LM):
                    pe.wait_ge(pt_out[g % 2], (LM * t + g) // 2 + 1)
                    if g == 0 and t >= 2:
                        pe.wait_ge(s["out"], t - 1)
                    for hh in range(2):
                        for kt in kts:
                            h = 2 * g + hh
                            ins = pe.matmul(K.bank[6 + t % 2][hh * LHD:(hh + 1) * LHD, g * P:(g + 1) * P], V[:, t - 1 + kt, h * LHD:(h + 1) * LHD],
                                            PT[:, g, (2 * hh + kt) * P:(2 * hh + kt + 1) * P], start=(kt == kts[0]), stop=(kt == 1))
                    ins.then_inc(s["pv_done"], 1)

        @block.vector
        def _(dve):
            def spread(t):
                if t >= 2:
                    dve.wait_ge(s["scored"], LM * (t - 1))
                for hh in range(2):
                    dve.tensor_scalar(Qh[:, t % 2, :, hh, :], QT[:, :, t * P:(t + 1) * P], half[:, hh:hh + 1], None, ALU.mult).then_inc(s["q_spread"], 1)

            def take_turned(n):
                dve.wait_ge(s["turned"], n + 1)
                if n >= LM:
                    dve.wait_ge(s["pv_done"], n - LM + 1)
                src, dst = turned_probs(n)
                dve.tensor_copy(dst, src).then_inc(s["pt_out_even"], 1)

            spread(0)
            for t in range(NTB):
                if t + 1 < NTB:
                    spread(t + 1)
                ks = keys(t)
                if t >= 2:
                    dve.wait_ge(s["exp_done"], LH * (t - 1))
                def recip(g):
                    dve.wait_ge(s["exp_done"], LH * t + 2 * (g + 1))
                    if g == 0 and t >= 2:
                        dve.wait_ge(s["normed"], LM * (t - 1))
                    dve.reciprocal(stat[:, t % 2, 2, 2 * g:2 * g + 2], stat[:, t % 2, 1, 2 * g:2 * g + 2]).then_inc(s["recip_done"], 1)

                for g in range(LM):
                    dve.wait_ge(s["scored"], LM * t + g + 1)
                    mx = stat[:, t % 2, 0, 2 * g:2 * g + 2]
                    dve.reduce_max(mx, K.bank[g][:].rearrange("p (h k) -> p h k", h=2)[:, :, ks], AX)
                    dve.drain()
                    dve.tensor_scalar(mx, mx, -QK_SCALE, None, ALU.mult).then_inc(s["max_done"], 1)
                    if g:
                        recip(g - 1)
                    if t and g == 1:
                        take_turned(LM * (t - 1))
                if t:
                    take_turned(LM * (t - 1) + 2)
                recip(LM - 1)
                if t:
                    dve.wait_ge(s["pv_done"], LM * t)
                    dve.tensor_copy(OT[:, :, b * S + (t - 1) * P:b * S + t * P], K.bank[6 + (t - 1) % 2][:].rearrange("p (g k) -> p g k", g=LM)).then_inc(s["out"], 1)
            for n in (LM * (NTB - 1), LM * (NTB - 1) + 2):
                take_turned(n)
            dve.wait_ge(s["pv_done"], LM * NTB)
            t = NTB
            dve.tensor_copy(OT[:, :, b * S + (t - 1) * P:b * S + t * P], K.bank[6 + (t - 1) % 2][:].rearrange("p (g k) -> p g k", g=LM)).then_inc(s["out"], 1)

        @block.gpsimd
        def _(pool):
            for t in range(NTB):
                ks = keys(t)
                for g in range(LM):
                    pool.wait_ge(s["recip_done"], LM * t + g + 1)
                    v = Pr[:, t % 2, 2 * g:2 * g + 2, ks]
                    pool.tensor_tensor(v, v, inner(stat[:, t % 2, 2, 2 * g:2 * g + 2], ks.stop - ks.start), ALU.mult).then_inc(s["normed"], 1)

        @block.scalar
        def _(act):
            def exps(t, g):
                ks = keys(t)
                act.wait_ge(s["max_done"], LM * t + g + 1)
                if t >= 2:
                    act.wait_ge(s["turned"], LM * (t - 2) + g + 1)
                    act.wait_ge(s["recip_done"], LM * (t - 2) + g + 1)
                for hh in range(2):
                    h = 2 * g + hh
                    act.activation(Pr[:, t % 2, h, ks], K.bank[g][:, hh * 2 * P + ks.start:hh * 2 * P + ks.stop], ACT.Exp, bias=stat[:, t % 2, 0, h:h + 1],
                                   scale=QK_SCALE, accum_out=stat[:, t % 2, 1, h:h + 1]).then_inc(s["exp_done"], 1)

            for g in range(LM):
                exps(0, g)
            for t in range(NTB):
                for g in range(LM):
                    if t + 1 < NTB:
                        exps(t + 1, g)
                    if g >= 2:
                        n = LM * t + 2 * g - 3
                        act.wait_ge(s["turned"], n + 1)
                        if t:
                            act.wait_ge(s["pv_done"], n - LM + 1)
                        src, dst = turned_probs(n)
                        act.activation(dst, src, ACT.Copy).then_inc(s["pt_out_odd"], 1)


def add_residual(nc, K, n_k, wt, src, bias, old, new):
    with phase(nc, K.sems, "done out") as (block, s):
        steps = [(h, j) for j in range(NB) for h in range(DC)]

        @block.tensor
        def _(pe):
            for n, (h, j) in enumerate(steps):
                for k in range(n_k):
                    ins = pe.matmul(K.bank[n][:], wt(k, h), src(k, j), start=(k == 0), stop=(k == n_k - 1))
                ins.then_inc(s["done"], 1)

        @block.vector
        def _(dve):
            for n, (h, j) in enumerate(steps):
                dve.wait_ge(s["done"], n + 1)
                o, d = (v[:, h, j * BLK:(j + 1) * BLK] for v in (old, new))
                if bias is None:
                    dve.tensor_tensor(d, K.bank[n][:], o, ALU.add)
                else:
                    dve.scalar_tensor_tensor(out=d, in0=K.bank[n][:], scalar=bias[:, h:h + 1], in1=o, op0=ALU.add, op1=ALU.add)


def L2_ffn(nc, K, w):
    x0, x1 = K.XT[K.cur], K.XT[1 - K.cur]
    with ExitStack() as es:
        sh = sbuf(es, nc, "shifted", [P, B, 1 + S])
        half = sbuf(es, nc, "head_half", [P, 2])
        ones64 = sbuf(es, nc, "ones64", [P, P])
        J = sbuf(es, nc, "J", [P, P])
        wm = sbuf(es, nc, "window_mask", [P, 2 * P], BF16)
        block_mean(nc, K, ones64[:], LHD)
        block_mean(nc, K, J[:], P)
        with phase(nc, K.sems, "step") as (block, s):
            @block.vector
            def _(dve):
                dve.tensor_scalar(ones64[:], ones64[:], float(LHD), None, ALU.mult)
                dve.tensor_scalar(J[:], J[:], 0.5, None, ALU.mult)
                dve.tensor_copy(wm[:, 0:P], K.below[:])
                dve.tensor_copy(wm[:, P:2 * P], K.above[:])
                dve.drain()
                for hh in range(2):
                    dve.tensor_copy(half[:, hh:hh + 1], ones64[:, hh * LHD:hh * LHD + 1])
                dve.memset(sh[:, :, 0:1], 0.0)
        h_of = lambda X: lambda k, j: X[:, 0, j * BLK:(j + 1) * BLK] if k == 0 else sh[:, j // 2, (j % 2) * BLK:(j % 2) * BLK + BLK]
        for l in range(L2D):
            X = x0 if l == 0 else x1
            pre = f"L2f{l}_"
            shift_half(nc, K, X, sh)
            with ExitStack() as att:
                OT = sbuf(att, nc, "OT", [P, LM, TOK])
                with ExitStack() as inn:
                    W = sbuf(inn, nc, "Wqkv", [P, DC, 3 * LM * P])
                    tab = sbuf(inn, nc, "tables", [P, 4, S // P, LHD])
                    sc = sbuf(inn, nc, "scales", [P, 4, LHD])
                    QT, KT = (sbuf(inn, nc, n, [P, LM, S]) for n in ("QT", "KT"))
                    V = K.Xtok[:].rearrange("p (t c) d -> p t (c d)", c=2)
                    load(nc, K, (W[:], w[pre + "Wqkv"]), (tab[:], w["L2f_tab"]), (sc[:].rearrange("p i d -> p (i d)"), spread(w[pre + "s"])))
                    with phase(nc, K.sems, "step") as (block, s):
                        @block.vector
                        def _(dve):
                            for i in range(4):
                                dve.tensor_tensor(tab[:, i], tab[:, i], middle(sc[:, i, :], S // P), ALU.mult)
                    for b in range(B):
                        tile_of = lambda k, t: X[:, 0, b * S + t * P:b * S + (t + 1) * P] if k == 0 else sh[:, b, t * P:(t + 1) * P]
                        local_qkv(nc, K, tile_of, W, tab, QT, KT, V)
                        local_attention(nc, K, b, QT, KT, V, half, wm, OT)
                with ExitStack() as inn:
                    Wo = sbuf(inn, nc, "Wo", [P, LM, D])
                    load(nc, K, (Wo[:], w[pre + "Wo"]))
                    add_residual(nc, K, LM, lambda k, h: Wo[:, k, h * P:(h + 1) * P], block_of(OT), None, X, x1)
            shift_half(nc, K, x1, sh)
            with ExitStack() as ff:
                W2 = sbuf(ff, nc, "W2", [P, HIDP // P, D])
                b2 = sbuf(ff, nc, "b2", [P, DC])
                GT = sbuf(ff, nc, "GT", [P, HIDP // P, TOK])
                with ExitStack() as inn:
                    W1 = sbuf(inn, nc, "W1", [P, DC, 2 * HIDP])
                    b1 = sbuf(inn, nc, "b1", [P, 2 * HIDP // P])
                    g, b_ = (sbuf(inn, nc, n, [P, DC]) for n in ("g", "b"))
                    Hn = sbuf(inn, nc, "Hn", [P, DC, TOK])
                    ge = sbuf(inn, nc, "gelu", [P, 2, BLK])
                    load(nc, K, (g[:], w[pre + "g"]), (b_[:], w[pre + "b"]),
                         later=((W1[:], w[pre + "W1"]), (b1[:], w[pre + "b1"]), (W2[:], w[pre + "W2"]), (b2[:], w[pre + "b2"])))
                    feature_ln_rows(nc, K, J[:], NB, DC, lambda j, h: h_of(x1)(h, j), lambda j, h: Hn[:, h, j * BLK:(j + 1) * BLK], lambda j: g[:], lambda j: b_[:])
                    arrive(nc, K)
                    HC = HIDP // P
                    steps = [(m, j) for m in range(HC) for j in range(NB)]
                    with phase(nc, K.sems, "done gelu_done out") as (block, s):
                        @block.tensor
                        def _(pe):
                            for n, (m, j) in enumerate(steps):
                                if n >= 4:
                                    pe.wait_ge(s["out"], n - 3)
                                for part in range(2):
                                    for k in range(DC):
                                        ins = pe.matmul(K.bank[2 * (n % 4) + part][:], W1[:, k, (part * HC + m) * P:(part * HC + m + 1) * P],
                                                        Hn[:, k, j * BLK:(j + 1) * BLK], start=(k == 0), stop=(k == DC - 1))
                                ins.then_inc(s["done"], 1)

                        @block.scalar
                        def _(act):
                            for n, (m, j) in enumerate(steps):
                                act.wait_ge(s["done"], n + 1)
                                if n >= 2:
                                    act.wait_ge(s["out"], n - 1)
                                act.activation(ge[:, n % 2, :], K.bank[2 * (n % 4) + 1][:], ACT.Gelu, bias=b1[:, HC + m:HC + m + 1]).then_inc(s["gelu_done"], 1)

                        @block.vector
                        def _(dve):
                            for n, (m, j) in enumerate(steps):
                                dve.wait_ge(s["gelu_done"], n + 1)
                                dve.scalar_tensor_tensor(out=GT[:, m, j * BLK:(j + 1) * BLK], in0=K.bank[2 * (n % 4)][:], scalar=b1[:, m:m + 1],
                                                         in1=ge[:, n % 2, :], op0=ALU.add, op1=ALU.mult).then_inc(s["out"], 1)
                if l < L2D - 1:
                    add_residual(nc, K, HIDP // P, lambda k, h: W2[:, k, h * P:(h + 1) * P], block_of(GT), b2, x1, x1)
                else:
                    with phase(nc, K.sems, "step") as (block, s):
                        @block.vector
                        def _(dve):
                            dve.tensor_tensor(x1[:, 0, :], x1[:, 0, :], x0[:, 0, :], ALU.add)

                        @block.gpsimd
                        def _(pool):
                            pool.tensor_tensor(x1[:, 1, :], x1[:, 1, :], x0[:, 1, :], ALU.add)
                    finish(nc, K, lambda k, h, j: W2[:, k, h * P:(h + 1) * P], block_of(GT), HIDP // P, bias=b2, res=x1)


def program(nc, w, out, first=0, last=12):
    with ExitStack() as es:
        K = Fixed()
        K.sems, K.cur = [], 0
        K.out, K.stored = out, nc.alloc_semaphore("stored")
        K.late, K.late_count = nc.alloc_semaphore("late_weights"), 0
        K.XT = [sbuf(es, nc, f"XT{i}", [P, DC, TOK])[:] for i in range(2)]
        K.Xtok = sbuf(es, nc, "Xtok", [P, NT, D])
        K.ctxT = sbuf(es, nc, "ctxT", [P, DC, B, 256])
        K.ones = sbuf(es, nc, "ones", [P, 8 * P])
        K.ident = sbuf(es, nc, "ident", [P, P])
        K.identb = sbuf(es, nc, "identb", [P, P], BF16)
        K.causal_T = sbuf(es, nc, "causal_T", [P, P])
        K.head_cols = sbuf(es, nc, "head_cols", [P, 8, P])
        K.head_rows = sbuf(es, nc, "head_rows", [P, 8])
        K.above = sbuf(es, nc, "above", [P, P], BF16)
        K.below = sbuf(es, nc, "below", [P, P], BF16)
        K.live_keys = sbuf(es, nc, "live_keys", [P, 1])
        K.eps = sbuf(es, nc, "eps", [P, 1])
        K.psum = es.enter_context(nc.psum_tensor("psum", [P, 8, BLK], F32))
        K.bank = [K.psum[:, i, :] for i in range(8)]
        setup(nc, K, w)
        for sublayer in SUBLAYERS[first:last]:
            sublayer(nc, K, w)
        if last < len(SUBLAYERS):
            with nc.Block() as block:
                @block.sync
                def _(sp):
                    sp.dma_start(out.rearrange("b (t p) d -> p (b t) d", p=P), K.Xtok[:]).then_inc(K.stored, 16)
                    sp.wait_ge(K.stored, 16)


def layouts(i):
    x = np.asarray(i["x"]).reshape(TOK, D)
    out = {"xT": rows(x.T), "xtok": rows(x)}
    ctx = np.concatenate([pad(np.asarray(i["ctx_1024"])[b].T, 1, 2 * P) for b in range(B)], axis=1)
    out["ctxT"] = rows(ctx).reshape(P, DC, B, 2 * P)
    for f in LAYOUTS:
        out.update(f(i))
    return out


LAYOUTS = (L0_attn_layout, L0_xattn_layout, L0_ffn_layout, L1_attn_layout, L1_xattn_layout, L1_ffn_layout,
           L2_attn_layout, L2_xattn_layout, L2_ffn_layout, L3_attn_layout, L3_xattn_layout, L3_ffn_layout)
SUBLAYERS = (L0_attn, L0_xattn, L0_ffn, L1_attn, L1_xattn, L1_ffn, L2_attn, L2_xattn, L2_ffn, L3_attn, L3_xattn, L3_ffn)


def kernel(**inputs):
    import concourse.bacc as _bacc
    from concourse import mybir as _mybir
    from concourse.bass_utils import run_bass_kernel_spmd as _run

    nc = _bacc.Bacc("TRN2", target_bir_lowering=False, num_devices=1)
    arrays, w = {}, {}
    for name, a in layouts(inputs).items():
        a = np.ascontiguousarray(a)
        arrays[f"in_{name}"] = a
        w[name] = nc.dram_tensor(f"in_{name}", a.shape, _mybir.dt.from_np(a.dtype), kind="ExternalInput").ap()
    out = nc.dram_tensor("out", (B, S, D), _mybir.dt.float32, kind="ExternalOutput").ap()
    program(nc, w, out)
    return _run(nc, [arrays], core_ids=[0]).results[0]["out"]
```
